# Optimizing a Trainium2 kernel written in Bass

```python
import numpy as np
import jax
import jax.numpy as jnp

def _softmax(x, axis=-1):
    return jax.nn.softmax(x, axis=axis)

def _gelu(x):
    return jax.nn.gelu(x, approximate=True)

def _silu(x):
    return jax.nn.silu(x)

def _sigmoid(x):
    return jax.nn.sigmoid(x)

def _layernorm(x, axis=-1, eps=1e-05):
    m = jnp.mean(x, axis=axis, keepdims=True)
    v = jnp.var(x, axis=axis, keepdims=True)
    return (x - m) / jnp.sqrt(v + eps)

def _scatter_add(tgt, idx, src, axis=0):
    return tgt.at[idx].add(src)

def _segment_sum(src, seg, n):
    return jax.ops.segment_sum(src, seg, n)
kernel_name = 'mk_recurrent_d4_jaxref_r4_0c06dc'

def setup_inputs(seed: int=0):
    np.random.seed(seed)
    _w = jnp.asarray

    def _L0_attn_setup():
        import jax, jax.numpy as jnp
        import numpy as np
        from jax import lax
        D_MODEL, D_STATE, D_CONV, D_INNER, DT_RANK = (256, 16, 4, 512, 64)
        CHUNK = 32

        def _selective_scan(x, dt, A, Bp, Cp):
            Bb, L, d_inner = x.shape
            n_chunks = L // CHUNK

            def to_chunks(t):
                return t.reshape(Bb, n_chunks, CHUNK, t.shape[-1]).transpose(1, 2, 0, 3)
            xs, dts, Bs, Cs = (to_chunks(x), to_chunks(dt), to_chunks(Bp), to_chunks(Cp))

            def step(h, inp):
                x_i, dt_i, B_i, C_i = inp
                dA = jnp.exp(dt_i[..., None] * A)
                h = dA * h + dt_i[..., None] * B_i[:, None, :] * x_i[..., None]
                y = jnp.einsum('bds,bs->bd', h, C_i)
                return (h, y)

            def chunk_step(h, inp):
                h, ys = lax.scan(step, h, inp)
                return (lax.stop_gradient(h), ys)
            h0 = jnp.zeros((Bb, d_inner, D_STATE), dtype=x.dtype)
            _, ys = lax.scan(chunk_step, h0, (xs, dts, Bs, Cs))
            return ys.reshape(L, Bb, d_inner).transpose(1, 0, 2)
        key = jax.random.key(seed)
        ks = jax.random.split(key, 8)
        x = jax.random.normal(ks[0], (2, 1024, D_MODEL), dtype=jnp.float32)
        W_in = jax.random.normal(ks[1], (D_MODEL, 2 * D_INNER), dtype=jnp.float32) * D_MODEL ** (-0.5)
        conv_w = jax.random.normal(ks[2], (D_INNER, 1, D_CONV), dtype=jnp.float32) * D_CONV ** (-0.5)
        conv_b = jax.random.normal(ks[3], (D_INNER,), dtype=jnp.float32) * 0.02
        W_x = jax.random.normal(ks[4], (D_INNER, DT_RANK + 2 * D_STATE), dtype=jnp.float32) * D_INNER ** (-0.5)
        W_dt = jax.random.uniform(ks[5], (DT_RANK, D_INNER), dtype=jnp.float32, minval=-DT_RANK ** (-0.5), maxval=DT_RANK ** (-0.5))
        dt = jnp.exp(jax.random.uniform(ks[6], (D_INNER,), dtype=jnp.float32) * (np.log(0.1) - np.log(0.001)) + np.log(0.001))
        b_dt = dt + jnp.log(-jnp.expm1(-dt))
        A_log = jnp.log(jnp.broadcast_to(jnp.arange(1, D_STATE + 1, dtype=jnp.float32), (D_INNER, D_STATE)))
        D = jnp.ones((D_INNER,), dtype=jnp.float32)
        W_out = jax.random.normal(ks[7], (D_INNER, D_MODEL), dtype=jnp.float32) * D_INNER ** (-0.5)
        return {'x': x, 'W_in': W_in, 'conv_w': conv_w, 'conv_b': conv_b, 'W_x': W_x, 'W_dt': W_dt, 'b_dt': b_dt, 'A_log': A_log, 'D': D, 'W_out': W_out}
    _L0_attn_in = _L0_attn_setup()

    def _L0_ffn_setup():
        import jax, jax.numpy as jnp
        import numpy as np
        D_MODEL, D_FF, RANK = (256, 1024, 64)
        B, S = (4, 1024)
        key = jax.random.key(seed)
        ks = jax.random.split(key, 7)
        return {'x': jax.random.normal(ks[0], (B, S, D_MODEL), dtype=jnp.float32), 'U1': jax.random.normal(ks[1], (D_MODEL, RANK), dtype=jnp.float32) * 0.02, 'V1': jax.random.normal(ks[2], (RANK, D_FF), dtype=jnp.float32) * 0.02, 'b1': jnp.zeros((D_FF,), dtype=jnp.float32), 'U2': jax.random.normal(ks[3], (D_FF, RANK), dtype=jnp.float32) * 0.02, 'V2': jax.random.normal(ks[4], (RANK, D_MODEL), dtype=jnp.float32) * 0.02, 'b2': jnp.zeros((D_MODEL,), dtype=jnp.float32)}
    _L0_ffn_in = _L0_ffn_setup()

    def _L1_attn_setup():
        import jax, jax.numpy as jnp
        import numpy as np
        EMBED_DIM = 256
        NUM_HEADS = 16
        CHUNK = 64

        def _mha_residual(x, Wq, Wk, Wv, Wo, num_heads):
            *lead, S, D = x.shape
            hd = D // num_heads
            scale = 1.0 / jnp.sqrt(jnp.asarray(hd, x.dtype))
            q = (x @ Wq).reshape(*lead, S, num_heads, hd)
            k = (x @ Wk).reshape(*lead, S, num_heads, hd)
            v = (x @ Wv).reshape(*lead, S, num_heads, hd)
            scores = jnp.einsum('...qhe,...khe->...hqk', q, k) * scale
            attn = jax.nn.softmax(scores, axis=-1)
            ctx = jnp.einsum('...hqk,...khe->...qhe', attn, v)
            ctx = ctx.reshape(*lead, S, D)
            return x + ctx @ Wo
        key = jax.random.key(seed)
        ks = jax.random.split(key, 9)
        B, S, D = (4, 2048, EMBED_DIM)
        w = lambda k: jax.random.normal(k, (D, D), dtype=jnp.float32) * (1.0 / np.sqrt(D))
        return {'x': jax.random.normal(ks[0], (B, S, D), dtype=jnp.float32), 'Wq_l': w(ks[1]), 'Wk_l': w(ks[2]), 'Wv_l': w(ks[3]), 'Wo_l': w(ks[4]), 'Wq_g': w(ks[5]), 'Wk_g': w(ks[6]), 'Wv_g': w(ks[7]), 'Wo_g': w(ks[8])}
    _L1_attn_in = _L1_attn_setup()

    def _L1_ffn_setup():
        import jax, jax.numpy as jnp
        import numpy as np
        B, T, D, E, TOP_K = (4, 1024, 256, 8, 2)
        CAPACITY_FACTOR = 1.5
        key = jax.random.key(seed)
        k1, k2, k3 = jax.random.split(key, 3)
        x = jax.random.normal(k1, (B, T, D), dtype=jnp.float32)
        Wr = jax.random.normal(k2, (E, D), dtype=jnp.float32) * 0.02
        We = jax.random.normal(k3, (E, D, D), dtype=jnp.float32) * 0.02
        return {'x': x, 'Wr': Wr, 'We': We}
    _L1_ffn_in = _L1_ffn_setup()

    def _L2_attn_setup():
        import jax, jax.numpy as jnp
        import numpy as np
        B, T, D_IN, D_OUT, NH = (4, 512, 256, 256, 16)
        HD = D_OUT // NH
        SCALE = 1.0 / float(np.sqrt(HD))
        key = jax.random.key(seed)
        k1, k2, k3 = jax.random.split(key, 3)
        x = jax.random.normal(k1, (B, T, D_IN), dtype=jnp.float32)
        w_qkv = jax.random.normal(k2, (3 * D_OUT, D_IN), dtype=jnp.float32) / np.sqrt(D_IN)
        w_out = jax.random.normal(k3, (D_OUT, D_OUT), dtype=jnp.float32) / np.sqrt(D_OUT)
        return {'x': x, 'w_qkv': w_qkv, 'w_out': w_out}
    _L2_attn_in = _L2_attn_setup()

    def _L2_ffn_setup():
        import jax, jax.numpy as jnp
        import numpy as np
        NUM_EXPERTS = 8
        EXPERT_CAPACITY = 2.0
        DIM = 256
        HIDDEN_DIM = 1024
        key = jax.random.key(seed)
        k_x, k_g, k_w1, k_w2 = jax.random.split(key, 4)
        n, t, d, f, e = (8, 256, DIM, HIDDEN_DIM, NUM_EXPERTS)
        x = jax.random.normal(k_x, (n, t, d), dtype=jnp.float32)
        gate_w = jax.random.normal(k_g, (e, d), dtype=jnp.float32) * 0.02
        w1 = jax.random.normal(k_w1, (e, d, f), dtype=jnp.float32) * 0.02
        w2 = jax.random.normal(k_w2, (e, f, d), dtype=jnp.float32) * 0.02
        return {'x': x, 'gate_w': gate_w, 'w1': w1, 'w2': w2}
    _L2_ffn_in = _L2_ffn_setup()

    def _L3_attn_setup():
        import jax, jax.numpy as jnp
        import numpy as np
        NUM_HEADS = 16

        def _heads(t, B, N, H, hd):
            return t.reshape(B, N, H, hd).transpose(0, 2, 1, 3)
        key = jax.random.key(seed)
        ks = jax.random.split(key, 9)
        B, N, D = (2, 512, 256)
        w = 0.02
        return {'x': jax.random.normal(ks[0], (B, N, D), dtype=jnp.float32), 'wq': jax.random.normal(ks[1], (D, D), dtype=jnp.float32) * w, 'bq': jax.random.normal(ks[2], (D,), dtype=jnp.float32) * w, 'wk': jax.random.normal(ks[3], (D, D), dtype=jnp.float32) * w, 'bk': jax.random.normal(ks[4], (D,), dtype=jnp.float32) * w, 'wv': jax.random.normal(ks[5], (D, D), dtype=jnp.float32) * w, 'bv': jax.random.normal(ks[6], (D,), dtype=jnp.float32) * w, 'wo': jax.random.normal(ks[7], (D, D), dtype=jnp.float32) * w, 'bo': jax.random.normal(ks[8], (D,), dtype=jnp.float32) * w}
    _L3_attn_in = _L3_attn_setup()

    def _L3_ffn_setup():
        import jax, jax.numpy as jnp
        import numpy as np
        DIM = 256

        def _reference_tuple_inner(x, W_r, W_k, W_v, mu_r, mu_k):
            B, T, C = x.shape
            x_prev = jnp.concatenate([jnp.zeros((B, 1, C), x.dtype), x[:, :-1, :]], axis=1)
            xr = mu_r * x + (1.0 - mu_r) * x_prev
            xk = mu_k * x + (1.0 - mu_k) * x_prev
            r = jax.nn.sigmoid(jnp.einsum('btc,dc->btd', xr, W_r))
            k = jnp.einsum('btc,dc->btd', xk, W_k)
            k_act = jnp.square(jax.nn.relu(k))
            out = r * jnp.einsum('btc,dc->btd', k_act, W_v)
            new_state = x[:, -1, :]
            return (out, new_state)
        key = jax.random.key(seed)
        ks = jax.random.split(key, 6)
        B, T, C = (8, 512, DIM)
        x = jax.random.normal(ks[0], (B, T, C), dtype=jnp.float32)
        s = 1.0 / np.sqrt(C)
        W_r = jax.random.uniform(ks[1], (C, C), jnp.float32, -s, s)
        W_k = jax.random.uniform(ks[2], (C, C), jnp.float32, -s, s)
        W_v = jax.random.uniform(ks[3], (C, C), jnp.float32, -s, s)
        mu_r = jax.random.uniform(ks[4], (C,), jnp.float32)
        mu_k = jax.random.uniform(ks[5], (C,), jnp.float32)
        return {'x': x, 'W_r': W_r, 'W_k': W_k, 'W_v': W_v, 'mu_r': mu_r, 'mu_k': mu_k}
    _L3_ffn_in = _L3_ffn_setup()
    _d = {'L0_attn_x': _L0_attn_in['x'], 'L0_attn_W_in': _L0_attn_in['W_in'], 'L0_attn_conv_w': _L0_attn_in['conv_w'], 'L0_attn_conv_b': _L0_attn_in['conv_b'], 'L0_attn_W_x': _L0_attn_in['W_x'], 'L0_attn_W_dt': _L0_attn_in['W_dt'], 'L0_attn_b_dt': _L0_attn_in['b_dt'], 'L0_attn_A_log': _L0_attn_in['A_log'], 'L0_attn_D': _L0_attn_in['D'], 'L0_attn_W_out': _L0_attn_in['W_out'], 'L0_ffn_U1': _L0_ffn_in['U1'], 'L0_ffn_V1': _L0_ffn_in['V1'], 'L0_ffn_b1': _L0_ffn_in['b1'], 'L0_ffn_U2': _L0_ffn_in['U2'], 'L0_ffn_V2': _L0_ffn_in['V2'], 'L0_ffn_b2': _L0_ffn_in['b2'], 'L1_attn_Wq_l': _L1_attn_in['Wq_l'], 'L1_attn_Wk_l': _L1_attn_in['Wk_l'], 'L1_attn_Wv_l': _L1_attn_in['Wv_l'], 'L1_attn_Wo_l': _L1_attn_in['Wo_l'], 'L1_attn_Wq_g': _L1_attn_in['Wq_g'], 'L1_attn_Wk_g': _L1_attn_in['Wk_g'], 'L1_attn_Wv_g': _L1_attn_in['Wv_g'], 'L1_attn_Wo_g': _L1_attn_in['Wo_g'], 'L1_ffn_Wr': _L1_ffn_in['Wr'], 'L1_ffn_We': _L1_ffn_in['We'], 'L2_attn_w_qkv': _L2_attn_in['w_qkv'], 'L2_attn_w_out': _L2_attn_in['w_out'], 'L2_ffn_gate_w': _L2_ffn_in['gate_w'], 'L2_ffn_w1': _L2_ffn_in['w1'], 'L2_ffn_w2': _L2_ffn_in['w2'], 'L3_attn_wq': _L3_attn_in['wq'], 'L3_attn_bq': _L3_attn_in['bq'], 'L3_attn_wk': _L3_attn_in['wk'], 'L3_attn_bk': _L3_attn_in['bk'], 'L3_attn_wv': _L3_attn_in['wv'], 'L3_attn_bv': _L3_attn_in['bv'], 'L3_attn_wo': _L3_attn_in['wo'], 'L3_attn_bo': _L3_attn_in['bo'], 'L3_ffn_W_r': _L3_ffn_in['W_r'], 'L3_ffn_W_k': _L3_ffn_in['W_k'], 'L3_ffn_W_v': _L3_ffn_in['W_v'], 'L3_ffn_mu_r': _L3_ffn_in['mu_r'], 'L3_ffn_mu_k': _L3_ffn_in['mu_k']}
    _x0 = _d['L0_attn_x']
    _d['L0_attn_x'] = jax.random.normal(jax.random.fold_in(jax.random.key(seed), 1), (8, 512, 256), dtype=_x0.dtype)
    del _x0
    return _d

def reference(L0_attn_x, L0_attn_W_in, L0_attn_conv_w, L0_attn_conv_b, L0_attn_W_x, L0_attn_W_dt, L0_attn_b_dt, L0_attn_A_log, L0_attn_D, L0_attn_W_out, L0_ffn_U1, L0_ffn_V1, L0_ffn_b1, L0_ffn_U2, L0_ffn_V2, L0_ffn_b2, L1_attn_Wq_l, L1_attn_Wk_l, L1_attn_Wv_l, L1_attn_Wo_l, L1_attn_Wq_g, L1_attn_Wk_g, L1_attn_Wv_g, L1_attn_Wo_g, L1_ffn_Wr, L1_ffn_We, L2_attn_w_qkv, L2_attn_w_out, L2_ffn_gate_w, L2_ffn_w1, L2_ffn_w2, L3_attn_wq, L3_attn_bq, L3_attn_wk, L3_attn_bk, L3_attn_wv, L3_attn_bv, L3_attn_wo, L3_attn_bo, L3_ffn_W_r, L3_ffn_W_k, L3_ffn_W_v, L3_ffn_mu_r, L3_ffn_mu_k):

    def _L0_attn_ref(x, W_in, conv_w, conv_b, W_x, W_dt, b_dt, A_log, D, W_out):
        import jax, jax.numpy as jnp
        import numpy as np
        from jax import lax
        D_MODEL, D_STATE, D_CONV, D_INNER, DT_RANK = (256, 16, 4, 512, 64)
        CHUNK = 32

        def _selective_scan(x, dt, A, Bp, Cp):
            Bb, L, d_inner = x.shape
            n_chunks = L // CHUNK

            def to_chunks(t):
                return t.reshape(Bb, n_chunks, CHUNK, t.shape[-1]).transpose(1, 2, 0, 3)
            xs, dts, Bs, Cs = (to_chunks(x), to_chunks(dt), to_chunks(Bp), to_chunks(Cp))

            def step(h, inp):
                x_i, dt_i, B_i, C_i = inp
                dA = jnp.exp(dt_i[..., None] * A)
                h = dA * h + dt_i[..., None] * B_i[:, None, :] * x_i[..., None]
                y = jnp.einsum('bds,bs->bd', h, C_i)
                return (h, y)

            def chunk_step(h, inp):
                h, ys = lax.scan(step, h, inp)
                return (lax.stop_gradient(h), ys)
            h0 = jnp.zeros((Bb, d_inner, D_STATE), dtype=x.dtype)
            _, ys = lax.scan(chunk_step, h0, (xs, dts, Bs, Cs))
            return ys.reshape(L, Bb, d_inner).transpose(1, 0, 2)
        Bb, L, _ = x.shape
        xz = x @ W_in
        xi, z = jnp.split(xz, 2, axis=-1)
        xc = xi.transpose(0, 2, 1)
        xc = lax.conv_general_dilated(xc, conv_w, window_strides=(1,), padding=[(D_CONV - 1, 0)], dimension_numbers=('NCH', 'OIH', 'NCH'), feature_group_count=D_INNER)
        xc = (xc + conv_b[None, :, None]).transpose(0, 2, 1)
        xc = jax.nn.silu(xc)
        xp = xc @ W_x
        dt_r, Bp, Cp = jnp.split(xp, [DT_RANK, DT_RANK + D_STATE], axis=-1)
        dt = jax.nn.softplus(dt_r @ W_dt + b_dt)
        A = -jnp.exp(A_log)
        y = _selective_scan(xc, dt, A, Bp, Cp)
        y = y + xc * D
        y = y * jax.nn.silu(z)
        return y @ W_out

    def _L0_ffn_ref(x, U1, V1, b1, U2, V2, b2):
        import jax, jax.numpy as jnp
        import numpy as np
        D_MODEL, D_FF, RANK = (256, 1024, 64)
        B, S = (4, 1024)
        P = jnp.einsum('bsd,dr->bsr', x, U1)
        H = jax.nn.gelu(jnp.einsum('bsr,rf->bsf', P, V1) + b1)
        Q = jnp.einsum('bsf,fr->bsr', H, U2)
        return jnp.einsum('bsr,rd->bsd', Q, V2) + b2

    def _L1_attn_ref(x, Wq_l, Wk_l, Wv_l, Wo_l, Wq_g, Wk_g, Wv_g, Wo_g):
        import jax, jax.numpy as jnp
        import numpy as np
        EMBED_DIM = 256
        NUM_HEADS = 16
        CHUNK = 64

        def _mha_residual(x, Wq, Wk, Wv, Wo, num_heads):
            *lead, S, D = x.shape
            hd = D // num_heads
            scale = 1.0 / jnp.sqrt(jnp.asarray(hd, x.dtype))
            q = (x @ Wq).reshape(*lead, S, num_heads, hd)
            k = (x @ Wk).reshape(*lead, S, num_heads, hd)
            v = (x @ Wv).reshape(*lead, S, num_heads, hd)
            scores = jnp.einsum('...qhe,...khe->...hqk', q, k) * scale
            attn = jax.nn.softmax(scores, axis=-1)
            ctx = jnp.einsum('...hqk,...khe->...qhe', attn, v)
            ctx = ctx.reshape(*lead, S, D)
            return x + ctx @ Wo
        B, S, D = x.shape
        nC = S // CHUNK
        chunks = x.reshape(B, nC, CHUNK, D)
        chunks = _mha_residual(chunks, Wq_l, Wk_l, Wv_l, Wo_l, NUM_HEADS)
        summaries = chunks.mean(axis=2)
        global_ctx = _mha_residual(summaries, Wq_g, Wk_g, Wv_g, Wo_g, NUM_HEADS)
        enhanced = chunks + global_ctx[:, :, None, :]
        return enhanced.reshape(B, S, D)

    def _L1_ffn_ref(x, Wr, We):
        import jax, jax.numpy as jnp
        import numpy as np
        B, T, D, E, TOP_K = (4, 1024, 256, 8, 2)
        CAPACITY_FACTOR = 1.5
        Bb, Tt, Dd = x.shape
        Ee = Wr.shape[0]
        K = TOP_K
        C = int(Tt * K / Ee * CAPACITY_FACTOR) + 1
        logits = jnp.einsum('btd,ed->bte', x, Wr)
        top_vals, top_idx = jax.lax.top_k(logits, K)
        w = jax.nn.softmax(top_vals, axis=-1)
        flat_e = top_idx.reshape(Bb, Tt * K)
        oh = jax.nn.one_hot(flat_e, Ee, dtype=jnp.int32)
        pos_all = jnp.cumsum(oh, axis=1) - oh
        pos = jnp.take_along_axis(pos_all, flat_e[..., None], axis=-1)[..., 0]
        keep = pos < C
        b_idx = jnp.arange(Bb, dtype=jnp.int32)[:, None]
        dst = (b_idx * Ee + flat_e) * C + pos
        dst = jnp.where(keep, dst, Bb * Ee * C).reshape(-1)
        x_rep = jnp.repeat(x, K, axis=1).reshape(-1, Dd)
        buf = jnp.zeros((Bb * Ee * C, Dd), dtype=x.dtype).at[dst].add(x_rep, mode='drop')
        expert_in = buf.reshape(Bb, Ee, C, Dd)
        expert_out = jnp.einsum('becd,edf->becf', expert_in, We)
        gathered = jnp.take(expert_out.reshape(Bb * Ee * C, Dd), dst, axis=0, mode='fill', fill_value=0.0)
        gathered = gathered.reshape(Bb, Tt, K, Dd)
        out = jnp.einsum('btk,btkd->btd', w, gathered)
        return out

    def _L2_attn_ref(x, w_qkv, w_out):
        import jax, jax.numpy as jnp
        import numpy as np
        B, T, D_IN, D_OUT, NH = (4, 512, 256, 256, 16)
        HD = D_OUT // NH
        SCALE = 1.0 / float(np.sqrt(HD))
        b, t, _ = x.shape
        qkv = jnp.einsum('btd,ed->bte', x, w_qkv)
        qkv = qkv.reshape(b, t, 3, NH, HD)
        q, k, v = jnp.moveaxis(qkv, 2, 0)
        scores = jnp.einsum('bqhd,bkhd->bhqk', q, k) * SCALE
        causal_bias = (1.0 - jnp.tril(jnp.ones((t, t), dtype=x.dtype))) * -10000.0
        scores = scores + causal_bias
        attn = jax.nn.softmax(scores, axis=-1)
        out = jnp.einsum('bhqk,bkhd->bqhd', attn, v)
        out = out.reshape(b, t, D_OUT)
        return jnp.einsum('btd,ed->bte', out, w_out)

    def _L2_ffn_ref(x, gate_w, w1, w2):
        import jax, jax.numpy as jnp
        import numpy as np
        NUM_EXPERTS = 8
        EXPERT_CAPACITY = 2.0
        DIM = 256
        HIDDEN_DIM = 1024
        n, t, d = x.shape
        e = gate_w.shape[0]
        k = int(EXPERT_CAPACITY * t / e)
        scores = jnp.einsum('ntd,ed->nte', x, gate_w)
        probs = jax.nn.softmax(scores, axis=-1)
        g, m = jax.lax.top_k(probs.transpose(0, 2, 1), k)
        batch_idx = jnp.arange(n)[:, None, None]
        xin = x[batch_idx, m]
        h = jnp.einsum('nekd,edf->nekf', xin, w1)
        h = jax.nn.gelu(h, approximate=False)
        h = jnp.einsum('nekf,efd->nekd', h, w2)
        out_tok = g[..., None] * h
        out = jnp.zeros((n, t, d), dtype=x.dtype).at[batch_idx, m].add(out_tok)
        return out

    def _L3_attn_ref(x, wq, bq, wk, bk, wv, bv, wo, bo):
        import jax, jax.numpy as jnp
        import numpy as np
        NUM_HEADS = 16

        def _heads(t, B, N, H, hd):
            return t.reshape(B, N, H, hd).transpose(0, 2, 1, 3)
        B, N, D = x.shape
        H = NUM_HEADS
        hd = D // H
        q = _heads(x @ wq.T + bq, B, N, H, hd)
        k = _heads(x @ wk.T + bk, B, N, H, hd)
        v = _heads(x @ wv.T + bv, B, N, H, hd)
        q2 = jnp.sum(q * q, axis=-1)
        k2 = jnp.sum(k * k, axis=-1)
        qk = jnp.einsum('bhid,bhjd->bhij', q, k)
        d2 = jnp.maximum(q2[..., :, None] + k2[..., None, :] - 2.0 * qk, 1e-12)
        attn = jax.nn.softmax(-jnp.sqrt(d2), axis=-1)
        out = jnp.einsum('bhij,bhjd->bhid', attn, v)
        out = out.transpose(0, 2, 1, 3).reshape(B, N, D)
        return out @ wo.T + bo

    def _L3_ffn_ref(x, W_r, W_k, W_v, mu_r, mu_k):
        import jax, jax.numpy as jnp
        import numpy as np
        DIM = 256

        def _reference_tuple_inner(x, W_r, W_k, W_v, mu_r, mu_k):
            B, T, C = x.shape
            x_prev = jnp.concatenate([jnp.zeros((B, 1, C), x.dtype), x[:, :-1, :]], axis=1)
            xr = mu_r * x + (1.0 - mu_r) * x_prev
            xk = mu_k * x + (1.0 - mu_k) * x_prev
            r = jax.nn.sigmoid(jnp.einsum('btc,dc->btd', xr, W_r))
            k = jnp.einsum('btc,dc->btd', xk, W_k)
            k_act = jnp.square(jax.nn.relu(k))
            out = r * jnp.einsum('btc,dc->btd', k_act, W_v)
            new_state = x[:, -1, :]
            return (out, new_state)
        return _reference_tuple_inner(x, W_r, W_k, W_v, mu_r, mu_k)[0]
    x = L0_attn_x
    xn = _layernorm(x, axis=-1)
    s = _L0_attn_ref(xn, L0_attn_W_in, L0_attn_conv_w, L0_attn_conv_b, L0_attn_W_x, L0_attn_W_dt, L0_attn_b_dt, L0_attn_A_log, L0_attn_D, L0_attn_W_out)
    g = _silu(_L0_ffn_ref(xn, L0_ffn_U1, L0_ffn_V1, L0_ffn_b1, L0_ffn_U2, L0_ffn_V2, L0_ffn_b2))
    x = x + s * g
    xn = _layernorm(x, axis=-1)
    s = _L1_attn_ref(xn, L1_attn_Wq_l, L1_attn_Wk_l, L1_attn_Wv_l, L1_attn_Wo_l, L1_attn_Wq_g, L1_attn_Wk_g, L1_attn_Wv_g, L1_attn_Wo_g)
    g = _silu(_L1_ffn_ref(xn, L1_ffn_Wr, L1_ffn_We))
    x = x + s * g
    xn = _layernorm(x, axis=-1)
    s = _L2_attn_ref(xn, L2_attn_w_qkv, L2_attn_w_out)
    g = _silu(_L2_ffn_ref(xn, L2_ffn_gate_w, L2_ffn_w1, L2_ffn_w2))
    x = x + s * g
    xn = _layernorm(x, axis=-1)
    s = _L3_attn_ref(xn, L3_attn_wq, L3_attn_bq, L3_attn_wk, L3_attn_bk, L3_attn_wv, L3_attn_bv, L3_attn_wo, L3_attn_bo)
    g = _silu(_L3_ffn_ref(xn, L3_ffn_W_r, L3_ffn_W_k, L3_ffn_W_v, L3_ffn_mu_r, L3_ffn_mu_k))
    x = x + s * g
    return x

_drawn_inputs = setup_inputs


def setup_inputs(seed=0):
    import zlib

    import numpy as np

    out = dict(_drawn_inputs(seed))
    spreads = {'L0_attn_D': (1.0, 0.2), 'L0_ffn_b1': (0.0, 0.1), 'L0_ffn_b2': (0.0, 0.1)}
    factors = {}
    for name, (base, spread) in spreads.items():
        noise = np.random.default_rng([zlib.crc32(name.encode()), seed]).standard_normal(out[name].shape)
        drawn = base * np.exp(spread * noise) if base else spread * noise
        out[name] = jnp.asarray(drawn.astype(out[name].dtype))
    for name, factor in factors.items():
        out[name] = (out[name] * factor).astype(out[name].dtype)
    return out
```

```python
import concourse.bass as bass
from concourse import mybir
from contextlib import ExitStack

F32 = mybir.dt.float32
BF16 = mybir.dt.bfloat16
ALU = mybir.AluOpType
ACT = mybir.ActivationFunctionType
AX = mybir.AxisListType

P = 128
NB, T, D = 8, 512, 256
TT = T // P
DT = D // P
LN_EPS = 1e-5
DMA = 16


class Chip:

    def __init__(self, nc, stage):
        self.nc, self.stage, self.stack, self.sems = nc, stage, ExitStack(), []

    def __enter__(self):
        self.stack.__enter__()
        return self

    def __exit__(self, *what):
        self.nc.clear_and_free_semaphores(self.sems)
        self.nc.all_engine_barrier()
        return self.stack.__exit__(*what)

    def sb(self, name, shape, dtype=F32):
        return self.stack.enter_context(self.nc.sbuf_tensor(f"{self.stage}_{name}", list(shape), dtype))

    def psum(self):
        return self.stack.enter_context(self.nc.psum_tensor(f"{self.stage}_psum", [P, 8, 512], F32))

    def sem(self, name):
        self.sems.append(self.nc.alloc_semaphore(f"{self.stage}_{name}"))
        return self.sems[-1]


def token_tiles(x, b):
    return x[b].rearrange("(i p) d -> p i d", p=P)


def column(v, n):
    return v.rearrange("(n p) -> p n", n=n)


def make_identity(pool, ident, made):
    pool.memset(ident[:, :], 0.0).then_inc(made, 1)
    pool.wait_ge(made, 1)
    pool.affine_select(out=ident[:, :], in_=ident[:, :], compare_op=ALU.not_equal, fill=1.0, base=0,
                       pattern=[[-1, P]], channel_multiplier=1).then_inc(made, 1)


NH, HD = 16, 16
GH = 4
NG = NH // GH
QUAD = 32
AUG = 2
SCALE = HD ** -0.5
NEG = -125.0


class LayerNorm:

    def __init__(self, c):
        self.eps = c.sb("ln_eps", [P, 1])
        self.stats = c.sb("ln_stats", [P, TT, 6])
        self.moments = c.sb("ln_moments", [P, TT, 2])
        self.std = c.sb("ln_std", [P, TT])
        self.rstd = c.sb("ln_rstd", [P, TT])
        self.xn = c.sb("xn", [P, TT, D])
        self.eps_set, self.stats_ready, self.begun, self.var_ready, self.std_ready, self.rstd_ready, self.ready = (
            c.sem(f"ln_{n}") for n in ("eps_set", "stats_ready", "begun", "var_ready", "std_ready", "rstd_ready", "xn"))

    def dve_setup(self, dve):
        dve.memset(self.eps[:, :], LN_EPS).then_inc(self.eps_set, 1)

    def act_setup(self, act):
        act.wait_ge(self.eps_set, 1)

    def dve(self, dve, b, x):
        for i in range(TT):
            dve.bn_stats(self.stats[:, i], x[:, i]).then_inc(self.stats_ready, 1)
        dve.wait_ge(self.stats_ready, b * TT + TT)
        dve.sem_inc(self.begun, 1)
        for i in range(TT):
            dve.bn_aggr(self.moments[:, i], self.stats[:, i]).then_inc(self.var_ready, 1)
        dve.wait_ge(self.std_ready, b + 1)
        dve.reciprocal(self.rstd[:, :], self.std[:, :]).then_inc(self.rstd_ready, 1)
        dve.wait_ge(self.rstd_ready, b + 1)
        for i in range(TT):
            dve.tensor_scalar(self.xn[:, i], x[:, i], self.moments[:, i, 0:1], self.rstd[:, i:i + 1],
                              ALU.subtract, ALU.mult).then_inc(self.ready, 1)

    def act(self, act, b):
        act.wait_ge(self.var_ready, b * TT + TT)
        act.activation(self.std[:, :], self.moments[:, :, 1], ACT.Sqrt, bias=self.eps[:, 0:1]).then_inc(self.std_ready, 1)


def load_head_columns(sp, dst, src, loaded, first=AUG):
    for k in range(DT):
        sp.dma_start(dst[:, k, :, first:first + HD],
                     src[k * P:(k + 1) * P, :].rearrange("p (h e) -> p h e", h=NH)).then_inc(loaded, DMA)


def load_head_rows(sp, dst, src, loaded, first=0):
    for j in range(GH):
        sp.dma_start(dst[j * QUAD + first:j * QUAD + first + HD, :, :],
                     src.rearrange("(g h e) n -> h e g n", g=NG, h=GH)[j]).then_inc(loaded, DMA)


class Turned:

    def __init__(self, c, ps, ident, pairs):
        self.ps, self.ident, self.pairs = ps, ident, pairs
        self.done, self.copied = c.sem("turn_done"), c.sem("turn_copied")

    def pe(self, pe):
        for n, (src, _) in enumerate(self.pairs):
            if n >= 4:
                pe.wait_ge(self.copied, n - 3)
            pe.transpose(self.ps[:, n % 4, 0:P], src, self.ident[:, :]).then_inc(self.done, 1)
        pe.wait_ge(self.copied, len(self.pairs))

    def act(self, act):
        for n, (_, dst) in enumerate(self.pairs):
            act.wait_ge(self.done, n + 1)
            act.copy(dst, self.ps[:, n % 4, 0:P]).then_inc(self.copied, 1)


class Attention:

    def __init__(self, c, ps, q, k, v, local, neg_ident, mask_a, mask_b, ident):
        self.ps, self.q, self.k, self.v, self.local = ps, q, k, v, local
        self.neg_ident, self.mask_a, self.mask_b, self.ident = neg_ident, mask_a, mask_b, ident
        self.UA = 2 if local else 2 * TT
        self.KB = 1 if local else TT
        self.row_max = c.sb("row_max", [P, TT, P])
        self.probs = c.sb("probs", [P, 2, GH, T])
        self.o = c.sb("o", [P, T])
        self.den_inv = c.sb("den_inv", [P, T])
        self.ctx = c.sb("ctx", [P, NG, T])
        self.den_sel = c.sb("den_sel", [P, P])
        (self.a_done, self.a_max, self.max_done, self.q_shifted, self.s_done, self.p_ready, self.pv_done, self.o_copied,
         self.den_done, self.den_inv_ready, self.ctx_ready, self.sel_made, self.max_zeroed) = (
            c.sem(f"att_{n}") for n in ("a_done", "a_max", "max_done", "q_shifted", "s_done", "p_ready", "pv_done",
                                        "o_copied", "den_done", "den_inv", "ctx", "sel_made", "max_zeroed"))

    def pool_setup(self, pool):
        pool.memset(self.den_sel[:, :], 0.0).then_inc(self.sel_made, 1)
        pool.wait_ge(self.sel_made, 1)
        pool.affine_select(out=self.den_sel[:, :], in_=self.den_sel[:, :], compare_op=ALU.not_equal, fill=1.0, base=-HD,
                           pattern=[[-QUAD, GH], [0, QUAD]], channel_multiplier=1).then_inc(self.sel_made, 1)

    def dve_setup(self, dve):
        dve.memset(self.row_max[:, :, :], 0.0).then_inc(self.max_zeroed, 1)
        dve.wait_ge(self.max_zeroed, 1)

    def pe_setup(self, pe):
        pe.wait_ge(self.sel_made, 2)

    def rows(self, h):
        return slice(h * QUAD, h * QUAD + AUG + HD)

    def pe_first(self, pe, b, g, units):
        for u in units:
            n = g * self.UA + u
            i, pair = divmod(u, 2)
            if n >= 1:
                pe.wait_ge(self.a_max, b * NG * self.UA + n)
            if self.local:
                for j in range(2):
                    pe.matmul(self.ps[:, j], self.neg_ident[:, :], self.mask_a[:, :], start=True, stop=False)
            for t in range(TT if self.local else 1):
                for j in range(2):
                    h = 2 * pair + j
                    r = self.rows(h)
                    if self.local:
                        cols = slice(t * P, (t + 1) * P)
                        last = pe.matmul(self.ps[:, j, cols], self.q[r, g, cols], self.k[r, g, cols], start=False,
                                         stop=(t == TT - 1))
                    else:
                        last = pe.matmul(self.ps[:, j], self.q[r, g, i * P:(i + 1) * P], self.k[r, g, :], start=True,
                                         stop=False)
            if not self.local:
                for j in range(2):
                    last = pe.matmul(self.ps[:, j, i * P:], self.neg_ident[:, :], self.mask_a[:, 0:T - i * P], start=False,
                                     stop=True)
            last.then_inc(self.a_done, 1)

    def dve_first(self, dve, b, g, units):
        for u in units:
            n = g * self.UA + u
            i, pair = divmod(u, 2)
            if g >= 1 and u == 0:
                dve.wait_ge(self.max_done, b * NG + g)
            dve.wait_ge(self.a_done, b * NG * self.UA + n + 1)
            scores = self.ps[:, 0:2]
            first = 2 * pair * QUAD
            if self.local:
                dve.reduce_max(self.row_max[:, :, first:first + QUAD + 1:QUAD].rearrange("p i j -> p j i"),
                               scores.rearrange("p j (i k) -> p j i k", k=P), AX.X).then_inc(self.a_max, 1)
            else:
                dve.reduce_max(self.row_max[:, i, first:first + QUAD + 1:QUAD], scores, AX.X).then_inc(self.a_max, 1)

    def pe_max(self, pe, b, g):
        pe.wait_ge(self.a_max, b * NG * self.UA + (g + 1) * self.UA)
        if g >= 2:
            pe.wait_ge(self.den_inv_ready, b * NG + g - 1)
        for i in range(TT):
            last = pe.transpose(self.ps[:, 6, i * P:(i + 1) * P], self.row_max[:, i], self.ident[:, :])
        last.then_inc(self.max_done, 1)

    def dve_shift(self, dve, b, g):
        dve.wait_ge(self.max_done, b * NG + g + 1)
        dve.tensor_tensor(self.q[:, g], self.q[:, g], self.ps[:, 6], ALU.subtract).then_inc(self.q_shifted, 1)

    def pe_second(self, pe, b, g, kt):
        n = g * self.KB + kt
        if kt == 0:
            pe.wait_ge(self.q_shifted, b * NG + g + 1)
        if n >= 1:
            pe.wait_ge(self.p_ready, b * NG * self.KB + n)
        if self.local:
            for h in range(GH):
                pe.matmul(self.ps[:, 2 + h], self.neg_ident[:, :], self.mask_b[:, :], start=True, stop=False)
            for t in range(TT):
                cols = slice(t * P, (t + 1) * P)
                for h in range(GH):
                    r = self.rows(h)
                    last = pe.matmul(self.ps[:, 2 + h, cols], self.k[r, g, cols], self.q[r, g, cols], start=False,
                                     stop=(t == TT - 1))
        else:
            for h in range(GH):
                r = self.rows(h)
                pe.matmul(self.ps[:, 2 + h], self.k[r, g, kt * P:(kt + 1) * P], self.q[r, g, :], start=True, stop=False)
            for h in range(GH):
                last = pe.matmul(self.ps[:, 2 + h, 0:(kt + 1) * P], self.neg_ident[:, :],
                                 self.mask_b[:, T - (kt + 1) * P:], start=False, stop=True)
        last.then_inc(self.s_done, 1)

    def act_exp(self, act, b, g, kt):
        n = g * self.KB + kt
        act.wait_ge(self.s_done, b * NG * self.KB + n + 1)
        if n >= 2:
            act.wait_ge(self.pv_done, b * NG * self.KB + n - 1)
        act.activation(self.probs[:, n % 2], self.ps[:, 2:6], ACT.Exp, scale=SCALE).then_inc(self.p_ready, 1)

    def pe_pv(self, pe, b, g, kt):
        n = g * self.KB + kt
        pe.wait_ge(self.p_ready, b * NG * self.KB + n + 1)
        if g >= 1 and kt == 0:
            pe.wait_ge(self.o_copied, b * NG + g)
        for t in range(TT if self.local else 1):
            cols = slice(t * P, (t + 1) * P) if self.local else slice(0, T)
            for h in range(GH):
                last = pe.matmul(self.ps[h * QUAD:(h + 1) * QUAD, 7, cols], self.v[:, t if self.local else kt, g * GH + h, :],
                                 self.probs[:, n % 2, h, cols], start=(kt == 0), stop=(kt == self.KB - 1))
        last.then_inc(self.pv_done, 1)

    def act_out(self, act, b, g):
        act.wait_ge(self.pv_done, b * NG * self.KB + (g + 1) * self.KB)
        if g >= 1:
            act.wait_ge(self.ctx_ready, b * NG + g)
        act.copy(self.o[:, :], self.ps[:, 7]).then_inc(self.o_copied, 1)

    def pe_den(self, pe, b, g):
        pe.wait_ge(self.o_copied, b * NG + g + 1)
        if g + 1 < NG:
            pe.wait_ge(self.q_shifted, b * NG + g + 2)
        pe.matmul(self.ps[:, 6], self.den_sel[:, :], self.o[:, :], start=True, stop=True).then_inc(self.den_done, 1)

    def dve_ctx(self, dve, b, g):
        dve.wait_ge(self.den_done, b * NG + g + 1)
        dve.reciprocal(self.den_inv[:, :], self.ps[:, 6]).then_inc(self.den_inv_ready, 1)
        dve.wait_ge(self.den_inv_ready, b * NG + g + 1)
        dve.tensor_tensor(self.ctx[:, g], self.o[:, :], self.den_inv[:, :], ALU.mult).then_inc(self.ctx_ready, 1)

    def pe(self, pe, b):
        self.pe_first(pe, b, 0, range(self.UA))
        self.pe_max(pe, b, 0)
        share = self.UA // self.KB
        for g in range(NG):
            for kt in range(self.KB):
                self.pe_second(pe, b, g, kt)
                if g + 1 < NG:
                    self.pe_first(pe, b, g + 1, range(kt * share, (kt + 1) * share))
                if kt >= 1:
                    self.pe_pv(pe, b, g, kt - 1)
            self.pe_pv(pe, b, g, self.KB - 1)
            if g + 1 < NG:
                self.pe_max(pe, b, g + 1)
            self.pe_den(pe, b, g)

    def act(self, act, b):
        for g in range(NG):
            for kt in range(self.KB):
                self.act_exp(act, b, g, kt)
            self.act_out(act, b, g)

    def dve(self, dve, b):
        self.dve_first(dve, b, 0, range(self.UA))
        self.dve_shift(dve, b, 0)
        for g in range(NG):
            if g + 1 < NG:
                self.dve_first(dve, b, g + 1, range(self.UA))
                self.dve_shift(dve, b, g + 1)
            self.dve_ctx(dve, b, g)




NPART = 3
STACK = ((0, 3, 0), (0, 2, 1), (0, 1, 2))
SLOTS = sum(n for _, n, _ in STACK)
KQK = SLOTS * HD


def parts_tensor(nc, name):
    return nc.dram_tensor(name, (NB, NG, NPART * HD, GH * T), BF16, kind="Internal").ap()


class Split:

    TILES = 2 * DT
    STORES = TILES * (P // (GH * HD)) * NPART

    def __init__(self, c, q_parts, k_parts):
        self.q_parts, self.k_parts = q_parts, k_parts
        self.full = c.sb("full", [P, self.TILES, T])
        self.rest = c.sb("rest", [P, self.TILES, T])
        self.parts = c.sb("parts", [P, self.TILES, NPART, T], BF16)
        self.copied, self.high, self.rest_ready, self.middle, self.ready, self.stored = (
            c.sem(f"split_{n}") for n in ("copied", "high", "rest", "middle", "ready", "stored"))

    def act_setup(self, act):
        act.sem_inc(self.copied, self.TILES)

    def dve_setup(self, dve):
        dve.sem_inc(self.rest_ready, self.TILES)

    def pool_setup(self, pool):
        pool.sem_inc(self.ready, self.TILES)

    def sp_setup(self, sp):
        sp.sem_inc(self.stored, self.STORES * DMA)

    def bank_free(self, eng, b, n):
        eng.wait_ge(self.copied, b * self.TILES + n + 1)

    def act(self, act, b, n, bank, **how):
        act.wait_ge(self.rest_ready, b * self.TILES + n + 1)
        act.activation(self.full[:, n], bank, ACT.Identity, **how).then_inc(self.copied, 1)

    def dve(self, dve, b, n):
        dve.wait_ge(self.copied, b * self.TILES + n + 1 + self.TILES)
        if n == 0:
            dve.wait_ge(self.stored, (b + 1) * self.STORES * DMA)
        dve.tensor_copy(self.parts[:, n, 0], self.full[:, n]).then_inc(self.high, 1)
        dve.wait_ge(self.high, b * self.TILES + n + 1)
        dve.wait_ge(self.ready, b * self.TILES + n + 1)
        dve.tensor_tensor(self.rest[:, n], self.full[:, n], self.parts[:, n, 0], ALU.subtract).then_inc(self.rest_ready, 1)

    def pool(self, pool, b, n):
        pool.wait_ge(self.rest_ready, b * self.TILES + n + 1 + self.TILES)
        pool.sem_inc(self.middle, 1)
        pool.tensor_copy(self.parts[:, n, 1], self.rest[:, n]).then_inc(self.middle, 1)
        pool.wait_ge(self.middle, (b * self.TILES + n + 1) * 2)
        pool.tensor_tensor(self.parts[:, n, 2], self.rest[:, n], self.parts[:, n, 1], ALU.subtract).then_inc(self.ready, 1)

    def sp(self, sp, b, n):
        sp.wait_ge(self.ready, b * self.TILES + n + 1 + self.TILES)
        to, m = (self.q_parts, n) if n < DT else (self.k_parts, n - DT)
        for j in range(P // (GH * HD)):
            for part in range(NPART):
                row = (part if n < DT else NPART - 1 - part) * HD
                dst = to[b, m * (P // (GH * HD)) + j, row:row + HD, :].rearrange("e (h t) -> h e t", h=GH)
                sp.dma_start(dst, self.parts[j * GH * HD:(j + 1) * GH * HD, n, part]).then_inc(self.stored, DMA)


def load_stack(sp, dst, parts, b, g, k_side, loaded):
    row = 0
    for first_q, n, first_k in STACK:
        first = first_k if k_side else first_q
        sp.dma_start(dst[row:row + n * HD], parts[b, g, first * HD:(first + n) * HD, :].rearrange(
            "r (h t) -> r h t", h=GH)).then_inc(loaded, DMA)
        row += n * HD
DI, DS, TAPS, RANK = 512, 16, 4, 64
MT = DI // P
F0, R0 = 1024, 64
FT0 = F0 // P
STEPS = DS * MT
RING = 4
CHUNK = 4
NCHUNK = DS // CHUNK


def stage_mamba(nc, w, x_in, x_out):
    with Chip(nc, "mamba") as c:
        ident = c.sb("ident", [P, P])
        eps = c.sb("eps", [P, 1])
        w_in = c.sb("w_in", [P, DT, 2 * DI])
        w_x = c.sb("w_x", [P, MT, RANK + 2 * DS])
        w_dt = c.sb("w_dt", [RANK, DI])
        w_out = c.sb("w_out", [P, MT, D])
        u1 = c.sb("u1", [P, DT, R0])
        v1 = c.sb("v1", [R0, F0])
        u2 = c.sb("u2", [P, FT0, R0])
        v2b = c.sb("v2b", [R0 + 1, D])
        conv_w = c.sb("conv_w", [P, MT, TAPS])
        conv_b = c.sb("conv_b", [P, MT])
        b_dt = c.sb("b_dt", [P, MT])
        a_neg = c.sb("a_neg", [P, MT, DS])
        skip = c.sb("skip", [P, MT])
        b1 = c.sb("b1", [P, FT0])
        x = c.sb("x", [P, TT, D])
        stats = c.sb("stats", [P, TT, 6])
        moments = c.sb("moments", [P, TT, 2])
        std = c.sb("std", [P, TT])
        rstd = c.sb("rstd", [P, TT])
        xn = c.sb("xn", [P, TT, D])
        xn_t = c.sb("xn_t", [P, DT, T])
        xi = c.sb("xi", [P, MT, TAPS - 1 + T])
        conv = c.sb("conv", [P, MT, T])
        xc = c.sb("xc", [P, MT, T])
        z_silu = c.sb("z_silu", [P, MT, T])
        low = c.sb("low", [R0, T])
        xp = c.sb("xp", [RANK + 2 * DS, T])
        sp_x = c.sb("sp_x", [P, MT, T])
        sp_e = c.sb("sp_e", [P, MT, T])
        sp_u = c.sb("sp_u", [P, MT, T])
        dt = c.sb("dt", [P, MT, T])
        u = c.sb("u", [P, MT, T])
        b_all = c.sb("b_all", [P, 2, CHUNK, T])
        c_all = c.sb("c_all", [P, 2, CHUNK, T])
        decay = c.sb("decay", [P, RING, T])
        drive = c.sb("drive", [P, RING, T])
        h = c.sb("h", [P, RING, T])
        hc = c.sb("hc", [P, RING, T])
        hidden = c.sb("hidden", [P, 2, T])
        q1 = c.sb("q1", [R0 + 1, T])
        gate = c.sb("gate", [P, TT, D])
        xo = c.sb("xo", [P, TT, D])
        bc_dram = nc.dram_tensor("mamba_bc", (2 * DS, T), F32, kind="Internal").ap()
        ps = c.psum()

        w_loaded, made, ident_made, a_made = (c.sem(n) for n in ("w_loaded", "made", "ident_made", "a_made"))
        x_loaded, x_free = c.sem("x_loaded"), c.sem("x_free")
        ln_stats, ln_begun, ln_var, ln_std, ln_rstd, xn_ready = (
            c.sem(n) for n in ("ln_stats", "ln_begun", "ln_var", "ln_std", "ln_rstd", "xn_ready"))
        pe_group, q_summed, act_evac = c.sem("pe_group"), c.sem("q_summed"), c.sem("act_evac")
        conv_step, xc_ready = c.sem("conv_step"), c.sem("xc_ready")
        bc_stored = c.sem("bc_stored")
        b_loaded, c_loaded = ([c.sem(f"{n}_loaded{k}") for k in range(2)] for n in "bc")
        sp_x_ready, sp_abs, sp_exp, sp_up, sp_err, sp_ln, sp_relu, dt_ready, u_ready = (
            c.sem(n) for n in ("sp_x", "sp_abs", "sp_exp", "sp_up", "sp_err", "sp_ln", "sp_relu", "dt", "u"))
        decay_ready, drive_ready, h_ready, hc_ready, y_summed = (
            c.sem(n) for n in ("decay", "drive", "h", "hc", "y_summed"))
        y_skip, y_gated, s_gated, xo_ready, x_stored = (
            c.sem(n) for n in ("y_skip", "y_gated", "s_gated", "xo", "x_stored"))

        G_XNT, G_XI, G_Z, G_LOW, G_XP, G_DT = 0, 2, 6, 10, 11, 12
        G_HID, G_FFN, G_S = 16, 24, 26
        GROUPS = 28
        Q_EVAC, EVACS = 21, 23

        def evac_count(g):
            return g + 1 if g < G_DT else g + 1 - MT + (g >= G_FFN)

        with nc.Block() as block:

            @block.sync
            def _(sp):
                for dst, src in (
                    (w_in[:, :, :], w["W_in"].rearrange("(k p) n -> p k n", p=P)),
                    (w_x[:, :, :], w["W_x"].rearrange("(k p) n -> p k n", p=P)),
                    (w_dt[:, :], w["W_dt"]),
                    (w_out[:, :, :], w["W_out"].rearrange("(k p) n -> p k n", p=P)),
                    (u1[:, :, :], w["U1"].rearrange("(k p) n -> p k n", p=P)),
                    (v1[:, :], w["V1"]),
                    (u2[:, :, :], w["U2"].rearrange("(k p) n -> p k n", p=P)),
                    (v2b[0:R0, :], w["V2"]),
                    (v2b[R0:R0 + 1, :], w["b2"].rearrange("(a n) -> a n", a=1)),
                    (conv_w[:, :, :], w["conv_w"].rearrange("(m p) a k -> p m (a k)", p=P)),
                    (a_neg[:, :, :], w["A_log"].rearrange("(m p) s -> p m s", p=P)),
                ):
                    sp.dma_start(dst, src).then_inc(w_loaded, DMA)
                with nc.allow_non_contiguous_dma(reason="short vectors, once"):
                    for dst, src in ((conv_b, w["conv_b"]), (b_dt, w["b_dt"]), (skip, w["D"])):
                        sp.dma_start(dst[:, :], column(src, MT)).then_inc(w_loaded, DMA)
                    sp.dma_start(b1[:, :], column(w["b1"], FT0)).then_inc(w_loaded, DMA)
                sp.sem_inc(x_free, 1)
                sp.sem_inc(x_stored, DMA)
                with sp.Fori(0, NB) as b:
                    sp.wait_ge(x_free, b + 1)
                    sp.dma_start(x[:, :, :], token_tiles(x_in, b)).then_inc(x_loaded, DMA)
                    sp.wait_ge(act_evac, b * EVACS + evac_count(G_XP))
                    sp.dma_start(bc_dram, xp[RANK:RANK + 2 * DS, :]).then_inc(bc_stored, DMA)
                    sp.wait_ge(bc_stored, b * DMA + DMA)
                    for k in range(NCHUNK):
                        if k >= 2:
                            sp.wait_ge(drive_ready, b * STEPS + (k - 1) * CHUNK * MT)
                            sp.wait_ge(hc_ready, b * STEPS + (k - 1) * CHUNK * MT)
                        rows = bc_dram[k * CHUNK:(k + 1) * CHUNK, :]
                        sp.dma_start(b_all[:, k % 2], rows.partition_broadcast(P)).then_inc(b_loaded[k % 2], DMA)
                        rows = bc_dram[DS + k * CHUNK:DS + (k + 1) * CHUNK, :]
                        sp.dma_start(c_all[:, k % 2], rows.partition_broadcast(P)).then_inc(c_loaded[k % 2], DMA)
                    sp.wait_ge(xo_ready, b * 2 + 2)
                    sp.dma_start(token_tiles(x_out, b), xo[:, :, :]).then_inc(x_stored, DMA)
                sp.wait_ge(x_stored, (NB + 1) * DMA)

            @block.gpsimd
            def _(pool):
                make_identity(pool, ident, ident_made)
                with pool.Fori(0, NB) as b:
                    for m in range(MT):
                        pool.wait_ge(xc_ready, b * MT + m + 1)
                        pool.wait_ge(dt_ready, b * MT + m + 1)
                        pool.tensor_tensor(u[:, m], dt[:, m], xc[:, m], ALU.mult).then_inc(u_ready, 1)
                    for n in range(STEPS):
                        s, m = divmod(n, MT)
                        if n < MT:
                            pool.wait_ge(u_ready, b * MT + m + 1)
                        if n % (CHUNK * MT) == 0:
                            k = s // CHUNK
                            pool.wait_ge(b_loaded[k % 2], (b * (NCHUNK // 2) + k // 2 + 1) * DMA)
                        if n >= RING:
                            pool.wait_ge(h_ready, b * STEPS + n - RING + 1)
                        pool.tensor_tensor(drive[:, n % RING], u[:, m], b_all[:, s // CHUNK % 2, s % CHUNK],
                                           ALU.mult).then_inc(drive_ready, 1)

            @block.scalar
            def _(act):
                act.wait_ge(w_loaded, 15 * DMA)
                act.wait_ge(made, 3)
                act.activation(a_neg[:, :, :], a_neg[:, :, :], ACT.Exp).then_inc(a_made, 1)
                act.wait_ge(a_made, 1)
                act.mul(a_neg[:, :, :], a_neg[:, :, :], -1.0).then_inc(a_made, 1)
                act.wait_ge(a_made, 2)
                with act.Fori(0, NB) as b:
                    act.wait_ge(ln_var, b * TT + TT)
                    act.activation(std[:, :], moments[:, :, 1], ACT.Sqrt, bias=eps[:, 0:1]).then_inc(ln_std, 1)
                    for k in range(DT):
                        act.wait_ge(pe_group, b * GROUPS + G_XNT + k + 1)
                        act.copy(xn_t[:, k], ps[:, (G_XNT + k) % 4]).then_inc(act_evac, 1)
                    for m in range(MT):
                        act.wait_ge(pe_group, b * GROUPS + G_XI + m + 1)
                        act.copy(xi[:, m, TAPS - 1:], ps[:, (G_XI + m) % 4]).then_inc(act_evac, 1)
                    for m in range(MT):
                        act.wait_ge(pe_group, b * GROUPS + G_Z + m + 1)
                        act.activation(z_silu[:, m], ps[:, (G_Z + m) % 4], ACT.Silu).then_inc(act_evac, 1)
                    act.wait_ge(pe_group, b * GROUPS + G_LOW + 1)
                    act.copy(low[:, :], ps[0:R0, G_LOW % 4]).then_inc(act_evac, 1)
                    for m in range(MT):
                        act.wait_ge(conv_step, b * TAPS * MT + (TAPS - 1) * MT + m + 1)
                        act.activation(xc[:, m], conv[:, m], ACT.Silu, bias=conv_b[:, m:m + 1]).then_inc(xc_ready, 1)
                    act.wait_ge(pe_group, b * GROUPS + G_XP + 1)
                    act.copy(xp[:, :], ps[0:RANK + 2 * DS, G_XP % 4]).then_inc(act_evac, 1)
                    for m in range(MT):
                        act.wait_ge(sp_x_ready, b * MT + m + 1)
                        act.activation(sp_e[:, m], sp_x[:, m], ACT.Abs).then_inc(sp_abs, 1)
                    for m in range(MT):
                        act.wait_ge(sp_abs, b * MT + m + 1)
                        act.activation(sp_e[:, m], sp_e[:, m], ACT.Exp, scale=-1.0).then_inc(sp_exp, 1)
                    for m in range(MT):
                        act.wait_ge(sp_err, b * MT + m + 1)
                        act.activation(sp_u[:, m], sp_u[:, m], ACT.Ln).then_inc(sp_ln, 1)
                    for f in range(FT0):
                        act.wait_ge(pe_group, b * GROUPS + G_HID + f + 1)
                        if f >= 2:
                            act.wait_ge(q_summed, b * FT0 + f - 1)
                        act.activation(hidden[:, f % 2], ps[:, (G_HID + f) % 4], ACT.Gelu_apprx_tanh,
                                       bias=b1[:, f:f + 1]).then_inc(act_evac, 1)
                    act.wait_ge(q_summed, b * FT0 + FT0)
                    act.copy(q1[0:R0, :], ps[0:R0, 4]).then_inc(act_evac, 1)
                    for j in range(2):
                        act.wait_ge(pe_group, b * GROUPS + G_FFN + j + 1)
                        act.activation(gate[:, 2 * j:2 * j + 2, :], ps[:, (G_FFN + j) % 4], ACT.Silu).then_inc(act_evac, 1)
                    for n in range(STEPS):
                        s, m = divmod(n, MT)
                        if n < MT:
                            act.wait_ge(dt_ready, b * MT + m + 1)
                        if n >= RING:
                            act.wait_ge(h_ready, b * STEPS + n - RING + 1)
                        act.activation(decay[:, n % RING], dt[:, m], ACT.Exp,
                                       scale=a_neg[:, m, s:s + 1]).then_inc(decay_ready, 1)

            @block.vector
            def _(dve):
                dve.memset(eps[:, :], LN_EPS).then_inc(made, 1)
                dve.memset(xi[:, :, 0:TAPS - 1], 0.0).then_inc(made, 1)
                dve.memset(q1[R0:R0 + 1, :], 1.0).then_inc(made, 1)
                dve.wait_ge(w_loaded, 15 * DMA)
                dve.wait_ge(made, 3)
                with dve.Fori(0, NB) as b:
                    dve.wait_ge(x_loaded, b * DMA + DMA)
                    for i in range(TT):
                        dve.bn_stats(stats[:, i], x[:, i]).then_inc(ln_stats, 1)
                    dve.wait_ge(ln_stats, b * TT + TT)
                    dve.sem_inc(ln_begun, 1)
                    for i in range(TT):
                        dve.bn_aggr(moments[:, i], stats[:, i]).then_inc(ln_var, 1)
                    dve.wait_ge(ln_std, b + 1)
                    dve.reciprocal(rstd[:, :], std[:, :]).then_inc(ln_rstd, 1)
                    dve.wait_ge(ln_rstd, b + 1)
                    for i in range(TT):
                        dve.tensor_scalar(xn[:, i], x[:, i], moments[:, i, 0:1], rstd[:, i:i + 1],
                                          ALU.subtract, ALU.mult).then_inc(xn_ready, 1)
                    for k in range(TAPS):
                        for m in range(MT):
                            if k == 0:
                                dve.wait_ge(act_evac, b * EVACS + evac_count(G_XI + m))
                                dve.tensor_scalar(conv[:, m], xi[:, m, 0:T], conv_w[:, m, 0:1], None,
                                                  ALU.mult).then_inc(conv_step, 1)
                            else:
                                dve.wait_ge(conv_step, b * TAPS * MT + (k - 1) * MT + m + 1)
                                dve.scalar_tensor_tensor(conv[:, m], xi[:, m, k:k + T], conv_w[:, m, k:k + 1],
                                                         conv[:, m], ALU.mult, ALU.add).then_inc(conv_step, 1)
                    for m in range(MT):
                        dve.wait_ge(pe_group, b * GROUPS + G_DT + m + 1)
                        dve.tensor_scalar(sp_x[:, m], ps[:, (G_DT + m) % 4], b_dt[:, m:m + 1], None,
                                          ALU.add).then_inc(sp_x_ready, 1)
                    for m in range(MT):
                        dve.wait_ge(sp_exp, b * MT + m + 1)
                        dve.tensor_scalar(sp_u[:, m], sp_e[:, m], 1.0, None, ALU.add).then_inc(sp_up, 1)
                    for m in range(MT):
                        dve.wait_ge(sp_up, b * MT + m + 1)
                        dve.scalar_tensor_tensor(sp_e[:, m], sp_u[:, m], 1.0, sp_e[:, m], ALU.subtract,
                                                 ALU.subtract).then_inc(sp_err, 1)
                    for m in range(MT):
                        dve.wait_ge(sp_err, b * MT + m + 1)
                        dve.scalar_tensor_tensor(sp_x[:, m], sp_x[:, m], 0.0, sp_e[:, m], ALU.max,
                                                 ALU.subtract).then_inc(sp_relu, 1)
                    for m in range(MT):
                        dve.wait_ge(sp_relu, b * MT + m + 1)
                        dve.wait_ge(sp_ln, b * MT + m + 1)
                        dve.tensor_tensor(dt[:, m], sp_x[:, m], sp_u[:, m], ALU.add).then_inc(dt_ready, 1)
                    for n in range(STEPS + 1):
                        if n < STEPS:
                            dve.wait_ge(decay_ready, b * STEPS + n + 1)
                            dve.wait_ge(drive_ready, b * STEPS + n + 1)
                            if n >= RING:
                                dve.wait_ge(hc_ready, b * STEPS + n - RING + 1)
                            dve.tensor_tensor_scan(h[:, n % RING], decay[:, n % RING], drive[:, n % RING], 0.0,
                                                   ALU.mult, ALU.add).then_inc(h_ready, 1)
                        if n >= 1:
                            s = (n - 1) // MT
                            dve.wait_ge(h_ready, b * STEPS + n)
                            if (n - 1) % (CHUNK * MT) == 0:
                                k = s // CHUNK
                                dve.wait_ge(c_loaded[k % 2], (b * (NCHUNK // 2) + k // 2 + 1) * DMA)
                            if n - 1 >= RING:
                                dve.wait_ge(y_summed, b * STEPS + n - RING)
                            dve.tensor_tensor(hc[:, (n - 1) % RING], h[:, (n - 1) % RING],
                                              c_all[:, s // CHUNK % 2, s % CHUNK], ALU.mult).then_inc(hc_ready, 1)
                    for m in range(MT):
                        dve.wait_ge(y_summed, b * STEPS + STEPS - MT + m + 1)
                        dve.scalar_tensor_tensor(conv[:, m], xc[:, m], skip[:, m:m + 1], ps[:, 4 + m], ALU.mult,
                                                 ALU.add).then_inc(y_skip, 1)
                    for m in range(MT):
                        dve.wait_ge(y_skip, b * MT + m + 1)
                        dve.tensor_tensor(conv[:, m], conv[:, m], z_silu[:, m], ALU.mult).then_inc(y_gated, 1)
                    dve.wait_ge(act_evac, b * EVACS + EVACS)
                    dve.wait_ge(x_stored, b * DMA + DMA)
                    for j in range(2):
                        dve.wait_ge(pe_group, b * GROUPS + G_S + j + 1)
                        dve.tensor_tensor(xo[:, 2 * j:2 * j + 2, :], gate[:, 2 * j:2 * j + 2, :],
                                          ps[:, (G_S + j) % 4].rearrange("p (i d) -> p i d", d=D), ALU.mult).then_inc(s_gated, 1)
                    for j in range(2):
                        dve.wait_ge(s_gated, b * 2 + j + 1)
                        dve.tensor_tensor(xo[:, 2 * j:2 * j + 2, :], xo[:, 2 * j:2 * j + 2, :],
                                          x[:, 2 * j:2 * j + 2, :], ALU.add).then_inc(xo_ready, 1)
                    dve.wait_ge(xo_ready, b * 2 + 2)
                    dve.sem_inc(x_free, 1)

            @block.tensor
            def _(pe):
                pe.wait_ge(w_loaded, 15 * DMA)
                pe.wait_ge(made, 3)
                pe.wait_ge(ident_made, 2)
                with pe.Fori(0, NB) as b:
                    def bank(g):
                        return ps[:, g % 4]

                    pe.wait_ge(xn_ready, b * TT + TT)
                    for k in range(DT):
                        for i in range(TT):
                            last = pe.transpose(bank(G_XNT + k)[:, i * P:(i + 1) * P], xn[:, i, k * P:(k + 1) * P], ident[:, :])
                        last.then_inc(pe_group, 1)
                    pe.wait_ge(act_evac, b * EVACS + evac_count(G_XNT + 1))
                    for g in range(G_XI, G_XI + 2 * MT):
                        if g >= 4:
                            pe.wait_ge(act_evac, b * EVACS + evac_count(g - 4))
                        for k in range(DT):
                            last = pe.matmul(bank(g), w_in[:, k, (g - G_XI) * P:(g - G_XI + 1) * P], xn_t[:, k],
                                             start=(k == 0), stop=(k == DT - 1))
                        last.then_inc(pe_group, 1)
                    pe.wait_ge(act_evac, b * EVACS + evac_count(G_LOW - 4))
                    for k in range(DT):
                        last = pe.matmul(bank(G_LOW)[0:R0], u1[:, k], xn_t[:, k], start=(k == 0), stop=(k == DT - 1))
                    last.then_inc(pe_group, 1)
                    pe.wait_ge(act_evac, b * EVACS + evac_count(G_XP - 4))
                    pe.wait_ge(xc_ready, b * MT + MT)
                    for m in range(MT):
                        last = pe.matmul(bank(G_XP)[0:RANK + 2 * DS], w_x[:, m], xc[:, m], start=(m == 0), stop=(m == MT - 1))
                    last.then_inc(pe_group, 1)
                    pe.wait_ge(act_evac, b * EVACS + evac_count(G_XP))
                    for m in range(MT):
                        pe.matmul(bank(G_DT + m), w_dt[:, m * P:(m + 1) * P], xp[0:RANK, :], start=True,
                                  stop=True).then_inc(pe_group, 1)

                    def sum_q(f):
                        pe.wait_ge(act_evac, b * EVACS + evac_count(G_HID + f))
                        pe.matmul(ps[0:R0, 4], u2[:, f], hidden[:, f % 2], start=(f == 0),
                                  stop=(f == FT0 - 1)).then_inc(q_summed, 1)

                    for f in range(FT0):
                        if f < 4:
                            pe.wait_ge(sp_x_ready, b * MT + f + 1)
                        else:
                            pe.wait_ge(act_evac, b * EVACS + evac_count(G_HID + f - 4))
                        pe.matmul(bank(G_HID + f), v1[:, f * P:(f + 1) * P], low[:, :], start=True,
                                  stop=True).then_inc(pe_group, 1)
                        if f >= 1:
                            sum_q(f - 1)
                    sum_q(FT0 - 1)
                    pe.wait_ge(act_evac, b * EVACS + Q_EVAC)
                    for j in range(2):
                        for i in (2 * j, 2 * j + 1):
                            last = pe.matmul(bank(G_FFN + j)[:, i % 2 * D:(i % 2 + 1) * D], q1[:, i * P:(i + 1) * P],
                                             v2b[:, :], start=True, stop=True)
                        last.then_inc(pe_group, 1)
                    for n in range(STEPS):
                        s, m = divmod(n, MT)
                        pe.wait_ge(hc_ready, b * STEPS + n + 1)
                        pe.matmul(ps[:, 4 + m], ident[:, :], hc[:, n % RING], start=(s == 0),
                                  stop=(s == DS - 1)).then_inc(y_summed, 1)
                    pe.wait_ge(y_gated, b * MT + MT)
                    for j in range(2):
                        for i in (2 * j, 2 * j + 1):
                            for m in range(MT):
                                last = pe.matmul(bank(G_S + j)[:, i % 2 * D:(i % 2 + 1) * D],
                                                 conv[:, m, i * P:(i + 1) * P], w_out[:, m], start=(m == 0),
                                                 stop=(m == MT - 1))
                        last.then_inc(pe_group, 1)
LC = 64
NC = T // LC
NE1, TOP1 = 8, 2
CAP1 = int(T * TOP1 / NE1 * 1.5) + 1
APART = 2.0 ** 90


def stage_chunks(nc, w, x_in, x_out):
    with Chip(nc, "chunks") as c:
        ident = c.sb("ident", [P, P])
        neg_ident = c.sb("neg_ident", [P, P], BF16)
        apart = c.sb("apart", [P, T], BF16)
        wq = c.sb("wq", [P, DT, NH, QUAD])
        wk = c.sb("wk", [P, DT, NH, QUAD])
        wv = c.sb("wv", [P, DT, D])
        wo = c.sb("wo", [P, NG, D])
        wq_g, wk_g, wv_g, wo_g = (c.sb(n, [P, DT, D]) for n in ("wq_g", "wk_g", "wv_g", "wo_g"))
        wr = c.sb("wr", [P, DT, NE1])
        we = c.sb("we", [P, DT, NE1, D])
        k_one = c.sb("k_one", [P, 1])
        chunk_mean = c.sb("chunk_mean", [P, TT, NC])
        chunk_of = c.sb("chunk_of", [NC, TT, P])
        head_rows = c.sb("head_rows", [P, DT, NH, NC])
        head_keys = c.sb("head_keys", [P, NH, HD])
        key_rows = c.sb("key_rows", [NC, NH, NC])
        before = c.sb("before", [P, P])
        ones = c.sb("ones", [P, P])
        order = c.sb("order", [P, NE1])
        x = c.sb("x", [P, TT, D])
        ln = LayerNorm(c)
        xn = ln.xn
        xn_t = c.sb("xn_t", [P, DT, T])
        q = c.sb("q", [P, NG, T])
        k = c.sb("k", [P, NG, T])
        v = c.sb("v", [P, TT, NH, QUAD])
        chunks = c.sb("chunks", [P, TT, D])
        lg, eq, val, sel1, lg2, sel2, t1, t2, any_, keep, coef = (
            c.sb(n, [P, TT, NE1]) for n in ("lg", "eq", "val", "sel1", "lg2", "sel2", "t1", "t2", "any", "keep", "coef"))
        m1, m2, best, w1, w2 = (c.sb(n, [P, TT]) for n in ("m1", "m2", "best", "w1", "w2"))
        moe = c.sb("moe", [P, TT, D])
        gate = c.sb("gate", [P, TT, D])
        xo = c.sb("xo", [P, TT, D])
        sum_t = c.sb("sum_t", [P, DT, NC])
        sum_tok = c.sb("sum_tok", [NC, D])
        q_g = c.sb("q_g", [P, DT, NC])
        k_g = c.sb("k_g", [P, DT, NC])
        v_g = c.sb("v_g", [NC, D])
        k_bd = c.sb("k_bd", [P, DT, NH, NC])
        v_bd = c.sb("v_bd", [P, NH, HD])
        g_max = c.sb("g_max", [NC, NH])
        g_s = c.sb("g_s", [NC, NH, NC])
        g_sum = c.sb("g_sum", [NC, NH])
        g_inv = c.sb("g_inv", [NC, NH])
        g_p = c.sb("g_p", [NC, NH, NC])
        g_pt = c.sb("g_pt", [P, NC])
        g_ctx = c.sb("g_ctx", [P, DT, NC])
        g_out = c.sb("g_out", [NC, D])
        ps = c.psum()
        att = Attention(c, ps, q, k, v, True, neg_ident, apart, apart, ident)

        w_loaded, filled, made, ident_made, neg_made = (c.sem(n) for n in ("w_loaded", "filled", "made", "ident_made", "neg_made"))
        x_loaded, x_free, x_stored, xo_ready = (c.sem(n) for n in ("x_loaded", "x_free", "x_stored", "xo"))
        pe_proj, act_evac, v_done, v_copied = (c.sem(n) for n in ("pe_proj", "act_evac", "v_done", "v_copied"))
        route, any_ready, pos_done, w2_ready, gap_ready, coef_step, coef_ready = (
            c.sem(n) for n in ("route", "any", "pos_done", "w2", "gap", "coef_step", "coef"))
        moe_done, moe_sum, gate_ready = (c.sem(n) for n in ("moe_done", "moe_sum", "gate"))
        c_done, chunks_ready = (c.sem(n) for n in ("c_done", "chunks"))
        sums_done, sums_copied, gproj_done, gproj_copied, kbd_ready, vrep_done, vbd_ready = (
            c.sem(n) for n in ("sums_done", "sums_copied", "gproj_done", "gproj_copied", "kbd", "vrep_done", "vbd"))
        gs_done, gmax_step, gexp_ready, gp_step, gpt_done, gpt_copied, gctx_done, gctx_copied, gout_done, gout_ready = (
            c.sem(n) for n in ("gs_done", "gmax_step", "gexp", "gp_step", "gpt_done", "gpt_copied", "gctx_done",
                               "gctx_copied", "gout_done", "gout"))
        gbc_done, s_step, gpt_begun = c.sem("gbc_done"), c.sem("s_step"), c.sem("gpt_begun")

        EVACS = DT + 2 * NG
        ROUTE = 16
        UNITS = TT * NE1 // 2
        LOADS = 2 * DT + 1 + NG + 4 + DT + DT
        FILLS, WINDOWS = 22, 12

        def all_made(eng):
            eng.wait_ge(w_loaded, LOADS * DMA)
            eng.wait_ge(ident_made, 2)
            eng.wait_ge(neg_made, 2)
            eng.wait_ge(made, WINDOWS)
            eng.wait_ge(filled, FILLS)

        with nc.Block() as block:

            @block.sync
            def _(sp):
                sp.wait_ge(filled, FILLS)
                load_head_columns(sp, wq, w["Wq_l"], w_loaded)
                load_head_columns(sp, wk, w["Wk_l"], w_loaded)
                sp.dma_start(wv[:, :, :], w["Wv_l"].rearrange("(k p) n -> p k n", p=P)).then_inc(w_loaded, DMA)
                load_head_rows(sp, wo, w["Wo_l"], w_loaded)
                for dst, name in ((wq_g, "Wq_g"), (wk_g, "Wk_g"), (wv_g, "Wv_g"), (wo_g, "Wo_g")):
                    sp.dma_start(dst[:, :, :], w[name].rearrange("(k p) n -> p k n", p=P)).then_inc(w_loaded, DMA)
                with nc.allow_non_contiguous_dma(reason="the router's weight transposed, once"):
                    for m in range(DT):
                        sp.dma_start(wr[:, m, :], w["Wr"][:, m * P:(m + 1) * P].rearrange("e p -> p e")).then_inc(w_loaded, DMA)
                for m in range(DT):
                    sp.dma_start(we[:, m], w["We"][:, m * P:(m + 1) * P, :].rearrange("e p n -> p e n")).then_inc(w_loaded, DMA)
                sp.sem_inc(x_free, 1)
                sp.sem_inc(x_stored, DMA)
                with sp.Fori(0, NB) as b:
                    sp.wait_ge(x_free, b + 1)
                    sp.dma_start(x[:, :, :], token_tiles(x_in, b)).then_inc(x_loaded, DMA)
                    sp.wait_ge(xo_ready, b + 1)
                    sp.dma_start(token_tiles(x_out, b), xo[:, :, :]).then_inc(x_stored, DMA)
                sp.wait_ge(x_stored, (NB + 1) * DMA)

            @block.gpsimd
            def _(pool):
                make_identity(pool, ident, ident_made)
                pool.memset(neg_ident[:, :], 0.0).then_inc(neg_made, 1)
                pool.wait_ge(neg_made, 1)
                pool.affine_select(out=neg_ident[:, :], in_=neg_ident[:, :], compare_op=ALU.not_equal, fill=NEG, base=0,
                                   pattern=[[-1, P]], channel_multiplier=1).then_inc(neg_made, 1)
                att.pool_setup(pool)
                pool.wait_ge(filled, FILLS)

                def window(tile, pattern, step, size, n):
                    pool.affine_select(out=tile, in_=tile, compare_op=ALU.is_ge, fill=0.0, base=0,
                                       pattern=pattern, channel_multiplier=step).then_inc(made, 1)
                    pool.wait_ge(made, n + 1)
                    pool.affine_select(out=tile, in_=tile, compare_op=ALU.is_ge, fill=0.0, base=size - 1,
                                       pattern=[[-p, k] for p, k in pattern], channel_multiplier=-step).then_inc(made, 1)
                    pool.wait_ge(made, n + 2)

                window(chunk_mean[:, :, :], [[P, TT], [-LC, NC]], 1, LC, 0)
                window(chunk_of[:, :, :], [[P, TT], [1, P]], -LC, LC, 2)
                window(head_rows[:, :, :, :], [[P, DT], [-HD, NH], [0, NC]], 1, HD, 4)
                window(head_keys[:, :, :], [[-NC, NH], [0, HD]], 1, NC, 6)
                window(key_rows[:, :, :], [[0, NH], [-1, NC]], 1, 1, 8)
                pool.affine_select(out=before[:, :], in_=before[:, :], compare_op=ALU.is_gt, fill=0.0, base=0,
                                   pattern=[[1, P]], channel_multiplier=-1).then_inc(made, 1)
                pool.wait_ge(made, 11)
                pool.iota(order[:, :], [[-1, NE1]], base=NE1, channel_multiplier=0,
                          allow_small_or_imprecise_dtypes=True).then_inc(made, 1)

            @block.scalar
            def _(act):
                ln.act_setup(act)
                all_made(act)
                with act.Fori(0, NB) as b:
                    ln.act(act, b)
                    first = [xn_t[:, m] for m in range(DT)] + [q[:, g] for g in range(NG)] + [k[:, g] for g in range(NG)]
                    for n, dst in enumerate(first):
                        act.wait_ge(pe_proj, b * EVACS + n + 1)
                        if n < DT + NG:
                            act.copy(dst, ps[:, n % 8]).then_inc(act_evac, 1)
                        else:
                            act.activation(dst, ps[:, n % 8], ACT.Identity, bias=k_one[:, 0:1]).then_inc(act_evac, 1)
                    act.wait_ge(gap_ready, b + 1)
                    act.activation(w2[:, :], w2[:, :], ACT.Exp).then_inc(w2_ready, 1)
                    att.act(act, b)
                    act.wait_ge(sums_done, b + 1)
                    act.copy(sum_t[:, :, :], ps[:, 6, 0:DT * NC].rearrange("p (m n) -> p m n", n=NC)).then_inc(sums_copied, 1)
                    act.copy(sum_tok[:, :], ps[0:NC, 7, 0:D]).then_inc(sums_copied, 1)
                    act.wait_ge(gproj_done, b + 1)
                    act.copy(q_g[:, :, :], ps[:, 6, 16:32].rearrange("p (m n) -> p m n", n=NC)).then_inc(gproj_copied, 1)
                    act.copy(k_g[:, :, :], ps[:, 6, 32:48].rearrange("p (m n) -> p m n", n=NC)).then_inc(gproj_copied, 1)
                    act.copy(v_g[:, :], ps[0:NC, 7, D:2 * D]).then_inc(gproj_copied, 1)
                    act.wait_ge(gmax_step, b * 2 + 2)
                    act.activation(g_s[:, :, :], g_s[:, :, :], ACT.Exp, scale=SCALE).then_inc(gexp_ready, 1)
                    act.wait_ge(gpt_done, b + 1)
                    act.copy(g_pt[:, :], ps[:, 6, 200:200 + NC]).then_inc(gpt_copied, 1)
                    act.wait_ge(gctx_done, b + 1)
                    act.copy(g_ctx[:, :, :], ps[:, 6, 208:224].rearrange("p (m n) -> p m n", n=NC)).then_inc(gctx_copied, 1)
                    act.wait_ge(moe_sum, b * TT * NE1 + TT * NE1)
                    act.activation(gate[:, :, :], moe[:, :, :], ACT.Silu).then_inc(gate_ready, 1)

            @block.vector
            def _(dve):
                steps = [0]

                def fill(tile, value):
                    dve.memset(tile, value).then_inc(filled, 1)
                    steps[0] += 1
                    dve.wait_ge(filled, steps[0])

                for tile in (wq[:, :, :, :], wk[:, :, :, :], wo[:, :, :], v[:, :, :, :], k_one[:, :]):
                    fill(tile, 0.0)
                fill(v[:, :, :, HD:HD + 1], 1.0)
                for h in range(GH):
                    fill(k_one[h * QUAD:h * QUAD + 1, :], 1.0)
                fill(apart[:, :], APART)
                for r in range(P // LC):
                    rows = slice(r * LC, (r + 1) * LC)
                    fill(apart[rows, :].rearrange("p (i k) -> p i k", k=P)[:, :, rows], 0.0)
                fill(chunk_mean[:, :, :], 1.0 / LC)
                for tile in (chunk_of[:, :, :], head_rows[:, :, :, :], head_keys[:, :, :], key_rows[:, :, :], before[:, :],
                             ones[:, :]):
                    fill(tile, 1.0)
                fill(any_[:, :, :], 0.0)
                fill(moe[:, :, :], 0.0)
                assert steps[0] == FILLS
                ln.dve_setup(dve)
                att.dve_setup(dve)
                all_made(dve)
                with dve.Fori(0, NB) as b:
                    dve.wait_ge(x_loaded, b * DMA + DMA)
                    ln.dve(dve, b, x)
                    for j in range(2):
                        dve.wait_ge(v_done, b * 3 + j + 1)
                        dve.tensor_copy(v[:, 2 * j:2 * j + 2, :, 0:HD],
                                        ps[:, 2 + j].rearrange("p (i h e) -> p i h e", i=2, h=NH)).then_inc(v_copied, 1)
                    dve.wait_ge(v_done, b * 3 + 3)
                    count = [0]

                    def link(ins):
                        ins.then_inc(route, 1)
                        count[0] += 1
                        dve.wait_ge(route, b * ROUTE + count[0])

                    def wide(column):
                        return column[:, :].unsqueeze(2).broadcast_to([P, TT, NE1])

                    order_b = order[:, :].unsqueeze(1).broadcast_to([P, TT, NE1])
                    link(dve.tensor_copy(lg[:, :, :], ps[:, 4, 0:TT * NE1].rearrange("p (i e) -> p i e", e=NE1)))
                    for logits, top, sel in ((lg, m1, sel1), (lg2, m2, sel2)):
                        link(dve.reduce_max(top[:, :], logits[:, :, :], AX.X))
                        link(dve.tensor_tensor(eq[:, :, :], logits[:, :, :], wide(top), ALU.is_equal))
                        link(dve.tensor_tensor(val[:, :, :], eq[:, :, :], order_b, ALU.mult))
                        link(dve.reduce_max(best[:, :], val[:, :, :], AX.X))
                        link(dve.tensor_tensor(sel[:, :, :], val[:, :, :], wide(best), ALU.is_equal))
                        if sel is sel1:
                            link(dve.scalar_tensor_tensor(lg2[:, :, :], sel1[:, :, :], -3.0e38, lg[:, :, :], ALU.mult, ALU.add))
                    dve.tensor_tensor(any_[:, :, :], sel1[:, :, :], sel2[:, :, :], ALU.add).then_inc(any_ready, 1)
                    dve.tensor_tensor(w2[:, :], m2[:, :], m1[:, :], ALU.subtract).then_inc(gap_ready, 1)
                    dve.wait_ge(w2_ready, b + 1)
                    link(dve.tensor_scalar(w1[:, :], w2[:, :], 1.0, None, ALU.add))
                    link(dve.reciprocal(w1[:, :], w1[:, :]))
                    link(dve.tensor_tensor(w2[:, :], w2[:, :], w1[:, :], ALU.mult))
                    dve.wait_ge(pos_done, b + 1)
                    dve.tensor_scalar(keep[:, :, :], ps[:, 5, 0:TT * NE1].rearrange("p (i e) -> p i e", e=NE1), float(CAP1),
                                      None, ALU.is_lt).then_inc(coef_step, 1)
                    dve.tensor_tensor(t1[:, :, :], sel1[:, :, :], wide(w1), ALU.mult).then_inc(coef_step, 1)
                    dve.tensor_tensor(t2[:, :, :], sel2[:, :, :], wide(w2), ALU.mult).then_inc(coef_step, 1)
                    dve.wait_ge(coef_step, b * 3 + 3)
                    link(dve.tensor_tensor(t1[:, :, :], t1[:, :, :], t2[:, :, :], ALU.add))
                    dve.tensor_tensor(coef[:, :, :], t1[:, :, :], keep[:, :, :], ALU.mult).then_inc(coef_ready, 1)
                    assert count[0] == ROUTE
                    att.dve(dve, b)
                    for j in range(2):
                        dve.wait_ge(c_done, b * 2 + j + 1)
                        dve.tensor_tensor(chunks[:, 2 * j:2 * j + 2, :], xn[:, 2 * j:2 * j + 2, :],
                                          ps[:, j].rearrange("p (i n) -> p i n", n=D), ALU.add).then_inc(chunks_ready, 1)
                    dve.wait_ge(coef_ready, b + 1)

                    def experts(i):
                        for e in range(NE1):
                            n = i * NE1 + e
                            if e % 2 == 0:
                                dve.wait_ge(moe_done, b * UNITS + n // 2 + 1)
                            product = ps[:, 2 + e // 2, e % 2 * D:(e % 2 + 1) * D]
                            if e == 0:
                                dve.tensor_scalar(moe[:, i], product, coef[:, i, e:e + 1], None, ALU.mult).then_inc(moe_sum, 1)
                            else:
                                dve.wait_ge(moe_sum, b * TT * NE1 + n)
                                dve.scalar_tensor_tensor(moe[:, i], product, coef[:, i, e:e + 1], moe[:, i], ALU.mult,
                                                         ALU.add).then_inc(moe_sum, 1)

                    experts(0)
                    dve.wait_ge(gproj_copied, b * 3 + 3)
                    for m in range(DT):
                        dve.tensor_tensor(k_bd[:, m], head_rows[:, m], k_g[:, m].unsqueeze(1).broadcast_to([P, NH, NC]),
                                          ALU.mult).then_inc(kbd_ready, 1)
                    experts(1)
                    dve.wait_ge(vrep_done, b + 1)
                    dve.tensor_tensor(v_bd[:, :, :], head_keys[:, :, :], ps[:, 1, 0:D].rearrange("p (h e) -> p h e", e=HD),
                                      ALU.mult).then_inc(vbd_ready, 1)
                    dve.wait_ge(gs_done, b + 1)
                    scores = ps[0:NC, 6, 64:64 + P].rearrange("p (h k) -> p h k", k=NC)
                    dve.reduce_max(g_max[:, :], scores, AX.X).then_inc(gmax_step, 1)
                    dve.wait_ge(gmax_step, b * 2 + 1)
                    dve.tensor_tensor(g_s[:, :, :], scores, g_max[:, :].unsqueeze(2).broadcast_to([NC, NH, NC]),
                                      ALU.subtract).then_inc(gmax_step, 1)
                    experts(2)
                    dve.wait_ge(gexp_ready, b + 1)
                    dve.reduce_sum(g_sum[:, :], g_s[:, :, :], AX.X).then_inc(gp_step, 1)
                    dve.wait_ge(gp_step, b * 3 + 1)
                    dve.reciprocal(g_inv[:, :], g_sum[:, :]).then_inc(gp_step, 1)
                    dve.wait_ge(gp_step, b * 3 + 2)
                    dve.tensor_tensor(g_p[:, :, :], g_s[:, :, :], g_inv[:, :].unsqueeze(2).broadcast_to([NC, NH, NC]),
                                      ALU.mult).then_inc(gp_step, 1)
                    experts(3)
                    dve.wait_ge(gout_done, b + 1)
                    dve.tensor_tensor(g_out[:, :], ps[0:NC, 7, 0:D], sum_tok[:, :], ALU.add).then_inc(gout_ready, 1)
                    dve.wait_ge(gbc_done, b + 1)
                    dve.tensor_tensor(chunks[:, :, :], chunks[:, :, :], ps[:, 0:2].rearrange("p j (i n) -> p (j i) n", n=D),
                                      ALU.add).then_inc(s_step, 1)
                    dve.wait_ge(s_step, b * 2 + 1)
                    dve.wait_ge(gate_ready, b + 1)
                    dve.wait_ge(x_stored, b * DMA + DMA)
                    dve.tensor_tensor(xo[:, :, :], chunks[:, :, :], gate[:, :, :], ALU.mult).then_inc(s_step, 1)
                    dve.wait_ge(s_step, b * 2 + 2)
                    dve.tensor_tensor(xo[:, :, :], xo[:, :, :], x[:, :, :], ALU.add).then_inc(xo_ready, 1)
                    dve.wait_ge(xo_ready, b + 1)
                    dve.sem_inc(x_free, 1)

            @block.tensor
            def _(pe):
                att.pe_setup(pe)
                all_made(pe)
                with pe.Fori(0, NB) as b:
                    pe.wait_ge(ln.ready, b * TT + TT)
                    for m in range(DT):
                        for i in range(TT):
                            last = pe.transpose(ps[:, m, i * P:(i + 1) * P], xn[:, i, m * P:(m + 1) * P], ident[:, :])
                        last.then_inc(pe_proj, 1)
                    pe.wait_ge(act_evac, b * EVACS + DT)
                    for n in range(DT, EVACS):
                        weight, g = (wq, n - DT) if n < DT + NG else (wk, n - DT - NG)
                        for m in range(DT):
                            last = pe.matmul(ps[:, n % 8], weight[:, m, g * GH:(g + 1) * GH, :].rearrange("p h e -> p (h e)"),
                                             xn_t[:, m], start=(m == 0), stop=(m == DT - 1))
                        last.then_inc(pe_proj, 1)
                    for j in range(2):
                        pe.wait_ge(act_evac, b * EVACS + DT + j + 1)
                        for i in (2 * j, 2 * j + 1):
                            for m in range(DT):
                                last = pe.matmul(ps[:, 2 + j, i % 2 * D:(i % 2 + 1) * D], xn_t[:, m, i * P:(i + 1) * P],
                                                 wv[:, m], start=(m == 0), stop=(m == DT - 1))
                        last.then_inc(v_done, 1)
                    pe.wait_ge(act_evac, b * EVACS + DT + 3)
                    for i in range(TT):
                        for m in range(DT):
                            last = pe.matmul(ps[:, 4, i * NE1:(i + 1) * NE1], xn_t[:, m, i * P:(i + 1) * P], wr[:, m],
                                             start=(m == 0), stop=(m == DT - 1))
                    last.then_inc(v_done, 1)
                    pe.wait_ge(act_evac, b * EVACS + EVACS)
                    pe.wait_ge(any_ready, b + 1)
                    queue = ps[:, 5, 0:TT * NE1]
                    pe.matmul(queue, before[:, :], any_[:, :, :].rearrange("p i e -> p (i e)"), start=True, stop=False)
                    for j in range(1, TT):
                        last = pe.matmul(queue[:, j * NE1:], ones[:, :], any_[:, 0:TT - j, :].rearrange("p i e -> p (i e)"),
                                         start=False, stop=(j == TT - 1))
                    last.then_inc(pos_done, 1)
                    pe.wait_ge(v_copied, b * 2 + 2)
                    pe.wait_ge(coef_ready, b + 1)
                    att.pe(pe, b)
                    pe.wait_ge(att.ctx_ready, b * NG + NG)
                    for j in range(2):
                        for i in (2 * j, 2 * j + 1):
                            for g in range(NG):
                                last = pe.matmul(ps[:, j, i % 2 * D:(i % 2 + 1) * D], att.ctx[:, g, i * P:(i + 1) * P],
                                                 wo[:, g], start=(g == 0), stop=(g == NG - 1))
                        last.then_inc(c_done, 1)

                    def experts(i):
                        for j in range(NE1 // 2):
                            if i >= 1:
                                pe.wait_ge(moe_sum, b * TT * NE1 + (i - 1) * NE1 + 2 * j + 2)
                            for m in range(DT):
                                last = pe.matmul(ps[:, 2 + j], xn_t[:, m, i * P:(i + 1) * P],
                                                 we[:, m, 2 * j:2 * j + 2, :].rearrange("p e n -> p (e n)"),
                                                 start=(m == 0), stop=(m == DT - 1))
                            last.then_inc(moe_done, 1)

                    experts(0)
                    pe.wait_ge(chunks_ready, b * 2 + 2)
                    for m in range(DT):
                        for i in range(TT):
                            pe.matmul(ps[:, 6, m * NC:(m + 1) * NC], chunks[:, i, m * P:(m + 1) * P], chunk_mean[:, i],
                                      start=(i == 0), stop=(i == TT - 1))
                    for i in range(TT):
                        last = pe.matmul(ps[0:NC, 7, 0:D], chunk_mean[:, i], chunks[:, i], start=(i == 0), stop=(i == TT - 1))
                    last.then_inc(sums_done, 1)
                    pe.wait_ge(sums_copied, b * 2 + 2)
                    for first, weight in ((16, wq_g), (32, wk_g)):
                        for n in range(DT):
                            for m in range(DT):
                                pe.matmul(ps[:, 6, first + n * NC:first + (n + 1) * NC], weight[:, m, n * P:(n + 1) * P],
                                          sum_t[:, m], start=(m == 0), stop=(m == DT - 1))
                    for m in range(DT):
                        last = pe.matmul(ps[0:NC, 7, D:2 * D], sum_t[:, m], wv_g[:, m], start=(m == 0), stop=(m == DT - 1))
                    last.then_inc(gproj_done, 1)
                    experts(1)
                    pe.wait_ge(gproj_copied, b * 3 + 3)
                    pe.matmul(ps[:, 1, 0:D], key_rows[:, :, :].rearrange("p h k -> p (h k)"), v_g[:, :], start=True,
                              stop=True).then_inc(vrep_done, 1)
                    pe.wait_ge(kbd_ready, b * DT + DT)
                    for m in range(DT):
                        last = pe.matmul(ps[0:NC, 6, 64:64 + P], q_g[:, m], k_bd[:, m].rearrange("p h k -> p (h k)"),
                                         start=(m == 0), stop=(m == DT - 1))
                    last.then_inc(gs_done, 1)
                    experts(2)
                    pe.wait_ge(gp_step, b * 3 + 3)
                    pe.sem_inc(gpt_begun, 1)
                    pe.transpose(ps[:, 6, 200:200 + NC], g_p[:, :, :].rearrange("p h k -> p (h k)"),
                                 ident[0:NC, 0:NC]).then_inc(gpt_done, 1)
                    pe.wait_ge(gpt_copied, b + 1)
                    pe.wait_ge(vbd_ready, b + 1)
                    for m in range(DT):
                        last = pe.matmul(ps[:, 6, 208 + m * NC:208 + (m + 1) * NC],
                                         v_bd[:, :, :].rearrange("p h e -> p (h e)")[:, m * P:(m + 1) * P], g_pt[:, :],
                                         start=True, stop=True)
                    last.then_inc(gctx_done, 1)
                    experts(3)
                    pe.wait_ge(gctx_copied, b + 1)
                    for m in range(DT):
                        last = pe.matmul(ps[0:NC, 7, 0:D], g_ctx[:, m], wo_g[:, m], start=(m == 0), stop=(m == DT - 1))
                    last.then_inc(gout_done, 1)
                    pe.wait_ge(gout_ready, b + 1)
                    for i in range(TT):
                        last = pe.matmul(ps[:, i // 2, i % 2 * D:(i % 2 + 1) * D], chunk_of[:, i], g_out[:, :], start=True,
                                         stop=True)
                    last.then_inc(gbc_done, 1)




NE2 = 8
V_WIDTH = NH * QUAD


def stage_causal_in(nc, w, x_in, xn_out, q_out, k_out, v_out, probs_out):
    with Chip(nc, "causal_in") as c:
        ident = c.sb("ident", [P, P])
        w_rows = c.sb("w_rows", [P, 3 * DT, D])
        w_qkv = c.sb("w_qkv", [P, DT, 3 * D])
        wg = c.sb("wg", [P, DT, NE2])
        x = c.sb("x", [P, TT, D])
        ln = LayerNorm(c)
        xn = ln.xn
        xn_t = c.sb("xn_t", [P, DT, T])
        v = c.sb("v", [P, TT, NH, QUAD])
        lg, probs = c.sb("lg", [P, TT, NE2]), c.sb("gate_probs", [P, TT, NE2])
        top, total = c.sb("top", [P, TT]), c.sb("total", [P, TT])
        probs_t = c.sb("probs_t", [NE2, T])
        ps = c.psum()
        split = Split(c, q_out, k_out)
        turned = Turned(c, ps, ident, [
            (w_rows[:, n, m * P:(m + 1) * P], w_qkv[:, m, n * P:(n + 1) * P]) for n in range(3 * DT) for m in range(DT)])

        w_loaded, filled, ident_made = (c.sem(n) for n in ("w_loaded", "filled", "ident_made"))
        x_loaded, x_free, xn_stored, v_stored, probs_stored = (
            c.sem(n) for n in ("x_loaded", "x_free", "xn_stored", "v_stored", "probs_stored"))
        xt_done, xt_copied, qk_done, v_done, v_copied, gate_done = (
            c.sem(n) for n in ("xt_done", "xt_copied", "qk_done", "v_done", "v_copied", "gate_done"))
        gate_step, shifted, gate_exp, turn_done, probs_copied = (
            c.sem(n) for n in ("gate_step", "shifted", "gate_exp", "probs_turned", "probs_copied"))
        LOADS, FILLS, GATE = 1 + DT, 2, 4

        with nc.Block() as block:

            @block.sync
            def _(sp):
                sp.dma_start(w_rows[:, :, :], w["w_qkv"].rearrange("(n p) k -> p n k", p=P)).then_inc(w_loaded, DMA)
                with nc.allow_non_contiguous_dma(reason="the gate's weight transposed, once"):
                    for m in range(DT):
                        sp.dma_start(wg[:, m, :], w["gate_w"][:, m * P:(m + 1) * P].rearrange("e p -> p e")).then_inc(w_loaded, DMA)
                sp.sem_inc(x_free, 1)
                for stored in (xn_stored, v_stored, probs_stored):
                    sp.sem_inc(stored, DMA)
                split.sp_setup(sp)
                with sp.Fori(0, NB) as b:
                    sp.wait_ge(x_free, b + 1)
                    sp.dma_start(x[:, :, :], token_tiles(x_in, b)).then_inc(x_loaded, DMA)
                    sp.wait_ge(ln.ready, b * TT + TT)
                    sp.dma_start(token_tiles(xn_out, b), xn[:, :, :]).then_inc(xn_stored, DMA)
                    for n in range(split.TILES):
                        split.sp(sp, b, n)
                    sp.wait_ge(v_copied, b * 2 + 4)
                    sp.dma_start(token_tiles(v_out, b), v[:, :, :, :].rearrange("p i h e -> p i (h e)")).then_inc(v_stored, DMA)
                    sp.wait_ge(probs_copied, b + 2)
                    sp.dma_start(probs_out.rearrange("(b e) t -> b e t", e=NE2)[b], probs_t[:, :]).then_inc(probs_stored, DMA)
                for stored in (xn_stored, v_stored, probs_stored):
                    sp.wait_ge(stored, (NB + 1) * DMA)
                sp.wait_ge(split.stored, (NB + 1) * split.STORES * DMA)

            @block.gpsimd
            def _(pool):
                make_identity(pool, ident, ident_made)
                split.pool_setup(pool)
                with pool.Fori(0, NB) as b:
                    for n in range(split.TILES):
                        split.pool(pool, b, n)

            @block.scalar
            def _(act):
                ln.act_setup(act)
                turned.act(act)
                split.act_setup(act)
                act.sem_inc(probs_copied, 1)
                with act.Fori(0, NB) as b:
                    ln.act(act, b)
                    for m in range(DT):
                        act.wait_ge(xt_done, b * DT + m + 3)
                        act.copy(xn_t[:, m], ps[:, m]).then_inc(xt_copied, 1)
                    for n in range(split.TILES):
                        act.wait_ge(qk_done, b * split.TILES + n + 1)
                        split.act(act, b, n, ps[:, 2 + n])
                    act.wait_ge(shifted, b + 2)
                    act.activation(lg[:, :, :], lg[:, :, :], ACT.Exp).then_inc(gate_exp, 1)
                    act.wait_ge(turn_done, b + 1)
                    act.wait_ge(probs_stored, b * DMA + DMA)
                    act.copy(probs_t[:, :], ps[0:NE2, 1]).then_inc(probs_copied, 1)

            @block.vector
            def _(dve):
                dve.memset(v[:, :, :, :], 0.0).then_inc(filled, 1)
                dve.wait_ge(filled, 1)
                dve.memset(v[:, :, :, HD:HD + 1], 1.0).then_inc(filled, 1)
                dve.wait_ge(filled, 2)
                ln.dve_setup(dve)
                split.dve_setup(dve)
                dve.sem_inc(v_copied, 2)
                dve.sem_inc(shifted, 1)
                with dve.Fori(0, NB) as b:
                    dve.wait_ge(x_loaded, b * DMA + DMA)
                    dve.wait_ge(xn_stored, b * DMA + DMA)
                    dve.wait_ge(xt_done, b * DT + 2)
                    ln.dve(dve, b, x)
                    dve.wait_ge(ln.ready, b * TT + TT)
                    dve.sem_inc(x_free, 1)
                    for n in range(split.TILES):
                        split.dve(dve, b, n)
                    dve.wait_ge(v_stored, b * DMA + DMA)
                    for j in range(2):
                        dve.wait_ge(v_done, b * 2 + j + 1)
                        dve.tensor_copy(v[:, 2 * j:2 * j + 2, :, 0:HD],
                                        ps[:, 6 + j].rearrange("p (i h e) -> p i h e", i=2, h=NH)).then_inc(v_copied, 1)
                    dve.wait_ge(gate_done, b + 1)
                    scores = ps[:, 0, 0:TT * NE2].rearrange("p (i e) -> p i e", e=NE2)

                    def wide(column):
                        return column[:, :].unsqueeze(2).broadcast_to([P, TT, NE2])

                    dve.reduce_max(top[:, :], scores, AX.X).then_inc(gate_step, 1)
                    dve.wait_ge(gate_step, b * GATE + 1)
                    dve.tensor_tensor(lg[:, :, :], scores, wide(top), ALU.subtract).then_inc(shifted, 1)
                    dve.wait_ge(gate_exp, b + 1)
                    dve.reduce_sum(total[:, :], lg[:, :, :], AX.X).then_inc(gate_step, 1)
                    dve.wait_ge(gate_step, b * GATE + 2)
                    dve.reciprocal(total[:, :], total[:, :]).then_inc(gate_step, 1)
                    dve.wait_ge(gate_step, b * GATE + 3)
                    dve.tensor_tensor(probs[:, :, :], lg[:, :, :], wide(total), ALU.mult).then_inc(gate_step, 1)

            @block.tensor
            def _(pe):
                pe.wait_ge(w_loaded, LOADS * DMA)
                pe.wait_ge(ident_made, 2)
                turned.pe(pe)
                pe.sem_inc(xt_done, 2)
                with pe.Fori(0, NB) as b:
                    pe.wait_ge(ln.ready, b * TT + TT)
                    pe.wait_ge(shifted, b + 1)
                    pe.wait_ge(probs_copied, b + 1)
                    for m in range(DT):
                        for i in range(TT):
                            last = pe.transpose(ps[:, m, i * P:(i + 1) * P], xn[:, i, m * P:(m + 1) * P], ident[:, :])
                        last.then_inc(xt_done, 1)
                    pe.wait_ge(xt_copied, b * DT + DT)
                    for n in range(split.TILES):
                        split.bank_free(pe, b, n)
                        for m in range(DT):
                            last = pe.matmul(ps[:, 2 + n], w_qkv[:, m, n * P:(n + 1) * P], xn_t[:, m], start=(m == 0),
                                             stop=(m == DT - 1))
                        last.then_inc(qk_done, 1)
                    for j in range(2):
                        pe.wait_ge(v_copied, b * 2 + j + 1)
                        for i in (2 * j, 2 * j + 1):
                            for m in range(DT):
                                last = pe.matmul(ps[:, 6 + j, i % 2 * D:(i % 2 + 1) * D], xn_t[:, m, i * P:(i + 1) * P],
                                                 w_qkv[:, m, 2 * D:], start=(m == 0), stop=(m == DT - 1))
                        last.then_inc(v_done, 1)
                    for i in range(TT):
                        for m in range(DT):
                            last = pe.matmul(ps[:, 0, i * NE2:(i + 1) * NE2], xn_t[:, m, i * P:(i + 1) * P], wg[:, m],
                                             start=(m == 0), stop=(m == DT - 1))
                    last.then_inc(gate_done, 1)
                    pe.wait_ge(gate_step, b * GATE + GATE)
                    for i in range(TT):
                        last = pe.transpose(ps[0:NE2, 1, i * P:(i + 1) * P], probs[:, i, :], ident[:, :])
                    last.then_inc(turn_done, 1)


CAUSAL = -1.0e4 / SCALE / NEG
ROW_MASK, ROW_SHIFT = KQK, KQK + TT
KA, KB = ROW_SHIFT, ROW_SHIFT + NPART


def stage_causal_attend(nc, w, q_in, k_in, v_in, s_out):
    with Chip(nc, "causal") as c:
        ident = c.sb("ident", [P, P])
        ident_b = c.sb("ident_b", [P, P], BF16)
        neg_ident = c.sb("neg_ident", [P, P], BF16)
        later_keys = c.sb("later_keys", [P, P], BF16)
        earlier_queries = c.sb("earlier_queries", [P, P], BF16)
        wo_cols = c.sb("wo_cols", [P, DT, NH, QUAD])
        wo = c.sb("wo", [P, NG, D])
        den_sel = c.sb("den_sel", [P, P])
        qs = c.sb("qs", [P, NG, GH, T], BF16)
        ks = c.sb("ks", [P, NG, GH, T], BF16)
        v = c.sb("v", [P, NG, TT, GH * QUAD])
        row_max = c.sb("row_max", [P, 2, GH * TT])
        rest = c.sb("rest", [P, 2, GH * TT])
        shift = c.sb("shift", [P, 2, GH * TT, QUAD], BF16)
        probs = c.sb("probs", [P, 2, TT, GH, T])
        o = c.sb("o", [P, T])
        den_inv = c.sb("den_inv", [P, T])
        ctx = c.sb("ctx", [P, NG, T])
        so = c.sb("so", [P, TT, D])
        ps = c.psum()
        turned = Turned(c, ps, ident, [
            (wo_cols[:, n, g * GH:(g + 1) * GH, :].rearrange("p h e -> p (h e)"), wo[:, g, n * P:(n + 1) * P])
            for n in range(DT) for g in range(NG)])

        w_loaded, filled, made, ident_made = (c.sem(n) for n in ("w_loaded", "filled", "made", "ident_made"))
        qk_loaded, v_loaded = ([c.sem(f"{n}_loaded{g}") for g in range(NG)] for n in ("qk", "v"))
        a_done, a_max, shift_step, shift_ready, max_turned, max_copied = (
            c.sem(n) for n in ("a_done", "a_max", "shift_step", "shift_ready", "max_turned", "max_copied"))
        s_done, p_ready, pv_done, o_copied, den_done, den_inv_ready, ctx_ready = (
            c.sem(n) for n in ("s_done", "p_ready", "pv_done", "o_copied", "den_done", "den_inv", "ctx"))
        proj_done, proj_copied, s_stored = c.sem("proj_done"), c.sem("proj_copied"), c.sem("s_stored")

        UA, UB = GH * TT, 2 * TT
        CHAIN = 3
        LOADS = DT
        FILLS, MADE = 8 + 3 * NG, 6 + 3 * NG
        K_LOADS, V_LOADS = 2 * len(STACK), 1

        def all_made(eng):
            eng.wait_ge(w_loaded, LOADS * DMA)
            eng.wait_ge(ident_made, 2)
            eng.wait_ge(made, MADE)
            eng.wait_ge(filled, FILLS)

        def run(eng, step):
            step(0, 0, (0, 2), None, None)
            step(0, 1, (0, 3), (0, 0), None)
            with eng.Fori(0, NB - 1) as b:
                step(b, 2, (b + 1, 0), (b, 1), None)
                step(b, 3, (b + 1, 1), (b, 2), None)
                step(b + 1, 0, (b + 1, 2), (b, 3), b)
                step(b + 1, 1, (b + 1, 3), (b + 1, 0), None)
            step(NB - 1, 2, None, (NB - 1, 1), None)
            step(NB - 1, 3, None, (NB - 1, 2), None)
            step(None, None, None, (NB - 1, 3), NB - 1)

        with nc.Block() as block:

            @block.sync
            def _(sp):
                sp.wait_ge(filled, FILLS)
                load_head_columns(sp, wo_cols, w["w_out"], w_loaded, 0)

                def load_qk(b, g):
                    load_stack(sp, qs[:, g], q_in, b, g, False, qk_loaded[g])
                    load_stack(sp, ks[:, g], k_in, b, g, True, qk_loaded[g])

                def load_v(b, g):
                    sp.dma_start(v[:, g], token_tiles(v_in, b)[:, :, g * GH * QUAD:(g + 1) * GH * QUAD]).then_inc(v_loaded[g], DMA)

                sp.wait_ge(made, MADE)
                for g in range(NG):
                    load_qk(0, g)
                    load_v(0, g)
                with sp.Fori(0, NB - 1) as b:
                    for g in range(NG):
                        sp.wait_ge(s_done, b * NG * UB + (g + 1) * UB)
                        load_qk(b + 1, g)
                        sp.wait_ge(pv_done, b * NG * TT + (g + 1) * TT + 2 * TT)
                        load_v(b + 1, g)

            @block.gpsimd
            def _(pool):
                make_identity(pool, ident, ident_made)
                pool.wait_ge(filled, FILLS)
                count = [0]

                def select(tile, compare, fill, base, pattern, per_row):
                    pool.affine_select(out=tile, in_=tile, compare_op=compare, fill=fill, base=base, pattern=pattern,
                                       channel_multiplier=per_row).then_inc(made, 1)
                    count[0] += 1
                    pool.wait_ge(made, count[0])

                select(ident_b[:, :], ALU.not_equal, 1.0, 0, [[-1, P]], 1)
                select(neg_ident[:, :], ALU.not_equal, NEG, 0, [[-1, P]], 1)
                select(later_keys[:, :], ALU.is_gt, 0.0, 0, [[1, P]], -1)
                select(earlier_queries[:, :], ALU.is_gt, 0.0, 0, [[-1, P]], 1)
                select(den_sel[:, :], ALU.not_equal, 1.0, -HD, [[-QUAD, GH], [0, QUAD]], 1)
                for g in range(NG):
                    select(qs[ROW_MASK:ROW_MASK + TT, g], ALU.is_gt, 0.0, 0, [[0, GH], [-1, T]], P)
                    select(ks[ROW_MASK:ROW_MASK + TT, g], ALU.is_ge, 0.0, 0, [[0, GH], [1, T]], -P)
                    select(ks[ROW_MASK:ROW_MASK + TT, g], ALU.is_ge, 0.0, P - 1, [[0, GH], [-1, T]], P)
                select(shift[:, :, :, 0:TT].rearrange("p a (h i) j -> p (a h) i j", i=TT), ALU.is_gt, 0.0, 0,
                       [[0, 2 * GH], [-1, TT], [1, TT]], 0)
                assert count[0] == MADE

            @block.scalar
            def _(act):
                all_made(act)
                turned.act(act)
                act.sem_inc(max_copied, GH)
                act.sem_inc(p_ready, 2)
                act.sem_inc(proj_copied, 2)
                act.sem_inc(s_stored, DMA)

                def exp(b, g, kt):
                    for pair in range(2):
                        n = g * UB + kt * 2 + pair
                        act.wait_ge(s_done, b * NG * UB + n + 1)
                        if pair == 0:
                            act.wait_ge(pv_done, b * NG * TT + g * TT + kt + 1)
                        act.activation(probs[:, g % 2, kt, 2 * pair:2 * pair + 2], ps[:, 2 + n % 2 * 2:4 + n % 2 * 2], ACT.Exp,
                                       scale=SCALE).then_inc(p_ready, 1)

                def shifts(b, g, heads):
                    act.wait_ge(max_turned, b * NG + g + 3)
                    for h in heads:
                        act.copy(qs[ROW_MASK:KB, g, h], ps[h * QUAD:h * QUAD + KB - ROW_MASK, 7]).then_inc(max_copied, 1)

                def output(b, g):
                    act.wait_ge(pv_done, b * NG * TT + (g + 1) * TT + 2 * TT)
                    act.wait_ge(ctx_ready, b * NG + g + 1)
                    act.copy(o[:, :], ps[:, 6]).then_inc(o_copied, 1)

                def finish(b):
                    act.wait_ge(s_stored, b * DMA + DMA)
                    for j in (1, 0):
                        act.wait_ge(proj_done, b * 2 + 2 - j)
                        act.copy(so[:, 2 * j:2 * j + 2, :], ps[:, 6 + j].rearrange("p (i n) -> p i n", n=D)).then_inc(proj_copied, 1)
                    act.wait_ge(proj_copied, b * 2 + 4)
                    act.dma_start(token_tiles(s_out, b), so[:, :, :]).then_inc(s_stored, DMA)

                def step(b, g, first, before, done):
                    for kt in range(TT):
                        if g is not None:
                            exp(b, g, kt)
                        if kt == 1 and before is not None:
                            output(*before)
                        if kt in (1, 2) and g is not None and not (g == NG - 1 and first is None):
                            nxt = (b, g + 1) if g + 1 < NG else (b + 1, 0)
                            shifts(*nxt, range(2 * kt - 2, 2 * kt))
                    if done is not None:
                        finish(done)

                shifts(0, 0, range(GH))
                run(act, step)
                act.wait_ge(s_stored, (NB + 1) * DMA)

            @block.vector
            def _(dve):
                count = [0]

                def fill(tile, value):
                    dve.memset(tile, value).then_inc(filled, 1)
                    count[0] += 1
                    dve.wait_ge(filled, count[0])

                for tile in (ident_b[:, :], neg_ident[:, :], den_sel[:, :], wo_cols[:, :, :, :], shift[:, :, :, :]):
                    fill(tile, 0.0)
                fill(later_keys[:, :], CAUSAL)
                fill(earlier_queries[:, :], CAUSAL)
                fill(shift[:, :, :, 0:TT], NEG)
                for g in range(NG):
                    fill(qs[ROW_MASK:ROW_MASK + TT, g], NEG)
                    fill(ks[ROW_MASK:KB, g], 1.0)
                    fill(ks[ROW_MASK:ROW_MASK + TT, g], CAUSAL)
                assert count[0] == FILLS
                all_made(dve)
                dve.sem_inc(a_max, 2)
                dve.sem_inc(den_inv_ready, 1)
                dve.sem_inc(ctx_ready, 1)

                def maxima(b, g, units):
                    for u in units:
                        dve.wait_ge(a_done, b * NG * UA + g * UA + u + 1)
                        dve.reduce_max(row_max[:, g % 2, u:u + 1], ps[:, u % 2], AX.X).then_inc(a_max, 1)

                def split_maxima(b, g):
                    n = b * NG + g
                    dve.wait_ge(a_max, b * NG * UA + (g + 1) * UA + 2)
                    dve.wait_ge(max_turned, n + 1)
                    part = [shift[:, g % 2, :, TT + k] for k in range(NPART)]
                    dve.tensor_scalar(part[0], row_max[:, g % 2], -1.0, None, ALU.mult).then_inc(shift_step, 1)
                    dve.wait_ge(shift_step, n * CHAIN + 1)
                    dve.scalar_tensor_tensor(rest[:, g % 2], row_max[:, g % 2], -1.0, part[0], ALU.mult,
                                             ALU.subtract).then_inc(shift_step, 1)
                    dve.wait_ge(shift_step, n * CHAIN + 2)
                    dve.tensor_copy(part[1], rest[:, g % 2]).then_inc(shift_step, 1)
                    dve.wait_ge(shift_step, n * CHAIN + 3)
                    dve.tensor_tensor(part[2], rest[:, g % 2], part[1], ALU.subtract).then_inc(shift_ready, 1)

                def context(b, g):
                    n = b * NG + g
                    dve.wait_ge(den_done, n + 1)
                    dve.reciprocal(den_inv[:, :], ps[:, 6]).then_inc(den_inv_ready, 1)
                    dve.wait_ge(den_inv_ready, n + 2)
                    if g == 0 and not isinstance(b, int):
                        dve.wait_ge(proj_done, b * 2)
                    dve.tensor_tensor(ctx[:, g], o[:, :], den_inv[:, :], ALU.mult).then_inc(ctx_ready, 1)

                def step(b, g, first, before, done):
                    if first is not None:
                        maxima(*first, range(0, 12))
                    if before is not None:
                        context(*before)
                    if first is not None:
                        maxima(*first, range(12, UA))
                        split_maxima(*first)

                for g in range(2):
                    maxima(0, g, range(UA))
                    split_maxima(0, g)
                run(dve, step)

            @block.tensor
            def _(pe):
                all_made(pe)
                turned.pe(pe)
                pe.sem_inc(pv_done, 2 * TT)
                pe.sem_inc(max_turned, 2)

                def first_scores(b, g, units):
                    for u in units:
                        h, i = divmod(u, TT)
                        if u == 0:
                            pe.wait_ge(qk_loaded[g], (b + 1) * K_LOADS * DMA)
                        pe.wait_ge(a_max, b * NG * UA + g * UA + u + 1)
                        pe.matmul(ps[:, u % 2], qs[0:KA, g, h, i * P:(i + 1) * P], ks[0:KA, g, h, :], start=True, stop=False)
                        pe.matmul(ps[:, u % 2, i * P:(i + 1) * P], neg_ident[:, :], later_keys[:, :], start=False,
                                  stop=True).then_inc(a_done, 1)

                def turn_maxima(b, g):
                    pe.wait_ge(shift_ready, b * NG + g + 1)
                    pe.wait_ge(max_copied, (b * NG + g) * GH + GH)
                    for h in range(GH):
                        for i in range(TT):
                            last = pe.matmul(ps[h * QUAD:(h + 1) * QUAD, 7, i * P:(i + 1) * P], shift[:, g % 2, h * TT + i, :],
                                             ident_b[:, :], start=True, stop=True)
                    last.then_inc(max_turned, 1)

                def second_scores(b, g, kt):
                    if kt == 0:
                        pe.wait_ge(max_copied, (b * NG + g) * GH + 2 * GH)
                    for pair in range(2):
                        n = g * UB + kt * 2 + pair
                        pe.wait_ge(p_ready, b * NG * UB + n + 1)
                        for j in range(2):
                            bank = ps[:, 2 + n % 2 * 2 + j]
                            h = 2 * pair + j
                            pe.matmul(bank, ks[0:KB, g, h, kt * P:(kt + 1) * P], qs[0:KB, g, h, :], start=True, stop=False)
                            last = pe.matmul(bank[:, kt * P:(kt + 1) * P], neg_ident[:, :], earlier_queries[:, :], start=False,
                                             stop=True)
                        last.then_inc(s_done, 1)

                def output(b, g, kt):
                    if kt == 0:
                        pe.wait_ge(v_loaded[g], (b + 1) * V_LOADS * DMA)
                        pe.wait_ge(den_inv_ready, b * NG + g + 1)
                        pe.wait_ge(proj_copied, b * 2 + 2)
                    pe.wait_ge(p_ready, b * NG * UB + g * UB + 2 * kt + 4)
                    for h in range(GH):
                        last = pe.matmul(ps[h * QUAD:(h + 1) * QUAD, 6], v[:, g, kt, h * QUAD:(h + 1) * QUAD],
                                         probs[:, g % 2, kt, h], start=(kt == 0), stop=(kt == TT - 1))
                    last.then_inc(pv_done, 1)

                def denominators(b, g):
                    pe.wait_ge(o_copied, b * NG + g + 1)
                    pe.matmul(ps[:, 6], den_sel[:, :], o[:, :], start=True, stop=True).then_inc(den_done, 1)

                def project(b):
                    pe.wait_ge(ctx_ready, b * NG + NG + 1)
                    for j in (1, 0):
                        for i in (2 * j, 2 * j + 1):
                            for g in range(NG):
                                last = pe.matmul(ps[:, 6 + j, i % 2 * D:(i % 2 + 1) * D], ctx[:, g, i * P:(i + 1) * P], wo[:, g],
                                                 start=(g == 0), stop=(g == NG - 1))
                        last.then_inc(proj_done, 1)

                def step(b, g, first, before, done):
                    for kt in range(TT):
                        if g is not None:
                            second_scores(b, g, kt)
                        if before is not None and kt < 2:
                            output(*before, 2 * kt)
                            output(*before, 2 * kt + 1)
                        if first is not None:
                            first_scores(*first, range(kt * TT, (kt + 1) * TT))
                        if before is not None and kt == 2:
                            denominators(*before)
                    if done is not None:
                        if g is not None:
                            pe.wait_ge(max_copied, done * NG * GH + (NG + 2) * GH + GH)
                        project(done)
                    if first is not None:
                        if done is not None:
                            pe.wait_ge(proj_copied, done * 2 + 3)
                        turn_maxima(*first)

                for g in range(2):
                    first_scores(0, g, range(UA))
                    turn_maxima(0, g)
                run(pe, step)


F2 = 1024
FT2 = F2 // P
TOP2 = int(2.0 * T / NE2)
ROUNDS = TOP2 // 8
assert TOP2 == P


def stage_experts(nc, w, x_in, xn_in, s_in, probs_in, x_out):
    with Chip(nc, "experts") as c:
        ident = c.sb("ident", [P, P])
        token = c.sb("token", [P, TT])
        tokens = c.sb("tokens", [P, T])
        work = c.sb("work", [NB * NE2, T])
        best = c.sb("best", [NB * NE2, TOP2])
        place = c.sb("place", [NB * NE2, TOP2], mybir.dt.uint32)
        place_f = c.sb("place_f", [NB * NE2, TOP2])
        prob_t = c.sb("prob_t", [P, NB * NE2])
        place_t = c.sb("place_t", [P, NB * NE2])
        place_all = c.sb("place_all", [P, 2, NE2 * TOP2])
        xn = c.sb("xn", [P, 2, TT, D])
        x = c.sb("x", [P, 2, TT, D])
        out = c.sb("out", [P, 2, TT, D])
        picks = c.sb("picks", [P, 2, NE2 * T])
        slots = c.sb("slots", [P, NE2, NB, D])
        w1 = c.sb("w1", [P, 2, DT, F2])
        w2 = c.sb("w2", [P, 2, FT2, D])
        hidden = c.sb("hidden", [P, 2, FT2, 4 * TOP2])
        place_dram = nc.dram_tensor("experts_place_rows", (NB, NE2 * TOP2), F32, kind="Internal").ap()
        ps = c.psum()

        ident_made, made, probs_loaded, top_step, found, place_stored = (
            c.sem(n) for n in ("ident_made", "made", "probs_loaded", "top_step", "found", "place_stored"))
        turn_done, turn_copied = c.sem("turn_done"), c.sem("turn_copied")
        in_loaded, s_loaded, w_loaded, stored = ([c.sem(f"{n}{r}") for r in range(2)] for n in (
            "in_loaded", "s_loaded", "w_loaded", "stored"))
        gather_ready, gather_done, gather_copied, copy_begun = (
            c.sem(n) for n in ("gather_ready", "gather_done", "gather_copied", "copy_begun"))
        h_done, h_ready, o_done, o_copied, o_begun = (c.sem(n) for n in ("h_done", "h_ready", "o_done", "o_copied", "o_begun"))
        scatter_ready, scatter_begun, scatter_done, gate_ready, gated, added = (
            c.sem(n) for n in ("scatter_ready", "scatter_begun", "scatter_done", "gate_ready", "gated", "added"))

        GATHERS = 2 * DT
        HALF = NE2 // 2
        UNITS = 4

        with nc.Block() as block:

            @block.sync
            def _(sp):
                def weights(r, e):
                    sp.dma_start(w1[:, r], w["w1"][e].rearrange("(k p) f -> p k f", p=P)).then_inc(w_loaded[r], DMA)
                    sp.dma_start(w2[:, r], w["w2"][e].rearrange("(k p) d -> p k d", p=P)).then_inc(w_loaded[r], DMA)

                sp.dma_start(work[:, :], probs_in).then_inc(probs_loaded, DMA)
                for r in range(2):
                    weights(r, r)
                sp.wait_ge(found, 1)
                sp.dma_start(place_dram.rearrange("b (e j) -> (b e) j", e=NE2), place_f[:, :]).then_inc(place_stored, DMA)
                sp.wait_ge(place_stored, DMA)
                with sp.Fori(0, NB // 2) as i:
                    for r in range(2):
                        sp.wait_ge(gather_done, (i * 2 + r) * GATHERS + GATHERS)
                        sp.dma_start(xn[:, r], token_tiles(xn_in, i * 2 + r)).then_inc(in_loaded[r], DMA)
                        sp.dma_start(place_all[:, r], place_dram[i * 2 + r].partition_broadcast(P)).then_inc(in_loaded[r], DMA)
                with sp.Fori(0, NE2 // 2 - 1) as i:
                    for r in range(2):
                        sp.wait_ge(o_done, i * 2 * UNITS + 8 + 4 * r)
                        weights(r, i * 2 + 2 + r)
                with sp.Fori(0, NB // 2) as i:
                    for r in range(2):
                        sp.wait_ge(added, (i * 2 + r) * 2 + 2)
                        sp.dma_start(xn[:, r], token_tiles(s_in, i * 2 + r)).then_inc(s_loaded[r], DMA)
                        sp.dma_start(x[:, r], token_tiles(x_in, i * 2 + r)).then_inc(s_loaded[r], DMA)
                    for r in range(2):
                        sp.wait_ge(added, (i * 2 + r) * 2 + 6)
                        sp.dma_start(token_tiles(x_out, i * 2 + r), out[:, r]).then_inc(stored[r], DMA)
                for r in range(2):
                    sp.wait_ge(stored[r], (NB // 2 + 1) * DMA)

            @block.gpsimd
            def _(pool):
                make_identity(pool, ident, ident_made)
                pool.iota(token[:, :], [[P, TT]], base=0, channel_multiplier=1,
                          allow_small_or_imprecise_dtypes=True).then_inc(made, 1)
                pool.iota(tokens[:, :], [[1, T]], base=0, channel_multiplier=0,
                          allow_small_or_imprecise_dtypes=True).then_inc(made, 1)
                pool.sem_inc(added, 4)
                with pool.Fori(0, NB // 2) as i:
                    for r in range(2):
                        for j in range(2):
                            tiles = slice(2 * j, 2 * j + 2)
                            if j == 0:
                                pool.wait_ge(s_loaded[r], i * 2 * DMA + 2 * DMA)
                            pool.wait_ge(gate_ready, (i * 2 + r) * 2 + j + 5)
                            pool.tensor_tensor(out[:, r, tiles], out[:, r, tiles], xn[:, r, tiles], ALU.mult).then_inc(gated, 1)
                        for j in range(2):
                            tiles = slice(2 * j, 2 * j + 2)
                            pool.wait_ge(gated, (i * 2 + r) * 2 + j + 1)
                            pool.tensor_tensor(out[:, r, tiles], out[:, r, tiles], x[:, r, tiles], ALU.add).then_inc(added, 1)

            @block.scalar
            def _(act):
                act.wait_ge(turn_done, 2)
                act.copy(prob_t[:, :], ps[:, 0, 0:NB * NE2]).then_inc(turn_copied, 1)
                act.copy(place_t[:, :], ps[:, 1, 0:NB * NE2]).then_inc(turn_copied, 1)
                act.wait_ge(turn_copied, 2)
                act.sem_inc(gather_copied, 2 * GATHERS)
                with act.Fori(0, NB // 2) as i:
                    for r in range(2):
                        for n in range(GATHERS):
                            m, half = divmod(n, 2)
                            act.wait_ge(gather_done, (i * 2 + r) * GATHERS + n + 1 + 2 * GATHERS)
                            act.sem_inc(copy_begun, 1)
                            act.copy(slots[:, half * HALF:(half + 1) * HALF, i * 2 + r, m * P:(m + 1) * P],
                                     ps[:, r * GATHERS + n].rearrange("p (e j) -> p e j", e=HALF)).then_inc(gather_copied, 1)
                act.sem_inc(h_ready, 4)
                with act.Fori(0, NE2 // 2) as i:
                    for u in range(UNITS):
                        for f in range(FT2):
                            n = u * FT2 + f
                            act.wait_ge(h_done, i * UNITS * FT2 + n + 1)
                            if f == 0:
                                act.wait_ge(o_done, i * UNITS * 2 + 2 * u + 2)
                            act.activation(hidden[:, u % 2, f], ps[:, n % 4], ACT.Gelu).then_inc(h_ready, 1)
                act.sem_inc(gate_ready, 4)
                for r in range(2):
                    act.sem_inc(stored[r], DMA)
                with act.Fori(0, NB // 2) as i:
                    for r in range(2):
                        act.wait_ge(stored[r], i * DMA + DMA)
                        for j in range(2):
                            act.wait_ge(scatter_done, (i * 2 + r) * 2 + j + 5)
                            act.activation(out[:, r, 2 * j:2 * j + 2], ps[:, r * 2 + j].rearrange("p (i d) -> p i d", d=D),
                                           ACT.Silu).then_inc(gate_ready, 1)

            @block.vector
            def _(dve):
                dve.wait_ge(probs_loaded, DMA)
                for k in range(ROUNDS):
                    eight = slice(8 * k, 8 * k + 8)
                    if k >= 1:
                        dve.wait_ge(top_step, 3 * k)
                    dve.max(best[:, eight], work[:, :]).then_inc(top_step, 1)
                    dve.wait_ge(top_step, 3 * k + 1)
                    dve.max_index(place[:, eight], best[:, eight], work[:, :]).then_inc(top_step, 1)
                    dve.wait_ge(top_step, 3 * k + 2)
                    dve.match_replace(work[:, :], best[:, eight], work[:, :], -1.0).then_inc(top_step, 1)
                dve.wait_ge(top_step, 3 * ROUNDS)
                dve.tensor_copy(place_f[:, :], place[:, :]).then_inc(found, 1)
                dve.wait_ge(made, 2)
                with dve.Fori(0, NB // 2) as i:
                    for r in range(2):
                        dve.wait_ge(in_loaded[r], i * 2 * DMA + 2 * DMA)
                        dve.wait_ge(gather_done, (i * 2 + r) * GATHERS + GATHERS)
                        for t in range(TT):
                            dve.tensor_scalar(picks[:, r, t * NE2 * TOP2:(t + 1) * NE2 * TOP2], place_all[:, r],
                                              token[:, t:t + 1], None, ALU.is_equal).then_inc(gather_ready, 1)
                dve.sem_inc(o_copied, 4)
                with dve.Fori(0, NE2 // 2) as i:
                    for u in range(UNITS):
                        for j in range(2):
                            n = u * 2 + j
                            dve.wait_ge(o_done, i * UNITS * 2 + n + 5)
                            dve.sem_inc(o_begun, 1)
                            dve.tensor_copy(slots[:, i * 2 + u // 2, u % 2 * 4 + j * 2:u % 2 * 4 + j * 2 + 2, :],
                                            ps[:, 4 + n % 4].rearrange("p (b d) -> p b d", d=D)).then_inc(o_copied, 1)
                with dve.Fori(0, NB // 2) as i:
                    for r in range(2):
                        dve.wait_ge(scatter_done, (i * 2 + r) * 2 + 2)
                        dve.sem_inc(scatter_begun, 1)
                        for e in range(NE2):
                            col = (i * 2 + r) * NE2 + e
                            dve.tensor_scalar(picks[:, r, e * T:(e + 1) * T], tokens[:, :], place_t[:, bass.ds(col, 1)],
                                              prob_t[:, bass.ds(col, 1)], ALU.is_equal, ALU.mult).then_inc(scatter_ready, 1)

            @block.tensor
            def _(pe):
                pe.wait_ge(ident_made, 2)
                pe.wait_ge(found, 1)
                pe.transpose(ps[:, 0, 0:NB * NE2], best[:, :], ident[0:NB * NE2, 0:NB * NE2]).then_inc(turn_done, 1)
                pe.transpose(ps[:, 1, 0:NB * NE2], place_f[:, :], ident[0:NB * NE2, 0:NB * NE2]).then_inc(turn_done, 1)
                pe.sem_inc(gather_done, 2 * GATHERS)
                with pe.Fori(0, NB // 2) as i:
                    for r in range(2):
                        pe.wait_ge(gather_ready, (i * 2 + r) * TT + TT)
                        for n in range(GATHERS):
                            m, half = divmod(n, 2)
                            pe.wait_ge(gather_copied, (i * 2 + r) * GATHERS + n + 1)
                            for t in range(TT):
                                first = t * NE2 * TOP2 + half * HALF * TOP2
                                last = pe.matmul(ps[:, r * GATHERS + n], xn[:, r, t, m * P:(m + 1) * P],
                                                 picks[:, r, first:first + HALF * TOP2], start=(t == 0), stop=(t == TT - 1))
                            last.then_inc(gather_done, 1)
                pe.wait_ge(gather_copied, (NB + 2) * GATHERS)
                pe.sem_inc(o_done, 4)
                with pe.Fori(0, NE2 // 2) as i:

                    def first_product(u):
                        r, half = divmod(u, 2)
                        if half == 0:
                            pe.wait_ge(w_loaded[r], i * 2 * DMA + 2 * DMA)
                        for f in range(FT2):
                            n = u * FT2 + f
                            pe.wait_ge(h_ready, i * UNITS * FT2 + n + 1)
                            for m in range(DT):
                                last = pe.matmul(ps[:, n % 4], w1[:, r, m, f * P:(f + 1) * P],
                                                 slots[:, i * 2 + r, half * 4:half * 4 + 4, m * P:(m + 1) * P],
                                                 start=(m == 0), stop=(m == DT - 1))
                            last.then_inc(h_done, 1)

                    def second_product(u):
                        r = u // 2
                        pe.wait_ge(h_ready, i * UNITS * FT2 + (u + 1) * FT2 + 4)
                        for j in range(2):
                            n = u * 2 + j
                            pe.wait_ge(o_copied, i * UNITS * 2 + n + 1)
                            for b in range(2):
                                for f in range(FT2):
                                    last = pe.matmul(ps[:, 4 + n % 4, b * D:(b + 1) * D],
                                                     hidden[:, u % 2, f, (2 * j + b) * TOP2:(2 * j + b + 1) * TOP2], w2[:, r, f],
                                                     start=(f == 0), stop=(f == FT2 - 1))
                            last.then_inc(o_done, 1)

                    first_product(0)
                    for u in range(UNITS):
                        if u + 1 < UNITS:
                            first_product(u + 1)
                        second_product(u)
                pe.wait_ge(o_copied, NE2 * 4 + 4)
                pe.sem_inc(scatter_done, 4)
                with pe.Fori(0, NB // 2) as i:
                    for r in range(2):
                        pe.wait_ge(scatter_ready, (i * 2 + r) * NE2 + NE2)
                        for j in range(2):
                            pe.wait_ge(gate_ready, (i * 2 + r) * 2 + j + 1)
                            for t in (2 * j, 2 * j + 1):
                                for e in range(NE2):
                                    last = pe.matmul(ps[:, r * 2 + j, t % 2 * D:(t % 2 + 1) * D],
                                                     picks[:, r, e * T + t * P:e * T + (t + 1) * P], slots[:, e, i * 2 + r, :],
                                                     start=(e == 0), stop=(e == NE2 - 1))
                            last.then_inc(scatter_done, 1)


KD = KQK + 2 * NPART


def norms_tensor(nc, name):
    return nc.dram_tensor(name, (NB, NPART, NH * T), BF16, kind="Internal").ap()


def stage_distance_in(nc, w, x_in, q_out, k_out, q2_out, k2_out, v_out, gate_out):
    with Chip(nc, "distance_in") as c:
        ident = c.sb("ident", [P, P])
        NAMES = ("wq", "wk", "wv", "W_r", "W_k", "W_v")
        Q, K, V, MIX_R, MIX_K, MIX_V = range(len(NAMES))
        w_rows = c.sb("w_rows", [P, len(NAMES), DT, D])
        w_t = c.sb("w_t", [P, len(NAMES), DT, D])
        bias = c.sb("bias", [P, 2, DT])
        bv = c.sb("bv", [P, D])
        mu = c.sb("mu", [P, 2, DT])
        mu_not = c.sb("mu_not", [P, 2, DT])
        head_of = c.sb("head_of", [P, DT, NH])
        x = c.sb("x", [P, TT, D])
        ln = LayerNorm(c)
        xn = ln.xn
        xn_t = c.sb("xn_t", [P, DT, 1 + T])
        squares = c.sb("squares", [P, 2 * DT, T])
        norm = c.sb("norm", [NH, 2, T])
        norm_rest = c.sb("norm_rest", [NH, 2, T])
        norm_parts = c.sb("norm_parts", [NH, 2, NPART, T], BF16)
        v = c.sb("v", [P, TT, NH, QUAD])
        mixed = c.sb("mixed", [P, 2, DT, T])
        act_k = c.sb("act_k", [P, DT, T])
        r = c.sb("r", [P, TT, D])
        ffn = c.sb("ffn", [P, TT, D])
        gate = c.sb("gate", [P, TT, D])
        ps = c.psum()
        split = Split(c, q_out, k_out)
        turned = Turned(c, ps, ident, [
            (w_rows[:, a, n, m * P:(m + 1) * P], w_t[:, a, m, n * P:(n + 1) * P])
            for a in range(len(NAMES)) for n in range(DT) for m in range(DT)])

        w_loaded, filled, made, ident_made = (c.sem(n) for n in ("w_loaded", "filled", "made", "ident_made"))
        x_loaded, x_free, v_stored, norm_stored, gate_stored = (
            c.sem(n) for n in ("x_loaded", "x_free", "v_stored", "norm_stored", "gate_stored"))
        xt_done, xt_copied, qk_done, v_done, v_copied = (
            c.sem(n) for n in ("xt_done", "xt_copied", "qk_done", "v_done", "v_copied"))
        squared, norm_done, norm_copied, norm_step, norm_ready = (
            c.sem(n) for n in ("squared", "norm_done", "norm_copied", "norm_step", "norm_ready"))
        mix_half, mixed_ready, mix_k_done, relu_ready, act_k_ready, mix_r_done, r_ready, mix_v_done, ffn_ready, sig_ready, gate_ready = (
            c.sem(n) for n in ("mix_half", "mixed", "mix_k_done", "relu", "act_k", "mix_r_done", "r", "mix_v_done", "ffn", "sig", "gate"))
        LOADS = len(NAMES) + 5
        FILLS, MADE = 6, 2

        def all_made(eng):
            eng.wait_ge(w_loaded, LOADS * DMA)
            eng.wait_ge(ident_made, 2)
            eng.wait_ge(made, MADE)
            eng.wait_ge(filled, FILLS)

        with nc.Block() as block:

            @block.sync
            def _(sp):
                for a, name in enumerate(NAMES):
                    sp.dma_start(w_rows[:, a], w[name].rearrange("(n p) k -> p n k", p=P)).then_inc(w_loaded, DMA)
                with nc.allow_non_contiguous_dma(reason="short vectors, once"):
                    for a, name in enumerate(("bq", "bk")):
                        sp.dma_start(bias[:, a], column(w[name], DT)).then_inc(w_loaded, DMA)
                    for a, name in enumerate(("mu_r", "mu_k")):
                        sp.dma_start(mu[:, a], column(w[name], DT)).then_inc(w_loaded, DMA)
                sp.dma_start(bv[:, :], w["bv"].partition_broadcast(P)).then_inc(w_loaded, DMA)
                sp.sem_inc(x_free, 1)
                for stored in (v_stored, gate_stored):
                    sp.sem_inc(stored, DMA)
                sp.sem_inc(norm_stored, 2 * DMA)
                split.sp_setup(sp)
                with sp.Fori(0, NB) as b:
                    sp.wait_ge(x_free, b + 1)
                    sp.dma_start(x[:, :, :], token_tiles(x_in, b)).then_inc(x_loaded, DMA)
                    for n in range(split.TILES):
                        split.sp(sp, b, n)
                    sp.wait_ge(v_copied, b * 2 + 4)
                    sp.dma_start(token_tiles(v_out, b), v[:, :, :, :].rearrange("p i h e -> p i (h e)")).then_inc(v_stored, DMA)
                    for side, to in enumerate((q2_out, k2_out)):
                        sp.wait_ge(norm_ready, b * 2 + side + 1)
                        sp.dma_start(to[b].rearrange("a (h t) -> h a t", h=NH), norm_parts[:, side]).then_inc(norm_stored, DMA)
                    sp.wait_ge(gate_ready, b + 1)
                    sp.dma_start(token_tiles(gate_out, b), gate[:, :, :]).then_inc(gate_stored, DMA)
                for stored, per_batch in ((v_stored, 1), (gate_stored, 1), (norm_stored, 2)):
                    sp.wait_ge(stored, (NB + 1) * per_batch * DMA)
                sp.wait_ge(split.stored, (NB + 1) * split.STORES * DMA)

            @block.gpsimd
            def _(pool):
                make_identity(pool, ident, ident_made)
                pool.wait_ge(filled, FILLS - 2)
                pool.affine_select(out=head_of[:, :, :], in_=head_of[:, :, :], compare_op=ALU.is_ge, fill=0.0, base=0,
                                   pattern=[[P, DT], [-HD, NH]], channel_multiplier=1).then_inc(made, 1)
                pool.wait_ge(made, 1)
                pool.affine_select(out=head_of[:, :, :], in_=head_of[:, :, :], compare_op=ALU.is_ge, fill=0.0, base=HD - 1,
                                   pattern=[[-P, DT], [HD, NH]], channel_multiplier=-1).then_inc(made, 1)
                split.pool_setup(pool)
                with pool.Fori(0, NB) as b:
                    for n in range(split.TILES):
                        split.pool(pool, b, n)
                    pool.wait_ge(sig_ready, b + 1)
                    pool.wait_ge(gate_stored, b * DMA + DMA)
                    pool.tensor_tensor(gate[:, :, :], gate[:, :, :], ffn[:, :, :], ALU.mult).then_inc(gate_ready, 1)

            @block.scalar
            def _(act):
                ln.act_setup(act)
                all_made(act)
                turned.act(act)
                split.act_setup(act)
                act.sem_inc(relu_ready, DT)
                act.sem_inc(r_ready, 2)
                act.sem_inc(norm_copied, 2)
                with act.Fori(0, NB) as b:
                    ln.act(act, b)
                    for m in range(DT):
                        act.wait_ge(xt_done, b * DT + m + 3)
                        act.copy(xn_t[:, m, 1:], ps[:, m]).then_inc(xt_copied, 1)
                    for n in range(split.TILES):
                        act.wait_ge(qk_done, b * split.TILES + n + 1)
                        side, m = divmod(n, DT)
                        split.act(act, b, n, ps[:, 2 + n], bias=bias[:, side, m:m + 1], scale=1.0 if side == 0 else -2.0)
                    for n in range(split.TILES):
                        act.wait_ge(split.copied, b * split.TILES + n + 1 + split.TILES)
                        act.activation(squares[:, n], split.full[:, n], ACT.Square).then_inc(squared, 1)
                    for m in range(DT):
                        act.wait_ge(mix_k_done, b * DT + m + 1)
                        act.activation(act_k[:, m], ps[:, m], ACT.Relu).then_inc(relu_ready, 1)
                    for m in range(DT):
                        act.wait_ge(relu_ready, b * DT + m + 1 + DT)
                        act.activation(act_k[:, m], act_k[:, m], ACT.Square).then_inc(act_k_ready, 1)
                    for j in range(2):
                        act.wait_ge(mix_r_done, b * 2 + j + 1)
                        act.activation(r[:, 2 * j:2 * j + 2, :], ps[:, 2 + j].rearrange("p (i d) -> p i d", d=D),
                                       ACT.Sigmoid).then_inc(r_ready, 1)
                    for side in range(2):
                        act.wait_ge(norm_done, b * 2 + side + 1)
                        act.activation(norm[:, side], ps[0:NH, 4 + side], ACT.Identity,
                                       scale=1.0 if side == 0 else 0.25).then_inc(norm_copied, 1)
                    act.wait_ge(ffn_ready, b * 2 + 4)
                    act.wait_ge(gate_stored, b * DMA + DMA)
                    act.activation(gate[:, :, :], ffn[:, :, :], ACT.Sigmoid).then_inc(sig_ready, 1)

            @block.vector
            def _(dve):
                count = [0]

                def step(ins):
                    ins.then_inc(filled, 1)
                    count[0] += 1
                    dve.wait_ge(filled, count[0])

                step(dve.memset(v[:, :, :, :], 0.0))
                step(dve.memset(v[:, :, :, HD:HD + 1], 1.0))
                step(dve.memset(xn_t[:, :, 0:1], 0.0))
                step(dve.memset(head_of[:, :, :], 1.0))
                dve.wait_ge(w_loaded, LOADS * DMA)
                step(dve.tensor_scalar(mu_not[:, :, :], mu[:, :, :], -1.0, 1.0, ALU.mult, ALU.add))
                step(dve.tensor_scalar(bias[:, 1], bias[:, 1], -2.0, None, ALU.mult))
                assert count[0] == FILLS
                ln.dve_setup(dve)
                all_made(dve)
                split.dve_setup(dve)
                dve.sem_inc(v_copied, 2)
                dve.sem_inc(ffn_ready, 2)
                with dve.Fori(0, NB) as b:
                    dve.wait_ge(x_loaded, b * DMA + DMA)
                    dve.wait_ge(xt_done, b * DT + 2)
                    ln.dve(dve, b, x)
                    dve.wait_ge(ln.ready, b * TT + TT)
                    dve.sem_inc(x_free, 1)
                    dve.wait_ge(xt_copied, b * DT + DT)
                    for a in range(2):
                        for m in range(DT):
                            dve.tensor_scalar(mixed[:, a, m], xn_t[:, m, 0:T], mu_not[:, a, m:m + 1], None,
                                              ALU.mult).then_inc(mix_half, 1)
                    for a in range(2):
                        for m in range(DT):
                            dve.wait_ge(mix_half, b * 2 * DT + a * DT + m + 1)
                            dve.scalar_tensor_tensor(mixed[:, a, m], xn_t[:, m, 1:], mu[:, a, m:m + 1], mixed[:, a, m], ALU.mult,
                                                     ALU.add).then_inc(mixed_ready, 1)
                    for n in range(split.TILES):
                        split.dve(dve, b, n)
                    dve.wait_ge(v_stored, b * DMA + DMA)
                    for j in range(2):
                        dve.wait_ge(v_done, b * 2 + j + 1)
                        dve.tensor_tensor(v[:, 2 * j:2 * j + 2, :, 0:HD],
                                          ps[:, 6 + j].rearrange("p (i h e) -> p i h e", i=2, h=NH),
                                          bv[:, :].rearrange("p (h e) -> p h e", h=NH).unsqueeze(1).broadcast_to([P, 2, NH, HD]),
                                          ALU.add).then_inc(v_copied, 1)
                    dve.wait_ge(norm_stored, b * 2 * DMA + 2 * DMA)
                    for side in range(2):
                        dve.wait_ge(norm_copied, b * 2 + side + 3)
                        chain = (b * 2 + side) * 3
                        dve.tensor_copy(norm_parts[:, side, 0], norm[:, side]).then_inc(norm_step, 1)
                        dve.wait_ge(norm_step, chain + 1)
                        dve.tensor_tensor(norm_rest[:, side], norm[:, side], norm_parts[:, side, 0], ALU.subtract).then_inc(norm_step, 1)
                        dve.wait_ge(norm_step, chain + 2)
                        dve.tensor_copy(norm_parts[:, side, 1], norm_rest[:, side]).then_inc(norm_step, 1)
                        dve.wait_ge(norm_step, chain + 3)
                        dve.tensor_tensor(norm_parts[:, side, 2], norm_rest[:, side], norm_parts[:, side, 1],
                                          ALU.subtract).then_inc(norm_ready, 1)
                    for j in range(2):
                        dve.wait_ge(r_ready, b * 2 + j + 3)
                        dve.wait_ge(mix_v_done, b * 2 + j + 1)
                        tiles = slice(2 * j, 2 * j + 2)
                        dve.tensor_tensor(ffn[:, tiles, :], r[:, tiles, :], ps[:, 6 + j].rearrange("p (i d) -> p i d", d=D),
                                          ALU.mult).then_inc(ffn_ready, 1)

            @block.tensor
            def _(pe):
                all_made(pe)
                turned.pe(pe)
                pe.sem_inc(xt_done, 2)
                with pe.Fori(0, NB) as b:
                    pe.wait_ge(ln.ready, b * TT + TT)
                    pe.wait_ge(relu_ready, b * DT + DT)
                    for m in range(DT):
                        for i in range(TT):
                            last = pe.transpose(ps[:, m, i * P:(i + 1) * P], xn[:, i, m * P:(m + 1) * P], ident[:, :])
                        last.then_inc(xt_done, 1)
                    pe.wait_ge(xt_copied, b * DT + DT)
                    pe.wait_ge(r_ready, b * 2 + 2)
                    pe.wait_ge(norm_copied, b * 2 + 2)
                    for n in range(split.TILES):
                        split.bank_free(pe, b, n)
                        side, n2 = divmod(n, DT)
                        for m in range(DT):
                            last = pe.matmul(ps[:, 2 + n], w_t[:, Q + side, m, n2 * P:(n2 + 1) * P], xn_t[:, m, 1:], start=(m == 0),
                                             stop=(m == DT - 1))
                        last.then_inc(qk_done, 1)
                    for j in range(2):
                        pe.wait_ge(v_copied, b * 2 + j + 1)
                        pe.wait_ge(ffn_ready, b * 2 + j + 1)
                        for i in (2 * j, 2 * j + 1):
                            for m in range(DT):
                                last = pe.matmul(ps[:, 6 + j, i % 2 * D:(i % 2 + 1) * D], xn_t[:, m, 1 + i * P:1 + (i + 1) * P],
                                                 w_t[:, V, m], start=(m == 0), stop=(m == DT - 1))
                        last.then_inc(v_done, 1)
                    pe.wait_ge(mixed_ready, (b + 1) * 2 * DT)
                    for n in range(DT):
                        for m in range(DT):
                            last = pe.matmul(ps[:, n], w_t[:, MIX_K, m, n * P:(n + 1) * P], mixed[:, 1, m], start=(m == 0),
                                             stop=(m == DT - 1))
                        last.then_inc(mix_k_done, 1)
                    for j in range(2):
                        pe.wait_ge(split.copied, b * split.TILES + j + 1 + split.TILES)
                        for i in (2 * j, 2 * j + 1):
                            for m in range(DT):
                                last = pe.matmul(ps[:, 2 + j, i % 2 * D:(i % 2 + 1) * D], mixed[:, 0, m, i * P:(i + 1) * P],
                                                 w_t[:, MIX_R, m], start=(m == 0), stop=(m == DT - 1))
                        last.then_inc(mix_r_done, 1)
                    for side in range(2):
                        pe.wait_ge(squared, b * 2 * DT + (side + 1) * DT)
                        pe.wait_ge(split.copied, b * split.TILES + DT + side + 1 + split.TILES)
                        for m in range(DT):
                            last = pe.matmul(ps[0:NH, 4 + side], head_of[:, m], squares[:, side * DT + m], start=(m == 0),
                                             stop=(m == DT - 1))
                        last.then_inc(norm_done, 1)
                    pe.wait_ge(act_k_ready, b * DT + DT)
                    for j in range(2):
                        pe.wait_ge(v_copied, b * 2 + j + 3)
                        for i in (2 * j, 2 * j + 1):
                            for m in range(DT):
                                last = pe.matmul(ps[:, 6 + j, i % 2 * D:(i % 2 + 1) * D], act_k[:, m, i * P:(i + 1) * P],
                                                 w_t[:, MIX_V, m], start=(m == 0), stop=(m == DT - 1))
                        last.then_inc(mix_v_done, 1)


D2_MIN = 1e-12


def stage_distance_attend(nc, w, x_in, q_in, k_in, q2_in, k2_in, v_in, gate_in, x_out):
    with Chip(nc, "distance") as c:
        ident = c.sb("ident", [P, P])
        wo_cols = c.sb("wo_cols", [P, DT, NH, QUAD])
        wo = c.sb("wo", [P, NG, D])
        bo = c.sb("bo", [P, D])
        den_sel = c.sb("den_sel", [P, P])
        qs = c.sb("qs", [P, NG, GH, T], BF16)
        ks = c.sb("ks", [P, NG, GH, T], BF16)
        v = c.sb("v", [P, NG, TT, GH * QUAD])
        least = c.sb("least", [P, 2, GH * TT])
        least_t = c.sb("least_t", [GH * TT, 2, P])
        least_all = c.sb("least_all", [P, 2, GH * T])
        dist = c.sb("dist", [P, 2, TT, GH * T])
        o = c.sb("o", [P, T])
        den_inv = c.sb("den_inv", [P, T])
        ctx = c.sb("ctx", [P, NG, T])
        gate = c.sb("gate", [P, TT, D])
        x = c.sb("x", [P, TT, D])
        xo = c.sb("xo", [P, TT, D])
        least_dram = nc.dram_tensor("distance_least_rows", (2, GH * TT, P), F32, kind="Internal").ap()
        ps = c.psum()
        turned = Turned(c, ps, ident, [
            (wo_cols[:, n, g * GH:(g + 1) * GH, :].rearrange("p h e -> p (h e)"), wo[:, g, n * P:(n + 1) * P])
            for n in range(DT) for g in range(NG)])

        w_loaded, filled, made, ident_made = (c.sem(n) for n in ("w_loaded", "filled", "made", "ident_made"))
        qk_loaded, v_loaded = ([c.sem(f"{n}_loaded{g}") for g in range(NG)] for n in ("qk", "v"))
        least_stored, least_loaded = ([c.sem(f"{n}{g}") for g in range(2)] for n in ("least_stored", "least_loaded"))
        a_done, a_min, least_clamped, least_ready, least_turned, least_copied = (
            c.sem(n) for n in ("a_done", "a_min", "least_clamped", "least_ready", "least_turned", "least_copied"))
        s_done, clamped, sqrt_ready, shifted, p_ready, pv_done, o_copied, den_done, den_inv_ready, ctx_ready = (
            c.sem(n) for n in ("s_done", "clamped", "sqrt_ready", "shifted", "p_ready", "pv_done", "o_copied", "den_done",
                               "den_inv", "ctx"))
        gx_loaded, proj_done, proj_copied, gated, xo_ready, xo_stored = (
            c.sem(n) for n in ("gx_loaded", "proj_done", "proj_copied", "gated", "xo", "xo_stored"))

        UA, UB = GH * TT, 2 * TT
        LOADS = DT + 1
        FILLS, MADE = 2 + 2 * NG, 1
        K_LOADS = 2 * (len(STACK) + 1)

        def all_made(eng):
            eng.wait_ge(w_loaded, LOADS * DMA)
            eng.wait_ge(ident_made, 2)
            eng.wait_ge(made, MADE)
            eng.wait_ge(filled, FILLS)

        def run(eng, step):
            step(None, (0, 0), (0, 1), None, None)
            step((0, 0), (0, 1), (0, 2), None, None)
            step((0, 1), (0, 2), (0, 3), (0, 0), None)
            with eng.Fori(0, NB - 1) as b:
                step((b, 2), (b, 3), (b + 1, 0), (b, 1), None)
                step((b, 3), (b + 1, 0), (b + 1, 1), (b, 2), None)
                step((b + 1, 0), (b + 1, 1), (b + 1, 2), (b, 3), (b, 0))
                step((b + 1, 1), (b + 1, 2), (b + 1, 3), (b + 1, 0), (b, 1))
            step((NB - 1, 2), (NB - 1, 3), None, (NB - 1, 1), None)
            step((NB - 1, 3), None, None, (NB - 1, 2), None)
            step(None, None, None, (NB - 1, 3), (NB - 1, 0))
            step(None, None, None, None, (NB - 1, 1))

        with nc.Block() as block:

            @block.sync
            def _(sp):
                sp.wait_ge(filled, FILLS)
                load_head_columns(sp, wo_cols, w["wo"], w_loaded, 0)
                sp.dma_start(bo[:, :], w["bo"].partition_broadcast(P)).then_inc(w_loaded, DMA)

                def load_qk(b, g):
                    load_stack(sp, qs[:, g], q_in, b, g, False, qk_loaded[g])
                    load_stack(sp, ks[:, g], k_in, b, g, True, qk_loaded[g])
                    for dst, src in ((qs[KQK:KQK + NPART, g], q2_in), (ks[KQK + NPART:KD, g], k2_in)):
                        sp.dma_start(dst, src[b][:, g * GH * T:(g + 1) * GH * T].rearrange("a (h t) -> a h t", h=GH)).then_inc(
                            qk_loaded[g], DMA)

                def load_v(b, g):
                    sp.dma_start(v[:, g], token_tiles(v_in, b)[:, :, g * GH * QUAD:(g + 1) * GH * QUAD]).then_inc(v_loaded[g], DMA)

                def spread_least(b, g):
                    sp.wait_ge(least_copied, b * NG + g + 1)
                    sp.wait_ge(shifted, (b * NG + g) * TT + TT)
                    sp.dma_start(least_dram[g % 2], least_t[:, g % 2]).then_inc(least_stored[g % 2], DMA)
                    sp.wait_ge(least_stored[g % 2], (b * 2 + g // 2 + 1) * DMA)
                    sp.dma_start(least_all[:, g % 2], least_dram[g % 2].rearrange("n q -> (n q)").partition_broadcast(P)).then_inc(
                        least_loaded[g % 2], DMA)

                def load_gx(b):
                    sp.wait_ge(xo_ready, b * 2 + 2)
                    sp.dma_start(gate[:, :, :], token_tiles(gate_in, b)).then_inc(gx_loaded, DMA)
                    sp.dma_start(x[:, :, :], token_tiles(x_in, b)).then_inc(gx_loaded, DMA)

                def second_used(b, g):
                    sp.wait_ge(s_done, (b * NG + g) * UB + UB)

                def values_used(b, g):
                    sp.wait_ge(pv_done, (b * NG + g) * TT + 3 * TT)

                def store(b):
                    sp.wait_ge(xo_ready, b * 2 + 4)
                    sp.dma_start(token_tiles(x_out, b), xo[:, :, :]).then_inc(xo_stored, DMA)

                sp.sem_inc(xo_stored, DMA)
                for g in range(NG):
                    load_qk(0, g)
                    load_v(0, g)
                for g in range(3):
                    spread_least(0, g)
                with sp.Fori(0, NB - 1) as b:
                    for g in range(2):
                        second_used(b, g)
                        load_qk(b + 1, g)
                    load_gx(b)
                    spread_least(b, 3)
                    second_used(b, 2)
                    load_qk(b + 1, 2)
                    values_used(b, 0)
                    load_v(b + 1, 0)
                    spread_least(b + 1, 0)
                    second_used(b, 3)
                    load_qk(b + 1, 3)
                    values_used(b, 1)
                    load_v(b + 1, 1)
                    spread_least(b + 1, 1)
                    for g in (2, 3):
                        values_used(b, g)
                        load_v(b + 1, g)
                    spread_least(b + 1, 2)
                    store(b)
                load_gx(NB - 1)
                spread_least(NB - 1, 3)
                store(NB - 1)
                sp.wait_ge(xo_stored, (NB + 1) * DMA)

            @block.gpsimd
            def _(pool):
                make_identity(pool, ident, ident_made)
                pool.wait_ge(filled, FILLS)
                pool.affine_select(out=den_sel[:, :], in_=den_sel[:, :], compare_op=ALU.not_equal, fill=1.0, base=-HD,
                                   pattern=[[-QUAD, GH], [0, QUAD]], channel_multiplier=1).then_inc(made, 1)
                pool.sem_inc(shifted, 2 * TT)
                pool.sem_inc(xo_ready, 2)

                def step(out, mid, first, before, proj):
                    if mid is not None:
                        b, g = mid
                        pool.wait_ge(least_loaded[g % 2], (b * 2 + g // 2 + 1) * DMA)
                        for kt in range(TT):
                            pool.wait_ge(sqrt_ready, (b * NG + g) * TT + kt + 1)
                            pool.tensor_tensor(dist[:, g % 2, kt], dist[:, g % 2, kt], least_all[:, g % 2],
                                               ALU.subtract).then_inc(shifted, 1)
                    if proj is not None and proj[1] == 1:
                        b = proj[0]
                        pool.wait_ge(gx_loaded, b * 2 * DMA + 2 * DMA)
                        for j in range(2):
                            tiles = slice(2 * j, 2 * j + 2)
                            pool.wait_ge(proj_copied, b * 2 + j + 2)
                            pool.tensor_tensor(xo[:, tiles], xo[:, tiles], gate[:, tiles], ALU.mult).then_inc(gated, 1)
                        for j in range(2):
                            tiles = slice(2 * j, 2 * j + 2)
                            pool.wait_ge(gated, b * 2 + j + 1)
                            pool.tensor_tensor(xo[:, tiles], xo[:, tiles], x[:, tiles], ALU.add).then_inc(xo_ready, 1)

                run(pool, step)

            @block.scalar
            def _(act):
                all_made(act)
                turned.act(act)

                def step(out, mid, first, before, proj):
                    if mid is not None:
                        b, g = mid
                        n = b * NG + g
                        act.wait_ge(least_clamped, n + 1)
                        act.activation(least[:, g % 2], least[:, g % 2], ACT.Sqrt).then_inc(least_ready, 1)
                    if before is not None:
                        pb, pg = before
                        act.wait_ge(pv_done, (pb * NG + pg) * TT + 3 * TT)
                        act.wait_ge(ctx_ready, pb * NG + pg + 1)
                        act.copy(o[:, :], ps[:, 6]).then_inc(o_copied, 1)
                    if mid is not None:
                        for kt in range(TT):
                            act.wait_ge(clamped, n * UB + 2 * kt + 4)
                            act.activation(dist[:, g % 2, kt], dist[:, g % 2, kt], ACT.Sqrt).then_inc(sqrt_ready, 1)
                            if kt == 0:
                                act.wait_ge(least_turned, n + 3)
                                act.copy(least_t[:, g % 2], ps[0:GH * TT, 7, 0:P]).then_inc(least_copied, 1)
                    if out is not None:
                        b, g = out
                        for kt in range(TT):
                            act.wait_ge(shifted, (b * NG + g) * TT + kt + 1 + 2 * TT)
                            act.activation(dist[:, g % 2, kt], dist[:, g % 2, kt], ACT.Exp, scale=-1.0).then_inc(p_ready, 1)

                run(act, step)

            @block.vector
            def _(dve):
                count = [0]

                def fill(tile, value):
                    dve.memset(tile, value).then_inc(filled, 1)
                    count[0] += 1
                    dve.wait_ge(filled, count[0])

                fill(den_sel[:, :], 0.0)
                fill(wo_cols[:, :, :, :], 0.0)
                for g in range(NG):
                    fill(qs[KQK:KD, g], 1.0)
                    fill(ks[KQK:KD, g], 1.0)
                assert count[0] == FILLS
                all_made(dve)
                dve.sem_inc(a_min, 2)
                dve.sem_inc(clamped, 2)
                dve.sem_inc(den_inv_ready, 1)
                dve.sem_inc(ctx_ready, 1)
                dve.sem_inc(proj_copied, 1)

                def minima(b, g):
                    n = b * NG + g
                    for u in range(UA):
                        dve.wait_ge(a_done, n * UA + u + 1)
                        if u == 0:
                            dve.wait_ge(least_turned, n + 1)
                        dve.tensor_reduce(least[:, g % 2, u:u + 1], ps[:, u % 2], op=ALU.min, axis=AX.X).then_inc(a_min, 1)
                    dve.wait_ge(a_min, n * UA + UA + 2)
                    dve.tensor_scalar(least[:, g % 2], least[:, g % 2], D2_MIN, None, ALU.max).then_inc(least_clamped, 1)

                def add_bias(b, j):
                    dve.wait_ge(proj_done, b * 2 + j + 1)
                    if j == 0:
                        dve.wait_ge(xo_stored, b * DMA + DMA)
                    dve.tensor_tensor(xo[:, 2 * j:2 * j + 2, :], ps[:, 7].rearrange("p (i n) -> p i n", n=D),
                                      bo[:, :].unsqueeze(1).broadcast_to([P, 2, D]), ALU.add).then_inc(proj_copied, 1)

                def step(out, mid, first, before, proj):
                    if proj is not None and proj[1] == 1:
                        add_bias(*proj)
                    if mid is not None:
                        b, g = mid
                        n = b * NG + g
                        for u in range(UB):
                            kt, pair = divmod(u, 2)
                            dve.wait_ge(s_done, n * UB + u + 1)
                            if pair == 0:
                                dve.wait_ge(pv_done, n * TT + kt + 1)
                            dve.tensor_scalar(dist[:, g % 2, kt, pair * 2 * T:(pair + 1) * 2 * T],
                                              ps[:, 2 + u % 2 * 2:4 + u % 2 * 2].rearrange("p h t -> p (h t)"), D2_MIN, None,
                                              ALU.max).then_inc(clamped, 1)
                    if before is not None:
                        b, g = before
                        n = b * NG + g
                        dve.wait_ge(den_done, n + 1)
                        dve.reciprocal(den_inv[:, :], ps[:, 6]).then_inc(den_inv_ready, 1)
                        dve.wait_ge(den_inv_ready, n + 2)
                        if g == 0 and not isinstance(b, int):
                            dve.wait_ge(proj_done, b * 2)
                        dve.tensor_tensor(ctx[:, g], o[:, :], den_inv[:, :], ALU.mult).then_inc(ctx_ready, 1)
                    if first is not None:
                        minima(*first)
                    if proj is not None and proj[1] == 0:
                        add_bias(*proj)

                minima(0, 0)
                run(dve, step)

            @block.tensor
            def _(pe):
                all_made(pe)
                turned.pe(pe)
                pe.sem_inc(pv_done, 2 * TT)
                pe.sem_inc(least_turned, 2)

                def first_scores(b, g, units):
                    for u in units:
                        h, i = divmod(u, TT)
                        if u == 0:
                            pe.wait_ge(qk_loaded[g], (b + 1) * K_LOADS * DMA)
                        pe.wait_ge(a_min, (b * NG + g) * UA + u + 1)
                        pe.matmul(ps[:, u % 2], qs[0:KD, g, h, i * P:(i + 1) * P], ks[0:KD, g, h, :], start=True,
                                  stop=True).then_inc(a_done, 1)

                def second_scores(b, g, kt):
                    for pair in range(2):
                        u = kt * 2 + pair
                        pe.wait_ge(clamped, (b * NG + g) * UB + u + 1)
                        for j in range(2):
                            h = 2 * pair + j
                            last = pe.matmul(ps[:, 2 + u % 2 * 2 + j], ks[0:KD, g, h, kt * P:(kt + 1) * P], qs[0:KD, g, h, :],
                                             start=True, stop=True)
                        last.then_inc(s_done, 1)

                def turn_least(b, g):
                    pe.wait_ge(least_ready, b * NG + g + 1)
                    due = (-1, -1, 1, 1)[g]
                    if due > 0 or not isinstance(b, int):
                        pe.wait_ge(proj_copied, b * 2 + due)
                    if not (isinstance(b, int) and b == 0 and g == 0):
                        pe.wait_ge(least_copied, b * NG + g)
                    pe.transpose(ps[0:GH * TT, 7, 0:P], least[:, g % 2], ident[:, :]).then_inc(least_turned, 1)

                def output(b, g, kt):
                    n = b * NG + g
                    if kt == 0:
                        pe.wait_ge(v_loaded[g], (b + 1) * DMA)
                        pe.wait_ge(den_inv_ready, n + 1)
                    pe.wait_ge(p_ready, n * TT + kt + 1)
                    for h in range(GH):
                        last = pe.matmul(ps[h * QUAD:(h + 1) * QUAD, 6], v[:, g, kt, h * QUAD:(h + 1) * QUAD],
                                         dist[:, g % 2, kt, h * T:(h + 1) * T], start=(kt == 0), stop=(kt == TT - 1))
                    last.then_inc(pv_done, 1)

                def project(b, j, mid):
                    if j == 0:
                        pe.wait_ge(ctx_ready, b * NG + NG + 1)
                    if mid is not None:
                        pe.wait_ge(least_copied, mid[0] * NG + mid[1] + 1 - j)
                    pe.wait_ge(proj_copied, b * 2 + j + 1)
                    for i in (2 * j, 2 * j + 1):
                        for g in range(NG):
                            last = pe.matmul(ps[:, 7, i % 2 * D:(i % 2 + 1) * D], ctx[:, g, i * P:(i + 1) * P], wo[:, g],
                                             start=(g == 0), stop=(g == NG - 1))
                    last.then_inc(proj_done, 1)

                def step(out, mid, first, before, proj):
                    if proj is not None and proj[1] == 1:
                        project(*proj, mid)
                    for kt in range(TT):
                        if mid is not None:
                            second_scores(*mid, kt)
                            if kt == 1:
                                turn_least(*mid)
                        if kt == 2 and before is not None:
                            pe.wait_ge(o_copied, before[0] * NG + before[1] + 1)
                            pe.matmul(ps[:, 6], den_sel[:, :], o[:, :], start=True, stop=True).then_inc(den_done, 1)
                    for kt in range(TT):
                        if first is not None:
                            first_scores(*first, range(kt * TT, (kt + 1) * TT))
                        if out is not None:
                            output(*out, kt)
                    if proj is not None and proj[1] == 0:
                        project(*proj, mid)

                first_scores(0, 0, range(UA))
                run(pe, step)


def build(nc, a, out):
    def scratch(name, shape):
        return nc.dram_tensor(name, shape, F32, kind="Internal").ap()

    def weights(prefix, names):
        return {n: a[f"{prefix}_{n}"] for n in names}

    x1, x2, x3, xn2, s2, gate3 = (scratch(n, (NB, T, D)) for n in ("x1", "x2", "x3", "xn2", "s2", "gate3"))
    probs2 = scratch("probs2", (NB * NE2, T))
    v2, v3 = (scratch(n, (NB, T, V_WIDTH)) for n in ("v2", "v3"))
    q2, k2, q3, k3 = (parts_tensor(nc, n) for n in ("q2_parts", "k2_parts", "q3_parts", "k3_parts"))
    q3_norm, k3_norm = (norms_tensor(nc, n) for n in ("q3_norm", "k3_norm"))

    stage_mamba(nc, weights("L0_attn", ("W_in", "conv_w", "conv_b", "W_x", "W_dt", "b_dt", "A_log", "D", "W_out"))
                | weights("L0_ffn", ("U1", "V1", "b1", "U2", "V2", "b2")), a["L0_attn_x"], x1)
    stage_chunks(nc, weights("L1_attn", ("Wq_l", "Wk_l", "Wv_l", "Wo_l", "Wq_g", "Wk_g", "Wv_g", "Wo_g"))
                 | weights("L1_ffn", ("Wr", "We")), x1, x2)
    stage_causal_in(nc, weights("L2_attn", ("w_qkv",)) | weights("L2_ffn", ("gate_w",)), x2, xn2, q2, k2, v2, probs2)
    stage_causal_attend(nc, weights("L2_attn", ("w_out",)), q2, k2, v2, s2)
    stage_experts(nc, weights("L2_ffn", ("w1", "w2")), x2, xn2, s2, probs2, x3)
    stage_distance_in(nc, weights("L3_attn", ("wq", "bq", "wk", "bk", "wv", "bv"))
                      | weights("L3_ffn", ("W_r", "W_k", "W_v", "mu_r", "mu_k")), x3, q3, k3, q3_norm, k3_norm, v3, gate3)
    stage_distance_attend(nc, weights("L3_attn", ("wo", "bo")), x3, q3, k3, q3_norm, k3_norm, v3, gate3, out)


def kernel(**inputs):
    import numpy as np
    import concourse.bacc as bacc
    from concourse.bass_utils import run_bass_kernel_spmd

    nc = bacc.Bacc("TRN2", target_bir_lowering=False, num_devices=1)
    arrays, handles = {}, {}
    for name, value in inputs.items():
        arrays[name] = np.ascontiguousarray(value)
        handles[name] = nc.dram_tensor(name, arrays[name].shape, mybir.dt.from_np(arrays[name].dtype), kind="ExternalInput").ap()
    out = nc.dram_tensor("out", (NB, T, D), F32, kind="ExternalOutput").ap()
    build(nc, handles, out)
    return run_bass_kernel_spmd(nc, [arrays], core_ids=[0]).results[0]["out"]
```

```python
import concourse.bass as bass
from concourse import mybir
from contextlib import ExitStack

F32 = mybir.dt.float32
BF16 = mybir.dt.bfloat16
ALU = mybir.AluOpType
ACT = mybir.ActivationFunctionType
AX = mybir.AxisListType

P = 128
NB, T, D = 8, 512, 256
TT = T // P
DT = D // P
LN_EPS = 1e-5
DMA = 16


class Chip:

    def __init__(self, nc, stage):
        self.nc, self.stage, self.stack, self.sems = nc, stage, ExitStack(), []

    def __enter__(self):
        self.stack.__enter__()
        return self

    def __exit__(self, *what):
        self.nc.clear_and_free_semaphores(self.sems)
        self.nc.all_engine_barrier()
        return self.stack.__exit__(*what)

    def sb(self, name, shape, dtype=F32):
        return self.stack.enter_context(self.nc.sbuf_tensor(f"{self.stage}_{name}", list(shape), dtype))

    def psum(self):
        return self.stack.enter_context(self.nc.psum_tensor(f"{self.stage}_psum", [P, 8, 512], F32))

    def sem(self, name):
        self.sems.append(self.nc.alloc_semaphore(f"{self.stage}_{name}"))
        return self.sems[-1]


def token_tiles(x, b):
    return x[b].rearrange("(i p) d -> p i d", p=P)


def column(v, n):
    return v.rearrange("(n p) -> p n", n=n)


def make_identity(pool, ident, made):
    pool.memset(ident[:, :], 0.0).then_inc(made, 1)
    pool.wait_ge(made, 1)
    pool.affine_select(out=ident[:, :], in_=ident[:, :], compare_op=ALU.not_equal, fill=1.0, base=0,
                       pattern=[[-1, P]], channel_multiplier=1).then_inc(made, 1)


NH, HD = 16, 16
GH = 4
NG = NH // GH
QUAD = 32
AUG = 2
SCALE = HD ** -0.5
NEG = -125.0


class LayerNorm:

    def __init__(self, c):
        self.eps = c.sb("ln_eps", [P, 1])
        self.stats = c.sb("ln_stats", [P, TT, 6])
        self.moments = c.sb("ln_moments", [P, TT, 2])
        self.std = c.sb("ln_std", [P, TT])
        self.rstd = c.sb("ln_rstd", [P, TT])
        self.xn = c.sb("xn", [P, TT, D])
        self.eps_set, self.stats_ready, self.begun, self.var_ready, self.std_ready, self.rstd_ready, self.ready = (
            c.sem(f"ln_{n}") for n in ("eps_set", "stats_ready", "begun", "var_ready", "std_ready", "rstd_ready", "xn"))

    def dve_setup(self, dve):
        dve.memset(self.eps[:, :], LN_EPS).then_inc(self.eps_set, 1)

    def act_setup(self, act):
        act.wait_ge(self.eps_set, 1)

    def dve(self, dve, b, x):
        for i in range(TT):
            dve.bn_stats(self.stats[:, i], x[:, i]).then_inc(self.stats_ready, 1)
        dve.wait_ge(self.stats_ready, b * TT + TT)
        dve.sem_inc(self.begun, 1)
        for i in range(TT):
            dve.bn_aggr(self.moments[:, i], self.stats[:, i]).then_inc(self.var_ready, 1)
        dve.wait_ge(self.std_ready, b + 1)
        dve.reciprocal(self.rstd[:, :], self.std[:, :]).then_inc(self.rstd_ready, 1)
        dve.wait_ge(self.rstd_ready, b + 1)
        for i in range(TT):
            dve.tensor_scalar(self.xn[:, i], x[:, i], self.moments[:, i, 0:1], self.rstd[:, i:i + 1],
                              ALU.subtract, ALU.mult).then_inc(self.ready, 1)

    def act(self, act, b):
        act.wait_ge(self.var_ready, b * TT + TT)
        act.activation(self.std[:, :], self.moments[:, :, 1], ACT.Sqrt, bias=self.eps[:, 0:1]).then_inc(self.std_ready, 1)


def load_head_columns(sp, dst, src, loaded, first=AUG):
    for k in range(DT):
        sp.dma_start(dst[:, k, :, first:first + HD],
                     src[k * P:(k + 1) * P, :].rearrange("p (h e) -> p h e", h=NH)).then_inc(loaded, DMA)


def load_head_rows(sp, dst, src, loaded, first=0):
    for j in range(GH):
        sp.dma_start(dst[j * QUAD + first:j * QUAD + first + HD, :, :],
                     src.rearrange("(g h e) n -> h e g n", g=NG, h=GH)[j]).then_inc(loaded, DMA)


class Turned:

    def __init__(self, c, ps, ident, pairs):
        self.ps, self.ident, self.pairs = ps, ident, pairs
        self.done, self.copied = c.sem("turn_done"), c.sem("turn_copied")

    def pe(self, pe):
        for n, (src, _) in enumerate(self.pairs):
            if n >= 4:
                pe.wait_ge(self.copied, n - 3)
            pe.transpose(self.ps[:, n % 4, 0:P], src, self.ident[:, :]).then_inc(self.done, 1)
        pe.wait_ge(self.copied, len(self.pairs))

    def act(self, act):
        for n, (_, dst) in enumerate(self.pairs):
            act.wait_ge(self.done, n + 1)
            act.copy(dst, self.ps[:, n % 4, 0:P]).then_inc(self.copied, 1)


NPART = 3
STACK = ((0, 3, 0), (0, 2, 1), (0, 1, 2))
SLOTS = sum(n for _, n, _ in STACK)
KQK = SLOTS * HD


def parts_tensor(nc, name):
    return nc.dram_tensor(name, (NB, NG, NPART * HD, GH * T), BF16, kind="Internal").ap()


class Split:

    TILES = 2 * DT
    STORES = TILES * (P // (GH * HD)) * NPART

    def __init__(self, c, q_parts, k_parts):
        self.q_parts, self.k_parts = q_parts, k_parts
        self.full = c.sb("full", [P, self.TILES, T])
        self.rest = c.sb("rest", [P, self.TILES, T])
        self.parts = c.sb("parts", [P, self.TILES, NPART, T], BF16)
        self.copied, self.high, self.rest_ready, self.middle, self.ready, self.stored = (
            c.sem(f"split_{n}") for n in ("copied", "high", "rest", "middle", "ready", "stored"))

    def act_setup(self, act):
        act.sem_inc(self.copied, self.TILES)

    def dve_setup(self, dve):
        dve.sem_inc(self.rest_ready, self.TILES)

    def pool_setup(self, pool):
        pool.sem_inc(self.ready, self.TILES)

    def sp_setup(self, sp):
        sp.sem_inc(self.stored, self.STORES * DMA)

    def bank_free(self, eng, b, n):
        eng.wait_ge(self.copied, b * self.TILES + n + 1)

    def act(self, act, b, n, bank, **how):
        act.wait_ge(self.rest_ready, b * self.TILES + n + 1)
        act.activation(self.full[:, n], bank, ACT.Identity, **how).then_inc(self.copied, 1)

    def dve(self, dve, b, n):
        dve.wait_ge(self.copied, b * self.TILES + n + 1 + self.TILES)
        if n == 0:
            dve.wait_ge(self.stored, (b + 1) * self.STORES * DMA)
        dve.tensor_copy(self.parts[:, n, 0], self.full[:, n]).then_inc(self.high, 1)
        dve.wait_ge(self.high, b * self.TILES + n + 1)
        dve.wait_ge(self.ready, b * self.TILES + n + 1)
        dve.tensor_tensor(self.rest[:, n], self.full[:, n], self.parts[:, n, 0], ALU.subtract).then_inc(self.rest_ready, 1)

    def pool(self, pool, b, n):
        pool.wait_ge(self.rest_ready, b * self.TILES + n + 1 + self.TILES)
        pool.sem_inc(self.middle, 1)
        pool.tensor_copy(self.parts[:, n, 1], self.rest[:, n]).then_inc(self.middle, 1)
        pool.wait_ge(self.middle, (b * self.TILES + n + 1) * 2)
        pool.tensor_tensor(self.parts[:, n, 2], self.rest[:, n], self.parts[:, n, 1], ALU.subtract).then_inc(self.ready, 1)

    def sp(self, sp, b, n):
        sp.wait_ge(self.ready, b * self.TILES + n + 1 + self.TILES)
        to, m = (self.q_parts, n) if n < DT else (self.k_parts, n - DT)
        for j in range(P // (GH * HD)):
            for part in range(NPART):
                row = (part if n < DT else NPART - 1 - part) * HD
                dst = to[b, m * (P // (GH * HD)) + j, row:row + HD, :].rearrange("e (h t) -> h e t", h=GH)
                sp.dma_start(dst, self.parts[j * GH * HD:(j + 1) * GH * HD, n, part]).then_inc(self.stored, DMA)


def load_stack(sp, dst, parts, b, g, k_side, loaded):
    row = 0
    for first_q, n, first_k in STACK:
        first = first_k if k_side else first_q
        sp.dma_start(dst[row:row + n * HD], parts[b, g, first * HD:(first + n) * HD, :].rearrange(
            "r (h t) -> r h t", h=GH)).then_inc(loaded, DMA)
        row += n * HD


class Context:

    def __init__(self, c):
        self.turned = c.sb("out_turned", [P, T])
        self.den_inv = c.sb("den_inv", [P, T // QUAD])
        self.scaled = c.sb("out_scaled", [P, T])
        self.ctx = c.sb("ctx", [P, NG, T])
        self.out_turned, self.inverted, self.scaled_ready, self.ready = (
            c.sem(n) for n in ("out_turned", "den_inverted", "out_scaled", "ctx"))

    def dve_setup(self, dve):
        dve.sem_inc(self.out_turned, 1)

    def bank_free(self, pe, n):
        pe.wait_ge(self.out_turned, n + 1)

    def turn(self, dve, bank):
        dve.transpose(self.turned[:, :], bank).then_inc(self.out_turned, 1)

    def scale(self, dve, n):
        dve.wait_ge(self.out_turned, n + 2)
        blocks = self.turned[:, :].rearrange("p (c e) -> p c e", e=QUAD)
        dve.reciprocal(self.den_inv[:, :], blocks[:, :, HD]).then_inc(self.inverted, 1)
        dve.wait_ge(self.inverted, n + 1)
        dve.tensor_tensor(self.scaled[:, :].rearrange("p (c e) -> p c e", e=QUAD), blocks,
                          self.den_inv[:, :].unsqueeze(2).broadcast_to([P, T // QUAD, QUAD]), ALU.mult).then_inc(self.scaled_ready, 1)

    def turn_back(self, dve, n, g):
        dve.wait_ge(self.scaled_ready, n + 1)
        dve.transpose(self.ctx[:, g], self.scaled[:, :]).then_inc(self.ready, 1)
DI, DS, TAPS, RANK = 512, 16, 4, 64
MT = DI // P
F0, R0 = 1024, 64
FT0 = F0 // P
STEPS = DS * MT
RING = 4
CHUNK = 4
NCHUNK = DS // CHUNK


def stage_mamba(nc, w, x_in, x_out):
    with Chip(nc, "mamba") as c:
        ident = c.sb("ident", [P, P])
        eps = c.sb("eps", [P, 1])
        w_in = c.sb("w_in", [P, DT, 2 * DI])
        w_x = c.sb("w_x", [P, MT, RANK + 2 * DS])
        w_dt = c.sb("w_dt", [RANK, DI])
        w_out = c.sb("w_out", [P, MT, D])
        u1 = c.sb("u1", [P, DT, R0])
        v1 = c.sb("v1", [R0, F0])
        u2 = c.sb("u2", [P, FT0, R0])
        v2b = c.sb("v2b", [R0 + 1, D])
        conv_w = c.sb("conv_w", [P, MT, TAPS])
        conv_b = c.sb("conv_b", [P, MT])
        b_dt = c.sb("b_dt", [P, MT])
        a_neg = c.sb("a_neg", [P, MT, DS])
        skip = c.sb("skip", [P, MT])
        b1 = c.sb("b1", [P, FT0])
        x = c.sb("x", [P, TT, D])
        stats = c.sb("stats", [P, TT, 6])
        moments = c.sb("moments", [P, TT, 2])
        std = c.sb("std", [P, TT])
        rstd = c.sb("rstd", [P, TT])
        xn = c.sb("xn", [P, TT, D])
        xn_t = c.sb("xn_t", [P, DT, T])
        xi = c.sb("xi", [P, MT, TAPS - 1 + T])
        conv = c.sb("conv", [P, MT, T])
        xc = c.sb("xc", [P, MT, T])
        z_silu = c.sb("z_silu", [P, MT, T])
        low = c.sb("low", [R0, T])
        xp = c.sb("xp", [RANK + 2 * DS, T])
        sp_x = c.sb("sp_x", [P, MT, T])
        sp_e = c.sb("sp_e", [P, MT, T])
        sp_u = c.sb("sp_u", [P, MT, T])
        dt = c.sb("dt", [P, MT, T])
        u = c.sb("u", [P, MT, T])
        b_all = c.sb("b_all", [P, 2, CHUNK, T])
        c_all = c.sb("c_all", [P, 2, CHUNK, T])
        decay = c.sb("decay", [P, RING, T])
        drive = c.sb("drive", [P, RING, T])
        h = c.sb("h", [P, RING, T])
        hc = c.sb("hc", [P, RING, T])
        hidden = c.sb("hidden", [P, 2, T])
        q1 = c.sb("q1", [R0 + 1, T])
        gate = c.sb("gate", [P, TT, D])
        xo = c.sb("xo", [P, TT, D])
        bc_dram = nc.dram_tensor("mamba_bc", (2 * DS, T), F32, kind="Internal").ap()
        ps = c.psum()

        w_loaded, made, ident_made, a_made = (c.sem(n) for n in ("w_loaded", "made", "ident_made", "a_made"))
        x_loaded, x_free = c.sem("x_loaded"), c.sem("x_free")
        ln_stats, ln_begun, ln_var, ln_std, ln_rstd, xn_ready = (
            c.sem(n) for n in ("ln_stats", "ln_begun", "ln_var", "ln_std", "ln_rstd", "xn_ready"))
        pe_group, q_summed, act_evac = c.sem("pe_group"), c.sem("q_summed"), c.sem("act_evac")
        conv_step, xc_ready = c.sem("conv_step"), c.sem("xc_ready")
        bc_stored = c.sem("bc_stored")
        b_loaded, c_loaded = ([c.sem(f"{n}_loaded{k}") for k in range(2)] for n in "bc")
        sp_x_ready, sp_abs, sp_exp, sp_up, sp_err, sp_ln, sp_relu, dt_ready, u_ready = (
            c.sem(n) for n in ("sp_x", "sp_abs", "sp_exp", "sp_up", "sp_err", "sp_ln", "sp_relu", "dt", "u"))
        decay_ready, drive_ready, h_ready, hc_ready, y_summed = (
            c.sem(n) for n in ("decay", "drive", "h", "hc", "y_summed"))
        y_skip, y_gated, s_gated, xo_ready, x_stored = (
            c.sem(n) for n in ("y_skip", "y_gated", "s_gated", "xo", "x_stored"))

        G_XNT, G_XI, G_Z, G_LOW, G_XP, G_DT = 0, 2, 6, 10, 11, 12
        G_HID, G_FFN, G_S = 16, 24, 26
        GROUPS = 28
        Q_EVAC, EVACS = 21, 23

        def evac_count(g):
            return g + 1 if g < G_DT else g + 1 - MT + (g >= G_FFN)

        with nc.Block() as block:

            @block.sync
            def _(sp):
                for dst, src in (
                    (w_in[:, :, :], w["W_in"].rearrange("(k p) n -> p k n", p=P)),
                    (w_x[:, :, :], w["W_x"].rearrange("(k p) n -> p k n", p=P)),
                    (w_dt[:, :], w["W_dt"]),
                    (w_out[:, :, :], w["W_out"].rearrange("(k p) n -> p k n", p=P)),
                    (u1[:, :, :], w["U1"].rearrange("(k p) n -> p k n", p=P)),
                    (v1[:, :], w["V1"]),
                    (u2[:, :, :], w["U2"].rearrange("(k p) n -> p k n", p=P)),
                    (v2b[0:R0, :], w["V2"]),
                    (v2b[R0:R0 + 1, :], w["b2"].rearrange("(a n) -> a n", a=1)),
                    (conv_w[:, :, :], w["conv_w"].rearrange("(m p) a k -> p m (a k)", p=P)),
                    (a_neg[:, :, :], w["A_log"].rearrange("(m p) s -> p m s", p=P)),
                ):
                    sp.dma_start(dst, src).then_inc(w_loaded, DMA)
                with nc.allow_non_contiguous_dma(reason="short vectors, once"):
                    for dst, src in ((conv_b, w["conv_b"]), (b_dt, w["b_dt"]), (skip, w["D"])):
                        sp.dma_start(dst[:, :], column(src, MT)).then_inc(w_loaded, DMA)
                    sp.dma_start(b1[:, :], column(w["b1"], FT0)).then_inc(w_loaded, DMA)
                sp.sem_inc(x_free, 1)
                sp.sem_inc(x_stored, DMA)
                with sp.Fori(0, NB) as b:
                    sp.wait_ge(x_free, b + 1)
                    sp.dma_start(x[:, :, :], token_tiles(x_in, b)).then_inc(x_loaded, DMA)
                    sp.wait_ge(act_evac, b * EVACS + evac_count(G_XP))
                    sp.dma_start(bc_dram, xp[RANK:RANK + 2 * DS, :]).then_inc(bc_stored, DMA)
                    sp.wait_ge(bc_stored, b * DMA + DMA)
                    for k in range(NCHUNK):
                        if k >= 2:
                            sp.wait_ge(drive_ready, b * STEPS + (k - 1) * CHUNK * MT)
                            sp.wait_ge(hc_ready, b * STEPS + (k - 1) * CHUNK * MT)
                        rows = bc_dram[k * CHUNK:(k + 1) * CHUNK, :]
                        sp.dma_start(b_all[:, k % 2], rows.partition_broadcast(P)).then_inc(b_loaded[k % 2], DMA)
                        rows = bc_dram[DS + k * CHUNK:DS + (k + 1) * CHUNK, :]
                        sp.dma_start(c_all[:, k % 2], rows.partition_broadcast(P)).then_inc(c_loaded[k % 2], DMA)
                    sp.wait_ge(xo_ready, b * 2 + 2)
                    sp.dma_start(token_tiles(x_out, b), xo[:, :, :]).then_inc(x_stored, DMA)
                sp.wait_ge(x_stored, (NB + 1) * DMA)

            @block.gpsimd
            def _(pool):
                make_identity(pool, ident, ident_made)
                with pool.Fori(0, NB) as b:
                    for m in range(MT):
                        pool.wait_ge(xc_ready, b * MT + m + 1)
                        pool.wait_ge(dt_ready, b * MT + m + 1)
                        pool.tensor_tensor(u[:, m], dt[:, m], xc[:, m], ALU.mult).then_inc(u_ready, 1)
                    for n in range(STEPS):
                        s, m = divmod(n, MT)
                        if n < MT:
                            pool.wait_ge(u_ready, b * MT + m + 1)
                        if n % (CHUNK * MT) == 0:
                            k = s // CHUNK
                            pool.wait_ge(b_loaded[k % 2], (b * (NCHUNK // 2) + k // 2 + 1) * DMA)
                        if n >= RING:
                            pool.wait_ge(h_ready, b * STEPS + n - RING + 1)
                        pool.tensor_tensor(drive[:, n % RING], u[:, m], b_all[:, s // CHUNK % 2, s % CHUNK],
                                           ALU.mult).then_inc(drive_ready, 1)

            @block.scalar
            def _(act):
                act.wait_ge(w_loaded, 15 * DMA)
                act.wait_ge(made, 3)
                act.activation(a_neg[:, :, :], a_neg[:, :, :], ACT.Exp).then_inc(a_made, 1)
                act.wait_ge(a_made, 1)
                act.mul(a_neg[:, :, :], a_neg[:, :, :], -1.0).then_inc(a_made, 1)
                act.wait_ge(a_made, 2)
                with act.Fori(0, NB) as b:
                    act.wait_ge(ln_var, b * TT + TT)
                    act.activation(std[:, :], moments[:, :, 1], ACT.Sqrt, bias=eps[:, 0:1]).then_inc(ln_std, 1)
                    for k in range(DT):
                        act.wait_ge(pe_group, b * GROUPS + G_XNT + k + 1)
                        act.copy(xn_t[:, k], ps[:, (G_XNT + k) % 4]).then_inc(act_evac, 1)
                    for m in range(MT):
                        act.wait_ge(pe_group, b * GROUPS + G_XI + m + 1)
                        act.copy(xi[:, m, TAPS - 1:], ps[:, (G_XI + m) % 4]).then_inc(act_evac, 1)
                    for m in range(MT):
                        act.wait_ge(pe_group, b * GROUPS + G_Z + m + 1)
                        act.activation(z_silu[:, m], ps[:, (G_Z + m) % 4], ACT.Silu).then_inc(act_evac, 1)
                    act.wait_ge(pe_group, b * GROUPS + G_LOW + 1)
                    act.copy(low[:, :], ps[0:R0, G_LOW % 4]).then_inc(act_evac, 1)
                    for m in range(MT):
                        act.wait_ge(conv_step, b * TAPS * MT + (TAPS - 1) * MT + m + 1)
                        act.activation(xc[:, m], conv[:, m], ACT.Silu, bias=conv_b[:, m:m + 1]).then_inc(xc_ready, 1)
                    act.wait_ge(pe_group, b * GROUPS + G_XP + 1)
                    act.copy(xp[:, :], ps[0:RANK + 2 * DS, G_XP % 4]).then_inc(act_evac, 1)
                    for m in range(MT):
                        act.wait_ge(sp_x_ready, b * MT + m + 1)
                        act.activation(sp_e[:, m], sp_x[:, m], ACT.Abs).then_inc(sp_abs, 1)
                    for m in range(MT):
                        act.wait_ge(sp_abs, b * MT + m + 1)
                        act.activation(sp_e[:, m], sp_e[:, m], ACT.Exp, scale=-1.0).then_inc(sp_exp, 1)
                    for m in range(MT):
                        act.wait_ge(sp_err, b * MT + m + 1)
                        act.activation(sp_u[:, m], sp_u[:, m], ACT.Ln).then_inc(sp_ln, 1)
                    for f in range(FT0):
                        act.wait_ge(pe_group, b * GROUPS + G_HID + f + 1)
                        if f >= 2:
                            act.wait_ge(q_summed, b * FT0 + f - 1)
                        act.activation(hidden[:, f % 2], ps[:, (G_HID + f) % 4], ACT.Gelu_apprx_tanh,
                                       bias=b1[:, f:f + 1]).then_inc(act_evac, 1)
                    act.wait_ge(q_summed, b * FT0 + FT0)
                    act.copy(q1[0:R0, :], ps[0:R0, 4]).then_inc(act_evac, 1)
                    for j in range(2):
                        act.wait_ge(pe_group, b * GROUPS + G_FFN + j + 1)
                        act.activation(gate[:, 2 * j:2 * j + 2, :], ps[:, (G_FFN + j) % 4], ACT.Silu).then_inc(act_evac, 1)
                    for n in range(STEPS):
                        s, m = divmod(n, MT)
                        if n < MT:
                            act.wait_ge(dt_ready, b * MT + m + 1)
                        if n >= RING:
                            act.wait_ge(h_ready, b * STEPS + n - RING + 1)
                        act.activation(decay[:, n % RING], dt[:, m], ACT.Exp,
                                       scale=a_neg[:, m, s:s + 1]).then_inc(decay_ready, 1)

            @block.vector
            def _(dve):
                dve.memset(eps[:, :], LN_EPS).then_inc(made, 1)
                dve.memset(xi[:, :, 0:TAPS - 1], 0.0).then_inc(made, 1)
                dve.memset(q1[R0:R0 + 1, :], 1.0).then_inc(made, 1)
                dve.wait_ge(w_loaded, 15 * DMA)
                dve.wait_ge(made, 3)
                with dve.Fori(0, NB) as b:
                    dve.wait_ge(x_loaded, b * DMA + DMA)
                    for i in range(TT):
                        dve.bn_stats(stats[:, i], x[:, i]).then_inc(ln_stats, 1)
                    dve.wait_ge(ln_stats, b * TT + TT)
                    dve.sem_inc(ln_begun, 1)
                    for i in range(TT):
                        dve.bn_aggr(moments[:, i], stats[:, i]).then_inc(ln_var, 1)
                    dve.wait_ge(ln_std, b + 1)
                    dve.reciprocal(rstd[:, :], std[:, :]).then_inc(ln_rstd, 1)
                    dve.wait_ge(ln_rstd, b + 1)
                    for i in range(TT):
                        dve.tensor_scalar(xn[:, i], x[:, i], moments[:, i, 0:1], rstd[:, i:i + 1],
                                          ALU.subtract, ALU.mult).then_inc(xn_ready, 1)
                    for k in range(TAPS):
                        for m in range(MT):
                            if k == 0:
                                dve.wait_ge(act_evac, b * EVACS + evac_count(G_XI + m))
                                dve.tensor_scalar(conv[:, m], xi[:, m, 0:T], conv_w[:, m, 0:1], None,
                                                  ALU.mult).then_inc(conv_step, 1)
                            else:
                                dve.wait_ge(conv_step, b * TAPS * MT + (k - 1) * MT + m + 1)
                                dve.scalar_tensor_tensor(conv[:, m], xi[:, m, k:k + T], conv_w[:, m, k:k + 1],
                                                         conv[:, m], ALU.mult, ALU.add).then_inc(conv_step, 1)
                    for m in range(MT):
                        dve.wait_ge(pe_group, b * GROUPS + G_DT + m + 1)
                        dve.tensor_scalar(sp_x[:, m], ps[:, (G_DT + m) % 4], b_dt[:, m:m + 1], None,
                                          ALU.add).then_inc(sp_x_ready, 1)
                    for m in range(MT):
                        dve.wait_ge(sp_exp, b * MT + m + 1)
                        dve.tensor_scalar(sp_u[:, m], sp_e[:, m], 1.0, None, ALU.add).then_inc(sp_up, 1)
                    for m in range(MT):
                        dve.wait_ge(sp_up, b * MT + m + 1)
                        dve.scalar_tensor_tensor(sp_e[:, m], sp_u[:, m], 1.0, sp_e[:, m], ALU.subtract,
                                                 ALU.subtract).then_inc(sp_err, 1)
                    for m in range(MT):
                        dve.wait_ge(sp_err, b * MT + m + 1)
                        dve.scalar_tensor_tensor(sp_x[:, m], sp_x[:, m], 0.0, sp_e[:, m], ALU.max,
                                                 ALU.subtract).then_inc(sp_relu, 1)
                    for m in range(MT):
                        dve.wait_ge(sp_relu, b * MT + m + 1)
                        dve.wait_ge(sp_ln, b * MT + m + 1)
                        dve.tensor_tensor(dt[:, m], sp_x[:, m], sp_u[:, m], ALU.add).then_inc(dt_ready, 1)
                    for n in range(STEPS + 1):
                        if n < STEPS:
                            dve.wait_ge(decay_ready, b * STEPS + n + 1)
                            dve.wait_ge(drive_ready, b * STEPS + n + 1)
                            if n >= RING:
                                dve.wait_ge(hc_ready, b * STEPS + n - RING + 1)
                            dve.tensor_tensor_scan(h[:, n % RING], decay[:, n % RING], drive[:, n % RING], 0.0,
                                                   ALU.mult, ALU.add).then_inc(h_ready, 1)
                        if n >= 1:
                            s = (n - 1) // MT
                            dve.wait_ge(h_ready, b * STEPS + n)
                            if (n - 1) % (CHUNK * MT) == 0:
                                k = s // CHUNK
                                dve.wait_ge(c_loaded[k % 2], (b * (NCHUNK // 2) + k // 2 + 1) * DMA)
                            if n - 1 >= RING:
                                dve.wait_ge(y_summed, b * STEPS + n - RING)
                            dve.tensor_tensor(hc[:, (n - 1) % RING], h[:, (n - 1) % RING],
                                              c_all[:, s // CHUNK % 2, s % CHUNK], ALU.mult).then_inc(hc_ready, 1)
                    for m in range(MT):
                        dve.wait_ge(y_summed, b * STEPS + STEPS - MT + m + 1)
                        dve.scalar_tensor_tensor(conv[:, m], xc[:, m], skip[:, m:m + 1], ps[:, 4 + m], ALU.mult,
                                                 ALU.add).then_inc(y_skip, 1)
                    for m in range(MT):
                        dve.wait_ge(y_skip, b * MT + m + 1)
                        dve.tensor_tensor(conv[:, m], conv[:, m], z_silu[:, m], ALU.mult).then_inc(y_gated, 1)
                    dve.wait_ge(act_evac, b * EVACS + EVACS)
                    dve.wait_ge(x_stored, b * DMA + DMA)
                    for j in range(2):
                        dve.wait_ge(pe_group, b * GROUPS + G_S + j + 1)
                        dve.tensor_tensor(xo[:, 2 * j:2 * j + 2, :], gate[:, 2 * j:2 * j + 2, :],
                                          ps[:, (G_S + j) % 4].rearrange("p (i d) -> p i d", d=D), ALU.mult).then_inc(s_gated, 1)
                    for j in range(2):
                        dve.wait_ge(s_gated, b * 2 + j + 1)
                        dve.tensor_tensor(xo[:, 2 * j:2 * j + 2, :], xo[:, 2 * j:2 * j + 2, :],
                                          x[:, 2 * j:2 * j + 2, :], ALU.add).then_inc(xo_ready, 1)
                    dve.wait_ge(xo_ready, b * 2 + 2)
                    dve.sem_inc(x_free, 1)

            @block.tensor
            def _(pe):
                pe.wait_ge(w_loaded, 15 * DMA)
                pe.wait_ge(made, 3)
                pe.wait_ge(ident_made, 2)
                with pe.Fori(0, NB) as b:
                    def bank(g):
                        return ps[:, g % 4]

                    pe.wait_ge(xn_ready, b * TT + TT)
                    for k in range(DT):
                        for i in range(TT):
                            last = pe.transpose(bank(G_XNT + k)[:, i * P:(i + 1) * P], xn[:, i, k * P:(k + 1) * P], ident[:, :])
                        last.then_inc(pe_group, 1)
                    pe.wait_ge(act_evac, b * EVACS + evac_count(G_XNT + 1))
                    for g in range(G_XI, G_XI + 2 * MT):
                        if g >= 4:
                            pe.wait_ge(act_evac, b * EVACS + evac_count(g - 4))
                        for k in range(DT):
                            last = pe.matmul(bank(g), w_in[:, k, (g - G_XI) * P:(g - G_XI + 1) * P], xn_t[:, k],
                                             start=(k == 0), stop=(k == DT - 1))
                        last.then_inc(pe_group, 1)
                    pe.wait_ge(act_evac, b * EVACS + evac_count(G_LOW - 4))
                    for k in range(DT):
                        last = pe.matmul(bank(G_LOW)[0:R0], u1[:, k], xn_t[:, k], start=(k == 0), stop=(k == DT - 1))
                    last.then_inc(pe_group, 1)
                    pe.wait_ge(act_evac, b * EVACS + evac_count(G_XP - 4))
                    pe.wait_ge(xc_ready, b * MT + MT)
                    for m in range(MT):
                        last = pe.matmul(bank(G_XP)[0:RANK + 2 * DS], w_x[:, m], xc[:, m], start=(m == 0), stop=(m == MT - 1))
                    last.then_inc(pe_group, 1)
                    pe.wait_ge(act_evac, b * EVACS + evac_count(G_XP))
                    for m in range(MT):
                        pe.matmul(bank(G_DT + m), w_dt[:, m * P:(m + 1) * P], xp[0:RANK, :], start=True,
                                  stop=True).then_inc(pe_group, 1)

                    def sum_q(f):
                        pe.wait_ge(act_evac, b * EVACS + evac_count(G_HID + f))
                        pe.matmul(ps[0:R0, 4], u2[:, f], hidden[:, f % 2], start=(f == 0),
                                  stop=(f == FT0 - 1)).then_inc(q_summed, 1)

                    for f in range(FT0):
                        if f < 4:
                            pe.wait_ge(sp_x_ready, b * MT + f + 1)
                        else:
                            pe.wait_ge(act_evac, b * EVACS + evac_count(G_HID + f - 4))
                        pe.matmul(bank(G_HID + f), v1[:, f * P:(f + 1) * P], low[:, :], start=True,
                                  stop=True).then_inc(pe_group, 1)
                        if f >= 1:
                            sum_q(f - 1)
                    sum_q(FT0 - 1)
                    pe.wait_ge(act_evac, b * EVACS + Q_EVAC)
                    for j in range(2):
                        for i in (2 * j, 2 * j + 1):
                            last = pe.matmul(bank(G_FFN + j)[:, i % 2 * D:(i % 2 + 1) * D], q1[:, i * P:(i + 1) * P],
                                             v2b[:, :], start=True, stop=True)
                        last.then_inc(pe_group, 1)
                    for n in range(STEPS):
                        s, m = divmod(n, MT)
                        pe.wait_ge(hc_ready, b * STEPS + n + 1)
                        pe.matmul(ps[:, 4 + m], ident[:, :], hc[:, n % RING], start=(s == 0),
                                  stop=(s == DS - 1)).then_inc(y_summed, 1)
                    pe.wait_ge(y_gated, b * MT + MT)
                    for j in range(2):
                        for i in (2 * j, 2 * j + 1):
                            for m in range(MT):
                                last = pe.matmul(bank(G_S + j)[:, i % 2 * D:(i % 2 + 1) * D],
                                                 conv[:, m, i * P:(i + 1) * P], w_out[:, m], start=(m == 0),
                                                 stop=(m == MT - 1))
                        last.then_inc(pe_group, 1)


def batches(eng, body):
    with eng.Fori(0, NB - 1) as b:
        body(b, True)
    body(NB - 1, False)


LC = 64
NC = T // LC
NE1, TOP1 = 8, 2
CAP1 = int(T * TOP1 / NE1 * 1.5) + 1
V_WIDTH = NH * QUAD


def stage_chunks_in(nc, w, x_in, xn_out, q_out, k_out, v_out, gate_out):
    with Chip(nc, "chunks_in") as c:
        ident = c.sb("ident", [P, P])
        w_qkv = c.sb("w_qkv", [P, DT, 3 * D])
        wr = c.sb("wr", [P, DT, NE1])
        we = c.sb("we", [P, DT, NE1, D])
        earlier = c.sb("earlier", [P, P])
        ones = c.sb("ones", [P, P])
        order = c.sb("order", [P, NE1])
        x = c.sb("x", [P, TT, D])
        ln = LayerNorm(c)
        xn = ln.xn
        xn_t = c.sb("xn_t", [P, DT, T])
        v = c.sb("v", [P, TT, NH, QUAD])
        lg, eq, val, sel1, lg2, sel2, t1, t2, any_, keep, coef = (
            c.sb(n, [P, TT, NE1]) for n in ("lg", "eq", "val", "sel1", "lg2", "sel2", "t1", "t2", "any", "keep", "coef"))
        m1, m2, best, w1, w2 = (c.sb(n, [P, TT]) for n in ("m1", "m2", "best", "w1", "w2"))
        moe = c.sb("moe", [P, TT, D])
        gate = c.sb("gate", [P, TT, D])
        ps = c.psum()
        split = Split(c, q_out, k_out)

        w_loaded, filled, made, ident_made = (c.sem(n) for n in ("w_loaded", "filled", "made", "ident_made"))
        x_loaded, x_free, xn_stored, v_stored, gate_stored = (
            c.sem(n) for n in ("x_loaded", "x_free", "xn_stored", "v_stored", "gate_stored"))
        xt_done, xt_copied, qk_done, v_done, v_copied, logits_done = (
            c.sem(n) for n in ("xt_done", "xt_copied", "qk_done", "v_done", "v_copied", "logits_done"))
        route, any_ready, queue_done, w2_ready, gap_ready, coef_step, coef_ready = (
            c.sem(n) for n in ("route", "any", "queue_done", "w2", "gap", "coef_step", "coef"))
        moe_done, moe_sum, gate_ready = (c.sem(n) for n in ("moe_done", "moe_sum", "gate"))

        ROUTE = 16
        UNITS = TT * NE1 // 2
        SUMS = TT * NE1
        LOADS = 3 + 2 * DT
        FILLS = 6

        def all_made(eng):
            eng.wait_ge(w_loaded, LOADS * DMA)
            eng.wait_ge(ident_made, 2)
            eng.wait_ge(made, 2)
            eng.wait_ge(filled, FILLS)

        with nc.Block() as block:

            @block.sync
            def _(sp):
                def load_x(b):
                    sp.dma_start(x[:, :, :], token_tiles(x_in, b)).then_inc(x_loaded, DMA)

                load_x(0)
                for n, name in enumerate(("Wq_l", "Wk_l", "Wv_l")):
                    sp.dma_start(w_qkv[:, :, n * D:(n + 1) * D], w[name].rearrange("(k p) n -> p k n", p=P)).then_inc(w_loaded, DMA)
                with nc.allow_non_contiguous_dma(reason="the router's weight transposed, once"):
                    for m in range(DT):
                        sp.dma_start(wr[:, m, :], w["Wr"][:, m * P:(m + 1) * P].rearrange("e p -> p e")).then_inc(w_loaded, DMA)
                for m in range(DT):
                    sp.dma_start(we[:, m], w["We"][:, m * P:(m + 1) * P, :].rearrange("e p n -> p e n")).then_inc(w_loaded, DMA)
                for stored in (xn_stored, v_stored, gate_stored):
                    sp.sem_inc(stored, DMA)
                split.sp_setup(sp)

                def body(b, more):
                    sp.wait_ge(ln.ready, b * TT + TT)
                    sp.dma_start(token_tiles(xn_out, b), xn[:, :, :]).then_inc(xn_stored, DMA)
                    if more:
                        sp.wait_ge(x_free, b + 1)
                        load_x(b + 1)
                    for n in range(split.TILES):
                        split.sp(sp, b, n)
                    sp.wait_ge(v_copied, b * 2 + 4)
                    sp.dma_start(token_tiles(v_out, b), v[:, :, :, :].rearrange("p i h e -> p i (h e)")).then_inc(v_stored, DMA)
                    sp.wait_ge(gate_ready, b + 2)
                    sp.dma_start(token_tiles(gate_out, b), gate[:, :, :]).then_inc(gate_stored, DMA)

                batches(sp, body)
                for stored in (xn_stored, v_stored, gate_stored):
                    sp.wait_ge(stored, (NB + 1) * DMA)
                sp.wait_ge(split.stored, (NB + 1) * split.STORES * DMA)

            @block.gpsimd
            def _(pool):
                make_identity(pool, ident, ident_made)
                pool.wait_ge(filled, FILLS)
                pool.affine_select(out=earlier[:, :], in_=earlier[:, :], compare_op=ALU.is_gt, fill=0.0, base=0,
                                   pattern=[[1, P]], channel_multiplier=-1).then_inc(made, 1)
                pool.iota(order[:, :], [[-1, NE1]], base=NE1, channel_multiplier=0,
                          allow_small_or_imprecise_dtypes=True).then_inc(made, 1)
                split.pool_setup(pool)
                with pool.Fori(0, NB) as b:
                    for n in range(split.TILES):
                        split.pool(pool, b, n)

            @block.scalar
            def _(act):
                ln.act_setup(act)
                all_made(act)
                split.act_setup(act)
                act.sem_inc(gate_ready, 1)

                def turn_copies(b):
                    for m in range(DT):
                        act.wait_ge(xt_done, b * DT + m + 3)
                        act.copy(xn_t[:, m], ps[:, m]).then_inc(xt_copied, 1)

                def body(b, more):
                    for n in range(split.TILES):
                        act.wait_ge(qk_done, b * split.TILES + n + 1)
                        split.act(act, b, n, ps[:, 2 + n])
                    act.wait_ge(gap_ready, b + 1)
                    act.activation(w2[:, :], w2[:, :], ACT.Exp).then_inc(w2_ready, 1)
                    if more:
                        ln.act(act, b + 1)
                        turn_copies(b + 1)
                    act.wait_ge(moe_sum, (b + 1) * SUMS + 1)
                    act.wait_ge(gate_stored, b * DMA + DMA)
                    act.activation(gate[:, :, :], moe[:, :, :], ACT.Silu).then_inc(gate_ready, 1)

                ln.act(act, 0)
                turn_copies(0)
                batches(act, body)

            @block.vector
            def _(dve):
                steps = [0]

                def fill(tile, value):
                    dve.memset(tile, value).then_inc(filled, 1)
                    steps[0] += 1
                    dve.wait_ge(filled, steps[0])

                fill(v[:, :, :, :], 0.0)
                fill(v[:, :, :, HD:HD + 1], 1.0)
                fill(earlier[:, :], 1.0)
                fill(ones[:, :], 1.0)
                fill(any_[:, :, :], 0.0)
                fill(moe[:, :, :], 0.0)
                assert steps[0] == FILLS
                ln.dve_setup(dve)
                split.dve_setup(dve)
                all_made(dve)
                dve.sem_inc(v_copied, 2)
                dve.sem_inc(moe_sum, 1)

                def norm(b):
                    dve.wait_ge(x_loaded, b * DMA + DMA)
                    dve.wait_ge(xn_stored, b * DMA + DMA)
                    dve.wait_ge(xt_done, b * DT + 2)
                    ln.dve(dve, b, x)
                    dve.wait_ge(ln.ready, b * TT + TT)
                    dve.sem_inc(x_free, 1)

                def body(b, more):
                    for n in range(split.TILES):
                        split.dve(dve, b, n)
                    dve.wait_ge(v_stored, b * DMA + DMA)
                    for j in range(2):
                        dve.wait_ge(v_done, b * 2 + j + 1)
                        dve.tensor_copy(v[:, 2 * j:2 * j + 2, :, 0:HD],
                                        ps[:, 6 + j].rearrange("p (i h e) -> p i h e", i=2, h=NH)).then_inc(v_copied, 1)
                    dve.wait_ge(logits_done, b + 1)
                    count = [0]

                    def link(ins):
                        ins.then_inc(route, 1)
                        count[0] += 1
                        dve.wait_ge(route, b * ROUTE + count[0])

                    def wide(column):
                        return column[:, :].unsqueeze(2).broadcast_to([P, TT, NE1])

                    order_b = order[:, :].unsqueeze(1).broadcast_to([P, TT, NE1])
                    link(dve.tensor_copy(lg[:, :, :], ps[:, 0, 0:TT * NE1].rearrange("p (i e) -> p i e", e=NE1)))
                    for logits, top, sel in ((lg, m1, sel1), (lg2, m2, sel2)):
                        link(dve.reduce_max(top[:, :], logits[:, :, :], AX.X))
                        link(dve.tensor_tensor(eq[:, :, :], logits[:, :, :], wide(top), ALU.is_equal))
                        link(dve.tensor_tensor(val[:, :, :], eq[:, :, :], order_b, ALU.mult))
                        link(dve.reduce_max(best[:, :], val[:, :, :], AX.X))
                        link(dve.tensor_tensor(sel[:, :, :], val[:, :, :], wide(best), ALU.is_equal))
                        if sel is sel1:
                            link(dve.scalar_tensor_tensor(lg2[:, :, :], sel1[:, :, :], -3.0e38, lg[:, :, :], ALU.mult, ALU.add))
                    dve.tensor_tensor(any_[:, :, :], sel1[:, :, :], sel2[:, :, :], ALU.add).then_inc(any_ready, 1)
                    dve.tensor_tensor(w2[:, :], m2[:, :], m1[:, :], ALU.subtract).then_inc(gap_ready, 1)
                    dve.wait_ge(w2_ready, b + 1)
                    link(dve.tensor_scalar(w1[:, :], w2[:, :], 1.0, None, ALU.add))
                    link(dve.reciprocal(w1[:, :], w1[:, :]))
                    link(dve.tensor_tensor(w2[:, :], w2[:, :], w1[:, :], ALU.mult))
                    dve.wait_ge(queue_done, b + 1)
                    dve.tensor_scalar(keep[:, :, :], ps[:, 1, 0:TT * NE1].rearrange("p (i e) -> p i e", e=NE1), float(CAP1),
                                      None, ALU.is_lt).then_inc(coef_step, 1)
                    dve.tensor_tensor(t1[:, :, :], sel1[:, :, :], wide(w1), ALU.mult).then_inc(coef_step, 1)
                    dve.tensor_tensor(t2[:, :, :], sel2[:, :, :], wide(w2), ALU.mult).then_inc(coef_step, 1)
                    dve.wait_ge(coef_step, b * 3 + 3)
                    link(dve.tensor_tensor(t1[:, :, :], t1[:, :, :], t2[:, :, :], ALU.add))
                    dve.tensor_tensor(coef[:, :, :], t1[:, :, :], keep[:, :, :], ALU.mult).then_inc(coef_ready, 1)
                    assert count[0] == ROUTE
                    dve.wait_ge(coef_ready, b + 1)
                    dve.wait_ge(gate_ready, b + 1)

                    def experts(i):
                        for e in range(NE1):
                            n = i * NE1 + e
                            if e % 2 == 0:
                                dve.wait_ge(moe_done, b * UNITS + n // 2 + 1)
                            product = ps[:, 2 + e // 2, e % 2 * D:(e % 2 + 1) * D]
                            if e == 0:
                                dve.tensor_scalar(moe[:, i], product, coef[:, i, e:e + 1], None, ALU.mult).then_inc(moe_sum, 1)
                            else:
                                dve.wait_ge(moe_sum, b * SUMS + n + 1)
                                dve.scalar_tensor_tensor(moe[:, i], product, coef[:, i, e:e + 1], moe[:, i], ALU.mult,
                                                         ALU.add).then_inc(moe_sum, 1)

                    experts(0)
                    experts(1)
                    if more:
                        norm(b + 1)
                    experts(2)
                    experts(3)

                norm(0)
                batches(dve, body)

            @block.tensor
            def _(pe):
                all_made(pe)
                pe.sem_inc(xt_done, 2)

                def turn(b):
                    pe.wait_ge(ln.ready, b * TT + TT)
                    for m in range(DT):
                        for i in range(TT):
                            last = pe.transpose(ps[:, m, i * P:(i + 1) * P], xn[:, i, m * P:(m + 1) * P], ident[:, :])
                        last.then_inc(xt_done, 1)

                def body(b, more):
                    pe.wait_ge(xt_copied, b * DT + DT)
                    pe.wait_ge(moe_sum, b * SUMS + 1)
                    for n in range(split.TILES):
                        for m in range(DT):
                            last = pe.matmul(ps[:, 2 + n], w_qkv[:, m, n * P:(n + 1) * P], xn_t[:, m], start=(m == 0),
                                             stop=(m == DT - 1))
                        last.then_inc(qk_done, 1)
                    for i in range(TT):
                        for m in range(DT):
                            last = pe.matmul(ps[:, 0, i * NE1:(i + 1) * NE1], xn_t[:, m, i * P:(i + 1) * P], wr[:, m],
                                             start=(m == 0), stop=(m == DT - 1))
                    last.then_inc(logits_done, 1)
                    for j in range(2):
                        pe.wait_ge(v_copied, b * 2 + j + 1)
                        for i in (2 * j, 2 * j + 1):
                            for m in range(DT):
                                last = pe.matmul(ps[:, 6 + j, i % 2 * D:(i % 2 + 1) * D], xn_t[:, m, i * P:(i + 1) * P],
                                                 w_qkv[:, m, 2 * D:], start=(m == 0), stop=(m == DT - 1))
                        last.then_inc(v_done, 1)

                    def experts(units):
                        for u in units:
                            i, j = divmod(u, NE1 // 2)
                            if i == 0:
                                pe.wait_ge(split.copied, b * split.TILES + j + 1 + split.TILES)
                            else:
                                pe.wait_ge(moe_sum, b * SUMS + (i - 1) * NE1 + 2 * j + 3)
                            for m in range(DT):
                                last = pe.matmul(ps[:, 2 + j], xn_t[:, m, i * P:(i + 1) * P],
                                                 we[:, m, 2 * j:2 * j + 2, :].rearrange("p e n -> p (e n)"),
                                                 start=(m == 0), stop=(m == DT - 1))
                            last.then_inc(moe_done, 1)

                    experts(range(4))
                    pe.wait_ge(any_ready, b + 1)
                    queue = ps[:, 1, 0:TT * NE1]
                    pe.matmul(queue, earlier[:, :], any_[:, :, :].rearrange("p i e -> p (i e)"), start=True, stop=False)
                    for j in range(1, TT):
                        last = pe.matmul(queue[:, j * NE1:], ones[:, :], any_[:, 0:TT - j, :].rearrange("p i e -> p (i e)"),
                                         start=False, stop=(j == TT - 1))
                    last.then_inc(queue_done, 1)
                    experts(range(4, UNITS))
                    if more:
                        turn(b + 1)

                turn(0)
                batches(pe, body)


APART = 2.0 ** 90


def stage_chunks_attend(nc, w, xn_in, q_in, k_in, v_in, chunks_out, means_out):
    with Chip(nc, "chunks") as c:
        PARITY = P // LC
        MASK, SHIFT = KQK, KQK + PARITY
        KA, KB = SHIFT, SHIFT + NPART
        ident_b = c.sb("ident_b", [P, P], BF16)
        wo = c.sb("wo", [P, NG, D])
        chunk_mean = c.sb("chunk_mean", [P, TT, NC])
        qs = c.sb("qs", [P, NG, GH, T], BF16)
        ks = c.sb("ks", [P, NG, GH, T], BF16)
        v = c.sb("v", [P, NG, TT, GH * QUAD])
        xn = c.sb("xn", [P, TT, D])
        row_max = c.sb("row_max", [P, 2, GH * TT])
        rest = c.sb("rest", [P, 2, GH * TT])
        shift = c.sb("shift", [P, 2, GH * TT, QUAD], BF16)
        probs = c.sb("probs", [P, 2, GH, T])
        context = Context(c)
        chunks = c.sb("chunks", [P, TT, D])
        means = c.sb("means", [NC, D])
        ps = c.psum()

        w_loaded, filled, made = (c.sem(n) for n in ("w_loaded", "filled", "made"))
        qk_loaded, v_loaded = ([c.sem(f"{n}_loaded{g}") for g in range(NG)] for n in ("qk", "v"))
        xn_loaded, chunks_stored, means_stored = (c.sem(n) for n in ("xn_loaded", "chunks_stored", "means_stored"))
        a_done, a_max, shift_step, shift_ready, max_turned, max_copied = (
            c.sem(n) for n in ("a_done", "a_max", "shift_step", "shift_ready", "max_turned", "max_copied"))
        s_done, p_ready, pv_done = (c.sem(n) for n in ("s_done", "p_ready", "pv_done"))
        proj_done, chunks_ready, means_done, means_copied = (
            c.sem(n) for n in ("proj_done", "chunks", "means_done", "means_copied"))

        PAIRS = GH // 2
        CHAIN = 3
        LOADS = GH
        FILLS, MADE = 5 + 3 * NG, 1 + 2 * NG + PARITY + 2
        K_LOADS = 2 * len(STACK)

        def all_made(eng):
            eng.wait_ge(w_loaded, LOADS * DMA)
            eng.wait_ge(made, MADE)
            eng.wait_ge(filled, FILLS)

        def run(eng, step):
            step(0, 0, (0, 2), None, None, None)
            step(0, 1, (0, 3), (0, 0), None, None)
            with eng.Fori(0, NB - 1) as b:
                step(b, 2, (b + 1, 0), (b, 1), (b, 0), None)
                step(b, 3, (b + 1, 1), (b, 2), (b, 1), None)
                step(b + 1, 0, (b + 1, 2), (b, 3), (b, 2), None)
                step(b + 1, 1, (b + 1, 3), (b + 1, 0), (b, 3), b)
            step(NB - 1, 2, None, (NB - 1, 1), (NB - 1, 0), None)
            step(NB - 1, 3, None, (NB - 1, 2), (NB - 1, 1), None)
            step(None, None, None, (NB - 1, 3), (NB - 1, 2), None)
            step(None, None, None, None, (NB - 1, 3), NB - 1)

        with nc.Block() as block:

            @block.sync
            def _(sp):
                sp.wait_ge(filled, FILLS)
                sp.wait_ge(made, MADE)
                load_head_rows(sp, wo, w["Wo_l"], w_loaded)

                def load_qk(b, g):
                    load_stack(sp, qs[:, g], q_in, b, g, False, qk_loaded[g])
                    load_stack(sp, ks[:, g], k_in, b, g, True, qk_loaded[g])

                def load_v(b, g):
                    sp.dma_start(v[:, g], token_tiles(v_in, b)[:, :, g * GH * QUAD:(g + 1) * GH * QUAD]).then_inc(v_loaded[g], DMA)

                def load_xn(b):
                    sp.dma_start(xn[:, :, :], token_tiles(xn_in, b)).then_inc(xn_loaded, DMA)

                for g in range(NG):
                    load_qk(0, g)
                    load_v(0, g)
                load_xn(0)
                with sp.Fori(0, NB - 1) as b:
                    for g in range(NG):
                        sp.wait_ge(s_done, (b * NG + g + 1) * PAIRS)
                        load_qk(b + 1, g)
                        sp.wait_ge(pv_done, b * NG + g + 3)
                        load_v(b + 1, g)
                    sp.wait_ge(chunks_ready, b * 2 + 3)
                    load_xn(b + 1)

            @block.gpsimd
            def _(pool):
                pool.wait_ge(filled, FILLS)
                count = [0]

                def select(tile, compare, fill, base, pattern, per_row):
                    pool.affine_select(out=tile, in_=tile, compare_op=compare, fill=fill, base=base, pattern=pattern,
                                       channel_multiplier=per_row).then_inc(made, 1)
                    count[0] += 1
                    pool.wait_ge(made, count[0])

                select(ident_b[:, :], ALU.not_equal, 1.0, 0, [[-1, P]], 1)
                for g in range(NG):
                    for tile, value, base in ((qs, NEG, 0), (ks, APART, -1)):
                        select(tile[MASK:SHIFT, g].rearrange("p h (i c t) -> p (h i) c t", i=TT, c=PARITY), ALU.not_equal, value,
                               base, [[0, GH * TT], [1, PARITY], [0, LC]], -1 if base == 0 else 1)
                for r in range(PARITY):
                    select(shift[:, :, :, r], ALU.is_ge, 0.0, (LC - 1, -LC)[r], [[0, 2 * GH * TT]], (-1, 1)[r])
                select(chunk_mean[:, :, :], ALU.is_ge, 0.0, 0, [[P, TT], [-LC, NC]], 1)
                select(chunk_mean[:, :, :], ALU.is_ge, 0.0, LC - 1, [[-P, TT], [LC, NC]], -1)
                assert count[0] == MADE

            @block.scalar
            def _(act):
                all_made(act)
                act.sem_inc(max_copied, GH)
                act.sem_inc(p_ready, PAIRS)
                act.sem_inc(means_copied, 1)
                act.sem_inc(chunks_stored, DMA)
                act.sem_inc(means_stored, DMA)

                def exp(b, g, pair):
                    n = b * NG + g
                    act.wait_ge(s_done, n * PAIRS + pair + 1)
                    if pair == 0:
                        act.wait_ge(pv_done, n + 1)
                    act.activation(probs[:, g % 2, 2 * pair:2 * pair + 2], ps[:, 2 + 2 * pair:4 + 2 * pair], ACT.Exp,
                                   scale=SCALE).then_inc(p_ready, 1)

                def shifts(b, g, heads):
                    act.wait_ge(max_turned, b * NG + g + 3)
                    for h in heads:
                        act.copy(qs[MASK:KB, g, h], ps[h * QUAD:h * QUAD + KB - MASK, 7]).then_inc(max_copied, 1)

                def finish(b):
                    act.wait_ge(chunks_ready, b * 2 + 3)
                    act.dma_start(token_tiles(chunks_out, b), chunks[:, :, :]).then_inc(chunks_stored, DMA)
                    act.wait_ge(means_done, b + 1)
                    act.wait_ge(means_stored, b * DMA + DMA)
                    act.copy(means[:, :], ps[0:NC, 7, 0:D]).then_inc(means_copied, 1)
                    act.wait_ge(means_copied, b + 2)
                    act.dma_start(means_out[b], means[:, :]).then_inc(means_stored, DMA)

                def step(b, g, first, before, ended, done):
                    if g is not None:
                        for pair in range(PAIRS):
                            exp(b, g, pair)
                        if not (g == NG - 1 and first is None):
                            nxt = (b, g + 1) if g + 1 < NG else (b + 1, 0)
                            shifts(*nxt, range(GH))
                    if done is not None:
                        finish(done)

                shifts(0, 0, range(GH))
                run(act, step)
                act.wait_ge(chunks_stored, (NB + 1) * DMA)
                act.wait_ge(means_stored, (NB + 1) * DMA)

            @block.vector
            def _(dve):
                count = [0]

                def fill(tile, value):
                    dve.memset(tile, value).then_inc(filled, 1)
                    count[0] += 1
                    dve.wait_ge(filled, count[0])

                for tile in (ident_b[:, :], wo[:, :, :], shift[:, :, :, :]):
                    fill(tile, 0.0)
                fill(shift[:, :, :, 0:PARITY], NEG)
                fill(chunk_mean[:, :, :], 1.0 / LC)
                for g in range(NG):
                    fill(qs[MASK:SHIFT, g], 0.0)
                    fill(ks[MASK:KB, g], 1.0)
                    fill(ks[MASK:SHIFT, g], 0.0)
                assert count[0] == FILLS
                all_made(dve)
                dve.sem_inc(a_max, 1)
                dve.sem_inc(chunks_ready, 1)
                context.dve_setup(dve)

                def maxima(b, g, pair):
                    n = b * NG + g
                    dve.wait_ge(a_done, n * PAIRS + pair + 1)
                    dve.reduce_max(row_max[:, g % 2, pair * 2 * TT:(pair + 1) * 2 * TT],
                                   ps[:, 0:2].rearrange("p h (i k) -> p (h i) k", k=P), AX.X).then_inc(a_max, 1)

                def split_maxima(b, g):
                    n = b * NG + g
                    dve.wait_ge(a_max, (n + 1) * PAIRS + 1)
                    dve.wait_ge(max_turned, n + 1)
                    part = [shift[:, g % 2, :, PARITY + k] for k in range(NPART)]
                    dve.tensor_scalar(part[0], row_max[:, g % 2], -1.0, None, ALU.mult).then_inc(shift_step, 1)
                    dve.wait_ge(shift_step, n * CHAIN + 1)
                    dve.scalar_tensor_tensor(rest[:, g % 2], row_max[:, g % 2], -1.0, part[0], ALU.mult,
                                             ALU.subtract).then_inc(shift_step, 1)
                    dve.wait_ge(shift_step, n * CHAIN + 2)
                    dve.tensor_copy(part[1], rest[:, g % 2]).then_inc(shift_step, 1)
                    dve.wait_ge(shift_step, n * CHAIN + 3)
                    dve.tensor_tensor(part[2], rest[:, g % 2], part[1], ALU.subtract).then_inc(shift_ready, 1)

                def add_xn(b, j):
                    dve.wait_ge(proj_done, b * 2 + j + 1)
                    if j == 0:
                        dve.wait_ge(xn_loaded, b * DMA + DMA)
                        dve.wait_ge(chunks_stored, b * DMA + DMA)
                    tiles = slice(2 * j, 2 * j + 2)
                    dve.tensor_tensor(chunks[:, tiles, :], xn[:, tiles, :], ps[:, 7].rearrange("p (i n) -> p i n", n=D),
                                      ALU.add).then_inc(chunks_ready, 1)

                def step(b, g, first, before, ended, done):
                    if ended is not None:
                        b, g = ended
                        dve.wait_ge(pv_done, b * NG + g + 3)
                        context.turn(dve, ps[:, 6])
                    if first is not None:
                        maxima(*first, 0)
                    if ended is not None:
                        context.scale(dve, b * NG + g)
                        if g == 0 and not (isinstance(b, int) and b == 0):
                            dve.wait_ge(proj_done, b * 2)
                        context.turn_back(dve, b * NG + g, g)
                    if first is not None:
                        maxima(*first, 1)
                        split_maxima(*first)
                    if done is not None:
                        for j in range(2):
                            add_xn(done, j)

                for g in range(2):
                    for pair in range(PAIRS):
                        maxima(0, g, pair)
                    split_maxima(0, g)
                run(dve, step)

            @block.tensor
            def _(pe):
                all_made(pe)
                pe.sem_inc(pv_done, 2)
                pe.sem_inc(max_turned, 2)

                def first_scores(b, g, pair):
                    n = b * NG + g
                    if pair == 0:
                        pe.wait_ge(qk_loaded[g], (b + 1) * K_LOADS * DMA)
                    pe.wait_ge(a_max, n * PAIRS + pair + 1)
                    for j in range(2):
                        h = 2 * pair + j
                        for i in range(TT):
                            cols = slice(i * P, (i + 1) * P)
                            last = pe.matmul(ps[:, j, cols], qs[0:KA, g, h, cols], ks[0:KA, g, h, cols], start=True, stop=True)
                    last.then_inc(a_done, 1)

                def turn_maxima(b, g):
                    n = b * NG + g
                    pe.wait_ge(shift_ready, n + 1)
                    pe.wait_ge(max_copied, n * GH + GH)
                    if not (isinstance(b, int) and b == 0):
                        pe.wait_ge(means_copied, b + (1 if g == 3 else 0))
                    for h in range(GH):
                        for i in range(TT):
                            last = pe.matmul(ps[h * QUAD:(h + 1) * QUAD, 7, i * P:(i + 1) * P], shift[:, g % 2, h * TT + i, :],
                                             ident_b[:, :], start=True, stop=True)
                    last.then_inc(max_turned, 1)

                def second_scores(b, g, pair):
                    n = b * NG + g
                    if pair == 0:
                        pe.wait_ge(max_copied, n * GH + 2 * GH)
                    pe.wait_ge(p_ready, n * PAIRS + pair + 1)
                    for j in range(2):
                        h = 2 * pair + j
                        for i in range(TT):
                            cols = slice(i * P, (i + 1) * P)
                            last = pe.matmul(ps[:, 2 + h, cols], ks[0:KB, g, h, cols], qs[0:KB, g, h, cols], start=True, stop=True)
                    last.then_inc(s_done, 1)

                def output(b, g):
                    n = b * NG + g
                    pe.wait_ge(v_loaded[g], (b + 1) * DMA)
                    context.bank_free(pe, n)
                    pe.wait_ge(p_ready, (n + 1) * PAIRS + PAIRS)
                    for i in range(TT):
                        cols = slice(i * P, (i + 1) * P)
                        for h in range(GH):
                            last = pe.matmul(ps[h * QUAD:(h + 1) * QUAD, 6, cols], v[:, g, i, h * QUAD:(h + 1) * QUAD],
                                             probs[:, g % 2, h, cols], start=True, stop=True)
                    last.then_inc(pv_done, 1)

                def project(b, shifted):
                    pe.wait_ge(context.ready, b * NG + NG)
                    if shifted:
                        pe.wait_ge(max_copied, b * NG * GH + (NG + 3) * GH + GH)
                    for j in range(2):
                        pe.wait_ge(chunks_ready, b * 2 + j + 1)
                        for i in (2 * j, 2 * j + 1):
                            for g in range(NG):
                                last = pe.matmul(ps[:, 7, i % 2 * D:(i % 2 + 1) * D], context.ctx[:, g, i * P:(i + 1) * P], wo[:, g],
                                                 start=(g == 0), stop=(g == NG - 1))
                        last.then_inc(proj_done, 1)
                    pe.wait_ge(chunks_ready, b * 2 + 3)
                    for i in range(TT):
                        last = pe.matmul(ps[0:NC, 7, 0:D], chunk_mean[:, i], chunks[:, i], start=(i == 0), stop=(i == TT - 1))
                    last.then_inc(means_done, 1)

                def step(b, g, first, before, ended, done):
                    if first is not None:
                        first_scores(*first, 0)
                    if g is not None:
                        for pair in range(PAIRS):
                            second_scores(b, g, pair)
                        if not (g == NG - 1 and first is None):
                            turn_maxima(*((b, g + 1) if g + 1 < NG else (b + 1, 0)))
                    if before is not None:
                        output(*before)
                    if first is not None:
                        first_scores(*first, 1)
                    if done is not None:
                        project(done, g is not None)

                for g in range(2):
                    for pair in range(PAIRS):
                        first_scores(0, g, pair)
                turn_maxima(0, 0)
                run(pe, step)


def stage_chunk_means(nc, w, means_in, out):
    with Chip(nc, "means") as c:
        R = NB * NC
        ident = c.sb("ident", [P, P])
        wq, wk, wv, wo = (c.sb(n, [P, DT, D]) for n in ("wq", "wk", "wv", "wo"))
        head_rows = c.sb("head_rows", [P, DT, NH, R])
        apart = c.sb("apart", [R, NB, NC])
        x = c.sb("x", [R, D])
        x_t, q, k = (c.sb(n, [P, DT, R]) for n in ("x_t", "q", "k"))
        v = c.sb("v", [R, D])
        k_heads = c.sb("k_heads", [P, DT, NH, R])
        s = c.sb("s", [R, NH, R])
        top, den = (c.sb(n, [R, NH]) for n in ("top", "den"))
        p_t = c.sb("p_t", [R, NH, R])
        o = c.sb("o", [R, D])
        o_t = c.sb("o_t", [P, DT, R])
        y = c.sb("y", [R, D])
        ps = c.psum()
        loaded, stored, filled, made, ident_made = (c.sem(n) for n in ("loaded", "stored", "filled", "made", "ident_made"))
        pe_done, act_done, dve_done = (c.sem(n) for n in ("pe_done", "act_done", "dve_done"))
        MASKED = -1.0e30

        with nc.Block() as block:

            @block.sync
            def _(sp):
                sp.dma_start(x[:, :], means_in).then_inc(loaded, DMA)
                for dst, name in ((wq, "Wq_g"), (wk, "Wk_g"), (wv, "Wv_g"), (wo, "Wo_g")):
                    sp.dma_start(dst[:, :, :], w[name].rearrange("(k p) n -> p k n", p=P)).then_inc(loaded, DMA)
                sp.wait_ge(dve_done, 9)
                sp.dma_start(out, y[:, :]).then_inc(stored, DMA)
                sp.wait_ge(stored, DMA)

            @block.gpsimd
            def _(pool):
                make_identity(pool, ident, ident_made)
                pool.wait_ge(filled, 2)
                count = [0]

                def select(tile, fill, base, pattern, per_row):
                    pool.affine_select(out=tile, in_=tile, compare_op=ALU.is_ge, fill=fill, base=base, pattern=pattern,
                                       channel_multiplier=per_row).then_inc(made, 1)
                    count[0] += 1
                    pool.wait_ge(made, count[0])

                select(head_rows[:, :, :, :], 0.0, 0, [[P, DT], [-HD, NH], [0, R]], 1)
                select(head_rows[:, :, :, :], 0.0, HD - 1, [[-P, DT], [HD, NH], [0, R]], -1)
                select(apart[:, :, :], MASKED, 0, [[-NC, NB], [0, NC]], 1)
                select(apart[:, :, :], MASKED, NC - 1, [[NC, NB], [0, NC]], -1)

            @block.scalar
            def _(act):
                act.wait_ge(pe_done, 1)
                act.copy(x_t[:, :, :], ps[:, 0, 0:DT * R].rearrange("p (m r) -> p m r", r=R)).then_inc(act_done, 1)
                act.wait_ge(pe_done, 2)
                act.copy(k[:, :, :], ps[:, 1, 0:DT * R].rearrange("p (m r) -> p m r", r=R)).then_inc(act_done, 1)
                act.copy(q[:, :, :], ps[:, 2, 0:DT * R].rearrange("p (m r) -> p m r", r=R)).then_inc(act_done, 1)
                act.copy(v[:, :], ps[0:R, 3, 0:D]).then_inc(act_done, 1)
                act.wait_ge(dve_done, 5)
                act.activation(s[:, :, :], s[:, :, :], ACT.Exp, scale=SCALE).then_inc(act_done, 1)
                act.wait_ge(pe_done, 4)
                act.copy(p_t[:, :, :], ps[0:R, 4:6].rearrange("p j (h r) -> p (j h) r", r=R)).then_inc(act_done, 1)
                act.wait_ge(pe_done, 5)
                act.copy(o[:, :], ps[0:R, 0, 0:D]).then_inc(act_done, 1)
                act.wait_ge(pe_done, 6)
                act.copy(o_t[:, :, :], ps[:, 1, 0:DT * R].rearrange("p (m r) -> p m r", r=R)).then_inc(act_done, 1)

            @block.vector
            def _(dve):
                dve.memset(head_rows[:, :, :, :], 1.0).then_inc(filled, 1)
                dve.memset(apart[:, :, :], 0.0).then_inc(filled, 1)
                dve.wait_ge(made, 4)
                dve.wait_ge(act_done, 2)
                for m in range(DT):
                    dve.tensor_tensor(k_heads[:, m], head_rows[:, m], k[:, m].unsqueeze(1).broadcast_to([P, NH, R]),
                                      ALU.mult).then_inc(dve_done, 1)
                dve.wait_ge(pe_done, 3)
                dve.tensor_tensor(s[:, :, :], ps[0:R, 6:8].rearrange("p j (h r) -> p (j h) r", r=R),
                                  apart[:, :, :].rearrange("p b n -> p (b n)").unsqueeze(1).broadcast_to([R, NH, R]),
                                  ALU.add).then_inc(dve_done, 1)
                dve.wait_ge(dve_done, 3)
                dve.reduce_max(top[:, :], s[:, :, :], AX.X).then_inc(dve_done, 1)
                dve.wait_ge(dve_done, 4)
                dve.tensor_tensor(s[:, :, :], s[:, :, :], top[:, :].unsqueeze(2).broadcast_to([R, NH, R]),
                                  ALU.subtract).then_inc(dve_done, 1)
                dve.wait_ge(act_done, 5)
                dve.reduce_sum(den[:, :], s[:, :, :], AX.X).then_inc(dve_done, 1)
                dve.wait_ge(dve_done, 6)
                dve.reciprocal(den[:, :], den[:, :]).then_inc(dve_done, 1)
                dve.wait_ge(dve_done, 7)
                dve.tensor_tensor(s[:, :, :], s[:, :, :], den[:, :].unsqueeze(2).broadcast_to([R, NH, R]),
                                  ALU.mult).then_inc(dve_done, 1)
                dve.wait_ge(pe_done, 7)
                dve.tensor_tensor(y[:, :], x[:, :], ps[0:R, 2, 0:D], ALU.add).then_inc(dve_done, 1)

            @block.tensor
            def _(pe):
                pe.wait_ge(ident_made, 2)
                pe.wait_ge(loaded, 5 * DMA)
                for m in range(DT):
                    last = pe.transpose(ps[:, 0, m * R:(m + 1) * R], x[:, m * P:(m + 1) * P], ident[0:R, 0:R])
                last.then_inc(pe_done, 1)
                pe.wait_ge(act_done, 1)
                for bank, weight in ((1, wk), (2, wq)):
                    for n in range(DT):
                        for m in range(DT):
                            pe.matmul(ps[:, bank, n * R:(n + 1) * R], weight[:, m, n * P:(n + 1) * P], x_t[:, m], start=(m == 0),
                                      stop=(m == DT - 1))
                for m in range(DT):
                    last = pe.matmul(ps[0:R, 3, 0:D], x_t[:, m], wv[:, m], start=(m == 0), stop=(m == DT - 1))
                last.then_inc(pe_done, 1)
                pe.wait_ge(act_done, 4)
                pe.wait_ge(dve_done, 2)
                for j in range(2):
                    heads = slice(j * NH // 2, (j + 1) * NH // 2)
                    for m in range(DT):
                        last = pe.matmul(ps[0:R, 6 + j], q[:, m], k_heads[:, m, heads].rearrange("p h r -> p (h r)"),
                                         start=(m == 0), stop=(m == DT - 1))
                last.then_inc(pe_done, 1)
                pe.wait_ge(dve_done, 8)
                for h in range(NH):
                    j, n = divmod(h, NH // 2)
                    last = pe.transpose(ps[0:R, 4 + j, n * R:(n + 1) * R], s[:, h], ident[0:R, 0:R])
                last.then_inc(pe_done, 1)
                pe.wait_ge(act_done, 6)
                for h in range(NH):
                    last = pe.matmul(ps[0:R, 0, h * HD:(h + 1) * HD], p_t[:, h], v[:, h * HD:(h + 1) * HD], start=True, stop=True)
                last.then_inc(pe_done, 1)
                pe.wait_ge(act_done, 7)
                for m in range(DT):
                    last = pe.transpose(ps[:, 1, m * R:(m + 1) * R], o[:, m * P:(m + 1) * P], ident[0:R, 0:R])
                last.then_inc(pe_done, 1)
                pe.wait_ge(act_done, 8)
                for m in range(DT):
                    last = pe.matmul(ps[0:R, 2, 0:D], o_t[:, m], wo[:, m], start=(m == 0), stop=(m == DT - 1))
                last.then_inc(pe_done, 1)


NE2 = 8


def stage_causal_in(nc, w, x_in, chunks_in, context_in, gate_in, x_out, xn_out, q_out, k_out, v_out, probs_out):
    with Chip(nc, "causal_in") as c:
        ident = c.sb("ident", [P, P])
        chunk_of = c.sb("chunk_of", [NC, TT, P])
        w_rows = c.sb("w_rows", [P, 3 * DT, D])
        w_qkv = c.sb("w_qkv", [P, DT, 3 * D])
        wg = c.sb("wg", [P, DT, NE2])
        x1 = c.sb("x1", [P, TT, D])
        chunks = c.sb("chunks", [P, TT, D])
        context = c.sb("context", [NC, D])
        gate = c.sb("gate", [P, TT, D])
        part = c.sb("part", [P, TT, D])
        x = c.sb("x", [P, TT, D])
        ln = LayerNorm(c)
        xn = ln.xn
        xn_t = c.sb("xn_t", [P, DT, T])
        v = c.sb("v", [P, TT, NH, QUAD])
        lg, probs = c.sb("lg", [P, TT, NE2]), c.sb("gate_probs", [P, TT, NE2])
        top, total = c.sb("top", [P, TT]), c.sb("total", [P, TT])
        probs_t = c.sb("probs_t", [NE2, T])
        ps = c.psum()
        split = Split(c, q_out, k_out)
        turned = Turned(c, ps, ident, [
            (w_rows[:, n, m * P:(m + 1) * P], w_qkv[:, m, n * P:(n + 1) * P]) for n in range(3 * DT) for m in range(DT)])

        w_loaded, filled, made, ident_made = (c.sem(n) for n in ("w_loaded", "filled", "made", "ident_made"))
        loaded, x_stored, xn_stored, v_stored, probs_stored = (
            c.sem(n) for n in ("loaded", "x_stored", "xn_stored", "v_stored", "probs_stored"))
        spread, sum_ready, gated, x_ready = (c.sem(n) for n in ("context_spread", "sum_ready", "gated", "x_ready"))
        xt_done, xt_copied, qk_done, v_done, v_copied, gate_done = (
            c.sem(n) for n in ("xt_done", "xt_copied", "qk_done", "v_done", "v_copied", "gate_done"))
        gate_step, shifted, gate_exp, turn_done, probs_copied = (
            c.sem(n) for n in ("gate_step", "shifted", "gate_exp", "probs_turned", "probs_copied"))
        W_LOADS, LOADS, FILLS, GATE = 1 + DT, 4, 3, 4

        with nc.Block() as block:

            @block.sync
            def _(sp):
                def load(b):
                    for dst, src in ((x1, x_in), (chunks, chunks_in), (gate, gate_in)):
                        sp.dma_start(dst[:, :, :], token_tiles(src, b)).then_inc(loaded, DMA)
                    sp.dma_start(context[:, :], context_in[b]).then_inc(loaded, DMA)

                def sums(b, load_next):
                    sp.wait_ge(x_ready, b * 2 + 4)
                    sp.dma_start(token_tiles(x_out, b), x[:, :, :]).then_inc(x_stored, DMA)
                    if load_next:
                        load(b + 1)
                    sp.wait_ge(ln.ready, b * TT + TT)
                    sp.dma_start(token_tiles(xn_out, b), xn[:, :, :]).then_inc(xn_stored, DMA)

                load(0)
                sp.dma_start(w_rows[:, :, :], w["w_qkv"].rearrange("(n p) k -> p n k", p=P)).then_inc(w_loaded, DMA)
                with nc.allow_non_contiguous_dma(reason="the gate's weight transposed, once"):
                    for m in range(DT):
                        sp.dma_start(wg[:, m, :], w["gate_w"][:, m * P:(m + 1) * P].rearrange("e p -> p e")).then_inc(w_loaded, DMA)
                for stored in (x_stored, xn_stored, v_stored, probs_stored):
                    sp.sem_inc(stored, DMA)
                split.sp_setup(sp)

                def body(b, ahead):
                    if ahead > 0:
                        sums(b + 1, ahead > 1)
                    for n in range(split.TILES):
                        split.sp(sp, b, n)
                    sp.wait_ge(v_copied, b * 2 + 4)
                    sp.dma_start(token_tiles(v_out, b), v[:, :, :, :].rearrange("p i h e -> p i (h e)")).then_inc(v_stored, DMA)
                    sp.wait_ge(probs_copied, b + 2)
                    sp.dma_start(probs_out.rearrange("(b e) t -> b e t", e=NE2)[b], probs_t[:, :]).then_inc(probs_stored, DMA)

                sums(0, True)
                with sp.Fori(0, NB - 2) as b:
                    body(b, 2)
                body(NB - 2, 1)
                body(NB - 1, 0)
                for stored in (x_stored, xn_stored, v_stored, probs_stored):
                    sp.wait_ge(stored, (NB + 1) * DMA)
                sp.wait_ge(split.stored, (NB + 1) * split.STORES * DMA)

            @block.gpsimd
            def _(pool):
                make_identity(pool, ident, ident_made)
                pool.wait_ge(filled, FILLS)
                pool.affine_select(out=chunk_of[:, :, :], in_=chunk_of[:, :, :], compare_op=ALU.is_ge, fill=0.0, base=0,
                                   pattern=[[P, TT], [1, P]], channel_multiplier=-LC).then_inc(made, 1)
                pool.wait_ge(made, 1)
                pool.affine_select(out=chunk_of[:, :, :], in_=chunk_of[:, :, :], compare_op=ALU.is_ge, fill=0.0, base=LC - 1,
                                   pattern=[[-P, TT], [-1, P]], channel_multiplier=LC).then_inc(made, 1)
                split.pool_setup(pool)
                with pool.Fori(0, NB) as b:
                    for n in range(split.TILES):
                        split.pool(pool, b, n)

            @block.scalar
            def _(act):
                ln.act_setup(act)
                turned.act(act)
                split.act_setup(act)
                act.sem_inc(probs_copied, 1)

                def turn_copies(b):
                    for m in range(DT):
                        act.wait_ge(xt_done, b * DT + m + 3)
                        act.copy(xn_t[:, m], ps[:, m]).then_inc(xt_copied, 1)

                def body(b, more):
                    if more:
                        ln.act(act, b + 1)
                    for n in range(split.TILES):
                        act.wait_ge(qk_done, b * split.TILES + n + 1)
                        split.act(act, b, n, ps[:, 2 + n])
                    act.wait_ge(shifted, b + 2)
                    act.activation(lg[:, :, :], lg[:, :, :], ACT.Exp).then_inc(gate_exp, 1)
                    if more:
                        turn_copies(b + 1)
                    act.wait_ge(turn_done, b + 1)
                    act.wait_ge(probs_stored, b * DMA + DMA)
                    act.copy(probs_t[:, :], ps[0:NE2, 3]).then_inc(probs_copied, 1)

                ln.act(act, 0)
                turn_copies(0)
                batches(act, body)

            @block.vector
            def _(dve):
                steps = [0]

                def fill(tile, value):
                    dve.memset(tile, value).then_inc(filled, 1)
                    steps[0] += 1
                    dve.wait_ge(filled, steps[0])

                fill(chunk_of[:, :, :], 1.0)
                fill(v[:, :, :, :], 0.0)
                fill(v[:, :, :, HD:HD + 1], 1.0)
                assert steps[0] == FILLS
                ln.dve_setup(dve)
                split.dve_setup(dve)
                dve.sem_inc(v_copied, 2)
                dve.sem_inc(shifted, 1)
                dve.sem_inc(x_ready, 2)

                def sums(b):
                    halves = [slice(2 * j, 2 * j + 2) for j in range(2)]
                    dve.wait_ge(loaded, (b + 1) * LOADS * DMA)
                    for j, half in enumerate(halves):
                        dve.wait_ge(spread, b * 2 + j + 1)
                        dve.tensor_tensor(part[:, half, :], ps[:, 6 + j].rearrange("p (i d) -> p i d", d=D), chunks[:, half, :],
                                          ALU.add).then_inc(sum_ready, 1)
                    for j, half in enumerate(halves):
                        dve.wait_ge(sum_ready, b * 2 + j + 1)
                        dve.tensor_tensor(part[:, half, :], part[:, half, :], gate[:, half, :], ALU.mult).then_inc(gated, 1)
                    dve.wait_ge(x_stored, b * DMA + DMA)
                    for j, half in enumerate(halves):
                        dve.wait_ge(gated, b * 2 + j + 1)
                        dve.tensor_tensor(x[:, half, :], part[:, half, :], x1[:, half, :], ALU.add).then_inc(x_ready, 1)
                    dve.wait_ge(x_ready, b * 2 + 4)
                    dve.wait_ge(xn_stored, b * DMA + DMA)
                    dve.wait_ge(xt_done, b * DT + 2)
                    ln.dve(dve, b, x)

                def body(b, more):
                    if more:
                        sums(b + 1)
                    for n in range(split.TILES):
                        split.dve(dve, b, n)
                    dve.wait_ge(v_stored, b * DMA + DMA)
                    for j in range(2):
                        dve.wait_ge(v_done, b * 2 + j + 1)
                        dve.tensor_copy(v[:, 2 * j:2 * j + 2, :, 0:HD],
                                        ps[:, 6 + j].rearrange("p (i h e) -> p i h e", i=2, h=NH)).then_inc(v_copied, 1)
                    dve.wait_ge(gate_done, b + 1)
                    scores = ps[:, 2, 0:TT * NE2].rearrange("p (i e) -> p i e", e=NE2)

                    def wide(column):
                        return column[:, :].unsqueeze(2).broadcast_to([P, TT, NE2])

                    dve.reduce_max(top[:, :], scores, AX.X).then_inc(gate_step, 1)
                    dve.wait_ge(gate_step, b * GATE + 1)
                    dve.tensor_tensor(lg[:, :, :], scores, wide(top), ALU.subtract).then_inc(shifted, 1)
                    dve.wait_ge(gate_exp, b + 1)
                    dve.reduce_sum(total[:, :], lg[:, :, :], AX.X).then_inc(gate_step, 1)
                    dve.wait_ge(gate_step, b * GATE + 2)
                    dve.reciprocal(total[:, :], total[:, :]).then_inc(gate_step, 1)
                    dve.wait_ge(gate_step, b * GATE + 3)
                    dve.tensor_tensor(probs[:, :, :], lg[:, :, :], wide(total), ALU.mult).then_inc(gate_step, 1)

                sums(0)
                batches(dve, body)

            @block.tensor
            def _(pe):
                pe.wait_ge(ident_made, 2)
                pe.wait_ge(w_loaded, W_LOADS * DMA)
                turned.pe(pe)
                pe.wait_ge(made, 2)
                pe.sem_inc(xt_done, 2)

                def spread_context(b):
                    pe.wait_ge(loaded, (b + 1) * LOADS * DMA)
                    for j in range(2):
                        for i in (2 * j, 2 * j + 1):
                            last = pe.matmul(ps[:, 6 + j, i % 2 * D:(i % 2 + 1) * D], chunk_of[:, i], context[:, :], start=True,
                                             stop=True)
                        last.then_inc(spread, 1)

                def turn(b):
                    pe.wait_ge(ln.ready, b * TT + TT)
                    for m in range(DT):
                        for i in range(TT):
                            last = pe.transpose(ps[:, m, i * P:(i + 1) * P], xn[:, i, m * P:(m + 1) * P], ident[:, :])
                        last.then_inc(xt_done, 1)

                def body(b, more):
                    pe.wait_ge(v_copied, b * 2 + 2)
                    if more:
                        spread_context(b + 1)
                    pe.wait_ge(xt_copied, b * DT + DT)
                    pe.wait_ge(probs_copied, b + 1)
                    for n in range(split.TILES):
                        split.bank_free(pe, b, n)
                        for m in range(DT):
                            last = pe.matmul(ps[:, 2 + n], w_qkv[:, m, n * P:(n + 1) * P], xn_t[:, m], start=(m == 0),
                                             stop=(m == DT - 1))
                        last.then_inc(qk_done, 1)
                    if more:
                        pe.wait_ge(sum_ready, b * 2 + 4)
                    for j in range(2):
                        for i in (2 * j, 2 * j + 1):
                            for m in range(DT):
                                last = pe.matmul(ps[:, 6 + j, i % 2 * D:(i % 2 + 1) * D], xn_t[:, m, i * P:(i + 1) * P],
                                                 w_qkv[:, m, 2 * D:], start=(m == 0), stop=(m == DT - 1))
                        last.then_inc(v_done, 1)
                    pe.wait_ge(split.copied, b * split.TILES + 1 + split.TILES)
                    for i in range(TT):
                        for m in range(DT):
                            last = pe.matmul(ps[:, 2, i * NE2:(i + 1) * NE2], xn_t[:, m, i * P:(i + 1) * P], wg[:, m],
                                             start=(m == 0), stop=(m == DT - 1))
                    last.then_inc(gate_done, 1)
                    if more:
                        turn(b + 1)
                    pe.wait_ge(split.copied, b * split.TILES + 2 + split.TILES)
                    pe.wait_ge(gate_step, b * GATE + GATE)
                    for i in range(TT):
                        last = pe.transpose(ps[0:NE2, 3, i * P:(i + 1) * P], probs[:, i, :], ident[:, :])
                    last.then_inc(turn_done, 1)

                spread_context(0)
                turn(0)
                batches(pe, body)


CAUSAL = -1.0e4 / SCALE / NEG
ROW_MASK, ROW_SHIFT = KQK, KQK + TT
KA, KB = ROW_SHIFT, ROW_SHIFT + NPART


def stage_causal_attend(nc, w, q_in, k_in, v_in, s_out):
    with Chip(nc, "causal") as c:
        ident = c.sb("ident", [P, P])
        ident_b = c.sb("ident_b", [P, P], BF16)
        neg_ident = c.sb("neg_ident", [P, P], BF16)
        later_keys = c.sb("later_keys", [P, P], BF16)
        earlier_queries = c.sb("earlier_queries", [P, P], BF16)
        wo_cols = c.sb("wo_cols", [P, DT, NH, QUAD])
        wo = c.sb("wo", [P, NG, D])
        qs = c.sb("qs", [P, NG, GH, T], BF16)
        ks = c.sb("ks", [P, NG, GH, T], BF16)
        v = c.sb("v", [P, NG, TT, GH * QUAD])
        row_max = c.sb("row_max", [P, 2, GH * TT])
        rest = c.sb("rest", [P, 2, GH * TT])
        shift = c.sb("shift", [P, 2, GH * TT, QUAD], BF16)
        probs = c.sb("probs", [P, 2, TT, GH, T])
        context = Context(c)
        so = c.sb("so", [P, TT, D])
        ps = c.psum()
        turned = Turned(c, ps, ident, [
            (wo_cols[:, n, g * GH:(g + 1) * GH, :].rearrange("p h e -> p (h e)"), wo[:, g, n * P:(n + 1) * P])
            for n in range(DT) for g in range(NG)])

        w_loaded, filled, made, ident_made = (c.sem(n) for n in ("w_loaded", "filled", "made", "ident_made"))
        qk_loaded, v_loaded = ([c.sem(f"{n}_loaded{g}") for g in range(NG)] for n in ("qk", "v"))
        a_done, a_max, shift_step, shift_ready, max_turned, max_copied = (
            c.sem(n) for n in ("a_done", "a_max", "shift_step", "shift_ready", "max_turned", "max_copied"))
        s_done, p_ready, pv_done = (c.sem(n) for n in ("s_done", "p_ready", "pv_done"))
        proj_done, proj_copied, s_stored = c.sem("proj_done"), c.sem("proj_copied"), c.sem("s_stored")

        UA, UB = GH * TT, 2 * TT
        CHAIN = 3
        LOADS = DT
        FILLS, MADE = 7 + 3 * NG, 5 + 3 * NG
        K_LOADS, V_LOADS = 2 * len(STACK), 1

        def all_made(eng):
            eng.wait_ge(w_loaded, LOADS * DMA)
            eng.wait_ge(ident_made, 2)
            eng.wait_ge(made, MADE)
            eng.wait_ge(filled, FILLS)

        def run(eng, step):
            step(0, 0, (0, 2), None, None, None)
            step(0, 1, (0, 3), (0, 0), None, None)
            with eng.Fori(0, NB - 1) as b:
                step(b, 2, (b + 1, 0), (b, 1), (b, 0), None)
                step(b, 3, (b + 1, 1), (b, 2), (b, 1), None)
                step(b + 1, 0, (b + 1, 2), (b, 3), (b, 2), None)
                step(b + 1, 1, (b + 1, 3), (b + 1, 0), (b, 3), b)
            step(NB - 1, 2, None, (NB - 1, 1), (NB - 1, 0), None)
            step(NB - 1, 3, None, (NB - 1, 2), (NB - 1, 1), None)
            step(None, None, None, (NB - 1, 3), (NB - 1, 2), None)
            step(None, None, None, None, (NB - 1, 3), NB - 1)

        with nc.Block() as block:

            @block.sync
            def _(sp):
                sp.wait_ge(filled, FILLS)
                load_head_columns(sp, wo_cols, w["w_out"], w_loaded, 0)

                def load_qk(b, g):
                    load_stack(sp, qs[:, g], q_in, b, g, False, qk_loaded[g])
                    load_stack(sp, ks[:, g], k_in, b, g, True, qk_loaded[g])

                def load_v(b, g):
                    sp.dma_start(v[:, g], token_tiles(v_in, b)[:, :, g * GH * QUAD:(g + 1) * GH * QUAD]).then_inc(v_loaded[g], DMA)

                sp.wait_ge(made, MADE)
                for g in range(NG):
                    load_qk(0, g)
                    load_v(0, g)
                with sp.Fori(0, NB - 1) as b:
                    for g in range(NG):
                        sp.wait_ge(s_done, b * NG * UB + (g + 1) * UB)
                        load_qk(b + 1, g)
                        sp.wait_ge(pv_done, b * NG * TT + (g + 1) * TT + 2 * TT)
                        load_v(b + 1, g)

            @block.gpsimd
            def _(pool):
                make_identity(pool, ident, ident_made)
                pool.wait_ge(filled, FILLS)
                count = [0]

                def select(tile, compare, fill, base, pattern, per_row):
                    pool.affine_select(out=tile, in_=tile, compare_op=compare, fill=fill, base=base, pattern=pattern,
                                       channel_multiplier=per_row).then_inc(made, 1)
                    count[0] += 1
                    pool.wait_ge(made, count[0])

                select(ident_b[:, :], ALU.not_equal, 1.0, 0, [[-1, P]], 1)
                select(neg_ident[:, :], ALU.not_equal, NEG, 0, [[-1, P]], 1)
                select(later_keys[:, :], ALU.is_gt, 0.0, 0, [[1, P]], -1)
                select(earlier_queries[:, :], ALU.is_gt, 0.0, 0, [[-1, P]], 1)
                for g in range(NG):
                    select(qs[ROW_MASK:ROW_MASK + TT, g], ALU.is_gt, 0.0, 0, [[0, GH], [-1, T]], P)
                    select(ks[ROW_MASK:ROW_MASK + TT, g], ALU.is_ge, 0.0, 0, [[0, GH], [1, T]], -P)
                    select(ks[ROW_MASK:ROW_MASK + TT, g], ALU.is_ge, 0.0, P - 1, [[0, GH], [-1, T]], P)
                select(shift[:, :, :, 0:TT].rearrange("p a (h i) j -> p (a h) i j", i=TT), ALU.is_gt, 0.0, 0,
                       [[0, 2 * GH], [-1, TT], [1, TT]], 0)
                assert count[0] == MADE

            @block.scalar
            def _(act):
                all_made(act)
                turned.act(act)
                act.sem_inc(max_copied, GH)
                act.sem_inc(p_ready, 2)
                act.sem_inc(proj_copied, 1)
                act.sem_inc(s_stored, DMA)

                def exp(b, g, kt):
                    for pair in range(2):
                        n = g * UB + kt * 2 + pair
                        act.wait_ge(s_done, b * NG * UB + n + 1)
                        if pair == 0:
                            act.wait_ge(pv_done, b * NG * TT + g * TT + kt + 1)
                        act.activation(probs[:, g % 2, kt, 2 * pair:2 * pair + 2], ps[:, 2 + n % 2 * 2:4 + n % 2 * 2], ACT.Exp,
                                       scale=SCALE).then_inc(p_ready, 1)

                def shifts(b, g, heads):
                    act.wait_ge(max_turned, b * NG + g + 3)
                    for h in heads:
                        act.copy(qs[ROW_MASK:KB, g, h], ps[h * QUAD:h * QUAD + KB - ROW_MASK, 7]).then_inc(max_copied, 1)

                def finish(b, j):
                    if j == 0:
                        act.wait_ge(s_stored, b * DMA + DMA)
                    act.wait_ge(proj_done, b * 2 + j + 1)
                    act.copy(so[:, 2 * j:2 * j + 2, :], ps[:, 7].rearrange("p (i n) -> p i n", n=D)).then_inc(proj_copied, 1)
                    if j == 1:
                        act.wait_ge(proj_copied, b * 2 + 3)
                        act.dma_start(token_tiles(s_out, b), so[:, :, :]).then_inc(s_stored, DMA)

                def step(b, g, first, before, ended, done):
                    for kt in range(TT):
                        if g is not None:
                            exp(b, g, kt)
                        if kt < 2 and g is not None and not (g == NG - 1 and first is None):
                            nxt = (b, g + 1) if g + 1 < NG else (b + 1, 0)
                            shifts(*nxt, range(2 * kt, 2 * kt + 2))
                        if done is not None and kt >= 2:
                            finish(done, kt - 2)

                shifts(0, 0, range(GH))
                run(act, step)
                act.wait_ge(s_stored, (NB + 1) * DMA)

            @block.vector
            def _(dve):
                count = [0]

                def fill(tile, value):
                    dve.memset(tile, value).then_inc(filled, 1)
                    count[0] += 1
                    dve.wait_ge(filled, count[0])

                for tile in (ident_b[:, :], neg_ident[:, :], wo_cols[:, :, :, :], shift[:, :, :, :]):
                    fill(tile, 0.0)
                fill(later_keys[:, :], CAUSAL)
                fill(earlier_queries[:, :], CAUSAL)
                fill(shift[:, :, :, 0:TT], NEG)
                for g in range(NG):
                    fill(qs[ROW_MASK:ROW_MASK + TT, g], NEG)
                    fill(ks[ROW_MASK:KB, g], 1.0)
                    fill(ks[ROW_MASK:ROW_MASK + TT, g], CAUSAL)
                assert count[0] == FILLS
                all_made(dve)
                dve.sem_inc(a_max, 2)
                context.dve_setup(dve)

                def maxima(b, g, units):
                    for u in units:
                        dve.wait_ge(a_done, b * NG * UA + g * UA + u + 1)
                        dve.reduce_max(row_max[:, g % 2, u:u + 1], ps[:, u % 2], AX.X).then_inc(a_max, 1)

                def split_maxima(b, g):
                    n = b * NG + g
                    dve.wait_ge(a_max, b * NG * UA + (g + 1) * UA + 2)
                    dve.wait_ge(max_turned, n + 1)
                    part = [shift[:, g % 2, :, TT + k] for k in range(NPART)]
                    dve.tensor_scalar(part[0], row_max[:, g % 2], -1.0, None, ALU.mult).then_inc(shift_step, 1)
                    dve.wait_ge(shift_step, n * CHAIN + 1)
                    dve.scalar_tensor_tensor(rest[:, g % 2], row_max[:, g % 2], -1.0, part[0], ALU.mult,
                                             ALU.subtract).then_inc(shift_step, 1)
                    dve.wait_ge(shift_step, n * CHAIN + 2)
                    dve.tensor_copy(part[1], rest[:, g % 2]).then_inc(shift_step, 1)
                    dve.wait_ge(shift_step, n * CHAIN + 3)
                    dve.tensor_tensor(part[2], rest[:, g % 2], part[1], ALU.subtract).then_inc(shift_ready, 1)

                def step(b, g, first, before, ended, done):
                    def some(units):
                        if first is not None:
                            maxima(*first, units)

                    some(range(2))
                    if ended is not None:
                        b, g = ended
                        dve.wait_ge(pv_done, (b * NG + g) * TT + 3 * TT)
                        context.turn(dve, ps[:, 6])
                    some(range(2, 4))
                    if ended is not None:
                        context.scale(dve, b * NG + g)
                    some(range(4, 6))
                    if ended is not None:
                        if g == 0 and not (isinstance(b, int) and b == 0):
                            dve.wait_ge(proj_done, b * 2)
                        context.turn_back(dve, b * NG + g, g)
                    some(range(6, UA))
                    if first is not None:
                        split_maxima(*first)

                for g in range(2):
                    maxima(0, g, range(UA))
                    split_maxima(0, g)
                run(dve, step)

            @block.tensor
            def _(pe):
                all_made(pe)
                turned.pe(pe)
                pe.sem_inc(pv_done, 2 * TT)
                pe.sem_inc(max_turned, 2)

                def first_scores(b, g, units):
                    for u in units:
                        h, i = divmod(u, TT)
                        if u == 0:
                            pe.wait_ge(qk_loaded[g], (b + 1) * K_LOADS * DMA)
                        pe.wait_ge(a_max, b * NG * UA + g * UA + u + 1)
                        pe.matmul(ps[:, u % 2], qs[0:KA, g, h, i * P:(i + 1) * P], ks[0:KA, g, h, :], start=True, stop=False)
                        pe.matmul(ps[:, u % 2, i * P:(i + 1) * P], neg_ident[:, :], later_keys[:, :], start=False,
                                  stop=True).then_inc(a_done, 1)

                def turn_maxima(b, g):
                    pe.wait_ge(shift_ready, b * NG + g + 1)
                    pe.wait_ge(max_copied, (b * NG + g) * GH + GH)
                    if not (isinstance(b, int) and b == 0):
                        pe.wait_ge(proj_copied, b * 2 + (1 if g == 3 else -1))
                    for h in range(GH):
                        for i in range(TT):
                            last = pe.matmul(ps[h * QUAD:(h + 1) * QUAD, 7, i * P:(i + 1) * P], shift[:, g % 2, h * TT + i, :],
                                             ident_b[:, :], start=True, stop=True)
                    last.then_inc(max_turned, 1)

                def second_scores(b, g, kt, pair):
                    if kt == 0 and pair == 0:
                        pe.wait_ge(max_copied, (b * NG + g) * GH + 2 * GH)
                    n = g * UB + kt * 2 + pair
                    pe.wait_ge(p_ready, b * NG * UB + n + 1)
                    for j in range(2):
                        bank = ps[:, 2 + n % 2 * 2 + j]
                        h = 2 * pair + j
                        pe.matmul(bank, ks[0:KB, g, h, kt * P:(kt + 1) * P], qs[0:KB, g, h, :], start=True, stop=False)
                        last = pe.matmul(bank[:, kt * P:(kt + 1) * P], neg_ident[:, :], earlier_queries[:, :], start=False,
                                         stop=True)
                    last.then_inc(s_done, 1)

                def output(b, g, kt):
                    if kt == 0:
                        pe.wait_ge(v_loaded[g], (b + 1) * V_LOADS * DMA)
                        context.bank_free(pe, b * NG + g)
                    pe.wait_ge(p_ready, b * NG * UB + g * UB + 2 * kt + 4)
                    for h in range(GH):
                        last = pe.matmul(ps[h * QUAD:(h + 1) * QUAD, 6], v[:, g, kt, h * QUAD:(h + 1) * QUAD],
                                         probs[:, g % 2, kt, h], start=(kt == 0), stop=(kt == TT - 1))
                    last.then_inc(pv_done, 1)

                def project(b, j, shifted):
                    if j == 0:
                        pe.wait_ge(context.ready, b * NG + NG)
                        if shifted:
                            pe.wait_ge(max_copied, b * NG * GH + (NG + 3) * GH + GH)
                    pe.wait_ge(proj_copied, b * 2 + j + 1)
                    for i in (2 * j, 2 * j + 1):
                        for g in range(NG):
                            last = pe.matmul(ps[:, 7, i % 2 * D:(i % 2 + 1) * D], context.ctx[:, g, i * P:(i + 1) * P], wo[:, g],
                                             start=(g == 0), stop=(g == NG - 1))
                    last.then_inc(proj_done, 1)

                def step(b, g, first, before, ended, done):
                    for kt in range(TT):
                        units = [4 * kt, 4 * kt + 1], [4 * kt + 2], [4 * kt + 3]
                        for part in range(3):
                            if first is not None:
                                first_scores(*first, units[part])
                            if g is not None and part < 2:
                                second_scores(b, g, kt, part)
                            if kt == 0 and part == 1 and g is not None and not (g == NG - 1 and first is None):
                                turn_maxima(*((b, g + 1) if g + 1 < NG else (b + 1, 0)))
                        if before is not None:
                            output(*before, kt)
                        if done is not None and kt >= 2:
                            project(done, kt - 2, g is not None)

                for g in range(2):
                    first_scores(0, g, range(UA))
                turn_maxima(0, 0)
                run(pe, step)


F2 = 1024
FT2 = F2 // P
TOP2 = int(2.0 * T / NE2)
ROUNDS = TOP2 // 8
assert TOP2 == P


def stage_experts(nc, w, x_in, xn_in, s_in, probs_in, x_out):
    with Chip(nc, "experts") as c:
        ident = c.sb("ident", [P, P])
        token = c.sb("token", [P, TT])
        tokens = c.sb("tokens", [P, T])
        work = c.sb("work", [NB * NE2, T])
        best = c.sb("best", [NB * NE2, TOP2])
        place = c.sb("place", [NB * NE2, TOP2], mybir.dt.uint32)
        place_f = c.sb("place_f", [NB * NE2, TOP2])
        prob_t = c.sb("prob_t", [P, NB * NE2])
        place_t = c.sb("place_t", [P, NB * NE2])
        place_all = c.sb("place_all", [P, 2, NE2 * TOP2])
        xn = c.sb("xn", [P, 2, TT, D])
        x = c.sb("x", [P, 2, TT, D])
        out = c.sb("out", [P, 2, TT, D])
        picks = c.sb("picks", [P, 2, NE2 * T])
        slots = c.sb("slots", [P, NE2, NB, D])
        w1 = c.sb("w1", [P, 2, DT, F2])
        w2 = c.sb("w2", [P, 2, FT2, D])
        hidden = c.sb("hidden", [P, 2, FT2, 4 * TOP2])
        place_dram = nc.dram_tensor("experts_place_rows", (NB, NE2 * TOP2), F32, kind="Internal").ap()
        ps = c.psum()

        ident_made, made, probs_loaded, top_step, found, place_stored = (
            c.sem(n) for n in ("ident_made", "made", "probs_loaded", "top_step", "found", "place_stored"))
        turn_done, turn_copied = c.sem("turn_done"), c.sem("turn_copied")
        in_loaded, s_loaded, w_loaded, stored = ([c.sem(f"{n}{r}") for r in range(2)] for n in (
            "in_loaded", "s_loaded", "w_loaded", "stored"))
        gather_ready, gather_done, gather_copied, copy_begun = (
            c.sem(n) for n in ("gather_ready", "gather_done", "gather_copied", "copy_begun"))
        h_done, h_ready, o_done, o_copied, o_begun = (c.sem(n) for n in ("h_done", "h_ready", "o_done", "o_copied", "o_begun"))
        scatter_ready, scatter_begun, scatter_done, gate_ready, gated, added = (
            c.sem(n) for n in ("scatter_ready", "scatter_begun", "scatter_done", "gate_ready", "gated", "added"))

        GATHERS = 2 * DT
        HALF = NE2 // 2
        UNITS = 4

        with nc.Block() as block:

            @block.sync
            def _(sp):
                def weights(r, e):
                    sp.dma_start(w1[:, r], w["w1"][e].rearrange("(k p) f -> p k f", p=P)).then_inc(w_loaded[r], DMA)
                    sp.dma_start(w2[:, r], w["w2"][e].rearrange("(k p) d -> p k d", p=P)).then_inc(w_loaded[r], DMA)

                sp.dma_start(work[:, :], probs_in).then_inc(probs_loaded, DMA)
                for r in range(2):
                    weights(r, r)
                sp.wait_ge(found, 1)
                sp.dma_start(place_dram.rearrange("b (e j) -> (b e) j", e=NE2), place_f[:, :]).then_inc(place_stored, DMA)
                sp.wait_ge(place_stored, DMA)
                with sp.Fori(0, NB // 2) as i:
                    for r in range(2):
                        sp.wait_ge(gather_done, (i * 2 + r) * GATHERS + GATHERS)
                        sp.dma_start(xn[:, r], token_tiles(xn_in, i * 2 + r)).then_inc(in_loaded[r], DMA)
                        sp.dma_start(place_all[:, r], place_dram[i * 2 + r].partition_broadcast(P)).then_inc(in_loaded[r], DMA)
                with sp.Fori(0, NE2 // 2 - 1) as i:
                    for r in range(2):
                        sp.wait_ge(o_done, i * 2 * UNITS + 8 + 4 * r)
                        weights(r, i * 2 + 2 + r)
                with sp.Fori(0, NB // 2) as i:
                    for r in range(2):
                        sp.wait_ge(added, (i * 2 + r) * 2 + 2)
                        sp.dma_start(xn[:, r], token_tiles(s_in, i * 2 + r)).then_inc(s_loaded[r], DMA)
                        sp.dma_start(x[:, r], token_tiles(x_in, i * 2 + r)).then_inc(s_loaded[r], DMA)
                    for r in range(2):
                        sp.wait_ge(added, (i * 2 + r) * 2 + 6)
                        sp.dma_start(token_tiles(x_out, i * 2 + r), out[:, r]).then_inc(stored[r], DMA)
                for r in range(2):
                    sp.wait_ge(stored[r], (NB // 2 + 1) * DMA)

            @block.gpsimd
            def _(pool):
                make_identity(pool, ident, ident_made)
                pool.iota(token[:, :], [[P, TT]], base=0, channel_multiplier=1,
                          allow_small_or_imprecise_dtypes=True).then_inc(made, 1)
                pool.iota(tokens[:, :], [[1, T]], base=0, channel_multiplier=0,
                          allow_small_or_imprecise_dtypes=True).then_inc(made, 1)
                pool.sem_inc(added, 4)
                with pool.Fori(0, NB // 2) as i:
                    for r in range(2):
                        for j in range(2):
                            tiles = slice(2 * j, 2 * j + 2)
                            if j == 0:
                                pool.wait_ge(s_loaded[r], i * 2 * DMA + 2 * DMA)
                            pool.wait_ge(gate_ready, (i * 2 + r) * 2 + j + 5)
                            pool.tensor_tensor(out[:, r, tiles], out[:, r, tiles], xn[:, r, tiles], ALU.mult).then_inc(gated, 1)
                        for j in range(2):
                            tiles = slice(2 * j, 2 * j + 2)
                            pool.wait_ge(gated, (i * 2 + r) * 2 + j + 1)
                            pool.tensor_tensor(out[:, r, tiles], out[:, r, tiles], x[:, r, tiles], ALU.add).then_inc(added, 1)

            @block.scalar
            def _(act):
                act.wait_ge(turn_done, 2)
                act.copy(prob_t[:, :], ps[:, 0, 0:NB * NE2]).then_inc(turn_copied, 1)
                act.copy(place_t[:, :], ps[:, 1, 0:NB * NE2]).then_inc(turn_copied, 1)
                act.wait_ge(turn_copied, 2)
                act.sem_inc(gather_copied, 2 * GATHERS)
                with act.Fori(0, NB // 2) as i:
                    for r in range(2):
                        for n in range(GATHERS):
                            m, half = divmod(n, 2)
                            act.wait_ge(gather_done, (i * 2 + r) * GATHERS + n + 1 + 2 * GATHERS)
                            act.sem_inc(copy_begun, 1)
                            act.copy(slots[:, half * HALF:(half + 1) * HALF, i * 2 + r, m * P:(m + 1) * P],
                                     ps[:, r * GATHERS + n].rearrange("p (e j) -> p e j", e=HALF)).then_inc(gather_copied, 1)
                act.sem_inc(h_ready, 4)
                with act.Fori(0, NE2 // 2) as i:
                    for u in range(UNITS):
                        for f in range(FT2):
                            n = u * FT2 + f
                            act.wait_ge(h_done, i * UNITS * FT2 + n + 1)
                            if f == 0:
                                act.wait_ge(o_done, i * UNITS * 2 + 2 * u + 2)
                            act.activation(hidden[:, u % 2, f], ps[:, n % 4], ACT.Gelu).then_inc(h_ready, 1)
                act.sem_inc(gate_ready, 4)
                for r in range(2):
                    act.sem_inc(stored[r], DMA)
                with act.Fori(0, NB // 2) as i:
                    for r in range(2):
                        act.wait_ge(stored[r], i * DMA + DMA)
                        for j in range(2):
                            act.wait_ge(scatter_done, (i * 2 + r) * 2 + j + 5)
                            act.activation(out[:, r, 2 * j:2 * j + 2], ps[:, r * 2 + j].rearrange("p (i d) -> p i d", d=D),
                                           ACT.Silu).then_inc(gate_ready, 1)

            @block.vector
            def _(dve):
                dve.wait_ge(probs_loaded, DMA)
                for k in range(ROUNDS):
                    eight = slice(8 * k, 8 * k + 8)
                    if k >= 1:
                        dve.wait_ge(top_step, 3 * k)
                    dve.max(best[:, eight], work[:, :]).then_inc(top_step, 1)
                    dve.wait_ge(top_step, 3 * k + 1)
                    dve.max_index(place[:, eight], best[:, eight], work[:, :]).then_inc(top_step, 1)
                    dve.wait_ge(top_step, 3 * k + 2)
                    dve.match_replace(work[:, :], best[:, eight], work[:, :], -1.0).then_inc(top_step, 1)
                dve.wait_ge(top_step, 3 * ROUNDS)
                dve.tensor_copy(place_f[:, :], place[:, :]).then_inc(found, 1)
                dve.wait_ge(made, 2)
                with dve.Fori(0, NB // 2) as i:
                    for r in range(2):
                        dve.wait_ge(in_loaded[r], i * 2 * DMA + 2 * DMA)
                        dve.wait_ge(gather_done, (i * 2 + r) * GATHERS + GATHERS)
                        for t in range(TT):
                            dve.tensor_scalar(picks[:, r, t * NE2 * TOP2:(t + 1) * NE2 * TOP2], place_all[:, r],
                                              token[:, t:t + 1], None, ALU.is_equal).then_inc(gather_ready, 1)
                dve.sem_inc(o_copied, 4)
                with dve.Fori(0, NE2 // 2) as i:
                    for u in range(UNITS):
                        for j in range(2):
                            n = u * 2 + j
                            dve.wait_ge(o_done, i * UNITS * 2 + n + 5)
                            dve.sem_inc(o_begun, 1)
                            dve.tensor_copy(slots[:, i * 2 + u // 2, u % 2 * 4 + j * 2:u % 2 * 4 + j * 2 + 2, :],
                                            ps[:, 4 + n % 4].rearrange("p (b d) -> p b d", d=D)).then_inc(o_copied, 1)
                with dve.Fori(0, NB // 2) as i:
                    for r in range(2):
                        dve.wait_ge(scatter_done, (i * 2 + r) * 2 + 2)
                        dve.sem_inc(scatter_begun, 1)
                        for e in range(NE2):
                            col = (i * 2 + r) * NE2 + e
                            dve.tensor_scalar(picks[:, r, e * T:(e + 1) * T], tokens[:, :], place_t[:, bass.ds(col, 1)],
                                              prob_t[:, bass.ds(col, 1)], ALU.is_equal, ALU.mult).then_inc(scatter_ready, 1)

            @block.tensor
            def _(pe):
                pe.wait_ge(ident_made, 2)
                pe.wait_ge(found, 1)
                pe.transpose(ps[:, 0, 0:NB * NE2], best[:, :], ident[0:NB * NE2, 0:NB * NE2]).then_inc(turn_done, 1)
                pe.transpose(ps[:, 1, 0:NB * NE2], place_f[:, :], ident[0:NB * NE2, 0:NB * NE2]).then_inc(turn_done, 1)
                pe.sem_inc(gather_done, 2 * GATHERS)
                with pe.Fori(0, NB // 2) as i:
                    for r in range(2):
                        pe.wait_ge(gather_ready, (i * 2 + r) * TT + TT)
                        for n in range(GATHERS):
                            m, half = divmod(n, 2)
                            pe.wait_ge(gather_copied, (i * 2 + r) * GATHERS + n + 1)
                            for t in range(TT):
                                first = t * NE2 * TOP2 + half * HALF * TOP2
                                last = pe.matmul(ps[:, r * GATHERS + n], xn[:, r, t, m * P:(m + 1) * P],
                                                 picks[:, r, first:first + HALF * TOP2], start=(t == 0), stop=(t == TT - 1))
                            last.then_inc(gather_done, 1)
                pe.wait_ge(gather_copied, (NB + 2) * GATHERS)
                pe.sem_inc(o_done, 4)
                with pe.Fori(0, NE2 // 2) as i:

                    def first_product(u):
                        r, half = divmod(u, 2)
                        if half == 0:
                            pe.wait_ge(w_loaded[r], i * 2 * DMA + 2 * DMA)
                        for f in range(FT2):
                            n = u * FT2 + f
                            pe.wait_ge(h_ready, i * UNITS * FT2 + n + 1)
                            for m in range(DT):
                                last = pe.matmul(ps[:, n % 4], w1[:, r, m, f * P:(f + 1) * P],
                                                 slots[:, i * 2 + r, half * 4:half * 4 + 4, m * P:(m + 1) * P],
                                                 start=(m == 0), stop=(m == DT - 1))
                            last.then_inc(h_done, 1)

                    def second_product(u):
                        r = u // 2
                        pe.wait_ge(h_ready, i * UNITS * FT2 + (u + 1) * FT2 + 4)
                        for j in range(2):
                            n = u * 2 + j
                            pe.wait_ge(o_copied, i * UNITS * 2 + n + 1)
                            for b in range(2):
                                for f in range(FT2):
                                    last = pe.matmul(ps[:, 4 + n % 4, b * D:(b + 1) * D],
                                                     hidden[:, u % 2, f, (2 * j + b) * TOP2:(2 * j + b + 1) * TOP2], w2[:, r, f],
                                                     start=(f == 0), stop=(f == FT2 - 1))
                            last.then_inc(o_done, 1)

                    first_product(0)
                    for u in range(UNITS):
                        if u + 1 < UNITS:
                            first_product(u + 1)
                        second_product(u)
                pe.wait_ge(o_copied, NE2 * 4 + 4)
                pe.sem_inc(scatter_done, 4)
                with pe.Fori(0, NB // 2) as i:
                    for r in range(2):
                        pe.wait_ge(scatter_ready, (i * 2 + r) * NE2 + NE2)
                        for j in range(2):
                            pe.wait_ge(gate_ready, (i * 2 + r) * 2 + j + 1)
                            for t in (2 * j, 2 * j + 1):
                                for e in range(NE2):
                                    last = pe.matmul(ps[:, r * 2 + j, t % 2 * D:(t % 2 + 1) * D],
                                                     picks[:, r, e * T + t * P:e * T + (t + 1) * P], slots[:, e, i * 2 + r, :],
                                                     start=(e == 0), stop=(e == NE2 - 1))
                            last.then_inc(scatter_done, 1)


KD = KQK + 2 * NPART


def norms_tensor(nc, name):
    return nc.dram_tensor(name, (NB, NPART, NH * T), BF16, kind="Internal").ap()


def stage_distance_in(nc, w, x_in, q_out, k_out, q2_out, k2_out, v_out, gate_out):
    with Chip(nc, "distance_in") as c:
        ident = c.sb("ident", [P, P])
        NAMES = ("wq", "wk", "wv", "W_r", "W_k", "W_v")
        Q, K, V, MIX_R, MIX_K, MIX_V = range(len(NAMES))
        w_rows = c.sb("w_rows", [P, len(NAMES), DT, D])
        w_t = c.sb("w_t", [P, len(NAMES), DT, D])
        bias = c.sb("bias", [P, 2, DT])
        bv = c.sb("bv", [P, D])
        mu = c.sb("mu", [P, 2, DT])
        mu_not = c.sb("mu_not", [P, 2, DT])
        head_of = c.sb("head_of", [P, DT, NH])
        x = c.sb("x", [P, TT, D])
        ln = LayerNorm(c)
        xn = ln.xn
        xn_t = c.sb("xn_t", [P, DT, 1 + T])
        squares = c.sb("squares", [P, 2 * DT, T])
        norm = c.sb("norm", [NH, 2, T])
        norm_rest = c.sb("norm_rest", [NH, 2, T])
        norm_parts = c.sb("norm_parts", [NH, 2, NPART, T], BF16)
        v = c.sb("v", [P, TT, NH, QUAD])
        mixed = c.sb("mixed", [P, 2, DT, T])
        act_k = c.sb("act_k", [P, DT, T])
        r = c.sb("r", [P, TT, D])
        ffn = c.sb("ffn", [P, TT, D])
        gate = c.sb("gate", [P, TT, D])
        ps = c.psum()
        split = Split(c, q_out, k_out)
        turned = Turned(c, ps, ident, [
            (w_rows[:, a, n, m * P:(m + 1) * P], w_t[:, a, m, n * P:(n + 1) * P])
            for a in range(len(NAMES)) for n in range(DT) for m in range(DT)])

        w_loaded, filled, made, ident_made = (c.sem(n) for n in ("w_loaded", "filled", "made", "ident_made"))
        x_loaded, x_free, v_stored, norm_stored, gate_stored = (
            c.sem(n) for n in ("x_loaded", "x_free", "v_stored", "norm_stored", "gate_stored"))
        xt_done, xt_copied, qk_done, v_done, v_copied = (
            c.sem(n) for n in ("xt_done", "xt_copied", "qk_done", "v_done", "v_copied"))
        squared, norm_done, norm_copied, norm_step, norm_ready = (
            c.sem(n) for n in ("squared", "norm_done", "norm_copied", "norm_step", "norm_ready"))
        mix_half, mixed_ready, mix_k_done, relu_ready, act_k_ready, mix_r_done, r_ready, mix_v_done, ffn_ready, sig_ready, gate_ready = (
            c.sem(n) for n in ("mix_half", "mixed", "mix_k_done", "relu", "act_k", "mix_r_done", "r", "mix_v_done", "ffn", "sig", "gate"))
        LOADS = len(NAMES) + 5
        FILLS, MADE = 6, 2

        def all_made(eng):
            eng.wait_ge(w_loaded, LOADS * DMA)
            eng.wait_ge(ident_made, 2)
            eng.wait_ge(made, MADE)
            eng.wait_ge(filled, FILLS)

        with nc.Block() as block:

            @block.sync
            def _(sp):
                for a, name in enumerate(NAMES):
                    sp.dma_start(w_rows[:, a], w[name].rearrange("(n p) k -> p n k", p=P)).then_inc(w_loaded, DMA)
                with nc.allow_non_contiguous_dma(reason="short vectors, once"):
                    for a, name in enumerate(("bq", "bk")):
                        sp.dma_start(bias[:, a], column(w[name], DT)).then_inc(w_loaded, DMA)
                    for a, name in enumerate(("mu_r", "mu_k")):
                        sp.dma_start(mu[:, a], column(w[name], DT)).then_inc(w_loaded, DMA)
                sp.dma_start(bv[:, :], w["bv"].partition_broadcast(P)).then_inc(w_loaded, DMA)
                sp.sem_inc(x_free, 1)
                for stored in (v_stored, gate_stored):
                    sp.sem_inc(stored, DMA)
                sp.sem_inc(norm_stored, 2 * DMA)
                split.sp_setup(sp)
                with sp.Fori(0, NB) as b:
                    sp.wait_ge(x_free, b + 1)
                    sp.dma_start(x[:, :, :], token_tiles(x_in, b)).then_inc(x_loaded, DMA)
                    for n in range(split.TILES):
                        split.sp(sp, b, n)
                    sp.wait_ge(v_copied, b * 2 + 4)
                    sp.dma_start(token_tiles(v_out, b), v[:, :, :, :].rearrange("p i h e -> p i (h e)")).then_inc(v_stored, DMA)
                    for side, to in enumerate((q2_out, k2_out)):
                        sp.wait_ge(norm_ready, b * 2 + side + 1)
                        sp.dma_start(to[b].rearrange("a (h t) -> h a t", h=NH), norm_parts[:, side]).then_inc(norm_stored, DMA)
                    sp.wait_ge(gate_ready, b + 1)
                    sp.dma_start(token_tiles(gate_out, b), gate[:, :, :]).then_inc(gate_stored, DMA)
                for stored, per_batch in ((v_stored, 1), (gate_stored, 1), (norm_stored, 2)):
                    sp.wait_ge(stored, (NB + 1) * per_batch * DMA)
                sp.wait_ge(split.stored, (NB + 1) * split.STORES * DMA)

            @block.gpsimd
            def _(pool):
                make_identity(pool, ident, ident_made)
                pool.wait_ge(filled, FILLS - 2)
                pool.affine_select(out=head_of[:, :, :], in_=head_of[:, :, :], compare_op=ALU.is_ge, fill=0.0, base=0,
                                   pattern=[[P, DT], [-HD, NH]], channel_multiplier=1).then_inc(made, 1)
                pool.wait_ge(made, 1)
                pool.affine_select(out=head_of[:, :, :], in_=head_of[:, :, :], compare_op=ALU.is_ge, fill=0.0, base=HD - 1,
                                   pattern=[[-P, DT], [HD, NH]], channel_multiplier=-1).then_inc(made, 1)
                split.pool_setup(pool)
                with pool.Fori(0, NB) as b:
                    for n in range(split.TILES):
                        split.pool(pool, b, n)
                    pool.wait_ge(sig_ready, b + 1)
                    pool.wait_ge(gate_stored, b * DMA + DMA)
                    pool.tensor_tensor(gate[:, :, :], gate[:, :, :], ffn[:, :, :], ALU.mult).then_inc(gate_ready, 1)

            @block.scalar
            def _(act):
                ln.act_setup(act)
                all_made(act)
                turned.act(act)
                split.act_setup(act)
                act.sem_inc(relu_ready, DT)
                act.sem_inc(r_ready, 2)
                act.sem_inc(norm_copied, 2)
                with act.Fori(0, NB) as b:
                    ln.act(act, b)
                    for m in range(DT):
                        act.wait_ge(xt_done, b * DT + m + 3)
                        act.copy(xn_t[:, m, 1:], ps[:, m]).then_inc(xt_copied, 1)
                    for n in range(split.TILES):
                        act.wait_ge(qk_done, b * split.TILES + n + 1)
                        side, m = divmod(n, DT)
                        split.act(act, b, n, ps[:, 2 + n], bias=bias[:, side, m:m + 1], scale=1.0 if side == 0 else -2.0)
                    for n in range(split.TILES):
                        act.wait_ge(split.copied, b * split.TILES + n + 1 + split.TILES)
                        act.activation(squares[:, n], split.full[:, n], ACT.Square).then_inc(squared, 1)
                    for m in range(DT):
                        act.wait_ge(mix_k_done, b * DT + m + 1)
                        act.activation(act_k[:, m], ps[:, m], ACT.Relu).then_inc(relu_ready, 1)
                    for m in range(DT):
                        act.wait_ge(relu_ready, b * DT + m + 1 + DT)
                        act.activation(act_k[:, m], act_k[:, m], ACT.Square).then_inc(act_k_ready, 1)
                    for j in range(2):
                        act.wait_ge(mix_r_done, b * 2 + j + 1)
                        act.activation(r[:, 2 * j:2 * j + 2, :], ps[:, 2 + j].rearrange("p (i d) -> p i d", d=D),
                                       ACT.Sigmoid).then_inc(r_ready, 1)
                    for side in range(2):
                        act.wait_ge(norm_done, b * 2 + side + 1)
                        act.activation(norm[:, side], ps[0:NH, 4 + side], ACT.Identity,
                                       scale=1.0 if side == 0 else 0.25).then_inc(norm_copied, 1)
                    act.wait_ge(ffn_ready, b * 2 + 4)
                    act.wait_ge(gate_stored, b * DMA + DMA)
                    act.activation(gate[:, :, :], ffn[:, :, :], ACT.Sigmoid).then_inc(sig_ready, 1)

            @block.vector
            def _(dve):
                count = [0]

                def step(ins):
                    ins.then_inc(filled, 1)
                    count[0] += 1
                    dve.wait_ge(filled, count[0])

                step(dve.memset(v[:, :, :, :], 0.0))
                step(dve.memset(v[:, :, :, HD:HD + 1], 1.0))
                step(dve.memset(xn_t[:, :, 0:1], 0.0))
                step(dve.memset(head_of[:, :, :], 1.0))
                dve.wait_ge(w_loaded, LOADS * DMA)
                step(dve.tensor_scalar(mu_not[:, :, :], mu[:, :, :], -1.0, 1.0, ALU.mult, ALU.add))
                step(dve.tensor_scalar(bias[:, 1], bias[:, 1], -2.0, None, ALU.mult))
                assert count[0] == FILLS
                ln.dve_setup(dve)
                all_made(dve)
                split.dve_setup(dve)
                dve.sem_inc(v_copied, 2)
                dve.sem_inc(ffn_ready, 2)
                with dve.Fori(0, NB) as b:
                    dve.wait_ge(x_loaded, b * DMA + DMA)
                    dve.wait_ge(xt_done, b * DT + 2)
                    ln.dve(dve, b, x)
                    dve.wait_ge(ln.ready, b * TT + TT)
                    dve.sem_inc(x_free, 1)
                    dve.wait_ge(xt_copied, b * DT + DT)
                    for a in range(2):
                        for m in range(DT):
                            dve.tensor_scalar(mixed[:, a, m], xn_t[:, m, 0:T], mu_not[:, a, m:m + 1], None,
                                              ALU.mult).then_inc(mix_half, 1)
                    for a in range(2):
                        for m in range(DT):
                            dve.wait_ge(mix_half, b * 2 * DT + a * DT + m + 1)
                            dve.scalar_tensor_tensor(mixed[:, a, m], xn_t[:, m, 1:], mu[:, a, m:m + 1], mixed[:, a, m], ALU.mult,
                                                     ALU.add).then_inc(mixed_ready, 1)
                    for n in range(split.TILES):
                        split.dve(dve, b, n)
                    dve.wait_ge(v_stored, b * DMA + DMA)
                    for j in range(2):
                        dve.wait_ge(v_done, b * 2 + j + 1)
                        dve.tensor_tensor(v[:, 2 * j:2 * j + 2, :, 0:HD],
                                          ps[:, 6 + j].rearrange("p (i h e) -> p i h e", i=2, h=NH),
                                          bv[:, :].rearrange("p (h e) -> p h e", h=NH).unsqueeze(1).broadcast_to([P, 2, NH, HD]),
                                          ALU.add).then_inc(v_copied, 1)
                    dve.wait_ge(norm_stored, b * 2 * DMA + 2 * DMA)
                    for side in range(2):
                        dve.wait_ge(norm_copied, b * 2 + side + 3)
                        chain = (b * 2 + side) * 3
                        dve.tensor_copy(norm_parts[:, side, 0], norm[:, side]).then_inc(norm_step, 1)
                        dve.wait_ge(norm_step, chain + 1)
                        dve.tensor_tensor(norm_rest[:, side], norm[:, side], norm_parts[:, side, 0], ALU.subtract).then_inc(norm_step, 1)
                        dve.wait_ge(norm_step, chain + 2)
                        dve.tensor_copy(norm_parts[:, side, 1], norm_rest[:, side]).then_inc(norm_step, 1)
                        dve.wait_ge(norm_step, chain + 3)
                        dve.tensor_tensor(norm_parts[:, side, 2], norm_rest[:, side], norm_parts[:, side, 1],
                                          ALU.subtract).then_inc(norm_ready, 1)
                    for j in range(2):
                        dve.wait_ge(r_ready, b * 2 + j + 3)
                        dve.wait_ge(mix_v_done, b * 2 + j + 1)
                        tiles = slice(2 * j, 2 * j + 2)
                        dve.tensor_tensor(ffn[:, tiles, :], r[:, tiles, :], ps[:, 6 + j].rearrange("p (i d) -> p i d", d=D),
                                          ALU.mult).then_inc(ffn_ready, 1)

            @block.tensor
            def _(pe):
                all_made(pe)
                turned.pe(pe)
                pe.sem_inc(xt_done, 2)
                with pe.Fori(0, NB) as b:
                    pe.wait_ge(ln.ready, b * TT + TT)
                    pe.wait_ge(relu_ready, b * DT + DT)
                    for m in range(DT):
                        for i in range(TT):
                            last = pe.transpose(ps[:, m, i * P:(i + 1) * P], xn[:, i, m * P:(m + 1) * P], ident[:, :])
                        last.then_inc(xt_done, 1)
                    pe.wait_ge(xt_copied, b * DT + DT)
                    pe.wait_ge(r_ready, b * 2 + 2)
                    pe.wait_ge(norm_copied, b * 2 + 2)
                    for n in range(split.TILES):
                        split.bank_free(pe, b, n)
                        side, n2 = divmod(n, DT)
                        for m in range(DT):
                            last = pe.matmul(ps[:, 2 + n], w_t[:, Q + side, m, n2 * P:(n2 + 1) * P], xn_t[:, m, 1:], start=(m == 0),
                                             stop=(m == DT - 1))
                        last.then_inc(qk_done, 1)
                    for j in range(2):
                        pe.wait_ge(v_copied, b * 2 + j + 1)
                        pe.wait_ge(ffn_ready, b * 2 + j + 1)
                        for i in (2 * j, 2 * j + 1):
                            for m in range(DT):
                                last = pe.matmul(ps[:, 6 + j, i % 2 * D:(i % 2 + 1) * D], xn_t[:, m, 1 + i * P:1 + (i + 1) * P],
                                                 w_t[:, V, m], start=(m == 0), stop=(m == DT - 1))
                        last.then_inc(v_done, 1)
                    pe.wait_ge(mixed_ready, (b + 1) * 2 * DT)
                    for n in range(DT):
                        for m in range(DT):
                            last = pe.matmul(ps[:, n], w_t[:, MIX_K, m, n * P:(n + 1) * P], mixed[:, 1, m], start=(m == 0),
                                             stop=(m == DT - 1))
                        last.then_inc(mix_k_done, 1)
                    for j in range(2):
                        pe.wait_ge(split.copied, b * split.TILES + j + 1 + split.TILES)
                        for i in (2 * j, 2 * j + 1):
                            for m in range(DT):
                                last = pe.matmul(ps[:, 2 + j, i % 2 * D:(i % 2 + 1) * D], mixed[:, 0, m, i * P:(i + 1) * P],
                                                 w_t[:, MIX_R, m], start=(m == 0), stop=(m == DT - 1))
                        last.then_inc(mix_r_done, 1)
                    for side in range(2):
                        pe.wait_ge(squared, b * 2 * DT + (side + 1) * DT)
                        pe.wait_ge(split.copied, b * split.TILES + DT + side + 1 + split.TILES)
                        for m in range(DT):
                            last = pe.matmul(ps[0:NH, 4 + side], head_of[:, m], squares[:, side * DT + m], start=(m == 0),
                                             stop=(m == DT - 1))
                        last.then_inc(norm_done, 1)
                    pe.wait_ge(act_k_ready, b * DT + DT)
                    for j in range(2):
                        pe.wait_ge(v_copied, b * 2 + j + 3)
                        for i in (2 * j, 2 * j + 1):
                            for m in range(DT):
                                last = pe.matmul(ps[:, 6 + j, i % 2 * D:(i % 2 + 1) * D], act_k[:, m, i * P:(i + 1) * P],
                                                 w_t[:, MIX_V, m], start=(m == 0), stop=(m == DT - 1))
                        last.then_inc(mix_v_done, 1)


D2_MIN = 1e-12


def stage_distance_attend(nc, w, x_in, q_in, k_in, q2_in, k2_in, v_in, gate_in, x_out):
    with Chip(nc, "distance") as c:
        ident = c.sb("ident", [P, P])
        wo_cols = c.sb("wo_cols", [P, DT, NH, QUAD])
        wo = c.sb("wo", [P, NG, D])
        bo = c.sb("bo", [P, D])
        qs = c.sb("qs", [P, NG, GH, T], BF16)
        ks = c.sb("ks", [P, NG, GH, T], BF16)
        v = c.sb("v", [P, NG, TT, GH * QUAD])
        least = c.sb("least", [P, 2, GH * TT])
        least_t = c.sb("least_t", [GH * TT, 2, P])
        least_all = c.sb("least_all", [P, 2, GH * T])
        dist = c.sb("dist", [P, 2, TT, GH * T])
        context = Context(c)
        gate = c.sb("gate", [P, TT, D])
        x = c.sb("x", [P, TT, D])
        xo = c.sb("xo", [P, TT, D])
        least_dram = nc.dram_tensor("distance_least_rows", (2, GH * TT, P), F32, kind="Internal").ap()
        ps = c.psum()
        turned = Turned(c, ps, ident, [
            (wo_cols[:, n, g * GH:(g + 1) * GH, :].rearrange("p h e -> p (h e)"), wo[:, g, n * P:(n + 1) * P])
            for n in range(DT) for g in range(NG)])

        w_loaded, filled, ident_made = (c.sem(n) for n in ("w_loaded", "filled", "ident_made"))
        qk_loaded, v_loaded = ([c.sem(f"{n}_loaded{g}") for g in range(NG)] for n in ("qk", "v"))
        least_stored, least_loaded = ([c.sem(f"{n}{g}") for g in range(2)] for n in ("least_stored", "least_loaded"))
        a_done, a_min, least_clamped, least_ready, least_turned, least_copied = (
            c.sem(n) for n in ("a_done", "a_min", "least_clamped", "least_ready", "least_turned", "least_copied"))
        s_done, clamped, sqrt_ready, shifted, p_ready, pv_done = (
            c.sem(n) for n in ("s_done", "clamped", "sqrt_ready", "shifted", "p_ready", "pv_done"))
        gx_loaded, proj_done, proj_copied, gated, xo_ready, xo_stored = (
            c.sem(n) for n in ("gx_loaded", "proj_done", "proj_copied", "gated", "xo", "xo_stored"))

        UNITS = GH * TT // 2
        BUFFERS = 3
        LOADS = DT + 1
        FILLS = 1 + 2 * NG
        K_LOADS = 2 * (len(STACK) + 1)

        def all_made(eng):
            eng.wait_ge(w_loaded, LOADS * DMA)
            eng.wait_ge(ident_made, 2)
            eng.wait_ge(filled, FILLS)

        def pair(u):
            n = u % BUFFERS if u < 2 * UNITS - 1 else (u - 2) % BUFFERS
            return slice(2 * n, 2 * n + 2)

        def run(eng, step):
            step(None, (0, 0), (0, 1), None, None)
            step((0, 0), (0, 1), (0, 2), None, None)
            step((0, 1), (0, 2), (0, 3), (0, 0), None)
            with eng.Fori(0, NB - 1) as b:
                step((b, 2), (b, 3), (b + 1, 0), (b, 1), None)
                step((b, 3), (b + 1, 0), (b + 1, 1), (b, 2), None)
                step((b + 1, 0), (b + 1, 1), (b + 1, 2), (b, 3), None)
                step((b + 1, 1), (b + 1, 2), (b + 1, 3), (b + 1, 0), b)
            step((NB - 1, 2), (NB - 1, 3), None, (NB - 1, 1), None)
            step((NB - 1, 3), None, None, (NB - 1, 2), None)
            step(None, None, None, (NB - 1, 3), None)
            step(None, None, None, None, NB - 1)

        with nc.Block() as block:

            @block.sync
            def _(sp):
                sp.wait_ge(filled, FILLS)
                load_head_columns(sp, wo_cols, w["wo"], w_loaded, 0)
                sp.dma_start(bo[:, :], w["bo"].partition_broadcast(P)).then_inc(w_loaded, DMA)

                def spread_least(b, g):
                    sp.wait_ge(least_copied, b * NG + g + 1)
                    sp.wait_ge(shifted, (b * NG + g) * TT + TT)
                    sp.dma_start(least_dram[g % 2], least_t[:, g % 2]).then_inc(least_stored[g % 2], DMA)
                    sp.wait_ge(least_stored[g % 2], (b * 2 + g // 2 + 1) * DMA)
                    sp.dma_start(least_all[:, g % 2], least_dram[g % 2].rearrange("n q -> (n q)").partition_broadcast(P)).then_inc(
                        least_loaded[g % 2], DMA)

                def store(b):
                    sp.wait_ge(xo_ready, b * 2 + 4)
                    sp.dma_start(token_tiles(x_out, b), xo[:, :, :]).then_inc(xo_stored, DMA)

                sp.sem_inc(xo_stored, DMA)
                for g in range(3):
                    spread_least(0, g)
                with sp.Fori(0, NB - 1) as b:
                    spread_least(b, 3)
                    for g in range(3):
                        spread_least(b + 1, g)
                    store(b)
                spread_least(NB - 1, 3)
                store(NB - 1)
                sp.wait_ge(xo_stored, (NB + 1) * DMA)

            @block.gpsimd
            def _(pool):
                make_identity(pool, ident, ident_made)
                pool.sem_inc(shifted, 2 * TT)
                pool.sem_inc(xo_ready, 2)

                def step(out, mid, first, before, proj):
                    if mid is not None:
                        b, g = mid
                        pool.wait_ge(least_loaded[g % 2], (b * 2 + g // 2 + 1) * DMA)
                        for kt in range(TT):
                            pool.wait_ge(sqrt_ready, (b * NG + g) * TT + kt + 1)
                            pool.tensor_tensor(dist[:, g % 2, kt], dist[:, g % 2, kt], least_all[:, g % 2],
                                               ALU.subtract).then_inc(shifted, 1)
                    if proj is not None:
                        b = proj
                        pool.wait_ge(gx_loaded, b * 2 * DMA + 2 * DMA)
                        for j in range(2):
                            tiles = slice(2 * j, 2 * j + 2)
                            pool.wait_ge(proj_copied, b * 2 + j + 2)
                            pool.tensor_tensor(xo[:, tiles], xo[:, tiles], gate[:, tiles], ALU.mult).then_inc(gated, 1)
                        for j in range(2):
                            tiles = slice(2 * j, 2 * j + 2)
                            pool.wait_ge(gated, b * 2 + j + 1)
                            pool.tensor_tensor(xo[:, tiles], xo[:, tiles], x[:, tiles], ALU.add).then_inc(xo_ready, 1)

                run(pool, step)

            @block.scalar
            def _(act):
                def load_qk(b, g):
                    if not isinstance(b, int):
                        act.wait_ge(s_done, (b * NG + g - NG) * UNITS + UNITS)
                    load_stack(act, qs[:, g], q_in, b, g, False, qk_loaded[g])
                    load_stack(act, ks[:, g], k_in, b, g, True, qk_loaded[g])
                    for dst, src in ((qs[KQK:KQK + NPART, g], q2_in), (ks[KQK + NPART:KD, g], k2_in)):
                        act.dma_start(dst, src[b][:, g * GH * T:(g + 1) * GH * T].rearrange("a (h t) -> a h t", h=GH)).then_inc(
                            qk_loaded[g], DMA)

                def load_v(b, g):
                    if not isinstance(b, int):
                        act.wait_ge(pv_done, (b * NG + g - NG) * TT + 3 * TT)
                    act.dma_start(v[:, g], token_tiles(v_in, b)[:, :, g * GH * QUAD:(g + 1) * GH * QUAD]).then_inc(v_loaded[g], DMA)

                def load_gx(b):
                    act.wait_ge(xo_ready, b * 2 + 2)
                    act.dma_start(gate[:, :, :], token_tiles(gate_in, b)).then_inc(gx_loaded, DMA)
                    act.dma_start(x[:, :, :], token_tiles(x_in, b)).then_inc(gx_loaded, DMA)

                def step(out, mid, first, before, proj):
                    if first is not None and not isinstance(first[0], int):
                        b = first[0]
                        for g in ((0, 1), (2,), (3,), ())[first[1]]:
                            load_qk(b, g)
                        for g in ((), (0,), (1,), (2, 3))[first[1]]:
                            load_v(b, g)
                    if proj is not None and not isinstance(proj, int):
                        load_gx(proj)
                    if first is None and mid is not None:
                        load_gx(NB - 1)
                    if mid is not None:
                        b, g = mid
                        n = b * NG + g
                        act.wait_ge(least_clamped, n + 1)
                        act.activation(least[:, g % 2], least[:, g % 2], ACT.Sqrt).then_inc(least_ready, 1)
                    if mid is not None:
                        for kt in range(TT):
                            act.wait_ge(clamped, n * UNITS + 2 * kt + 4)
                            act.activation(dist[:, g % 2, kt], dist[:, g % 2, kt], ACT.Sqrt).then_inc(sqrt_ready, 1)
                            if kt == 0:
                                act.wait_ge(least_turned, n + 3)
                                act.copy(least_t[:, g % 2], ps[0:GH * TT, 7, 0:P]).then_inc(least_copied, 1)
                    if out is not None:
                        b, g = out
                        for kt in range(TT):
                            act.wait_ge(shifted, (b * NG + g) * TT + kt + 1 + 2 * TT)
                            act.activation(dist[:, g % 2, kt], dist[:, g % 2, kt], ACT.Exp, scale=-1.0).then_inc(p_ready, 1)

                act.wait_ge(filled, FILLS)
                for g in range(NG):
                    load_qk(0, g)
                    load_v(0, g)
                all_made(act)
                turned.act(act)
                run(act, step)

            @block.vector
            def _(dve):
                count = [0]

                def fill(tile, value):
                    dve.memset(tile, value).then_inc(filled, 1)
                    count[0] += 1
                    dve.wait_ge(filled, count[0])

                fill(wo_cols[:, :, :, :], 0.0)
                for g in range(NG):
                    fill(qs[KQK:KD, g], 1.0)
                    fill(ks[KQK:KD, g], 1.0)
                assert count[0] == FILLS
                all_made(dve)
                dve.sem_inc(a_min, 1)
                dve.sem_inc(clamped, 2)
                context.dve_setup(dve)
                dve.sem_inc(proj_copied, 1)

                def minima(b, g):
                    n = b * NG + g
                    for u in range(UNITS):
                        h, j = divmod(u, 2)
                        dve.wait_ge(a_done, n * UNITS + u + 1)
                        if u == 0:
                            dve.wait_ge(least_turned, n + 1)
                        dve.tensor_reduce(least[:, g % 2, h * TT + 2 * j:h * TT + 2 * j + 2], ps[:, pair(UNITS + u)], op=ALU.min,
                                          axis=AX.X).then_inc(a_min, 1)
                    dve.wait_ge(a_min, n * UNITS + UNITS + 1)
                    dve.tensor_scalar(least[:, g % 2], least[:, g % 2], D2_MIN, None, ALU.max).then_inc(least_clamped, 1)

                def add_bias(b, j):
                    dve.wait_ge(proj_done, b * 4 + 2 * j + 2)
                    if j == 0:
                        dve.wait_ge(xo_stored, b * DMA + DMA)
                    dve.tensor_tensor(xo[:, 2 * j:2 * j + 2, :], ps[:, 7].rearrange("p (i n) -> p i n", n=D),
                                      bo[:, :].unsqueeze(1).broadcast_to([P, 2, D]), ALU.add).then_inc(proj_copied, 1)

                def step(out, mid, first, before, proj):
                    for u in range(UNITS):
                        if mid is not None:
                            b, g = mid
                            kt, j = divmod(u, 2)
                            dve.wait_ge(s_done, (b * NG + g) * UNITS + u + 1)
                            if j == 0:
                                dve.wait_ge(pv_done, (b * NG + g) * TT + kt + 1)
                            dve.tensor_scalar(dist[:, g % 2, kt, j * 2 * T:(j + 1) * 2 * T],
                                              ps[:, pair(u)].rearrange("p h t -> p (h t)"), D2_MIN, None,
                                              ALU.max).then_inc(clamped, 1)
                        if proj is not None and u == 5:
                            add_bias(proj, 0)
                    if before is not None:
                        b, g = before
                        dve.wait_ge(pv_done, (b * NG + g) * TT + 3 * TT)
                        context.turn(dve, ps[:, 6])
                        context.scale(dve, b * NG + g)
                        if g == 0 and not (isinstance(b, int) and b == 0):
                            dve.wait_ge(proj_done, b * 4)
                        context.turn_back(dve, b * NG + g, g)
                    if proj is not None:
                        add_bias(proj, 1)
                    if first is not None:
                        minima(*first)

                minima(0, 0)
                run(dve, step)

            @block.tensor
            def _(pe):
                all_made(pe)
                turned.pe(pe)
                pe.sem_inc(pv_done, 2 * TT)
                pe.sem_inc(least_turned, 2)

                def first_scores(b, g, u, after_second=True):
                    h, j = divmod(u, 2)
                    n = b * NG + g
                    if u == 0:
                        pe.wait_ge(qk_loaded[g], (b + 1) * K_LOADS * DMA)
                    if u == UNITS - 1:
                        pe.wait_ge(a_min, n * UNITS + u)
                    elif u >= BUFFERS:
                        pe.wait_ge(a_min, n * UNITS + u - BUFFERS + 2)
                    elif after_second:
                        pe.wait_ge(clamped, n * UNITS - BUFFERS + u + 3)
                    for i in range(2):
                        last = pe.matmul(ps[:, pair(UNITS + u)][:, i], qs[0:KD, g, h, (2 * j + i) * P:(2 * j + i + 1) * P],
                                         ks[0:KD, g, h, :], start=True, stop=True)
                    last.then_inc(a_done, 1)

                def second_scores(b, g, u):
                    kt, j = divmod(u, 2)
                    n = b * NG + g
                    if u >= BUFFERS:
                        pe.wait_ge(clamped, n * UNITS + u - BUFFERS + 3)
                    elif u < 2:
                        pe.wait_ge(a_min, n * UNITS + UNITS + (-2, 1)[u])
                    for i in range(2):
                        h = 2 * j + i
                        last = pe.matmul(ps[:, pair(u)][:, i], ks[0:KD, g, h, kt * P:(kt + 1) * P], qs[0:KD, g, h, :],
                                         start=True, stop=True)
                    last.then_inc(s_done, 1)

                def turn_least(b, g):
                    pe.wait_ge(least_ready, b * NG + g + 1)
                    due = 1 if g == 3 else -1
                    if due > 0 or not isinstance(b, int):
                        pe.wait_ge(proj_copied, b * 2 + due)
                    if not (isinstance(b, int) and b == 0 and g == 0):
                        pe.wait_ge(least_copied, b * NG + g)
                    pe.transpose(ps[0:GH * TT, 7, 0:P], least[:, g % 2], ident[:, :]).then_inc(least_turned, 1)

                def output(b, g, kt):
                    n = b * NG + g
                    if kt == 0:
                        pe.wait_ge(v_loaded[g], (b + 1) * DMA)
                        context.bank_free(pe, n)
                    pe.wait_ge(p_ready, n * TT + kt + 1)
                    for h in range(GH):
                        last = pe.matmul(ps[h * QUAD:(h + 1) * QUAD, 6], v[:, g, kt, h * QUAD:(h + 1) * QUAD],
                                         dist[:, g % 2, kt, h * T:(h + 1) * T], start=(kt == 0), stop=(kt == TT - 1))
                    last.then_inc(pv_done, 1)

                def project(b, i, mid):
                    if i == 0:
                        pe.wait_ge(context.ready, b * NG + NG)
                        if mid is not None:
                            pe.wait_ge(least_copied, mid[0] * NG + mid[1] + 1)
                    if i % 2 == 0:
                        pe.wait_ge(proj_copied, b * 2 + i // 2 + 1)
                    for g in range(NG):
                        last = pe.matmul(ps[:, 7, i % 2 * D:(i % 2 + 1) * D], context.ctx[:, g, i * P:(i + 1) * P], wo[:, g],
                                         start=(g == 0), stop=(g == NG - 1))
                    last.then_inc(proj_done, 1)

                def step(out, mid, first, before, proj):
                    for u in range(UNITS):
                        if mid is not None:
                            second_scores(*mid, u)
                            if u == 1:
                                turn_least(*mid)
                        if before is not None and u in (1, 3):
                            output(*before, u // 2 + 2)
                        if proj is not None and u in (2, 3, 6, 7):
                            project(proj, u // 4 * 2 + u % 2, mid)
                    for u in range(UNITS):
                        if first is not None:
                            first_scores(*first, u)
                        if out is not None and u >= UNITS - 2:
                            output(*out, u - UNITS + 2)

                for u in range(UNITS):
                    first_scores(0, 0, u, False)
                run(pe, step)


def build(nc, a, out):
    def scratch(name, shape):
        return nc.dram_tensor(name, shape, F32, kind="Internal").ap()

    def weights(prefix, names):
        return {n: a[f"{prefix}_{n}"] for n in names}

    x1, x2, x3, xn1, chunks, gate1, xn2, s2, gate3 = (
        scratch(n, (NB, T, D)) for n in ("x1", "x2", "x3", "xn1", "chunks", "gate1", "xn2", "s2", "gate3"))
    means, context = (scratch(n, (NB, NC, D)) for n in ("means", "context"))
    probs2 = scratch("probs2", (NB * NE2, T))
    v1, v2, v3 = (scratch(n, (NB, T, V_WIDTH)) for n in ("v1", "v2", "v3"))
    q1, k1, q2, k2, q3, k3 = (parts_tensor(nc, f"{n}_parts") for n in ("q1", "k1", "q2", "k2", "q3", "k3"))
    q3_norm, k3_norm = (norms_tensor(nc, n) for n in ("q3_norm", "k3_norm"))

    stage_mamba(nc, weights("L0_attn", ("W_in", "conv_w", "conv_b", "W_x", "W_dt", "b_dt", "A_log", "D", "W_out"))
                | weights("L0_ffn", ("U1", "V1", "b1", "U2", "V2", "b2")), a["L0_attn_x"], x1)
    weights1 = weights("L1_attn", ("Wq_l", "Wk_l", "Wv_l", "Wo_l", "Wq_g", "Wk_g", "Wv_g", "Wo_g")) | weights("L1_ffn", ("Wr", "We"))
    stage_chunks_in(nc, weights1, x1, xn1, q1, k1, v1, gate1)
    stage_chunks_attend(nc, weights1, xn1, q1, k1, v1, chunks, means)
    stage_chunk_means(nc, weights1, means.rearrange("b n d -> (b n) d"), context.rearrange("b n d -> (b n) d"))
    stage_causal_in(nc, weights("L2_attn", ("w_qkv",)) | weights("L2_ffn", ("gate_w",)), x1, chunks, context, gate1,
                    x2, xn2, q2, k2, v2, probs2)
    stage_causal_attend(nc, weights("L2_attn", ("w_out",)), q2, k2, v2, s2)
    stage_experts(nc, weights("L2_ffn", ("w1", "w2")), x2, xn2, s2, probs2, x3)
    stage_distance_in(nc, weights("L3_attn", ("wq", "bq", "wk", "bk", "wv", "bv"))
                      | weights("L3_ffn", ("W_r", "W_k", "W_v", "mu_r", "mu_k")), x3, q3, k3, q3_norm, k3_norm, v3, gate3)
    stage_distance_attend(nc, weights("L3_attn", ("wo", "bo")), x3, q3, k3, q3_norm, k3_norm, v3, gate3, out)


def kernel(**inputs):
    import numpy as np
    import concourse.bacc as bacc
    from concourse.bass_utils import run_bass_kernel_spmd

    nc = bacc.Bacc("TRN2", target_bir_lowering=False, num_devices=1)
    arrays, handles = {}, {}
    for name, value in inputs.items():
        arrays[name] = np.ascontiguousarray(value)
        handles[name] = nc.dram_tensor(name, arrays[name].shape, mybir.dt.from_np(arrays[name].dtype), kind="ExternalInput").ap()
    out = nc.dram_tensor("out", (NB, T, D), F32, kind="ExternalOutput").ap()
    build(nc, handles, out)
    return run_bass_kernel_spmd(nc, [arrays], core_ids=[0]).results[0]["out"]
```

```python
import concourse.bass as bass
from concourse import mybir
from contextlib import ExitStack

F32 = mybir.dt.float32
BF16 = mybir.dt.bfloat16
ALU = mybir.AluOpType
ACT = mybir.ActivationFunctionType
AX = mybir.AxisListType

P = 128
NB, T, D = 8, 512, 256
TT = T // P
DT = D // P
LN_EPS = 1e-5
DMA = 16


class Chip:

    def __init__(self, nc, stage):
        self.nc, self.stage, self.stack, self.sems = nc, stage, ExitStack(), []

    def __enter__(self):
        self.stack.__enter__()
        return self

    def __exit__(self, *what):
        self.nc.clear_and_free_semaphores(self.sems)
        self.nc.all_engine_barrier()
        return self.stack.__exit__(*what)

    def sb(self, name, shape, dtype=F32):
        return self.stack.enter_context(self.nc.sbuf_tensor(f"{self.stage}_{name}", list(shape), dtype))

    def psum(self):
        return self.stack.enter_context(self.nc.psum_tensor(f"{self.stage}_psum", [P, 8, 512], F32))

    def sem(self, name):
        self.sems.append(self.nc.alloc_semaphore(f"{self.stage}_{name}"))
        return self.sems[-1]


def token_tiles(x, b):
    return x[b].rearrange("(i p) d -> p i d", p=P)


def column(v, n):
    return v.rearrange("(n p) -> p n", n=n)


def make_identity(pool, ident, made):
    pool.memset(ident[:, :], 0.0).then_inc(made, 1)
    pool.wait_ge(made, 1)
    pool.affine_select(out=ident[:, :], in_=ident[:, :], compare_op=ALU.not_equal, fill=1.0, base=0,
                       pattern=[[-1, P]], channel_multiplier=1).then_inc(made, 1)


def wait_past(eng, sem, count):
    if not isinstance(count, int) or count > 0:
        eng.wait_ge(sem, count)


def batches(eng, body):
    with eng.Fori(0, NB - 1) as b:
        body(b, True)
    body(NB - 1, False)


def in_turn(eng, sem):
    count = [0]

    def step(instruction):
        instruction.then_inc(sem, 1)
        count[0] += 1
        eng.wait_ge(sem, count[0])

    return step
NH, HD = 16, 16
GH = 4
NG = NH // GH
QUAD = 32
SCALE = HD ** -0.5
NEG = -125.0


class LayerNorm:

    def __init__(self, c):
        self.eps = c.sb("ln_eps", [P, 1])
        self.stats = c.sb("ln_stats", [P, TT, 6])
        self.moments = c.sb("ln_moments", [P, TT, 2])
        self.std = c.sb("ln_std", [P, TT])
        self.rstd = c.sb("ln_rstd", [P, TT])
        self.xn = c.sb("xn", [P, TT, D])
        self.eps_set, self.stats_ready, self.begun, self.var_ready, self.std_ready, self.rstd_ready, self.ready = (
            c.sem(f"ln_{n}") for n in ("eps_set", "stats_ready", "begun", "var_ready", "std_ready", "rstd_ready", "xn"))

    def dve_setup(self, dve):
        dve.memset(self.eps[:, :], LN_EPS).then_inc(self.eps_set, 1)

    def act_setup(self, act):
        act.wait_ge(self.eps_set, 1)

    def dve(self, dve, b, x):
        for i in range(TT):
            dve.bn_stats(self.stats[:, i], x[:, i]).then_inc(self.stats_ready, 1)
        dve.wait_ge(self.stats_ready, b * TT + TT)
        dve.sem_inc(self.begun, 1)
        for i in range(TT):
            dve.bn_aggr(self.moments[:, i], self.stats[:, i]).then_inc(self.var_ready, 1)
        dve.wait_ge(self.std_ready, b + 1)
        dve.reciprocal(self.rstd[:, :], self.std[:, :]).then_inc(self.rstd_ready, 1)
        dve.wait_ge(self.rstd_ready, b + 1)
        for i in range(TT):
            dve.tensor_scalar(self.xn[:, i], x[:, i], self.moments[:, i, 0:1], self.rstd[:, i:i + 1],
                              ALU.subtract, ALU.mult).then_inc(self.ready, 1)

    def act(self, act, b):
        act.wait_ge(self.var_ready, b * TT + TT)
        act.activation(self.std[:, :], self.moments[:, :, 1], ACT.Sqrt, bias=self.eps[:, 0:1]).then_inc(self.std_ready, 1)


def load_head_columns(sp, dst, src, loaded, first=0):
    for k in range(DT):
        sp.dma_start(dst[:, k, :, first:first + HD],
                     src[k * P:(k + 1) * P, :].rearrange("p (h e) -> p h e", h=NH)).then_inc(loaded, DMA)


def load_head_rows(sp, dst, src, loaded, first=0):
    for j in range(GH):
        sp.dma_start(dst[j * QUAD + first:j * QUAD + first + HD, :, :],
                     src.rearrange("(g h e) n -> h e g n", g=NG, h=GH)[j]).then_inc(loaded, DMA)


class Turned:

    def __init__(self, c, ps, ident, pairs):
        self.ps, self.ident, self.pairs = ps, ident, pairs
        self.done, self.copied = c.sem("turn_done"), c.sem("turn_copied")

    def pe(self, pe):
        for n, (src, _) in enumerate(self.pairs):
            if n >= 4:
                pe.wait_ge(self.copied, n - 3)
            pe.transpose(self.ps[:, n % 4, 0:P], src, self.ident[:, :]).then_inc(self.done, 1)
        pe.wait_ge(self.copied, len(self.pairs))

    def act(self, act):
        for n, (_, dst) in enumerate(self.pairs):
            act.wait_ge(self.done, n + 1)
            act.copy(dst, self.ps[:, n % 4, 0:P]).then_inc(self.copied, 1)


NPART = 3
STACK = ((0, 3, 0), (0, 2, 1), (0, 1, 2))
SLOTS = sum(n for _, n, _ in STACK)
KQK = SLOTS * HD


def parts_tensor(nc, name):
    return nc.dram_tensor(name, (NB, NPART * HD, NH * T), BF16, kind="Internal").ap()


class Split:

    TILES = 2 * DT
    STORES = TILES * NPART

    def __init__(self, c, q_parts, k_parts):
        self.q_parts, self.k_parts = q_parts, k_parts
        self.full = c.sb("full", [P, self.TILES, T])
        self.rest = c.sb("rest", [P, self.TILES, T])
        self.parts = c.sb("parts", [P, self.TILES, NPART, T], BF16)
        self.copied, self.high, self.rest_ready, self.middle, self.ready, self.stored = (
            c.sem(f"split_{n}") for n in ("copied", "high", "rest", "middle", "ready", "stored"))

    def act_setup(self, act):
        act.sem_inc(self.copied, self.TILES)

    def dve_setup(self, dve):
        dve.sem_inc(self.rest_ready, self.TILES)

    def pool_setup(self, pool):
        pool.sem_inc(self.ready, self.TILES)

    def sp_setup(self, sp):
        sp.sem_inc(self.stored, self.STORES * DMA)

    def bank_free(self, eng, b, n):
        eng.wait_ge(self.copied, b * self.TILES + n + 1)

    def act(self, act, b, n, bank, **how):
        act.wait_ge(self.rest_ready, b * self.TILES + n + 1)
        act.activation(self.full[:, n], bank, ACT.Identity, **how).then_inc(self.copied, 1)

    def act_middle(self, act, b):
        for n in range(self.TILES):
            act.wait_ge(self.rest_ready, b * self.TILES + n + 1 + self.TILES)
            act.copy(self.parts[:, n, 1], self.rest[:, n]).then_inc(self.middle, 1)

    def dve(self, dve, b, n):
        dve.wait_ge(self.copied, b * self.TILES + n + 1 + self.TILES)
        if n == 0:
            dve.wait_ge(self.stored, (b + 1) * self.STORES * DMA)
        dve.tensor_copy(self.parts[:, n, 0], self.full[:, n]).then_inc(self.high, 1)
        dve.wait_ge(self.high, b * self.TILES + n + 1)
        dve.wait_ge(self.ready, b * self.TILES + n + 1)
        dve.tensor_tensor(self.rest[:, n], self.full[:, n], self.parts[:, n, 0], ALU.subtract).then_inc(self.rest_ready, 1)

    def pool(self, pool, b, n):
        pool.wait_ge(self.middle, b * self.TILES + n + 1)
        pool.tensor_tensor(self.parts[:, n, 2], self.rest[:, n], self.parts[:, n, 1], ALU.subtract).then_inc(self.ready, 1)

    def sp(self, sp, b, n):
        sp.wait_ge(self.ready, b * self.TILES + n + 1 + self.TILES)
        to, m = (self.q_parts, n) if n < DT else (self.k_parts, n - DT)
        heads = P // HD
        for part in range(NPART):
            row = (part if n < DT else NPART - 1 - part) * HD
            dst = to[b, row:row + HD, m * heads * T:(m + 1) * heads * T].rearrange("e (h t) -> h e t", h=heads)
            sp.dma_start(dst, self.parts[:, n, part]).then_inc(self.stored, DMA)


def load_stack(sp, dst, parts, b, g, k_side, loaded):
    row = 0
    for first_q, n, first_k in STACK:
        first = first_k if k_side else first_q
        sp.dma_start(dst[row:row + n * HD], parts[b, first * HD:(first + n) * HD, g * GH * T:(g + 1) * GH * T].rearrange(
            "r (h t) -> r h t", h=GH)).then_inc(loaded, DMA)
        row += n * HD


class AttentionTiles:

    def __init__(self, c):
        self.qs, self.ks = (c.sb(n, [P, NG, GH, T], BF16) for n in ("q_stacks", "k_stacks"))
        self.wo = c.sb("wo", [P, NG, D])
        self.made, self.copied = c.sem("constants_made"), c.sem("constants_copied")

    def copy_rows(self, sp, q_rows, k_rows, made):
        sp.wait_ge(self.made, made)
        for g in range(1, NG):
            for stack, rows in ((self.qs, q_rows), (self.ks, k_rows)):
                sp.dma_start(stack[rows, g], stack[rows, 0]).then_inc(self.copied, DMA)

    def rows_copied(self, sp):
        sp.wait_ge(self.copied, 2 * (NG - 1) * DMA)

    def wo_blocks(self, wo_cols):
        return [(wo_cols[:, n, g * GH:(g + 1) * GH, :].rearrange("p h e -> p (h e)"), self.wo[:, g, n * P:(n + 1) * P])
                for n in range(DT) for g in range(NG)]


class Context:

    def __init__(self, c):
        self.turned = c.sb("out_turned", [P, T])
        self.den_inv = c.sb("den_inv", [P, T // QUAD])
        self.scaled = c.sb("out_scaled", [P, T])
        self.ctx = c.sb("ctx", [P, NG, T])
        self.out_turned, self.inverted, self.scaled_ready, self.ready = (
            c.sem(n) for n in ("out_turned", "den_inverted", "out_scaled", "ctx"))

    def dve_setup(self, dve):
        dve.sem_inc(self.out_turned, 1)

    def bank_free(self, pe, n):
        pe.wait_ge(self.out_turned, n + 1)

    def turn(self, dve, bank):
        dve.transpose(self.turned[:, :], bank).then_inc(self.out_turned, 1)

    def scale(self, dve, n):
        dve.wait_ge(self.out_turned, n + 2)
        blocks = self.turned[:, :].rearrange("p (c e) -> p c e", e=QUAD)
        dve.reciprocal(self.den_inv[:, :], blocks[:, :, HD]).then_inc(self.inverted, 1)
        dve.wait_ge(self.inverted, n + 1)
        dve.tensor_tensor(self.scaled[:, :].rearrange("p (c e) -> p c e", e=QUAD), blocks,
                          self.den_inv[:, :].unsqueeze(2).broadcast_to([P, T // QUAD, QUAD]), ALU.mult).then_inc(self.scaled_ready, 1)

    def turn_back(self, dve, n, g):
        dve.wait_ge(self.scaled_ready, n + 1)
        dve.transpose(self.ctx[:, g], self.scaled[:, :]).then_inc(self.ready, 1)


F32R = mybir.dt.float32r


class TwoParts:

    def __init__(self, c, name, shape):
        self.high, self.low = (c.sb(f"{name}_{part}", shape, F32R) for part in ("high", "low"))
        self.rounded, self.ready = c.sem(f"{name}_rounded"), c.sem(f"{name}_parts")

    def take_high(self, dve, x, piece):
        dve.tensor_copy(self.high[piece], x).then_inc(self.rounded, 1)

    def take_low(self, dve, x, piece, count, begun=None):
        dve.wait_ge(self.rounded, count)
        if begun is not None:
            dve.sem_inc(begun, 1)
        dve.tensor_tensor(self.low[piece], x, self.high[piece], ALU.subtract).then_inc(self.ready, 1)

    def both(self, piece):
        return self.high[piece], self.low[piece]


def three_passes(pe, out, left, right, first, final):
    for n, (a, b) in enumerate(((0, 0), (0, 1), (1, 0))):
        last = pe.matmul(out, left[a], right[b], start=(first and n == 0), stop=(final and n == 2))
    return last


DI, DS, TAPS, RANK = 512, 16, 4, 64
MT = DI // P
F0, R0 = 1024, 64
FT0 = F0 // P


def channels_tensor(nc, name):
    return nc.dram_tensor(name, (NB, P, MT * T), F32, kind="Internal").ap()


def halves(count):
    return [slice(j * count // 2, (j + 1) * count // 2) for j in range(2)]


def skewed(eng, step):
    step(0, None, None)
    step(1, 0, None)
    with eng.Fori(2, NB) as b:
        step(b, b - 1, b - 2)
    step(None, NB - 1, NB - 2)
    step(None, None, NB - 1)


def stage_mamba_in(nc, w, x_in, xc_out, z_out, dt_out, bc_out, low_out):
    with Chip(nc, "mamba_in") as c:
        ident = c.sb("ident", [P, P])
        eps = c.sb("eps", [P, 1])
        w_in = c.sb("w_in", [P, DT, 2 * DI])
        w_x = c.sb("w_x", [P, MT, RANK + 2 * DS])
        w_dt = c.sb("w_dt", [RANK, DI])
        u1 = c.sb("u1", [P, DT, R0])
        conv_w = c.sb("conv_w", [P, MT, TAPS])
        conv_b = c.sb("conv_b", [P, MT])
        b_dt = c.sb("b_dt", [P, MT])
        x = c.sb("x", [P, TT, D])
        ln = LayerNorm(c)
        xn = ln.xn
        xn_t = c.sb("xn_t", [P, DT, T])
        w_z_parts = TwoParts(c, "w_z", [P, DT, DI])
        xn_parts = TwoParts(c, "xn_t", [P, DT, T])
        xi = c.sb("xi", [P, MT, TAPS - 1 + T])
        conv = c.sb("conv", [P, MT, T])
        xc = c.sb("xc", [P, MT, T])
        z = c.sb("z", [P, MT, T])
        low = c.sb("low", [R0, T])
        xp = c.sb("xp", [RANK + 2 * DS, T])
        v = c.sb("v", [P, MT, T])
        expo = c.sb("expo", [P, MT, T])
        one_more = c.sb("one_more", [P, MT, T])
        dt = c.sb("dt", [P, MT, T])
        ps = c.psum()

        w_loaded, made, ident_made = (c.sem(n) for n in ("w_loaded", "made", "ident_made"))
        x_loaded, xc_stored, z_stored, dt_stored, bc_stored, low_stored = (
            c.sem(n) for n in ("x_loaded", "xc_stored", "z_stored", "dt_stored", "bc_stored", "low_stored"))
        xt_done, xi_done, z_done, low_done, xp_done, dt_done = (
            c.sem(n) for n in ("xt_done", "xi_done", "z_done", "low_done", "xp_done", "dt_done"))
        xt_copied, xi_copied, z_ready, low_copied, xp_copied = (
            c.sem(n) for n in ("xt_copied", "xi_copied", "z_ready", "low_copied", "xp_copied"))
        conv_step, xc_ready = c.sem("conv_step"), c.sem("xc_ready")
        v_ready, sp_abs, sp_exp, sp_up, sp_err, sp_ln, sp_relu, dt_ready = (
            c.sem(n) for n in ("v_ready", "sp_abs", "sp_exp", "sp_up", "sp_err", "sp_ln", "sp_relu", "dt_ready"))
        W_LOADS, MADE = 7, 1

        def all_made(eng):
            eng.wait_ge(w_loaded, W_LOADS * DMA)
            eng.wait_ge(ident_made, 2)
            eng.wait_ge(made, MADE)

        def tiles(t):
            return t.rearrange("p (m t) -> p m t", m=MT)

        with nc.Block() as block:

            @block.sync
            def _(sp):
                def load_x(b):
                    sp.dma_start(x[:, :, :], token_tiles(x_in, b)).then_inc(x_loaded, DMA)

                load_x(0)
                for dst, src in (
                    (w_in[:, :, :], w["W_in"].rearrange("(k p) n -> p k n", p=P)),
                    (w_x[:, :, :], w["W_x"].rearrange("(k p) n -> p k n", p=P)),
                    (w_dt[:, :], w["W_dt"]),
                    (u1[:, :, :], w["U1"].rearrange("(k p) n -> p k n", p=P)),
                    (conv_w[:, :, :], w["conv_w"].rearrange("(m p) a k -> p m (a k)", p=P)),
                ):
                    sp.dma_start(dst, src).then_inc(w_loaded, DMA)
                with nc.allow_non_contiguous_dma(reason="short vectors, once"):
                    for dst, src in ((conv_b, w["conv_b"]), (b_dt, w["b_dt"])):
                        sp.dma_start(dst[:, :], column(src, MT)).then_inc(w_loaded, DMA)

                def step(first, second, third, load_next=False):
                    if load_next:
                        sp.wait_ge(ln.ready, first * TT + TT)
                        load_x(first + 1)
                    if third is not None:
                        sp.wait_ge(xp_copied, third + 1)
                        sp.dma_start(bc_out[third], xp[RANK:RANK + 2 * DS, :]).then_inc(bc_stored, DMA)
                    if second is not None:
                        sp.wait_ge(low_copied, second + 1)
                        sp.dma_start(low_out[second], low[:, :]).then_inc(low_stored, DMA)
                        sp.wait_ge(z_ready, second * 2 + 2)
                        sp.dma_start(tiles(z_out[second]), z[:, :, :]).then_inc(z_stored, DMA)
                        sp.wait_ge(xc_ready, second * MT + MT)
                        sp.dma_start(tiles(xc_out[second]), xc[:, :, :]).then_inc(xc_stored, DMA)
                    if third is not None:
                        sp.wait_ge(dt_ready, third * MT + MT)
                        sp.dma_start(tiles(dt_out[third]), dt[:, :, :]).then_inc(dt_stored, DMA)

                step(0, None, None, True)
                step(1, 0, None, True)
                with sp.Fori(2, NB - 1) as b:
                    step(b, b - 1, b - 2, True)
                step(NB - 1, NB - 2, NB - 3)
                step(None, NB - 1, NB - 2)
                step(None, None, NB - 1)
                for stored in (xc_stored, z_stored, dt_stored, bc_stored, low_stored):
                    sp.wait_ge(stored, NB * DMA)

            @block.gpsimd
            def _(pool):
                make_identity(pool, ident, ident_made)

                def step(first, second, third):
                    if third is not None:
                        wait_past(pool, dt_stored, third * DMA)
                        for m in range(MT):
                            pool.wait_ge(sp_ln, third + 1)
                            pool.wait_ge(sp_relu, third * MT + m + 1)
                            pool.tensor_tensor(dt[:, m], v[:, m], one_more[:, m], ALU.add).then_inc(dt_ready, 1)

                skewed(pool, step)

            @block.scalar
            def _(act):
                ln.act_setup(act)
                all_made(act)

                def xi_copies(b, tiles):
                    for m in tiles:
                        act.wait_ge(xi_done, b * MT + m + 1)
                        act.copy(xi[:, m, TAPS - 1:], ps[:, m]).then_inc(xi_copied, 1)

                def step(first, second, third):
                    if second is not None:
                        xi_copies(second, (0, 1))
                    if first is not None:
                        ln.act(act, first)
                    if second is not None:
                        xi_copies(second, (2, 3))
                    if third is not None:
                        act.wait_ge(xp_done, third + 1)
                        wait_past(act, bc_stored, third * DMA)
                        act.copy(xp[:, :], ps[0:RANK + 2 * DS, 4]).then_inc(xp_copied, 1)
                    if second is not None:
                        act.wait_ge(low_done, second + 1)
                        wait_past(act, low_stored, second * DMA)
                        act.copy(low[:, :], ps[0:R0, 4]).then_inc(low_copied, 1)
                    if third is not None:
                        wait_past(act, dt_ready, third * MT)
                        for m in range(MT):
                            act.wait_ge(dt_done, third * MT + m + 1)
                            act.activation(v[:, m], ps[:, m], ACT.Identity, bias=b_dt[:, m:m + 1]).then_inc(v_ready, 1)
                        act.wait_ge(v_ready, third * MT + MT)
                        act.activation(expo[:, :, :], v[:, :, :], ACT.Abs).then_inc(sp_abs, 1)
                    if first is not None:
                        for m in range(DT):
                            act.wait_ge(xt_done, first * DT + m + 1)
                            act.copy(xn_t[:, m], ps[:, 1 + m]).then_inc(xt_copied, 1)
                    if third is not None:
                        act.wait_ge(sp_abs, third + 1)
                        act.activation(expo[:, :, :], expo[:, :, :], ACT.Exp, scale=-1.0).then_inc(sp_exp, 1)
                    if second is not None:
                        act.wait_ge(z_done, second * MT + MT)
                        wait_past(act, z_stored, second * DMA)
                        act.activation(z[:, 0], ps[:, 0], ACT.Silu).then_inc(z_ready, 1)
                        act.activation(z[:, 1:4], ps[:, 5:8], ACT.Silu).then_inc(z_ready, 1)
                        wait_past(act, xc_stored, second * DMA)
                        for m in range(MT):
                            act.wait_ge(conv_step, second * TAPS * MT + (TAPS - 1) * MT + m + 1)
                            act.activation(xc[:, m], conv[:, m], ACT.Silu, bias=conv_b[:, m:m + 1]).then_inc(xc_ready, 1)
                    if third is not None:
                        act.wait_ge(sp_err, third * MT + MT)
                        act.activation(one_more[:, :, :], one_more[:, :, :], ACT.Ln).then_inc(sp_ln, 1)

                skewed(act, step)

            @block.vector
            def _(dve):
                ln.dve_setup(dve)
                dve.memset(xi[:, :, 0:TAPS - 1], 0.0).then_inc(made, 1)
                all_made(dve)

                for k in range(DT):
                    w_z_parts.take_high(dve, w_in[:, k, DI:], (slice(None), k))
                for k in range(DT):
                    w_z_parts.take_low(dve, w_in[:, k, DI:], (slice(None), k), k + 1)

                def step(first, second, third):
                    if second is not None:
                        for k in range(DT):
                            dve.wait_ge(xt_copied, second * DT + k + 1)
                            xn_parts.take_high(dve, xn_t[:, k], (slice(None), k))
                        for k in range(DT):
                            xn_parts.take_low(dve, xn_t[:, k], (slice(None), k), second * DT + k + 1)
                    if first is not None:
                        dve.wait_ge(x_loaded, first * DMA + DMA)
                        wait_past(dve, xt_done, first * DT)
                        ln.dve(dve, first, x)
                    if second is not None:
                        wait_past(dve, xc_ready, second * MT)
                        for k in range(TAPS):
                            for m in range(MT):
                                if k == 0:
                                    dve.wait_ge(xi_copied, second * MT + m + 1)
                                    dve.tensor_scalar(conv[:, m], xi[:, m, 0:T], conv_w[:, m, 0:1], None, ALU.mult).then_inc(conv_step, 1)
                                else:
                                    dve.wait_ge(conv_step, second * TAPS * MT + (k - 1) * MT + m + 1)
                                    dve.scalar_tensor_tensor(conv[:, m], xi[:, m, k:k + T], conv_w[:, m, k:k + 1], conv[:, m],
                                                             ALU.mult, ALU.add).then_inc(conv_step, 1)
                    if third is not None:
                        wait_past(dve, dt_ready, third * MT)
                        dve.wait_ge(sp_exp, third + 1)
                        for m in range(MT):
                            dve.tensor_scalar(one_more[:, m], expo[:, m], 1.0, None, ALU.add).then_inc(sp_up, 1)
                        for m in range(MT):
                            dve.wait_ge(sp_up, third * MT + m + 1)
                            dve.scalar_tensor_tensor(expo[:, m], one_more[:, m], 1.0, expo[:, m], ALU.subtract,
                                                     ALU.subtract).then_inc(sp_err, 1)
                        for m in range(MT):
                            dve.wait_ge(sp_err, third * MT + m + 1)
                            dve.scalar_tensor_tensor(v[:, m], v[:, m], 0.0, expo[:, m], ALU.max, ALU.subtract).then_inc(sp_relu, 1)

                skewed(dve, step)

            @block.tensor
            def _(pe):
                all_made(pe)

                def project(bank, m, side, done):
                    for k in range(DT):
                        if side == 0:
                            last = pe.matmul(ps[:, bank], w_in[:, k, m * P:(m + 1) * P], xn_t[:, k], start=(k == 0),
                                             stop=(k == DT - 1))
                            continue
                        last = three_passes(pe, ps[:, bank],
                                            w_z_parts.both((slice(None), k, slice(m * P, (m + 1) * P))),
                                            xn_parts.both((slice(None), k)), k == 0, k == DT - 1)
                    last.then_inc(done, 1)

                def step(first, second, third):
                    if second is not None:
                        pe.wait_ge(xt_copied, second * DT + DT)
                        wait_past(pe, v_ready, (second - 1) * MT)
                        wait_past(pe, z_ready, second * 2 - 1)
                        for m in range(MT):
                            project(m, m, 0, xi_done)
                    if third is not None:
                        pe.wait_ge(xc_ready, third * MT + MT)
                        pe.wait_ge(low_copied, third + 1)
                        for m in range(MT):
                            last = pe.matmul(ps[0:RANK + 2 * DS, 4], w_x[:, m], xc[:, m], start=(m == 0), stop=(m == MT - 1))
                        last.then_inc(xp_done, 1)
                    if second is not None:
                        wait_past(pe, z_ready, second * 2)
                        pe.wait_ge(w_z_parts.ready, DT)
                        pe.wait_ge(xn_parts.ready, second * DT + DT)
                        project(5, 1, 1, z_done)
                    if third is not None:
                        pe.wait_ge(xp_copied, third + 1)
                        if second is not None:
                            pe.wait_ge(xi_copied, second * MT + MT)
                        for m in range(MT):
                            pe.matmul(ps[:, m], w_dt[:, m * P:(m + 1) * P], xp[0:RANK, :], start=True, stop=True).then_inc(dt_done, 1)
                    if second is not None:
                        for k in range(DT):
                            last = pe.matmul(ps[0:R0, 4], u1[:, k], xn_t[:, k], start=(k == 0), stop=(k == DT - 1))
                        last.then_inc(low_done, 1)
                        project(6, 2, 1, z_done)
                        project(7, 3, 1, z_done)
                        if third is not None:
                            pe.wait_ge(v_ready, third * MT + 1)
                        else:
                            pe.wait_ge(xi_copied, second * MT + 1)
                        project(0, 0, 1, z_done)
                    if first is not None:
                        pe.wait_ge(ln.ready, first * TT + TT)
                        if third is not None:
                            pe.wait_ge(v_ready, third * MT + 3)
                        elif second is not None:
                            pe.wait_ge(xi_copied, second * MT + 3)
                        for k in range(DT):
                            for i in range(TT):
                                last = pe.transpose(ps[:, 1 + k, i * P:(i + 1) * P], xn[:, i, k * P:(k + 1) * P], ident[:, :])
                            last.then_inc(xt_done, 1)

                skewed(pe, step)


STEPS = DS * MT
RING = 4
CHUNK = 4
NCHUNK = DS // CHUNK
HBANKS = 3


def alternate(eng, batch):
    batch(0, 0, False, True)
    with eng.Fori(0, NB // 2 - 1) as pair:
        batch(pair * 2 + 1, 1, True, True)
        batch(pair * 2 + 2, 0, True, True)
    batch(NB - 1, 1, True, False)


def beside_scan(eng, scan, ffn, finish, prepare):
    def batch(b, slot, before, after):
        for n in range(STEPS):
            if before:
                finish(n, b - 1, 1 - slot)
            ffn(n, b, slot)
            if after:
                prepare(n, b + 1, 1 - slot)
            scan(n, b, slot)

    for n in range(STEPS):
        prepare(n, 0, 0)
    alternate(eng, batch)
    for n in range(STEPS):
        finish(n, NB - 1, 1)


def nothing(n, b, slot):
    pass


def stage_mamba_scan(nc, w, x_in, xc_in, z_in, dt_in, bc_in, low_in, x_out):
    with Chip(nc, "mamba") as c:
        ident = c.sb("ident", [P, P])
        w_out = c.sb("w_out", [P, MT, D])
        v1 = c.sb("v1", [R0, F0])
        u2 = c.sb("u2", [P, FT0, R0])
        v2b = c.sb("v2b", [R0 + 1, D])
        a_neg = c.sb("a_neg", [P, MT, DS])
        skip = c.sb("skip", [P, MT])
        b1 = c.sb("b1", [P, FT0])
        xc = c.sb("xc", [P, 2, MT, T])
        z = c.sb("z", [P, 2, MT, T])
        dt = c.sb("dt", [P, 2, MT, T])
        u = c.sb("u", [P, 2, MT, T])
        b_all = c.sb("b_all", [P, 2, CHUNK, T])
        c_all = c.sb("c_all", [P, 2, CHUNK, T])
        decay = c.sb("decay", [P, RING, T])
        drive = c.sb("drive", [P, RING, T])
        h = c.sb("h", [P, RING, T])
        hc = c.sb("hc", [P, RING, T])
        low = c.sb("low", [R0, T])
        hidden = c.sb("hidden", [P, HBANKS, T])
        q1 = c.sb("q1", [R0 + 1, T])
        gate = c.sb("gate", [P, TT, D])
        xo = c.sb("xo", [P, TT, D])
        ps = c.psum()

        w_loaded, made, ident_made, a_made = (c.sem(n) for n in ("w_loaded", "made", "ident_made", "a_made"))
        ch_loaded = [c.sem(f"channels_loaded{k}") for k in range(2)]
        b_loaded, c_loaded = ([c.sem(f"{n}_loaded{k}") for k in range(2)] for n in "bc")
        low_loaded, xo_loaded, x_stored = (c.sem(n) for n in ("low_loaded", "xo_loaded", "x_stored"))
        u_ready, decay_ready, drive_ready, h_ready, hc_ready, y_summed = (
            c.sem(n) for n in ("u_ready", "decay_ready", "drive_ready", "h_ready", "hc_ready", "y_summed"))
        hid_done, hid_ready, q_summed, q_copied, ffn_done, gate_ready = (
            c.sem(n) for n in ("hid_done", "hid_ready", "q_summed", "q_copied", "ffn_done", "gate_ready"))
        y_skip, y_gated, s_done, s_gated, xo_ready = (c.sem(n) for n in ("y_skip", "y_gated", "s_done", "s_gated", "xo_ready"))
        W_LOADS, CHANNELS = 8, 3

        def loads_before(b, slot):
            return (b - slot) * (CHANNELS * DMA // 2)

        with nc.Block() as block:

            @block.sync
            def _(sp):
                def load_channels(b, slot):
                    for dst, src in ((dt, dt_in), (xc, xc_in), (z, z_in)):
                        sp.dma_start(dst[:, slot], src[b].rearrange("p (m t) -> p m t", m=MT)).then_inc(ch_loaded[slot], DMA)

                def load_low(b):
                    sp.dma_start(low[:, :], low_in[b]).then_inc(low_loaded, DMA)

                def load_chunk(b, k):
                    j = k % 2
                    rows = bc_in[b, k * CHUNK:(k + 1) * CHUNK, :]
                    sp.dma_start(b_all[:, j], rows.partition_broadcast(P)).then_inc(b_loaded[j], DMA)
                    rows = bc_in[b, DS + k * CHUNK:DS + (k + 1) * CHUNK, :]
                    sp.dma_start(c_all[:, j], rows.partition_broadcast(P)).then_inc(c_loaded[j], DMA)

                def chunk_used(b, k):
                    sp.wait_ge(drive_ready, b * STEPS + (k + 1) * CHUNK * MT)
                    sp.wait_ge(hc_ready, b * STEPS + (k + 1) * CHUNK * MT)

                def store(b):
                    sp.wait_ge(xo_ready, b * 2 + 2)
                    sp.dma_start(token_tiles(x_out, b), xo[:, :, :]).then_inc(x_stored, DMA)

                def batch(b, slot, before, after):
                    if before:
                        wait_past(sp, x_stored, (b - 1) * DMA)
                        sp.dma_start(xo[:, :, :], token_tiles(x_in, b - 1)).then_inc(xo_loaded, DMA)
                        sp.wait_ge(s_done, b * 2)
                    if after:
                        load_channels(b + 1, 1 - slot)
                    for k in range(NCHUNK - 2):
                        chunk_used(b, k)
                        load_chunk(b, k + 2)
                        if before and k == 0:
                            store(b - 1)
                    if after:
                        sp.wait_ge(hid_done, b * FT0 + FT0)
                        load_low(b + 1)
                        for k in range(2):
                            chunk_used(b, NCHUNK - 2 + k)
                            load_chunk(b + 1, k)

                load_channels(0, 0)
                for dst, src in (
                    (a_neg[:, :, :], w["A_log"].rearrange("(m p) s -> p m s", p=P)),
                    (w_out[:, :, :], w["W_out"].rearrange("(k p) n -> p k n", p=P)),
                    (v1[:, :], w["V1"]),
                    (u2[:, :, :], w["U2"].rearrange("(k p) n -> p k n", p=P)),
                    (v2b[0:R0, :], w["V2"]),
                    (v2b[R0:R0 + 1, :], w["b2"].rearrange("(a n) -> a n", a=1)),
                ):
                    sp.dma_start(dst, src).then_inc(w_loaded, DMA)
                with nc.allow_non_contiguous_dma(reason="short vectors, once"):
                    sp.dma_start(skip[:, :], column(w["D"], MT)).then_inc(w_loaded, DMA)
                    sp.dma_start(b1[:, :], column(w["b1"], FT0)).then_inc(w_loaded, DMA)
                for k in range(2):
                    load_chunk(0, k)
                load_low(0)
                alternate(sp, batch)
                sp.wait_ge(x_stored, (NB - 1) * DMA)
                sp.dma_start(xo[:, :, :], token_tiles(x_in, NB - 1)).then_inc(xo_loaded, DMA)
                store(NB - 1)
                sp.wait_ge(x_stored, NB * DMA)

            @block.gpsimd
            def _(pool):
                make_identity(pool, ident, ident_made)

                def prepare(n, b, slot):
                    m = n - 44
                    if 0 <= m < MT:
                        pool.wait_ge(ch_loaded[slot], loads_before(b, slot) + CHANNELS * DMA)
                        pool.tensor_tensor(u[:, slot, m], dt[:, slot, m], xc[:, slot, m], ALU.mult).then_inc(u_ready, 1)

                def scan(n, b, slot):
                    s, m = divmod(n, MT)
                    if n < MT:
                        pool.wait_ge(u_ready, b * MT + m + 1)
                    if n % (CHUNK * MT) == 0:
                        k = s // CHUNK
                        pool.wait_ge(b_loaded[k % 2], (b * (NCHUNK // 2) + k // 2 + 1) * DMA)
                    wait_past(pool, h_ready, b * STEPS + n - RING + 1)
                    pool.tensor_tensor(drive[:, n % RING], u[:, slot, m], b_all[:, s // CHUNK % 2, s % CHUNK],
                                       ALU.mult).then_inc(drive_ready, 1)

                beside_scan(pool, scan, nothing, nothing, prepare)

            @block.scalar
            def _(act):
                act.wait_ge(w_loaded, W_LOADS * DMA)
                act.activation(a_neg[:, :, :], a_neg[:, :, :], ACT.Exp).then_inc(a_made, 1)
                act.wait_ge(a_made, 1)
                act.mul(a_neg[:, :, :], a_neg[:, :, :], -1.0).then_inc(a_made, 1)
                act.wait_ge(a_made, 2)
                act.wait_ge(made, 1)

                def gelu(b, tiles):
                    for f in tiles:
                        act.wait_ge(hid_done, b * FT0 + f + 1)
                        wait_past(act, q_summed, b * FT0 + f - HBANKS + 1)
                        act.activation(hidden[:, f % HBANKS], ps[:, f % HBANKS], ACT.Gelu_apprx_tanh,
                                       bias=b1[:, f:f + 1]).then_inc(hid_ready, 1)

                def ffn(n, b, slot):
                    if n == 24:
                        gelu(b, range(0, 3))
                    if n == 34:
                        gelu(b, range(3, 6))
                    if n == 43:
                        gelu(b, range(6, FT0))
                    if n == 51:
                        act.wait_ge(q_summed, b * FT0 + FT0)
                        act.copy(q1[0:R0, :], ps[0:R0, 3]).then_inc(q_copied, 1)
                    if n == 59:
                        act.wait_ge(ffn_done, b + 1)
                        act.activation(gate[:, :, :].rearrange("p (j i) d -> p j (i d)", j=2), ps[:, 0:2], ACT.Silu).then_inc(gate_ready, 1)

                def scan(n, b, slot):
                    s, m = divmod(n, MT)
                    if n == 0:
                        act.wait_ge(ch_loaded[slot], loads_before(b, slot) + CHANNELS * DMA)
                    wait_past(act, h_ready, b * STEPS + n - RING + 1)
                    act.activation(decay[:, n % RING], dt[:, slot, m], ACT.Exp, scale=a_neg[:, m, s:s + 1]).then_inc(decay_ready, 1)

                beside_scan(act, scan, ffn, nothing, nothing)

            @block.vector
            def _(dve):
                dve.memset(q1[R0:R0 + 1, :], 1.0).then_inc(made, 1)
                dve.wait_ge(w_loaded, W_LOADS * DMA)

                def times_c(n, b):
                    s = n // MT
                    dve.wait_ge(h_ready, b * STEPS + n + 1)
                    if n % (CHUNK * MT) == 0:
                        k = s // CHUNK
                        dve.wait_ge(c_loaded[k % 2], (b * (NCHUNK // 2) + k // 2 + 1) * DMA)
                    wait_past(dve, y_summed, b * STEPS + n - RING + 1)
                    dve.tensor_tensor(hc[:, n % RING], h[:, n % RING], c_all[:, s // CHUNK % 2, s % CHUNK],
                                      ALU.mult).then_inc(hc_ready, 1)

                def scan(n, b, slot):
                    dve.wait_ge(decay_ready, b * STEPS + n + 1)
                    dve.wait_ge(drive_ready, b * STEPS + n + 1)
                    wait_past(dve, hc_ready, b * STEPS + n - RING + 1)
                    dve.tensor_tensor_scan(h[:, n % RING], decay[:, n % RING], drive[:, n % RING], 0.0,
                                           ALU.mult, ALU.add).then_inc(h_ready, 1)
                    if n >= 1:
                        times_c(n - 1, b)
                    if n == STEPS - 1:
                        times_c(n, b)

                def finish(n, b, slot):
                    if n < MT:
                        dve.wait_ge(y_summed, b * STEPS + STEPS - MT + n + 1)
                        dve.scalar_tensor_tensor(xc[:, slot, n], xc[:, slot, n], skip[:, n:n + 1], ps[:, 4 + n], ALU.mult,
                                                 ALU.add).then_inc(y_skip, 1)
                    if 1 <= n < MT + 1:
                        dve.wait_ge(y_skip, b * MT + n)
                        dve.tensor_tensor(z[:, slot, n - 1], z[:, slot, n - 1], xc[:, slot, n - 1], ALU.mult).then_inc(y_gated, 1)
                    if n in (14, 15):
                        half = halves(TT)[n - 14]
                        dve.wait_ge(s_done, b * 2 + n - 13)
                        dve.wait_ge(gate_ready, b + 1)
                        dve.tensor_tensor(gate[:, half, :], gate[:, half, :], ps[:, n - 12].rearrange("p (i d) -> p i d", d=D),
                                          ALU.mult).then_inc(s_gated, 1)
                    if n in (15, 16):
                        half = halves(TT)[n - 15]
                        dve.wait_ge(s_gated, b * 2 + n - 14)
                        dve.wait_ge(xo_loaded, b * DMA + DMA)
                        dve.tensor_tensor(xo[:, half, :], xo[:, half, :], gate[:, half, :], ALU.add).then_inc(xo_ready, 1)

                beside_scan(dve, scan, nothing, finish, nothing)

            @block.tensor
            def _(pe):
                pe.wait_ge(w_loaded, W_LOADS * DMA)
                pe.wait_ge(made, 1)
                pe.wait_ge(ident_made, 2)

                def hid(b, f):
                    if f == 0:
                        pe.wait_ge(low_loaded, b * DMA + DMA)
                        wait_past(pe, s_gated, b * 2)
                        wait_past(pe, gate_ready, b)
                    if f >= HBANKS:
                        pe.wait_ge(hid_ready, b * FT0 + f - HBANKS + 1)
                    pe.matmul(ps[:, f % HBANKS], v1[:, f * P:(f + 1) * P], low[:, :], start=True, stop=True).then_inc(hid_done, 1)

                def sum_q(b, tiles):
                    for f in tiles:
                        pe.wait_ge(hid_ready, b * FT0 + f + 1)
                        pe.matmul(ps[0:R0, 3], u2[:, f], hidden[:, f % HBANKS], start=(f == 0), stop=(f == FT0 - 1)).then_inc(q_summed, 1)

                def ffn(n, b, slot):
                    if n in (16, 17, 18):
                        hid(b, n - 16)
                    if n == 25:
                        sum_q(b, range(0, 3))
                    if n in (25, 26, 27):
                        hid(b, n - 22)
                    if n == 35:
                        sum_q(b, range(3, 6))
                    if n in (35, 36):
                        hid(b, n - 29)
                    if n == 44:
                        sum_q(b, range(6, FT0))
                    if n == 52:
                        pe.wait_ge(q_copied, b + 1)
                        for i in range(TT):
                            last = pe.matmul(ps[:, i // 2, i % 2 * D:(i % 2 + 1) * D], q1[:, i * P:(i + 1) * P], v2b[:, :],
                                             start=True, stop=True)
                        last.then_inc(ffn_done, 1)

                def scan(n, b, slot):
                    s, m = divmod(n, MT)
                    if s == 0:
                        wait_past(pe, y_skip, b * MT + m + 1 - MT)
                    pe.wait_ge(hc_ready, b * STEPS + n + 1)
                    pe.matmul(ps[:, 4 + m], ident[:, :], hc[:, n % RING], start=(s == 0), stop=(s == DS - 1)).then_inc(y_summed, 1)

                def finish(n, b, slot):
                    if n in (9, 10):
                        j = n - 9
                        pe.wait_ge(y_gated, b * MT + MT)
                        for i in (2 * j, 2 * j + 1):
                            for m in range(MT):
                                last = pe.matmul(ps[:, 2 + j, i % 2 * D:(i % 2 + 1) * D], z[:, slot, m, i * P:(i + 1) * P],
                                                 w_out[:, m], start=(m == 0), stop=(m == MT - 1))
                        last.then_inc(s_done, 1)

                beside_scan(pe, scan, ffn, finish, nothing)



LC = 64
NC = T // LC
NE1, TOP1 = 8, 2
CAP1 = int(T * TOP1 / NE1 * 1.5) + 1
V_WIDTH = NH * QUAD


APART = 2.0 ** 90


class ChunkTiles(AttentionTiles):

    PARITY = P // LC
    MASK, SHIFT = KQK, KQK + PARITY
    KA, KB = SHIFT, SHIFT + NPART

    def __init__(self, c):
        AttentionTiles.__init__(self, c)
        self.ident_b = c.sb("ident_b", [P, P], BF16)
        self.chunk_mean = c.sb("chunk_mean", [P, TT, NC])
        self.shift = c.sb("shift", [P, 2, GH * TT, QUAD], BF16)

    def select(self, constant, pool, tile, compare, fill, base, pattern, per_row):
        constant(pool.affine_select(out=tile, in_=tile, compare_op=compare, fill=fill, base=base, pattern=pattern,
                                    channel_multiplier=per_row))

    Q_ROWS, K_ROWS = slice(MASK, SHIFT), slice(MASK, KB)
    ROW_STEPS = 5

    def make_rows(self, constant, pool):
        constant(pool.memset(self.qs[self.Q_ROWS, 0], 0.0))
        constant(pool.memset(self.ks[self.K_ROWS, 0], 1.0))
        constant(pool.memset(self.ks[self.Q_ROWS, 0], 0.0))
        for tile, value, base in ((self.qs, NEG, 0), (self.ks, APART, -1)):
            rows = tile[self.Q_ROWS, 0].rearrange("p h (i c t) -> p (h i) c t", i=TT, c=self.PARITY)
            self.select(constant, pool, rows, ALU.not_equal, value, base, [[0, GH * TT], [1, self.PARITY], [0, LC]],
                        -1 if base == 0 else 1)

    def make_others(self, constant, pool):
        constant(pool.memset(self.ident_b[:, :], 0.0))
        self.select(constant, pool, self.ident_b[:, :], ALU.not_equal, 1.0, 0, [[-1, P]], 1)
        constant(pool.memset(self.shift[:, :, :, :], 0.0))
        constant(pool.memset(self.shift[:, :, :, 0:self.PARITY], NEG))
        for r in range(self.PARITY):
            self.select(constant, pool, self.shift[:, :, :, r], ALU.is_ge, 0.0, (LC - 1, -LC)[r], [[0, 2 * GH * TT]], (-1, 1)[r])
        constant(pool.memset(self.chunk_mean[:, :, :], 1.0 / LC))
        self.select(constant, pool, self.chunk_mean[:, :, :], ALU.is_ge, 0.0, 0, [[P, TT], [-LC, NC]], 1)
        self.select(constant, pool, self.chunk_mean[:, :, :], ALU.is_ge, 0.0, LC - 1, [[-P, TT], [LC, NC]], -1)


def stage_chunks(nc, w, x_in, xn, q_parts, k_parts, v, gate, chunks, means):
    with Chip(nc, "chunks_shared") as c:
        tiles = ChunkTiles(c)
        stage_chunks_in(nc, w, tiles, x_in, xn, q_parts, k_parts, v, gate)
        stage_chunks_attend(nc, tiles, xn, q_parts, k_parts, v, chunks, means)


def stage_chunks_in(nc, w, attention, x_in, xn_out, q_out, k_out, v_out, gate_out):
    with Chip(nc, "chunks_in") as c:
        ident = c.sb("ident", [P, P])
        w_qkv = c.sb("w_qkv", [P, DT, 3 * D])
        wr = c.sb("wr", [P, DT, NE1])
        we = c.sb("we", [P, DT, NE1, D])
        earlier = c.sb("earlier", [P, P])
        ones = c.sb("ones", [P, P])
        order = c.sb("order", [P, NE1])
        x = c.sb("x", [P, TT, D])
        ln = LayerNorm(c)
        xn = ln.xn
        xn_t = c.sb("xn_t", [P, DT, T])
        v = c.sb("v", [P, TT, NH, QUAD])
        lg, eq, val, sel1, lg2, sel2, t1, t2, any_, keep, coef = (
            c.sb(n, [P, TT, NE1]) for n in ("lg", "eq", "val", "sel1", "lg2", "sel2", "t1", "t2", "any", "keep", "coef"))
        m1, m2, best, w1, w2 = (c.sb(n, [P, TT]) for n in ("m1", "m2", "best", "w1", "w2"))
        moe = c.sb("moe", [P, TT, D])
        gate = c.sb("gate", [P, TT, D])
        ps = c.psum()
        split = Split(c, q_out, k_out)
        we_parts = TwoParts(c, "we", [P, DT, NE1, D])
        xn_parts = TwoParts(c, "xn_t", [P, DT, T])

        w_loaded, filled, made, ident_made = (c.sem(n) for n in ("w_loaded", "filled", "made", "ident_made"))
        x_loaded, x_free, xn_stored, v_stored, gate_stored = (
            c.sem(n) for n in ("x_loaded", "x_free", "xn_stored", "v_stored", "gate_stored"))
        xt_done, xt_copied, qk_done, v_done, v_copied, logits_done = (
            c.sem(n) for n in ("xt_done", "xt_copied", "qk_done", "v_done", "v_copied", "logits_done"))
        route, any_ready, queue_done, w2_ready, gap_ready, coef_step, coef_ready = (
            c.sem(n) for n in ("route", "any", "queue_done", "w2", "gap", "coef_step", "coef"))
        moe_done, moe_sum, gate_ready = (c.sem(n) for n in ("moe_done", "moe_sum", "gate"))

        ROUTE = 16
        UNITS = TT * NE1 // 2
        SUMS = TT * NE1
        LOADS = 3 + 2 * DT + GH
        FILLS = 7

        def all_made(eng):
            eng.wait_ge(w_loaded, LOADS * DMA)
            eng.wait_ge(ident_made, 2)
            eng.wait_ge(made, 2)
            eng.wait_ge(filled, FILLS)

        with nc.Block() as block:

            @block.sync
            def _(sp):
                def load_x(b):
                    sp.dma_start(x[:, :, :], token_tiles(x_in, b)).then_inc(x_loaded, DMA)

                load_x(0)
                for n, name in enumerate(("Wq_l", "Wk_l", "Wv_l")):
                    sp.dma_start(w_qkv[:, :, n * D:(n + 1) * D], w[name].rearrange("(k p) n -> p k n", p=P)).then_inc(w_loaded, DMA)
                with nc.allow_non_contiguous_dma(reason="the router's weight transposed, once"):
                    for m in range(DT):
                        sp.dma_start(wr[:, m, :], w["Wr"][:, m * P:(m + 1) * P].rearrange("e p -> p e")).then_inc(w_loaded, DMA)
                for m in range(DT):
                    sp.dma_start(we[:, m], w["We"][:, m * P:(m + 1) * P, :].rearrange("e p n -> p e n")).then_inc(w_loaded, DMA)
                sp.wait_ge(filled, 1)
                load_head_rows(sp, attention.wo, w["Wo_l"], w_loaded)
                for stored in (xn_stored, v_stored, gate_stored):
                    sp.sem_inc(stored, DMA)
                split.sp_setup(sp)
                attention.copy_rows(sp, attention.Q_ROWS, attention.K_ROWS, attention.ROW_STEPS)

                def body(b, more):
                    sp.wait_ge(ln.ready, b * TT + TT)
                    sp.dma_start(token_tiles(xn_out, b), xn[:, :, :]).then_inc(xn_stored, DMA)
                    if more:
                        sp.wait_ge(x_free, b + 1)
                        load_x(b + 1)
                    sp.wait_ge(v_copied, b * 2 + 4)
                    sp.dma_start(token_tiles(v_out, b), v[:, :, :, :].rearrange("p i h e -> p i (h e)")).then_inc(v_stored, DMA)
                    for n in range(split.TILES):
                        split.sp(sp, b, n)
                    sp.wait_ge(gate_ready, b + 2)
                    sp.dma_start(token_tiles(gate_out, b), gate[:, :, :]).then_inc(gate_stored, DMA)

                batches(sp, body)
                for stored in (xn_stored, v_stored, gate_stored):
                    sp.wait_ge(stored, (NB + 1) * DMA)
                sp.wait_ge(split.stored, (NB + 1) * split.STORES * DMA)
                attention.rows_copied(sp)

            @block.gpsimd
            def _(pool):
                make_identity(pool, ident, ident_made)
                pool.wait_ge(filled, FILLS)
                pool.affine_select(out=earlier[:, :], in_=earlier[:, :], compare_op=ALU.is_gt, fill=0.0, base=0,
                                   pattern=[[1, P]], channel_multiplier=-1).then_inc(made, 1)
                pool.iota(order[:, :], [[-1, NE1]], base=NE1, channel_multiplier=0,
                          allow_small_or_imprecise_dtypes=True).then_inc(made, 1)
                pool.wait_ge(made, 2)
                constant = in_turn(pool, attention.made)
                attention.make_rows(constant, pool)
                attention.make_others(constant, pool)
                split.pool_setup(pool)
                with pool.Fori(0, NB) as b:
                    for n in range(split.TILES):
                        split.pool(pool, b, n)

            @block.scalar
            def _(act):
                ln.act_setup(act)
                split.act_setup(act)
                act.sem_inc(gate_ready, 1)

                def turn_copies(b):
                    for m in range(DT):
                        act.wait_ge(xt_done, b * DT + m + 3)
                        act.copy(xn_t[:, m], ps[:, m]).then_inc(xt_copied, 1)

                def body(b, more):
                    act.wait_ge(gap_ready, b + 1)
                    act.activation(w2[:, :], w2[:, :], ACT.Exp).then_inc(w2_ready, 1)
                    for n in range(split.TILES):
                        act.wait_ge(qk_done, b * split.TILES + n + 1)
                        split.act(act, b, n, ps[:, 2 + n])
                    split.act_middle(act, b)
                    if more:
                        ln.act(act, b + 1)
                        turn_copies(b + 1)
                    act.wait_ge(moe_sum, (b + 1) * SUMS + 1)
                    act.wait_ge(gate_stored, b * DMA + DMA)
                    act.activation(gate[:, :, :], moe[:, :, :], ACT.Silu).then_inc(gate_ready, 1)

                ln.act(act, 0)
                turn_copies(0)
                batches(act, body)

            @block.vector
            def _(dve):
                steps = [0]

                def fill(tile, value):
                    dve.memset(tile, value).then_inc(filled, 1)
                    steps[0] += 1
                    dve.wait_ge(filled, steps[0])

                fill(attention.wo[:, :, :], 0.0)
                fill(v[:, :, :, :], 0.0)
                fill(v[:, :, :, HD:HD + 1], 1.0)
                fill(earlier[:, :], 1.0)
                fill(ones[:, :], 1.0)
                fill(any_[:, :, :], 0.0)
                fill(moe[:, :, :], 0.0)
                assert steps[0] == FILLS
                ln.dve_setup(dve)
                split.dve_setup(dve)
                dve.sem_inc(v_copied, 2)
                dve.sem_inc(moe_sum, 1)

                def norm(b):
                    dve.wait_ge(x_loaded, b * DMA + DMA)
                    dve.wait_ge(xn_stored, b * DMA + DMA)
                    dve.wait_ge(xt_done, b * DT + 2)
                    ln.dve(dve, b, x)
                    dve.wait_ge(ln.ready, b * TT + TT)
                    dve.sem_inc(x_free, 1)

                def body(b, more):
                    for m in range(DT):
                        dve.wait_ge(xt_copied, b * DT + m + 1)
                        xn_parts.take_high(dve, xn_t[:, m], (slice(None), m))
                    for m in range(DT):
                        xn_parts.take_low(dve, xn_t[:, m], (slice(None), m), b * DT + m + 1)
                    dve.wait_ge(logits_done, b + 1)
                    count = [0]

                    def link(ins):
                        ins.then_inc(route, 1)
                        count[0] += 1
                        dve.wait_ge(route, b * ROUTE + count[0])

                    def wide(column):
                        return column[:, :].unsqueeze(2).broadcast_to([P, TT, NE1])

                    order_b = order[:, :].unsqueeze(1).broadcast_to([P, TT, NE1])
                    link(dve.tensor_copy(lg[:, :, :], ps[:, 0, 0:TT * NE1].rearrange("p (i e) -> p i e", e=NE1)))
                    for logits, top, sel in ((lg, m1, sel1), (lg2, m2, sel2)):
                        link(dve.reduce_max(top[:, :], logits[:, :, :], AX.X))
                        link(dve.tensor_tensor(eq[:, :, :], logits[:, :, :], wide(top), ALU.is_equal))
                        link(dve.tensor_tensor(val[:, :, :], eq[:, :, :], order_b, ALU.mult))
                        link(dve.reduce_max(best[:, :], val[:, :, :], AX.X))
                        link(dve.tensor_tensor(sel[:, :, :], val[:, :, :], wide(best), ALU.is_equal))
                        if sel is sel1:
                            link(dve.scalar_tensor_tensor(lg2[:, :, :], sel1[:, :, :], -3.0e38, lg[:, :, :], ALU.mult, ALU.add))
                    dve.tensor_tensor(any_[:, :, :], sel1[:, :, :], sel2[:, :, :], ALU.add).then_inc(any_ready, 1)
                    dve.tensor_tensor(w2[:, :], m2[:, :], m1[:, :], ALU.subtract).then_inc(gap_ready, 1)
                    dve.wait_ge(v_stored, b * DMA + DMA)
                    for j in range(2):
                        dve.wait_ge(v_done, b * 2 + j + 1)
                        dve.tensor_copy(v[:, 2 * j:2 * j + 2, :, 0:HD],
                                        ps[:, 6 + j].rearrange("p (i h e) -> p i h e", i=2, h=NH)).then_inc(v_copied, 1)
                    for n in range(split.TILES):
                        split.dve(dve, b, n)
                    dve.wait_ge(w2_ready, b + 1)
                    link(dve.tensor_scalar(w1[:, :], w2[:, :], 1.0, None, ALU.add))
                    link(dve.reciprocal(w1[:, :], w1[:, :]))
                    link(dve.tensor_tensor(w2[:, :], w2[:, :], w1[:, :], ALU.mult))
                    dve.wait_ge(queue_done, b + 1)
                    dve.tensor_scalar(keep[:, :, :], ps[:, 1, 0:TT * NE1].rearrange("p (i e) -> p i e", e=NE1), float(CAP1),
                                      None, ALU.is_lt).then_inc(coef_step, 1)
                    dve.tensor_tensor(t1[:, :, :], sel1[:, :, :], wide(w1), ALU.mult).then_inc(coef_step, 1)
                    dve.tensor_tensor(t2[:, :, :], sel2[:, :, :], wide(w2), ALU.mult).then_inc(coef_step, 1)
                    dve.wait_ge(coef_step, b * 3 + 3)
                    link(dve.tensor_tensor(t1[:, :, :], t1[:, :, :], t2[:, :, :], ALU.add))
                    dve.tensor_tensor(coef[:, :, :], t1[:, :, :], keep[:, :, :], ALU.mult).then_inc(coef_ready, 1)
                    assert count[0] == ROUTE
                    dve.wait_ge(coef_ready, b + 1)
                    dve.wait_ge(gate_ready, b + 1)

                    def experts(i):
                        for e in range(NE1):
                            n = i * NE1 + e
                            if e % 2 == 0:
                                dve.wait_ge(moe_done, b * UNITS + n // 2 + 1)
                            product = ps[:, 2 + e // 2, e % 2 * D:(e % 2 + 1) * D]
                            if e == 0:
                                dve.tensor_scalar(moe[:, i], product, coef[:, i, e:e + 1], None, ALU.mult).then_inc(moe_sum, 1)
                            else:
                                dve.wait_ge(moe_sum, b * SUMS + n + 1)
                                dve.scalar_tensor_tensor(moe[:, i], product, coef[:, i, e:e + 1], moe[:, i], ALU.mult,
                                                         ALU.add).then_inc(moe_sum, 1)

                    experts(0)
                    experts(1)
                    if more:
                        norm(b + 1)
                    experts(2)
                    experts(3)

                norm(0)
                all_made(dve)
                for m in range(DT):
                    we_parts.take_high(dve, we[:, m], (slice(None), m))
                for m in range(DT):
                    we_parts.take_low(dve, we[:, m], (slice(None), m), m + 1)
                batches(dve, body)

            @block.tensor
            def _(pe):
                pe.wait_ge(ident_made, 2)
                pe.sem_inc(xt_done, 2)

                def turn(b):
                    pe.wait_ge(ln.ready, b * TT + TT)
                    for m in range(DT):
                        for i in range(TT):
                            last = pe.transpose(ps[:, m, i * P:(i + 1) * P], xn[:, i, m * P:(m + 1) * P], ident[:, :])
                        last.then_inc(xt_done, 1)

                def body(b, more):
                    pe.wait_ge(xt_copied, b * DT + DT)
                    for i in range(TT):
                        for m in range(DT):
                            last = pe.matmul(ps[:, 0, i * NE1:(i + 1) * NE1], xn_t[:, m, i * P:(i + 1) * P], wr[:, m],
                                             start=(m == 0), stop=(m == DT - 1))
                    last.then_inc(logits_done, 1)
                    for j in range(2):
                        pe.wait_ge(v_copied, b * 2 + j + 1)
                        for i in (2 * j, 2 * j + 1):
                            for m in range(DT):
                                last = pe.matmul(ps[:, 6 + j, i % 2 * D:(i % 2 + 1) * D], xn_t[:, m, i * P:(i + 1) * P],
                                                 w_qkv[:, m, 2 * D:], start=(m == 0), stop=(m == DT - 1))
                        last.then_inc(v_done, 1)
                    pe.wait_ge(moe_sum, b * SUMS + 1)
                    for n in range(split.TILES):
                        for m in range(DT):
                            last = pe.matmul(ps[:, 2 + n], w_qkv[:, m, n * P:(n + 1) * P], xn_t[:, m], start=(m == 0),
                                             stop=(m == DT - 1))
                        last.then_inc(qk_done, 1)
                    def experts(units):
                        for u in units:
                            i, j = divmod(u, NE1 // 2)
                            if i == 0:
                                pe.wait_ge(split.copied, b * split.TILES + j + 1 + split.TILES)
                            else:
                                pe.wait_ge(moe_sum, b * SUMS + (i - 1) * NE1 + 2 * j + 3)
                            for m in range(DT):
                                last = three_passes(pe, ps[:, 2 + j], xn_parts.both((slice(None), m, slice(i * P, (i + 1) * P))),
                                                    we_parts.both((slice(None), m, slice(2 * j, 2 * j + 2))), m == 0, m == DT - 1)
                            last.then_inc(moe_done, 1)

                    pe.wait_ge(any_ready, b + 1)
                    queue = ps[:, 1, 0:TT * NE1]
                    pe.matmul(queue, earlier[:, :], any_[:, :, :].rearrange("p i e -> p (i e)"), start=True, stop=False)
                    for j in range(1, TT):
                        last = pe.matmul(queue[:, j * NE1:], ones[:, :], any_[:, 0:TT - j, :].rearrange("p i e -> p (i e)"),
                                         start=False, stop=(j == TT - 1))
                    last.then_inc(queue_done, 1)
                    pe.wait_ge(we_parts.ready, DT)
                    pe.wait_ge(xn_parts.ready, b * DT + DT)
                    experts(range(12))
                    if more:
                        turn(b + 1)
                    experts(range(12, UNITS))

                turn(0)
                all_made(pe)
                batches(pe, body)


def stage_chunks_attend(nc, attention, xn_in, q_in, k_in, v_in, chunks_out, means_out):
    with Chip(nc, "chunks") as c:
        MASK, KA, KB = attention.MASK, attention.KA, attention.KB
        PARITY = attention.PARITY
        qs, ks, wo, shift, ident_b, chunk_mean = (
            attention.qs, attention.ks, attention.wo, attention.shift, attention.ident_b, attention.chunk_mean)
        v = c.sb("v", [P, NG, TT, GH * QUAD])
        xn = c.sb("xn", [P, TT, D])
        row_max = c.sb("row_max", [P, 2, GH * TT])
        rest = c.sb("rest", [P, 2, GH * TT])
        probs = c.sb("probs", [P, 2, GH, T])
        context = Context(c)
        chunks = c.sb("chunks", [P, TT, D])
        means = c.sb("means", [NC, D])
        ps = c.psum()

        qk_loaded, v_loaded = ([c.sem(f"{n}_loaded{g}") for g in range(NG)] for n in ("qk", "v"))
        xn_loaded, chunks_stored, means_stored = (c.sem(n) for n in ("xn_loaded", "chunks_stored", "means_stored"))
        a_done, a_max, shift_step, shift_ready, max_turned, max_copied = (
            c.sem(n) for n in ("a_done", "a_max", "shift_step", "shift_ready", "max_turned", "max_copied"))
        s_done, p_ready, pv_done = (c.sem(n) for n in ("s_done", "p_ready", "pv_done"))
        proj_done, chunks_ready, means_done, means_copied = (
            c.sem(n) for n in ("proj_done", "chunks", "means_done", "means_copied"))

        PAIRS = GH // 2
        PROJ_BANKS = (5, 7)
        CHAIN = 3
        K_LOADS = 2 * len(STACK)

        def run(eng, step):
            step(0, 0, (0, 2), None, None, None, None)
            step(0, 1, (0, 3), (0, 0), None, None, None)
            step(0, 2, (1, 0), (0, 1), (0, 0), None, None)
            step(0, 3, (1, 1), (0, 2), (0, 1), None, None)
            step(1, 0, (1, 2), (0, 3), (0, 2), None, None)
            with eng.Fori(1, NB - 1) as b:
                step(b, 1, (b, 3), (b, 0), (b - 1, 3), b - 1, None)
                step(b, 2, (b + 1, 0), (b, 1), (b, 0), None, b - 1)
                step(b, 3, (b + 1, 1), (b, 2), (b, 1), None, None)
                step(b + 1, 0, (b + 1, 2), (b, 3), (b, 2), None, None)
            step(NB - 1, 1, (NB - 1, 3), (NB - 1, 0), (NB - 2, 3), NB - 2, None)
            step(NB - 1, 2, None, (NB - 1, 1), (NB - 1, 0), None, NB - 2)
            step(NB - 1, 3, None, (NB - 1, 2), (NB - 1, 1), None, None)
            step(None, None, None, (NB - 1, 3), (NB - 1, 2), None, None)
            step(None, None, None, None, (NB - 1, 3), NB - 1, None)
            step(None, None, None, None, None, None, NB - 1)

        def load_v(eng, b, g):
            eng.dma_start(v[:, g], token_tiles(v_in, b)[:, :, g * GH * QUAD:(g + 1) * GH * QUAD]).then_inc(v_loaded[g], DMA)

        def load_xn(eng, b):
            eng.dma_start(xn[:, :, :], token_tiles(xn_in, b)).then_inc(xn_loaded, DMA)

        with nc.Block() as block:

            @block.sync
            def _(sp):
                def load_qk(b, g):
                    load_stack(sp, qs[:, g], q_in, b, g, False, qk_loaded[g])
                    load_stack(sp, ks[:, g], k_in, b, g, True, qk_loaded[g])

                def load_next_qk(b, g):
                    sp.wait_ge(s_done, (b * NG + g + 1) * PAIRS)
                    load_qk(b + 1, g)

                def load_next_v(b, g):
                    sp.wait_ge(pv_done, b * NG + g + 3)
                    load_v(sp, b + 1, g)

                for g in range(NG):
                    load_stack(sp, qs[:, g], q_in, 0, g, False, qk_loaded[g])
                with sp.Fori(0, NB - 1) as b:
                    load_next_qk(b, 0)
                    for g in range(1, NG):
                        load_next_qk(b, g)
                        load_next_v(b, g - 1)
                    load_next_v(b, NG - 1)

            @block.scalar
            def _(act):
                for g in range(NG):
                    load_stack(act, ks[:, g], k_in, 0, g, True, qk_loaded[g])
                    load_v(act, 0, g)
                load_xn(act, 0)
                act.sem_inc(max_copied, GH)
                act.sem_inc(p_ready, PAIRS)
                act.sem_inc(means_copied, 1)
                act.sem_inc(chunks_stored, DMA)
                act.sem_inc(means_stored, DMA)

                def exp(b, g, pair):
                    n = b * NG + g
                    act.wait_ge(s_done, n * PAIRS + pair + 1)
                    if pair == 0:
                        act.wait_ge(pv_done, n + 1)
                    act.activation(probs[:, g % 2, 2 * pair:2 * pair + 2], ps[:, 2 + 2 * pair:4 + 2 * pair], ACT.Exp,
                                   scale=SCALE).then_inc(p_ready, 1)

                def shifts(b, g, heads):
                    act.wait_ge(max_turned, b * NG + g + 3)
                    for h in heads:
                        act.copy(qs[MASK:KB, g, h], ps[h * QUAD:h * QUAD + KB - MASK, 7]).then_inc(max_copied, 1)

                def finish(b, more):
                    act.wait_ge(chunks_ready, b * 2 + 3)
                    act.dma_start(token_tiles(chunks_out, b), chunks[:, :, :]).then_inc(chunks_stored, DMA)
                    if more:
                        load_xn(act, b + 1)

                def finish_means(b):
                    act.wait_ge(means_done, b + 1)
                    act.wait_ge(means_stored, b * DMA + DMA)
                    act.copy(means[:, :], ps[0:NC, PROJ_BANKS[0], 0:D]).then_inc(means_copied, 1)
                    act.wait_ge(means_copied, b + 2)
                    act.dma_start(means_out[b], means[:, :]).then_inc(means_stored, DMA)

                def step(b, g, first, before, ended, done, rest):
                    if g is not None:
                        for pair in range(PAIRS):
                            exp(b, g, pair)
                        if not (g == NG - 1 and first is None):
                            nxt = (b, g + 1) if g + 1 < NG else (b + 1, 0)
                            shifts(*nxt, range(GH))
                    if rest is not None:
                        finish(rest, g is not None)
                        finish_means(rest)

                shifts(0, 0, range(GH))
                run(act, step)
                act.wait_ge(chunks_stored, (NB + 1) * DMA)
                act.wait_ge(means_stored, (NB + 1) * DMA)

            @block.vector
            def _(dve):
                dve.sem_inc(a_max, 1)
                dve.sem_inc(chunks_ready, 1)
                context.dve_setup(dve)

                def maxima(b, g, pair):
                    n = b * NG + g
                    dve.wait_ge(a_done, n * PAIRS + pair + 1)
                    dve.reduce_max(row_max[:, g % 2, pair * 2 * TT:(pair + 1) * 2 * TT],
                                   ps[:, 0:2].rearrange("p h (i k) -> p (h i) k", k=P), AX.X).then_inc(a_max, 1)

                def split_maxima(b, g):
                    n = b * NG + g
                    dve.wait_ge(a_max, (n + 1) * PAIRS + 1)
                    dve.wait_ge(max_turned, n + 1)
                    part = [shift[:, g % 2, :, PARITY + k] for k in range(NPART)]
                    dve.tensor_scalar(part[0], row_max[:, g % 2], -1.0, None, ALU.mult).then_inc(shift_step, 1)
                    dve.wait_ge(shift_step, n * CHAIN + 1)
                    dve.scalar_tensor_tensor(rest[:, g % 2], row_max[:, g % 2], -1.0, part[0], ALU.mult,
                                             ALU.subtract).then_inc(shift_step, 1)
                    dve.wait_ge(shift_step, n * CHAIN + 2)
                    dve.tensor_copy(part[1], rest[:, g % 2]).then_inc(shift_step, 1)
                    dve.wait_ge(shift_step, n * CHAIN + 3)
                    dve.tensor_tensor(part[2], rest[:, g % 2], part[1], ALU.subtract).then_inc(shift_ready, 1)

                def add_xn(b, j):
                    dve.wait_ge(proj_done, b * 2 + j + 1)
                    if j == 0:
                        dve.wait_ge(xn_loaded, b * DMA + DMA)
                        dve.wait_ge(means_copied, b + 1)
                        dve.wait_ge(chunks_stored, b * DMA + DMA)
                    tiles = slice(2 * j, 2 * j + 2)
                    dve.tensor_tensor(chunks[:, tiles, :], xn[:, tiles, :], ps[:, PROJ_BANKS[j]].rearrange("p (i n) -> p i n", n=D),
                                      ALU.add).then_inc(chunks_ready, 1)

                def step(b, g, first, before, ended, done, rest):
                    if ended is not None:
                        b, g = ended
                        dve.wait_ge(pv_done, b * NG + g + 3)
                        context.turn(dve, ps[:, 6])
                    if first is not None:
                        maxima(*first, 0)
                    if rest is not None:
                        add_xn(rest, 0)
                    if ended is not None:
                        context.scale(dve, b * NG + g)
                    if rest is not None:
                        add_xn(rest, 1)
                    if first is not None:
                        maxima(*first, 1)
                    if ended is not None:
                        if g == 0 and not (isinstance(b, int) and b == 0):
                            dve.wait_ge(proj_done, b * 2)
                        context.turn_back(dve, b * NG + g, g)
                    if first is not None:
                        split_maxima(*first)

                for g in range(2):
                    for pair in range(PAIRS):
                        maxima(0, g, pair)
                    split_maxima(0, g)
                run(dve, step)

            @block.tensor
            def _(pe):
                pe.sem_inc(pv_done, 2)
                pe.sem_inc(max_turned, 2)

                def first_scores(b, g, pair):
                    n = b * NG + g
                    if pair == 0:
                        pe.wait_ge(qk_loaded[g], (b + 1) * K_LOADS * DMA)
                    pe.wait_ge(a_max, n * PAIRS + pair + 1)
                    for j in range(2):
                        h = 2 * pair + j
                        for i in range(TT):
                            cols = slice(i * P, (i + 1) * P)
                            last = pe.matmul(ps[:, j, cols], qs[0:KA, g, h, cols], ks[0:KA, g, h, cols], start=True, stop=True)
                    last.then_inc(a_done, 1)

                def turn_maxima(b, g):
                    n = b * NG + g
                    pe.wait_ge(shift_ready, n + 1)
                    pe.wait_ge(max_copied, n * GH + GH)
                    if g == 3:
                        pe.wait_ge(chunks_ready, b * 2 + 1)
                    for h in range(GH):
                        for i in range(TT):
                            last = pe.matmul(ps[h * QUAD:(h + 1) * QUAD, 7, i * P:(i + 1) * P], shift[:, g % 2, h * TT + i, :],
                                             ident_b[:, :], start=True, stop=True)
                    last.then_inc(max_turned, 1)

                def second_scores(b, g, pair):
                    n = b * NG + g
                    if pair == 0:
                        pe.wait_ge(max_copied, n * GH + 2 * GH)
                    pe.wait_ge(p_ready, n * PAIRS + pair + 1)
                    if g == 2 and pair == 1:
                        wait_past(pe, chunks_ready, b * 2)
                    if g == 3 and pair == 1:
                        pe.wait_ge(means_copied, b + 1)
                    for j in range(2):
                        h = 2 * pair + j
                        for i in range(TT):
                            cols = slice(i * P, (i + 1) * P)
                            last = pe.matmul(ps[:, 2 + h, cols], ks[0:KB, g, h, cols], qs[0:KB, g, h, cols], start=True, stop=True)
                    last.then_inc(s_done, 1)

                def output(b, g):
                    n = b * NG + g
                    pe.wait_ge(v_loaded[g], (b + 1) * DMA)
                    context.bank_free(pe, n)
                    pe.wait_ge(p_ready, (n + 1) * PAIRS + PAIRS)
                    for i in range(TT):
                        cols = slice(i * P, (i + 1) * P)
                        for h in range(GH):
                            last = pe.matmul(ps[h * QUAD:(h + 1) * QUAD, 6, cols], v[:, g, i, h * QUAD:(h + 1) * QUAD],
                                             probs[:, g % 2, h, cols], start=True, stop=True)
                    last.then_inc(pv_done, 1)

                def project(b, j, shifted):
                    if j == 0:
                        pe.wait_ge(context.ready, b * NG + NG)
                    if shifted:
                        if j == 0:
                            pe.wait_ge(p_ready, (b * NG + NG + 2) * PAIRS + PAIRS)
                        else:
                            pe.wait_ge(max_copied, (b * NG + NG + 2) * GH + 2 * GH)
                    for i in (2 * j, 2 * j + 1):
                        for g in range(NG):
                            last = pe.matmul(ps[:, PROJ_BANKS[j], i % 2 * D:(i % 2 + 1) * D], context.ctx[:, g, i * P:(i + 1) * P],
                                             wo[:, g], start=(g == 0), stop=(g == NG - 1))
                    last.then_inc(proj_done, 1)

                def average(b, shifted):
                    pe.wait_ge(chunks_ready, b * 2 + 3)
                    if shifted:
                        pe.wait_ge(p_ready, (b * NG + NG + 3) * PAIRS + PAIRS)
                    for i in range(TT):
                        last = pe.matmul(ps[0:NC, PROJ_BANKS[0], 0:D], chunk_mean[:, i], chunks[:, i], start=(i == 0),
                                         stop=(i == TT - 1))
                    last.then_inc(means_done, 1)

                def step(b, g, first, before, ended, done, rest):
                    if first is not None:
                        first_scores(*first, 0)
                    if rest is not None:
                        project(rest, 1, g is not None)
                    if g is not None:
                        for pair in range(PAIRS):
                            second_scores(b, g, pair)
                        if not (g == NG - 1 and first is None):
                            turn_maxima(*((b, g + 1) if g + 1 < NG else (b + 1, 0)))
                    if first is not None:
                        first_scores(*first, 1)
                    if before is not None:
                        output(*before)
                    if done is not None:
                        project(done, 0, g is not None)
                    if rest is not None:
                        average(rest, g is not None)

                for g in range(2):
                    for pair in range(PAIRS):
                        first_scores(0, g, pair)
                turn_maxima(0, 0)
                run(pe, step)


def stage_chunk_means(nc, w, means_in, out):
    with Chip(nc, "means") as c:
        R = NB * NC
        ident = c.sb("ident", [P, P])
        wq, wk, wv, wo = (c.sb(n, [P, DT, D]) for n in ("wq", "wk", "wv", "wo"))
        head_rows = c.sb("head_rows", [P, DT, NH, R])
        apart = c.sb("apart", [R, NB, NC])
        x = c.sb("x", [R, D])
        x_t, q, k = (c.sb(n, [P, DT, R]) for n in ("x_t", "q", "k"))
        v = c.sb("v", [R, D])
        k_heads = c.sb("k_heads", [P, DT, NH, R])
        s = c.sb("s", [R, NH, R])
        top, den = (c.sb(n, [R, NH]) for n in ("top", "den"))
        p_t = c.sb("p_t", [R, NH, R])
        o = c.sb("o", [R, D])
        o_t = c.sb("o_t", [P, DT, R])
        y = c.sb("y", [R, D])
        ps = c.psum()
        loaded, stored, filled, made, ident_made = (c.sem(n) for n in ("loaded", "stored", "filled", "made", "ident_made"))
        pe_done, act_done, dve_done = (c.sem(n) for n in ("pe_done", "act_done", "dve_done"))
        MASKED = -1.0e30

        with nc.Block() as block:

            @block.sync
            def _(sp):
                sp.dma_start(x[:, :], means_in).then_inc(loaded, DMA)
                for dst, name in ((wq, "Wq_g"), (wk, "Wk_g"), (wv, "Wv_g"), (wo, "Wo_g")):
                    sp.dma_start(dst[:, :, :], w[name].rearrange("(k p) n -> p k n", p=P)).then_inc(loaded, DMA)
                sp.wait_ge(dve_done, 9)
                sp.dma_start(out, y[:, :]).then_inc(stored, DMA)
                sp.wait_ge(stored, DMA)

            @block.gpsimd
            def _(pool):
                make_identity(pool, ident, ident_made)
                pool.wait_ge(filled, 2)
                count = [0]

                def select(tile, fill, base, pattern, per_row):
                    pool.affine_select(out=tile, in_=tile, compare_op=ALU.is_ge, fill=fill, base=base, pattern=pattern,
                                       channel_multiplier=per_row).then_inc(made, 1)
                    count[0] += 1
                    pool.wait_ge(made, count[0])

                select(head_rows[:, :, :, :], 0.0, 0, [[P, DT], [-HD, NH], [0, R]], 1)
                select(head_rows[:, :, :, :], 0.0, HD - 1, [[-P, DT], [HD, NH], [0, R]], -1)
                select(apart[:, :, :], MASKED, 0, [[-NC, NB], [0, NC]], 1)
                select(apart[:, :, :], MASKED, NC - 1, [[NC, NB], [0, NC]], -1)

            @block.scalar
            def _(act):
                act.wait_ge(pe_done, 1)
                act.copy(x_t[:, :, :], ps[:, 0, 0:DT * R].rearrange("p (m r) -> p m r", r=R)).then_inc(act_done, 1)
                act.wait_ge(pe_done, 2)
                act.copy(k[:, :, :], ps[:, 1, 0:DT * R].rearrange("p (m r) -> p m r", r=R)).then_inc(act_done, 1)
                act.copy(q[:, :, :], ps[:, 2, 0:DT * R].rearrange("p (m r) -> p m r", r=R)).then_inc(act_done, 1)
                act.copy(v[:, :], ps[0:R, 3, 0:D]).then_inc(act_done, 1)
                act.wait_ge(dve_done, 5)
                act.activation(s[:, :, :], s[:, :, :], ACT.Exp, scale=SCALE).then_inc(act_done, 1)
                act.wait_ge(pe_done, 4)
                act.copy(p_t[:, :, :], ps[0:R, 4:6].rearrange("p j (h r) -> p (j h) r", r=R)).then_inc(act_done, 1)
                act.wait_ge(pe_done, 5)
                act.copy(o[:, :], ps[0:R, 0, 0:D]).then_inc(act_done, 1)
                act.wait_ge(pe_done, 6)
                act.copy(o_t[:, :, :], ps[:, 1, 0:DT * R].rearrange("p (m r) -> p m r", r=R)).then_inc(act_done, 1)

            @block.vector
            def _(dve):
                dve.memset(head_rows[:, :, :, :], 1.0).then_inc(filled, 1)
                dve.memset(apart[:, :, :], 0.0).then_inc(filled, 1)
                dve.wait_ge(made, 4)
                dve.wait_ge(act_done, 2)
                for m in range(DT):
                    dve.tensor_tensor(k_heads[:, m], head_rows[:, m], k[:, m].unsqueeze(1).broadcast_to([P, NH, R]),
                                      ALU.mult).then_inc(dve_done, 1)
                dve.wait_ge(pe_done, 3)
                dve.tensor_tensor(s[:, :, :], ps[0:R, 6:8].rearrange("p j (h r) -> p (j h) r", r=R),
                                  apart[:, :, :].rearrange("p b n -> p (b n)").unsqueeze(1).broadcast_to([R, NH, R]),
                                  ALU.add).then_inc(dve_done, 1)
                dve.wait_ge(dve_done, 3)
                dve.reduce_max(top[:, :], s[:, :, :], AX.X).then_inc(dve_done, 1)
                dve.wait_ge(dve_done, 4)
                dve.tensor_tensor(s[:, :, :], s[:, :, :], top[:, :].unsqueeze(2).broadcast_to([R, NH, R]),
                                  ALU.subtract).then_inc(dve_done, 1)
                dve.wait_ge(act_done, 5)
                dve.reduce_sum(den[:, :], s[:, :, :], AX.X).then_inc(dve_done, 1)
                dve.wait_ge(dve_done, 6)
                dve.reciprocal(den[:, :], den[:, :]).then_inc(dve_done, 1)
                dve.wait_ge(dve_done, 7)
                dve.tensor_tensor(s[:, :, :], s[:, :, :], den[:, :].unsqueeze(2).broadcast_to([R, NH, R]),
                                  ALU.mult).then_inc(dve_done, 1)
                dve.wait_ge(pe_done, 7)
                dve.tensor_tensor(y[:, :], x[:, :], ps[0:R, 2, 0:D], ALU.add).then_inc(dve_done, 1)

            @block.tensor
            def _(pe):
                pe.wait_ge(ident_made, 2)
                pe.wait_ge(loaded, 5 * DMA)
                for m in range(DT):
                    last = pe.transpose(ps[:, 0, m * R:(m + 1) * R], x[:, m * P:(m + 1) * P], ident[0:R, 0:R])
                last.then_inc(pe_done, 1)
                pe.wait_ge(act_done, 1)
                for bank, weight in ((1, wk), (2, wq)):
                    for n in range(DT):
                        for m in range(DT):
                            pe.matmul(ps[:, bank, n * R:(n + 1) * R], weight[:, m, n * P:(n + 1) * P], x_t[:, m], start=(m == 0),
                                      stop=(m == DT - 1))
                for m in range(DT):
                    last = pe.matmul(ps[0:R, 3, 0:D], x_t[:, m], wv[:, m], start=(m == 0), stop=(m == DT - 1))
                last.then_inc(pe_done, 1)
                pe.wait_ge(act_done, 4)
                pe.wait_ge(dve_done, 2)
                for j in range(2):
                    heads = slice(j * NH // 2, (j + 1) * NH // 2)
                    for m in range(DT):
                        last = pe.matmul(ps[0:R, 6 + j], q[:, m], k_heads[:, m, heads].rearrange("p h r -> p (h r)"),
                                         start=(m == 0), stop=(m == DT - 1))
                last.then_inc(pe_done, 1)
                pe.wait_ge(dve_done, 8)
                for h in range(NH):
                    j, n = divmod(h, NH // 2)
                    last = pe.transpose(ps[0:R, 4 + j, n * R:(n + 1) * R], s[:, h], ident[0:R, 0:R])
                last.then_inc(pe_done, 1)
                pe.wait_ge(act_done, 6)
                for h in range(NH):
                    last = pe.matmul(ps[0:R, 0, h * HD:(h + 1) * HD], p_t[:, h], v[:, h * HD:(h + 1) * HD], start=True, stop=True)
                last.then_inc(pe_done, 1)
                pe.wait_ge(act_done, 7)
                for m in range(DT):
                    last = pe.transpose(ps[:, 1, m * R:(m + 1) * R], o[:, m * P:(m + 1) * P], ident[0:R, 0:R])
                last.then_inc(pe_done, 1)
                pe.wait_ge(act_done, 8)
                for m in range(DT):
                    last = pe.matmul(ps[0:R, 2, 0:D], o_t[:, m], wo[:, m], start=(m == 0), stop=(m == DT - 1))
                last.then_inc(pe_done, 1)


NE2 = 8


CAUSAL = -1.0e4 / SCALE / NEG
ROW_MASK, ROW_SHIFT = KQK, KQK + TT
KA, KB = ROW_SHIFT, ROW_SHIFT + NPART


class CausalTiles(AttentionTiles):

    def __init__(self, c):
        AttentionTiles.__init__(self, c)
        self.ident_b = c.sb("ident_b", [P, P], BF16)
        self.neg_ident = c.sb("neg_ident", [P, P], BF16)
        self.later_keys = c.sb("later_keys", [P, P], BF16)
        self.earlier_queries = c.sb("earlier_queries", [P, P], BF16)
        self.shift = c.sb("shift", [P, 2, GH * TT, QUAD], BF16)

    def select(self, constant, pool, tile, compare, fill, base, pattern, per_row):
        constant(pool.affine_select(out=tile, in_=tile, compare_op=compare, fill=fill, base=base, pattern=pattern,
                                    channel_multiplier=per_row))

    Q_ROWS, K_ROWS = slice(ROW_MASK, ROW_MASK + TT), slice(ROW_MASK, KB)
    ROW_STEPS = 6

    def make_rows(self, constant, pool):
        q_rows, k_rows = (stack[self.Q_ROWS, 0] for stack in (self.qs, self.ks))
        constant(pool.memset(q_rows, NEG))
        self.select(constant, pool, q_rows, ALU.is_gt, 0.0, 0, [[0, GH], [-1, T]], P)
        constant(pool.memset(self.ks[self.K_ROWS, 0], 1.0))
        constant(pool.memset(k_rows, CAUSAL))
        self.select(constant, pool, k_rows, ALU.is_ge, 0.0, 0, [[0, GH], [1, T]], -P)
        self.select(constant, pool, k_rows, ALU.is_ge, 0.0, P - 1, [[0, GH], [-1, T]], P)

    def make_others(self, constant, pool):
        for tile, value, compare, fill, pattern, per_row in (
                (self.ident_b, 0.0, ALU.not_equal, 1.0, [[-1, P]], 1), (self.neg_ident, 0.0, ALU.not_equal, NEG, [[-1, P]], 1),
                (self.later_keys, CAUSAL, ALU.is_gt, 0.0, [[1, P]], -1), (self.earlier_queries, CAUSAL, ALU.is_gt, 0.0, [[-1, P]], 1)):
            constant(pool.memset(tile[:, :], value))
            self.select(constant, pool, tile[:, :], compare, fill, 0, pattern, per_row)
        constant(pool.memset(self.shift[:, :, :, :], 0.0))
        constant(pool.memset(self.shift[:, :, :, 0:TT], NEG))
        self.select(constant, pool, self.shift[:, :, :, 0:TT].rearrange("p a (h i) j -> p (a h) i j", i=TT), ALU.is_gt, 0.0, 0,
                    [[0, 2 * GH], [-1, TT], [1, TT]], 0)


def stage_causal(nc, w, x_in, chunks, context, gate, x_out, xn, q_parts, k_parts, v, s_out, probs):
    with Chip(nc, "causal_shared") as c:
        tiles = CausalTiles(c)
        stage_causal_in(nc, w, tiles, x_in, chunks, context, gate, x_out, xn, q_parts, k_parts, v, probs)
        stage_causal_attend(nc, tiles, q_parts, k_parts, v, s_out)


def stage_causal_in(nc, w, attention, x_in, chunks_in, context_in, gate_in, x_out, xn_out, q_out, k_out, v_out, probs_out):
    with Chip(nc, "causal_in") as c:
        ident = c.sb("ident", [P, P])
        chunk_of = c.sb("chunk_of", [NC, TT, P])
        w_rows = c.sb("w_rows", [P, 3 * DT, D])
        w_qkv = c.sb("w_qkv", [P, DT, 3 * D])
        wo_cols = c.sb("wo_cols", [P, DT, NH, QUAD])
        wg = c.sb("wg", [P, DT, NE2])
        x1 = c.sb("x1", [P, TT, D])
        chunks = c.sb("chunks", [P, TT, D])
        context = c.sb("context", [NC, D])
        gate = c.sb("gate", [P, TT, D])
        part = c.sb("part", [P, TT, D])
        x = c.sb("x", [P, TT, D])
        ln = LayerNorm(c)
        xn = ln.xn
        xn_t = c.sb("xn_t", [P, DT, T])
        v = c.sb("v", [P, TT, NH, QUAD])
        lg, probs = c.sb("lg", [P, TT, NE2]), c.sb("gate_probs", [P, TT, NE2])
        top, total = c.sb("top", [P, TT]), c.sb("total", [P, TT])
        probs_t = c.sb("probs_t", [NE2, T])
        ps = c.psum()
        split = Split(c, q_out, k_out)
        turned = Turned(c, ps, ident, [
            (w_rows[:, n, m * P:(m + 1) * P], w_qkv[:, m, n * P:(n + 1) * P]) for n in range(3 * DT) for m in range(DT)]
            + attention.wo_blocks(wo_cols))

        w_loaded, filled, made, ident_made = (c.sem(n) for n in ("w_loaded", "filled", "made", "ident_made"))
        loaded, x_stored, xn_stored, v_stored, probs_stored = (
            c.sem(n) for n in ("loaded", "x_stored", "xn_stored", "v_stored", "probs_stored"))
        spread, sum_ready, gated, x_ready = (c.sem(n) for n in ("context_spread", "sum_ready", "gated", "x_ready"))
        xt_done, xt_copied, qk_done, v_done, v_copied, gate_done = (
            c.sem(n) for n in ("xt_done", "xt_copied", "qk_done", "v_done", "v_copied", "gate_done"))
        gate_step, shifted, gate_exp, turn_done, probs_copied = (
            c.sem(n) for n in ("gate_step", "shifted", "gate_exp", "probs_turned", "probs_copied"))
        W_LOADS, LOADS, FILLS, GATE = 1 + 2 * DT, 4, 4, 4

        with nc.Block() as block:

            @block.sync
            def _(sp):
                def load(b):
                    for dst, src in ((x1, x_in), (chunks, chunks_in), (gate, gate_in)):
                        sp.dma_start(dst[:, :, :], token_tiles(src, b)).then_inc(loaded, DMA)
                    sp.dma_start(context[:, :], context_in[b]).then_inc(loaded, DMA)

                def sums(b, load_next):
                    sp.wait_ge(x_ready, b * 2 + 4)
                    sp.dma_start(token_tiles(x_out, b), x[:, :, :]).then_inc(x_stored, DMA)
                    if load_next:
                        load(b + 1)
                    sp.wait_ge(ln.ready, b * TT + TT)
                    sp.dma_start(token_tiles(xn_out, b), xn[:, :, :]).then_inc(xn_stored, DMA)

                load(0)
                sp.dma_start(w_rows[:, :, :], w["w_qkv"].rearrange("(n p) k -> p n k", p=P)).then_inc(w_loaded, DMA)
                with nc.allow_non_contiguous_dma(reason="the gate's weight transposed, once"):
                    for m in range(DT):
                        sp.dma_start(wg[:, m, :], w["gate_w"][:, m * P:(m + 1) * P].rearrange("e p -> p e")).then_inc(w_loaded, DMA)
                sp.wait_ge(filled, 1)
                load_head_columns(sp, wo_cols, w["w_out"], w_loaded, 0)
                for stored in (x_stored, xn_stored, v_stored, probs_stored):
                    sp.sem_inc(stored, DMA)
                split.sp_setup(sp)
                attention.copy_rows(sp, attention.Q_ROWS, attention.K_ROWS, attention.ROW_STEPS)

                def body(b, ahead):
                    if ahead > 0:
                        sums(b + 1, ahead > 1)
                    for n in range(split.TILES):
                        split.sp(sp, b, n)
                    sp.wait_ge(v_copied, b * 2 + 4)
                    sp.dma_start(token_tiles(v_out, b), v[:, :, :, :].rearrange("p i h e -> p i (h e)")).then_inc(v_stored, DMA)
                    sp.wait_ge(probs_copied, b + 2)
                    sp.dma_start(probs_out.rearrange("(b e) t -> b e t", e=NE2)[b], probs_t[:, :]).then_inc(probs_stored, DMA)

                sums(0, True)
                with sp.Fori(0, NB - 2) as b:
                    body(b, 2)
                body(NB - 2, 1)
                body(NB - 1, 0)
                for stored in (x_stored, xn_stored, v_stored, probs_stored):
                    sp.wait_ge(stored, (NB + 1) * DMA)
                sp.wait_ge(split.stored, (NB + 1) * split.STORES * DMA)
                attention.rows_copied(sp)

            @block.gpsimd
            def _(pool):
                make_identity(pool, ident, ident_made)
                pool.wait_ge(filled, FILLS)
                pool.affine_select(out=chunk_of[:, :, :], in_=chunk_of[:, :, :], compare_op=ALU.is_ge, fill=0.0, base=0,
                                   pattern=[[P, TT], [1, P]], channel_multiplier=-LC).then_inc(made, 1)
                pool.wait_ge(made, 1)
                pool.affine_select(out=chunk_of[:, :, :], in_=chunk_of[:, :, :], compare_op=ALU.is_ge, fill=0.0, base=LC - 1,
                                   pattern=[[-P, TT], [-1, P]], channel_multiplier=LC).then_inc(made, 1)
                pool.wait_ge(made, 2)
                constant = in_turn(pool, attention.made)
                attention.make_rows(constant, pool)
                attention.make_others(constant, pool)
                split.pool_setup(pool)
                with pool.Fori(0, NB) as b:
                    for n in range(split.TILES):
                        split.pool(pool, b, n)

            @block.scalar
            def _(act):
                ln.act_setup(act)
                turned.act(act)
                split.act_setup(act)
                act.sem_inc(probs_copied, 1)

                def turn_copies(b):
                    for m in range(DT):
                        act.wait_ge(xt_done, b * DT + m + 3)
                        act.copy(xn_t[:, m], ps[:, m]).then_inc(xt_copied, 1)

                def body(b, more):
                    if more:
                        ln.act(act, b + 1)
                    for n in range(split.TILES):
                        act.wait_ge(qk_done, b * split.TILES + n + 1)
                        split.act(act, b, n, ps[:, 2 + n])
                    split.act_middle(act, b)
                    act.wait_ge(shifted, b + 2)
                    act.activation(lg[:, :, :], lg[:, :, :], ACT.Exp).then_inc(gate_exp, 1)
                    if more:
                        turn_copies(b + 1)
                    act.wait_ge(turn_done, b + 1)
                    act.wait_ge(probs_stored, b * DMA + DMA)
                    act.copy(probs_t[:, :], ps[0:NE2, 3]).then_inc(probs_copied, 1)

                ln.act(act, 0)
                turn_copies(0)
                batches(act, body)

            @block.vector
            def _(dve):
                steps = [0]

                def fill(tile, value):
                    dve.memset(tile, value).then_inc(filled, 1)
                    steps[0] += 1
                    dve.wait_ge(filled, steps[0])

                fill(wo_cols[:, :, :, :], 0.0)
                fill(chunk_of[:, :, :], 1.0)
                fill(v[:, :, :, :], 0.0)
                fill(v[:, :, :, HD:HD + 1], 1.0)
                assert steps[0] == FILLS
                ln.dve_setup(dve)
                split.dve_setup(dve)
                dve.sem_inc(v_copied, 2)
                dve.sem_inc(shifted, 1)
                dve.sem_inc(x_ready, 2)

                def sums(b):
                    halves = [slice(2 * j, 2 * j + 2) for j in range(2)]
                    dve.wait_ge(loaded, (b + 1) * LOADS * DMA)
                    for j, half in enumerate(halves):
                        dve.wait_ge(spread, b * 2 + j + 1)
                        dve.tensor_tensor(part[:, half, :], ps[:, 6 + j].rearrange("p (i d) -> p i d", d=D), chunks[:, half, :],
                                          ALU.add).then_inc(sum_ready, 1)
                    for j, half in enumerate(halves):
                        dve.wait_ge(sum_ready, b * 2 + j + 1)
                        dve.tensor_tensor(part[:, half, :], part[:, half, :], gate[:, half, :], ALU.mult).then_inc(gated, 1)
                    dve.wait_ge(x_stored, b * DMA + DMA)
                    for j, half in enumerate(halves):
                        dve.wait_ge(gated, b * 2 + j + 1)
                        dve.tensor_tensor(x[:, half, :], part[:, half, :], x1[:, half, :], ALU.add).then_inc(x_ready, 1)
                    dve.wait_ge(x_ready, b * 2 + 4)
                    dve.wait_ge(xn_stored, b * DMA + DMA)
                    dve.wait_ge(xt_done, b * DT + 2)
                    ln.dve(dve, b, x)

                def body(b, more):
                    if more:
                        sums(b + 1)
                    for n in range(split.TILES):
                        split.dve(dve, b, n)
                    dve.wait_ge(v_stored, b * DMA + DMA)
                    for j in range(2):
                        dve.wait_ge(v_done, b * 2 + j + 1)
                        dve.tensor_copy(v[:, 2 * j:2 * j + 2, :, 0:HD],
                                        ps[:, 6 + j].rearrange("p (i h e) -> p i h e", i=2, h=NH)).then_inc(v_copied, 1)
                    dve.wait_ge(gate_done, b + 1)
                    scores = ps[:, 2, 0:TT * NE2].rearrange("p (i e) -> p i e", e=NE2)

                    def wide(column):
                        return column[:, :].unsqueeze(2).broadcast_to([P, TT, NE2])

                    dve.reduce_max(top[:, :], scores, AX.X).then_inc(gate_step, 1)
                    dve.wait_ge(gate_step, b * GATE + 1)
                    dve.tensor_tensor(lg[:, :, :], scores, wide(top), ALU.subtract).then_inc(shifted, 1)
                    dve.wait_ge(gate_exp, b + 1)
                    dve.reduce_sum(total[:, :], lg[:, :, :], AX.X).then_inc(gate_step, 1)
                    dve.wait_ge(gate_step, b * GATE + 2)
                    dve.reciprocal(total[:, :], total[:, :]).then_inc(gate_step, 1)
                    dve.wait_ge(gate_step, b * GATE + 3)
                    dve.tensor_tensor(probs[:, :, :], lg[:, :, :], wide(total), ALU.mult).then_inc(gate_step, 1)

                sums(0)
                batches(dve, body)

            @block.tensor
            def _(pe):
                pe.wait_ge(ident_made, 2)
                pe.wait_ge(w_loaded, W_LOADS * DMA)
                turned.pe(pe)
                pe.wait_ge(made, 2)
                pe.sem_inc(xt_done, 2)

                def spread_context(b):
                    pe.wait_ge(loaded, (b + 1) * LOADS * DMA)
                    for j in range(2):
                        for i in (2 * j, 2 * j + 1):
                            last = pe.matmul(ps[:, 6 + j, i % 2 * D:(i % 2 + 1) * D], chunk_of[:, i], context[:, :], start=True,
                                             stop=True)
                        last.then_inc(spread, 1)

                def turn(b):
                    pe.wait_ge(ln.ready, b * TT + TT)
                    for m in range(DT):
                        for i in range(TT):
                            last = pe.transpose(ps[:, m, i * P:(i + 1) * P], xn[:, i, m * P:(m + 1) * P], ident[:, :])
                        last.then_inc(xt_done, 1)

                def body(b, more):
                    pe.wait_ge(v_copied, b * 2 + 2)
                    if more:
                        spread_context(b + 1)
                    pe.wait_ge(xt_copied, b * DT + DT)
                    pe.wait_ge(probs_copied, b + 1)
                    for n in range(split.TILES):
                        split.bank_free(pe, b, n)
                        for m in range(DT):
                            last = pe.matmul(ps[:, 2 + n], w_qkv[:, m, n * P:(n + 1) * P], xn_t[:, m], start=(m == 0),
                                             stop=(m == DT - 1))
                        last.then_inc(qk_done, 1)
                    if more:
                        pe.wait_ge(sum_ready, b * 2 + 4)
                    for j in range(2):
                        for i in (2 * j, 2 * j + 1):
                            for m in range(DT):
                                last = pe.matmul(ps[:, 6 + j, i % 2 * D:(i % 2 + 1) * D], xn_t[:, m, i * P:(i + 1) * P],
                                                 w_qkv[:, m, 2 * D:], start=(m == 0), stop=(m == DT - 1))
                        last.then_inc(v_done, 1)
                    pe.wait_ge(split.copied, b * split.TILES + 1 + split.TILES)
                    for i in range(TT):
                        for m in range(DT):
                            last = pe.matmul(ps[:, 2, i * NE2:(i + 1) * NE2], xn_t[:, m, i * P:(i + 1) * P], wg[:, m],
                                             start=(m == 0), stop=(m == DT - 1))
                    last.then_inc(gate_done, 1)
                    if more:
                        turn(b + 1)
                    pe.wait_ge(split.copied, b * split.TILES + 2 + split.TILES)
                    pe.wait_ge(gate_step, b * GATE + GATE)
                    for i in range(TT):
                        last = pe.transpose(ps[0:NE2, 3, i * P:(i + 1) * P], probs[:, i, :], ident[:, :])
                    last.then_inc(turn_done, 1)

                spread_context(0)
                turn(0)
                batches(pe, body)


def stage_causal_attend(nc, attention, q_in, k_in, v_in, s_out):
    with Chip(nc, "causal") as c:
        qs, ks, wo, shift = attention.qs, attention.ks, attention.wo, attention.shift
        ident_b, neg_ident, later_keys, earlier_queries = (
            attention.ident_b, attention.neg_ident, attention.later_keys, attention.earlier_queries)
        v = c.sb("v", [P, NG, TT, GH * QUAD])
        row_max = c.sb("row_max", [P, 2, GH * TT])
        rest = c.sb("rest", [P, 2, GH * TT])
        probs = c.sb("probs", [P, 2, TT, GH, T])
        context = Context(c)
        so = c.sb("so", [P, TT, D])
        ps = c.psum()

        qk_loaded, v_loaded = ([c.sem(f"{n}_loaded{g}") for g in range(NG)] for n in ("qk", "v"))
        a_done, a_max, shift_step, shift_ready, max_turned, max_copied = (
            c.sem(n) for n in ("a_done", "a_max", "shift_step", "shift_ready", "max_turned", "max_copied"))
        s_done, p_ready, pv_done = (c.sem(n) for n in ("s_done", "p_ready", "pv_done"))
        proj_done, proj_copied, s_stored = c.sem("proj_done"), c.sem("proj_copied"), c.sem("s_stored")

        UA, UB = GH * TT, 2 * TT
        CHAIN = 3
        K_LOADS, V_LOADS = 2 * len(STACK), 1

        def load_v(eng, b, g):
            eng.dma_start(v[:, g], token_tiles(v_in, b)[:, :, g * GH * QUAD:(g + 1) * GH * QUAD]).then_inc(v_loaded[g], DMA)

        def run(eng, step):
            step(0, 0, (0, 2), None, None, None)
            step(0, 1, (0, 3), (0, 0), None, None)
            with eng.Fori(0, NB - 1) as b:
                step(b, 2, (b + 1, 0), (b, 1), (b, 0), None)
                step(b, 3, (b + 1, 1), (b, 2), (b, 1), None)
                step(b + 1, 0, (b + 1, 2), (b, 3), (b, 2), None)
                step(b + 1, 1, (b + 1, 3), (b + 1, 0), (b, 3), b)
            step(NB - 1, 2, None, (NB - 1, 1), (NB - 1, 0), None)
            step(NB - 1, 3, None, (NB - 1, 2), (NB - 1, 1), None)
            step(None, None, None, (NB - 1, 3), (NB - 1, 2), None)
            step(None, None, None, None, (NB - 1, 3), NB - 1)

        with nc.Block() as block:

            @block.sync
            def _(sp):
                def load_next_qk(b, g):
                    sp.wait_ge(s_done, b * NG * UB + (g + 1) * UB)
                    load_stack(sp, qs[:, g], q_in, b + 1, g, False, qk_loaded[g])
                    load_stack(sp, ks[:, g], k_in, b + 1, g, True, qk_loaded[g])

                def load_next_v(b, g):
                    sp.wait_ge(pv_done, b * NG * TT + (g + 1) * TT + 2 * TT)
                    load_v(sp, b + 1, g)

                for g in range(NG):
                    load_stack(sp, qs[:, g], q_in, 0, g, False, qk_loaded[g])
                with sp.Fori(0, NB - 1) as b:
                    load_next_qk(b, 0)
                    for g in range(1, NG):
                        load_next_qk(b, g)
                        load_next_v(b, g - 1)
                    load_next_v(b, NG - 1)

            @block.scalar
            def _(act):
                for g in range(NG):
                    load_stack(act, ks[:, g], k_in, 0, g, True, qk_loaded[g])
                    load_v(act, 0, g)
                act.sem_inc(max_copied, GH)
                act.sem_inc(p_ready, 2)
                act.sem_inc(proj_copied, 1)
                act.sem_inc(s_stored, DMA)

                def exp(b, g, kt):
                    for pair in range(2):
                        n = g * UB + kt * 2 + pair
                        act.wait_ge(s_done, b * NG * UB + n + 1)
                        if pair == 0:
                            act.wait_ge(pv_done, b * NG * TT + g * TT + kt + 1)
                        act.activation(probs[:, g % 2, kt, 2 * pair:2 * pair + 2], ps[:, 2 + n % 2 * 2:4 + n % 2 * 2], ACT.Exp,
                                       scale=SCALE).then_inc(p_ready, 1)

                def shifts(b, g, heads):
                    act.wait_ge(max_turned, b * NG + g + 3)
                    for h in heads:
                        act.copy(qs[ROW_MASK:KB, g, h], ps[h * QUAD:h * QUAD + KB - ROW_MASK, 7]).then_inc(max_copied, 1)

                def finish(b, j):
                    if j == 0:
                        act.wait_ge(s_stored, b * DMA + DMA)
                    act.wait_ge(proj_done, b * 2 + j + 1)
                    act.copy(so[:, 2 * j:2 * j + 2, :], ps[:, 7].rearrange("p (i n) -> p i n", n=D)).then_inc(proj_copied, 1)
                    if j == 1:
                        act.wait_ge(proj_copied, b * 2 + 3)
                        act.dma_start(token_tiles(s_out, b), so[:, :, :]).then_inc(s_stored, DMA)

                def step(b, g, first, before, ended, done):
                    for kt in range(TT):
                        if g is not None:
                            exp(b, g, kt)
                        if kt < 2 and g is not None and not (g == NG - 1 and first is None):
                            nxt = (b, g + 1) if g + 1 < NG else (b + 1, 0)
                            shifts(*nxt, range(2 * kt, 2 * kt + 2))
                        if done is not None and kt >= 2:
                            finish(done, kt - 2)

                shifts(0, 0, range(GH))
                run(act, step)
                act.wait_ge(s_stored, (NB + 1) * DMA)

            @block.vector
            def _(dve):
                dve.sem_inc(a_max, 2)
                context.dve_setup(dve)

                def maxima(b, g, units):
                    for u in units:
                        dve.wait_ge(a_done, b * NG * UA + g * UA + u + 1)
                        dve.reduce_max(row_max[:, g % 2, u:u + 1], ps[:, u % 2], AX.X).then_inc(a_max, 1)

                def split_maxima(b, g):
                    n = b * NG + g
                    dve.wait_ge(a_max, b * NG * UA + (g + 1) * UA + 2)
                    dve.wait_ge(max_turned, n + 1)
                    part = [shift[:, g % 2, :, TT + k] for k in range(NPART)]
                    dve.tensor_scalar(part[0], row_max[:, g % 2], -1.0, None, ALU.mult).then_inc(shift_step, 1)
                    dve.wait_ge(shift_step, n * CHAIN + 1)
                    dve.scalar_tensor_tensor(rest[:, g % 2], row_max[:, g % 2], -1.0, part[0], ALU.mult,
                                             ALU.subtract).then_inc(shift_step, 1)
                    dve.wait_ge(shift_step, n * CHAIN + 2)
                    dve.tensor_copy(part[1], rest[:, g % 2]).then_inc(shift_step, 1)
                    dve.wait_ge(shift_step, n * CHAIN + 3)
                    dve.tensor_tensor(part[2], rest[:, g % 2], part[1], ALU.subtract).then_inc(shift_ready, 1)

                def step(b, g, first, before, ended, done):
                    def some(units):
                        if first is not None:
                            maxima(*first, units)

                    some(range(2))
                    if ended is not None:
                        b, g = ended
                        dve.wait_ge(pv_done, (b * NG + g) * TT + 3 * TT)
                        context.turn(dve, ps[:, 6])
                    some(range(2, 4))
                    if ended is not None:
                        context.scale(dve, b * NG + g)
                    some(range(4, 6))
                    if ended is not None:
                        if g == 0 and not (isinstance(b, int) and b == 0):
                            dve.wait_ge(proj_done, b * 2)
                        context.turn_back(dve, b * NG + g, g)
                    some(range(6, UA))
                    if first is not None:
                        split_maxima(*first)

                for g in range(2):
                    maxima(0, g, range(UA))
                    split_maxima(0, g)
                run(dve, step)

            @block.tensor
            def _(pe):
                pe.sem_inc(pv_done, 2 * TT)
                pe.sem_inc(max_turned, 2)

                def first_scores(b, g, units):
                    for u in units:
                        h, i = divmod(u, TT)
                        if u == 0:
                            pe.wait_ge(qk_loaded[g], (b + 1) * K_LOADS * DMA)
                        pe.wait_ge(a_max, b * NG * UA + g * UA + u + 1)
                        pe.matmul(ps[:, u % 2], qs[0:KA, g, h, i * P:(i + 1) * P], ks[0:KA, g, h, :], start=True, stop=False)
                        pe.matmul(ps[:, u % 2, i * P:(i + 1) * P], neg_ident[:, :], later_keys[:, :], start=False,
                                  stop=True).then_inc(a_done, 1)

                def turn_maxima(b, g):
                    pe.wait_ge(shift_ready, b * NG + g + 1)
                    pe.wait_ge(max_copied, (b * NG + g) * GH + GH)
                    if not (isinstance(b, int) and b == 0):
                        pe.wait_ge(proj_copied, b * 2 + (1 if g == 3 else -1))
                    for h in range(GH):
                        for i in range(TT):
                            last = pe.matmul(ps[h * QUAD:(h + 1) * QUAD, 7, i * P:(i + 1) * P], shift[:, g % 2, h * TT + i, :],
                                             ident_b[:, :], start=True, stop=True)
                    last.then_inc(max_turned, 1)

                def second_scores(b, g, kt, pair):
                    if kt == 0 and pair == 0:
                        pe.wait_ge(max_copied, (b * NG + g) * GH + 2 * GH)
                    n = g * UB + kt * 2 + pair
                    pe.wait_ge(p_ready, b * NG * UB + n + 1)
                    for j in range(2):
                        bank = ps[:, 2 + n % 2 * 2 + j]
                        h = 2 * pair + j
                        pe.matmul(bank, ks[0:KB, g, h, kt * P:(kt + 1) * P], qs[0:KB, g, h, :], start=True, stop=False)
                        last = pe.matmul(bank[:, kt * P:(kt + 1) * P], neg_ident[:, :], earlier_queries[:, :], start=False,
                                         stop=True)
                    last.then_inc(s_done, 1)

                def output(b, g, kt):
                    if kt == 0:
                        pe.wait_ge(v_loaded[g], (b + 1) * V_LOADS * DMA)
                        context.bank_free(pe, b * NG + g)
                    pe.wait_ge(p_ready, b * NG * UB + g * UB + 2 * kt + 4)
                    for h in range(GH):
                        last = pe.matmul(ps[h * QUAD:(h + 1) * QUAD, 6], v[:, g, kt, h * QUAD:(h + 1) * QUAD],
                                         probs[:, g % 2, kt, h], start=(kt == 0), stop=(kt == TT - 1))
                    last.then_inc(pv_done, 1)

                def project(b, j, shifted):
                    if j == 0:
                        pe.wait_ge(context.ready, b * NG + NG)
                        if shifted:
                            pe.wait_ge(max_copied, b * NG * GH + (NG + 3) * GH + GH)
                    pe.wait_ge(proj_copied, b * 2 + j + 1)
                    for i in (2 * j, 2 * j + 1):
                        for g in range(NG):
                            last = pe.matmul(ps[:, 7, i % 2 * D:(i % 2 + 1) * D], context.ctx[:, g, i * P:(i + 1) * P], wo[:, g],
                                             start=(g == 0), stop=(g == NG - 1))
                    last.then_inc(proj_done, 1)

                def step(b, g, first, before, ended, done):
                    for kt in range(TT):
                        units = [4 * kt, 4 * kt + 1], [4 * kt + 2], [4 * kt + 3]
                        for part in range(3):
                            if first is not None:
                                first_scores(*first, units[part])
                            if g is not None and part < 2:
                                second_scores(b, g, kt, part)
                            if kt == 0 and part == 1 and g is not None and not (g == NG - 1 and first is None):
                                turn_maxima(*((b, g + 1) if g + 1 < NG else (b + 1, 0)))
                        if before is not None:
                            output(*before, kt)
                        if done is not None and kt >= 2:
                            project(done, kt - 2, g is not None)

                for g in range(2):
                    first_scores(0, g, range(UA))
                turn_maxima(0, 0)
                run(pe, step)


F2 = 1024
FT2 = F2 // P
TOP2 = int(2.0 * T / NE2)
ROUNDS = TOP2 // 8
assert TOP2 == P


def stage_experts(nc, w, x_in, xn_in, s_in, probs_in, x_out):
    with Chip(nc, "experts") as c:
        ident = c.sb("ident", [P, P])
        tokens = c.sb("tokens", [P, T])
        prob_t = c.sb("prob_t", [P, NB * NE2])
        place_t = c.sb("place_t", [P, NB * NE2])
        slots = c.sb("slots", [P, NE2, NB, D])
        ps = c.psum()
        with Chip(nc, "expert_weights") as c_w:
            w1 = c_w.sb("w1", [P, DT, F2])
            w2 = c_w.sb("w2", [P, FT2, D])
            w1_loaded, w2_loaded = c_w.sem("w1_loaded"), c_w.sem("w2_loaded")

            def load_w1(sp, e):
                sp.dma_start(w1[:, :, :], w["w1"][e].rearrange("(k p) f -> p k f", p=P)).then_inc(w1_loaded, DMA)

            def load_w2(sp, e):
                sp.dma_start(w2[:, :, :], w["w2"][e].rearrange("(k p) d -> p k d", p=P)).then_inc(w2_loaded, DMA)

            def load_first(sp):
                load_w1(sp, 0)
                load_w2(sp, 0)

            experts_gather(nc, xn_in, probs_in, ps, ident, tokens, prob_t, place_t, slots, load_first)
            experts_ffn(nc, ps, prob_t, slots, w1, w2, w1_loaded, w2_loaded, load_w1, load_w2)
        experts_scatter(nc, x_in, s_in, x_out, ps, tokens, place_t, slots)


def experts_gather(nc, xn_in, probs_in, ps, ident, tokens, prob_t, place_t, slots, load_first):
    with Chip(nc, "gather") as c:
        token = c.sb("token", [P, TT])
        work = c.sb("work", [NB * NE2, T])
        best = c.sb("best", [NB * NE2, TOP2])
        place = c.sb("place", [NB * NE2, TOP2], mybir.dt.uint32)
        place_f = c.sb("place_f", [NB * NE2, TOP2])
        place_all = c.sb("place_all", [P, 2, NE2 * TOP2])
        xn = c.sb("xn", [P, 2, TT, D])
        xn_parts = TwoParts(c, "xn", [P, 2, TT, D])
        picks = c.sb("picks", [P, 2, TT, NE2 * TOP2], F32R)
        place_dram = nc.dram_tensor("experts_place_rows", (NB, NE2 * TOP2), F32, kind="Internal").ap()

        ident_made, made, probs_loaded, top_step, found, place_stored = (
            c.sem(n) for n in ("ident_made", "made", "probs_loaded", "top_step", "found", "place_stored"))
        turn_done, turn_copied = c.sem("turn_done"), c.sem("turn_copied")
        in_loaded = [c.sem(f"in_loaded{r}") for r in range(2)]
        ready, done, copied, copy_begun = (c.sem(n) for n in ("ready", "done", "copied", "copy_begun"))
        HALF = NE2 // 2
        GROUPS = 2 * DT

        with nc.Block() as block:

            @block.sync
            def _(sp):
                sp.dma_start(work[:, :], probs_in).then_inc(probs_loaded, DMA)
                load_first(sp)
                sp.wait_ge(found, 1)
                sp.dma_start(place_dram.rearrange("b (e j) -> (b e) j", e=NE2), place_f[:, :]).then_inc(place_stored, DMA)
                sp.wait_ge(place_stored, DMA)
                with sp.Fori(0, NB // 2) as i:
                    for r in range(2):
                        sp.wait_ge(done, (i * 2 + r) * GROUPS + GROUPS)
                        sp.dma_start(xn[:, r], token_tiles(xn_in, i * 2 + r)).then_inc(in_loaded[r], DMA)
                        sp.dma_start(place_all[:, r], place_dram[i * 2 + r].partition_broadcast(P)).then_inc(in_loaded[r], DMA)

            @block.gpsimd
            def _(pool):
                make_identity(pool, ident, ident_made)
                pool.iota(token[:, :], [[P, TT]], base=0, channel_multiplier=1,
                          allow_small_or_imprecise_dtypes=True).then_inc(made, 1)
                pool.iota(tokens[:, :], [[1, T]], base=0, channel_multiplier=0,
                          allow_small_or_imprecise_dtypes=True).then_inc(made, 1)

            @block.scalar
            def _(act):
                act.wait_ge(turn_done, 2)
                act.copy(prob_t[:, :], ps[:, 0, 0:NB * NE2]).then_inc(turn_copied, 1)
                act.copy(place_t[:, :], ps[:, 1, 0:NB * NE2]).then_inc(turn_copied, 1)
                act.wait_ge(turn_copied, 2)
                act.sem_inc(copied, 2 * GROUPS)
                with act.Fori(0, NB // 2) as i:
                    for r in range(2):
                        for n in range(GROUPS):
                            m, half = divmod(n, 2)
                            act.wait_ge(done, (i * 2 + r) * GROUPS + n + 1 + 2 * GROUPS)
                            act.sem_inc(copy_begun, 1)
                            act.copy(slots[:, half * HALF:(half + 1) * HALF, i * 2 + r, m * P:(m + 1) * P],
                                     ps[:, r * GROUPS + n].rearrange("p (e j) -> p e j", e=HALF)).then_inc(copied, 1)

            @block.vector
            def _(dve):
                dve.wait_ge(probs_loaded, DMA)
                for k in range(ROUNDS):
                    eight = slice(8 * k, 8 * k + 8)
                    if k >= 1:
                        dve.wait_ge(top_step, 3 * k)
                    dve.max(best[:, eight], work[:, :]).then_inc(top_step, 1)
                    dve.wait_ge(top_step, 3 * k + 1)
                    dve.max_index(place[:, eight], best[:, eight], work[:, :]).then_inc(top_step, 1)
                    dve.wait_ge(top_step, 3 * k + 2)
                    dve.match_replace(work[:, :], best[:, eight], work[:, :], -1.0).then_inc(top_step, 1)
                dve.wait_ge(top_step, 3 * ROUNDS)
                dve.tensor_copy(place_f[:, :], place[:, :]).then_inc(found, 1)
                dve.wait_ge(made, 2)
                with dve.Fori(0, NB // 2) as i:
                    for r in range(2):
                        dve.wait_ge(in_loaded[r], i * 2 * DMA + 2 * DMA)
                        dve.wait_ge(done, (i * 2 + r) * GROUPS + GROUPS)
                        xn_parts.take_high(dve, xn[:, r], (slice(None), r))
                        for t in range(TT):
                            dve.tensor_scalar(picks[:, r, t], place_all[:, r], token[:, t:t + 1], None, ALU.is_equal).then_inc(ready, 1)
                        xn_parts.take_low(dve, xn[:, r], (slice(None), r), i * 2 + r + 1)

            @block.tensor
            def _(pe):
                pe.wait_ge(ident_made, 2)
                pe.wait_ge(found, 1)
                pe.transpose(ps[:, 0, 0:NB * NE2], best[:, :], ident[0:NB * NE2, 0:NB * NE2]).then_inc(turn_done, 1)
                pe.transpose(ps[:, 1, 0:NB * NE2], place_f[:, :], ident[0:NB * NE2, 0:NB * NE2]).then_inc(turn_done, 1)
                pe.sem_inc(done, 2 * GROUPS)
                with pe.Fori(0, NB // 2) as i:
                    for r in range(2):
                        pe.wait_ge(ready, (i * 2 + r) * TT + TT)
                        pe.wait_ge(xn_parts.ready, i * 2 + r + 1)
                        for n in range(GROUPS):
                            m, half = divmod(n, 2)
                            pe.wait_ge(copied, (i * 2 + r) * GROUPS + n + 1)
                            for t in range(TT):
                                for n_part, part in enumerate((xn_parts.high, xn_parts.low)):
                                    last = pe.matmul(ps[:, r * GROUPS + n], part[:, r, t, m * P:(m + 1) * P],
                                                     picks[:, r, t, half * HALF * TOP2:(half + 1) * HALF * TOP2],
                                                     start=(t == 0 and n_part == 0), stop=(t == TT - 1 and n_part == 1))
                            last.then_inc(done, 1)


def experts_ffn(nc, ps, prob_t, slots, w1, w2, w1_loaded, w2_loaded, load_w1, load_w2):
    with Chip(nc, "ffn") as c:
        HB = NB // 2
        UNITS = 2 * NE2
        RAW = 4
        x_parts = TwoParts(c, "x", [P, 2, HB, D])
        w1_parts = TwoParts(c, "w1", [P, DT, F2])
        w2_parts = TwoParts(c, "w2", [P, FT2, D])
        hidden = c.sb("hidden", [P, RAW, HB * TOP2])
        h_parts = TwoParts(c, "h", [P, FT2, HB * TOP2])
        h_done, h_ready, o_done, begun, o_copied = (c.sem(n) for n in ("h_done", "h_ready", "o_done", "begun", "o_copied"))

        def experts(eng, body):
            body(0, False)
            with eng.Fori(1, NE2 - 1) as e:
                body(e, False)
            body(NE2 - 1, True)

        with nc.Block() as block:

            @block.sync
            def _(sp):
                with sp.Fori(0, NE2 - 1) as e:
                    sp.wait_ge(w1_parts.ready, e * FT2 + FT2)
                    load_w1(sp, e + 1)
                    sp.wait_ge(w2_parts.ready, e * FT2 + FT2)
                    load_w2(sp, e + 1)

            @block.scalar
            def _(act):
                def body(e, final):
                    for n in range(2 * FT2):
                        tile = e * 2 * FT2 + n
                        act.wait_ge(h_done, tile + 1)
                        wait_past(act, h_parts.ready, tile + 1 - RAW)
                        act.activation(hidden[:, n % RAW], ps[:, n % 4], ACT.Gelu).then_inc(h_ready, 1)

                experts(act, body)

            @block.vector
            def _(dve):
                def split_w1(e, f):
                    part = (slice(None), slice(None), slice(f * P, (f + 1) * P))
                    dve.wait_ge(w1_loaded, e * DMA + DMA)
                    w1_parts.take_high(dve, w1[part], part)
                    w1_parts.take_low(dve, w1[part], part, e * FT2 + f + 1)

                def split_w2(e, f):
                    part = (slice(None), f)
                    dve.wait_ge(w2_loaded, e * DMA + DMA)
                    w2_parts.take_high(dve, w2[part], part)
                    w2_parts.take_low(dve, w2[part], part, e * FT2 + f + 1)

                def split_x(e, k):
                    wait_past(dve, h_done, (e * 2 + k - 1) * FT2)
                    dve.sem_inc(begun, 1)
                    taken = slots[:, e, k * HB:(k + 1) * HB, :]
                    x_parts.take_high(dve, taken, (slice(None), k))
                    x_parts.take_low(dve, taken, (slice(None), k), e * 2 + k + 1, begun)

                def outputs(e, k):
                    dve.wait_ge(o_done, (e * 2 + k + 1) * FT2)
                    dve.sem_inc(begun, 1)
                    for n in range(HB):
                        prob = prob_t[:, bass.ds(e + (k * HB + n) * NE2, 1)]
                        dve.tensor_scalar(slots[:, e, k * HB + n, :], ps[:, 4 + 2 * k + n // 2, n % 2 * D:(n % 2 + 1) * D], prob,
                                          None, ALU.mult).then_inc(o_copied, 1)

                def body(e, final):
                    for n in range(2 * FT2):
                        k, f = divmod(n, FT2)
                        tile = e * 2 * FT2 + n
                        dve.wait_ge(h_ready, tile + 1)
                        wait_past(dve, o_done, tile + 1 - FT2)
                        h_parts.take_high(dve, hidden[:, n % RAW], (slice(None), f))
                        h_parts.take_low(dve, hidden[:, n % RAW], (slice(None), f), tile + 1)
                        if k == 0:
                            split_w2(e, f)
                        elif not final:
                            dve.wait_ge(h_done, tile + 1)
                            split_w1(e + 1, f)
                        if f == 3 and not (final and k == 1):
                            split_x(e + k, 1 - k)
                        if f == 1 and not (isinstance(e, int) and e == 0):
                            outputs(e - 1, k)

                for f in range(FT2):
                    split_w1(0, f)
                split_x(0, 0)
                experts(dve, body)
                outputs(NE2 - 1, 0)
                outputs(NE2 - 1, 1)

            @block.tensor
            def _(pe):
                def first_product(e, k, f):
                    tile = (e * 2 + k) * FT2 + f
                    if f == 0:
                        pe.wait_ge(x_parts.ready, e * 2 + k + 1)
                    pe.wait_ge(w1_parts.ready, e * FT2 + f + 1)
                    wait_past(pe, h_ready, tile + 1 - 4)
                    for m in range(DT):
                        rows = slice(m * P, (m + 1) * P)
                        last = three_passes(pe, ps[:, f % 4], w1_parts.both((slice(None), m, slice(f * P, (f + 1) * P))),
                                            x_parts.both((slice(None), k, slice(None), rows)), m == 0, m == DT - 1)
                    last.then_inc(h_done, 1)

                def second_product(e, k, f):
                    tile = (e * 2 + k) * FT2 + f
                    if f == 0:
                        wait_past(pe, o_copied, (e * 2 + k - 1) * HB)
                    pe.wait_ge(h_parts.ready, tile + 1)
                    pe.wait_ge(w2_parts.ready, e * FT2 + f + 1)
                    for n in range(HB):
                        last = three_passes(pe, ps[:, 4 + 2 * k + n // 2, n % 2 * D:(n % 2 + 1) * D],
                                            h_parts.both((slice(None), f, slice(n * TOP2, (n + 1) * TOP2))),
                                            w2_parts.both((slice(None), f)), f == 0 and n % 2 == 0, f == FT2 - 1 and n % 2 == 1)
                    last.then_inc(o_done, 1)

                def body(e, final):
                    for n in range(2 * FT2):
                        k, f = divmod(n, FT2)
                        if not (isinstance(e, int) and e == 0 and k == 0):
                            second_product(e - 1 + k, 1 - k, f)
                        first_product(e, k, f)

                experts(pe, body)
                for f in range(FT2):
                    second_product(NE2 - 1, 1, f)


def experts_scatter(nc, x_in, s_in, x_out, ps, tokens, place_t, slots):
    with Chip(nc, "scatter") as c:
        s = c.sb("s", [P, 2, TT, D])
        x = c.sb("x", [P, 2, TT, D])
        out = c.sb("out", [P, 2, TT, D])
        given = TwoParts(c, "given", [P, 2, NE2, D])
        picks = c.sb("picks", [P, 2, NE2, T], F32R)
        loaded, stored = ([c.sem(f"{n}{r}") for r in range(2)] for n in ("loaded", "stored"))
        ready, begun, done, gate_ready, gated, added = (
            c.sem(n) for n in ("ready", "begun", "done", "gate_ready", "gated", "added"))

        with nc.Block() as block:

            @block.sync
            def _(sp):
                with sp.Fori(0, NB // 2) as i:
                    for r in range(2):
                        sp.wait_ge(added, (i * 2 + r) * 2 + 2)
                        sp.dma_start(s[:, r], token_tiles(s_in, i * 2 + r)).then_inc(loaded[r], DMA)
                        sp.dma_start(x[:, r], token_tiles(x_in, i * 2 + r)).then_inc(loaded[r], DMA)
                    for r in range(2):
                        sp.wait_ge(added, (i * 2 + r) * 2 + 6)
                        sp.dma_start(token_tiles(x_out, i * 2 + r), out[:, r]).then_inc(stored[r], DMA)
                for r in range(2):
                    sp.wait_ge(stored[r], (NB // 2 + 1) * DMA)

            @block.gpsimd
            def _(pool):
                pool.sem_inc(added, 4)
                with pool.Fori(0, NB // 2) as i:
                    for r in range(2):
                        for j in range(2):
                            tiles = slice(2 * j, 2 * j + 2)
                            if j == 0:
                                pool.wait_ge(loaded[r], i * 2 * DMA + 2 * DMA)
                            pool.wait_ge(gate_ready, (i * 2 + r) * 2 + j + 5)
                            pool.tensor_tensor(out[:, r, tiles], out[:, r, tiles], s[:, r, tiles], ALU.mult).then_inc(gated, 1)
                        for j in range(2):
                            tiles = slice(2 * j, 2 * j + 2)
                            pool.wait_ge(gated, (i * 2 + r) * 2 + j + 1)
                            pool.tensor_tensor(out[:, r, tiles], out[:, r, tiles], x[:, r, tiles], ALU.add).then_inc(added, 1)

            @block.scalar
            def _(act):
                act.sem_inc(gate_ready, 4)
                for r in range(2):
                    act.sem_inc(stored[r], DMA)
                with act.Fori(0, NB // 2) as i:
                    for r in range(2):
                        act.wait_ge(stored[r], i * DMA + DMA)
                        for j in range(2):
                            act.wait_ge(done, (i * 2 + r) * 2 + j + 5)
                            act.activation(out[:, r, 2 * j:2 * j + 2], ps[:, r * 2 + j].rearrange("p (i d) -> p i d", d=D),
                                           ACT.Silu).then_inc(gate_ready, 1)

            @block.vector
            def _(dve):
                with dve.Fori(0, NB // 2) as i:
                    for r in range(2):
                        dve.wait_ge(done, (i * 2 + r) * 2 + 2)
                        dve.sem_inc(begun, 1)
                        given.take_high(dve, slots[:, :, i * 2 + r, :], (slice(None), r))
                        for e in range(NE2):
                            place = place_t[:, bass.ds((i * 2 + r) * NE2 + e, 1)]
                            dve.tensor_scalar(picks[:, r, e], tokens[:, :], place, None, ALU.is_equal).then_inc(ready, 1)
                        given.take_low(dve, slots[:, :, i * 2 + r, :], (slice(None), r), i * 2 + r + 1, begun)

            @block.tensor
            def _(pe):
                pe.sem_inc(done, 4)
                with pe.Fori(0, NB // 2) as i:
                    for r in range(2):
                        pe.wait_ge(ready, (i * 2 + r) * NE2 + NE2)
                        pe.wait_ge(given.ready, i * 2 + r + 1)
                        for j in range(2):
                            pe.wait_ge(gate_ready, (i * 2 + r) * 2 + j + 1)
                            for t in (2 * j, 2 * j + 1):
                                for e in range(NE2):
                                    for n_part, part in enumerate((given.high, given.low)):
                                        last = pe.matmul(ps[:, r * 2 + j, t % 2 * D:(t % 2 + 1) * D],
                                                         picks[:, r, e, t * P:(t + 1) * P], part[:, r, e],
                                                         start=(e == 0 and n_part == 0), stop=(e == NE2 - 1 and n_part == 1))
                            last.then_inc(done, 1)


KD = KQK + 2 * NPART


def norms_tensor(nc, name):
    return nc.dram_tensor(name, (NB, NPART, NH * T), BF16, kind="Internal").ap()


def stage_distance(nc, w, x_in, q_parts, k_parts, q2, k2, v, gate, x_out):
    with Chip(nc, "distance_shared") as c:
        tiles = AttentionTiles(c)
        stage_distance_in(nc, w, tiles, x_in, q_parts, k_parts, q2, k2, v, gate)
        stage_distance_attend(nc, w, tiles, x_in, q_parts, k_parts, q2, k2, v, gate, x_out)


def stage_distance_in(nc, w, attention, x_in, q_out, k_out, q2_out, k2_out, v_out, gate_out):
    with Chip(nc, "distance_in") as c:
        ident = c.sb("ident", [P, P])
        NAMES = ("wq", "wk", "wv", "W_r", "W_k", "W_v")
        Q, K, V, MIX_R, MIX_K, MIX_V = range(len(NAMES))
        w_rows = c.sb("w_rows", [P, len(NAMES), DT, D])
        w_t = c.sb("w_t", [P, len(NAMES), DT, D])
        wo_cols = c.sb("wo_cols", [P, DT, NH, QUAD])
        bias = c.sb("bias", [P, 2, DT])
        bv = c.sb("bv", [P, D])
        mu = c.sb("mu", [P, 2, DT])
        mu_not = c.sb("mu_not", [P, 2, DT])
        head_of = c.sb("head_of", [P, DT, NH])
        x = c.sb("x", [P, TT, D])
        ln = LayerNorm(c)
        xn = ln.xn
        xn_t = c.sb("xn_t", [P, DT, 1 + T])
        squares = c.sb("squares", [P, 2 * DT, T])
        norm = c.sb("norm", [NH, 2, T])
        norm_rest = c.sb("norm_rest", [NH, 2, T])
        norm_parts = c.sb("norm_parts", [NH, 2, NPART, T], BF16)
        v = c.sb("v", [P, TT, NH, QUAD])
        mixed = c.sb("mixed", [P, 2, DT, T])
        act_k = c.sb("act_k", [P, DT, T])
        r = c.sb("r", [P, TT, D])
        ffn = c.sb("ffn", [P, TT, D])
        gate = c.sb("gate", [P, TT, D])
        ps = c.psum()
        split = Split(c, q_out, k_out)
        turned = Turned(c, ps, ident, [
            (w_rows[:, a, n, m * P:(m + 1) * P], w_t[:, a, m, n * P:(n + 1) * P])
            for a in range(len(NAMES)) for n in range(DT) for m in range(DT)] + attention.wo_blocks(wo_cols))

        w_loaded, filled, made, ident_made = (c.sem(n) for n in ("w_loaded", "filled", "made", "ident_made"))
        x_loaded, v_stored, norm_stored, gate_stored = (
            c.sem(n) for n in ("x_loaded", "v_stored", "norm_stored", "gate_stored"))
        xt_done, xt_copied, qk_done, v_done, v_copied = (
            c.sem(n) for n in ("xt_done", "xt_copied", "qk_done", "v_done", "v_copied"))
        squared, norm_done, norm_copied, norm_step, norm_ready = (
            c.sem(n) for n in ("squared", "norm_done", "norm_copied", "norm_step", "norm_ready"))
        mix_half, mixed_ready, mix_k_done, relu_ready, act_k_ready, mix_r_done, r_ready, mix_v_done, ffn_ready, sig_ready, gate_ready = (
            c.sem(n) for n in ("mix_half", "mixed", "mix_k_done", "relu", "act_k", "mix_r_done", "r", "mix_v_done", "ffn", "sig", "gate"))
        LOADS = len(NAMES) + 5 + DT
        FILLS, MADE = 7, 2

        def all_made(eng):
            eng.wait_ge(w_loaded, LOADS * DMA)
            eng.wait_ge(ident_made, 2)
            eng.wait_ge(made, MADE)
            eng.wait_ge(filled, FILLS)

        with nc.Block() as block:

            @block.sync
            def _(sp):
                def load_x(b):
                    sp.dma_start(x[:, :, :], token_tiles(x_in, b)).then_inc(x_loaded, DMA)

                load_x(0)
                for a, name in enumerate(NAMES):
                    sp.dma_start(w_rows[:, a], w[name].rearrange("(n p) k -> p n k", p=P)).then_inc(w_loaded, DMA)
                with nc.allow_non_contiguous_dma(reason="short vectors, once"):
                    for a, name in enumerate(("bq", "bk")):
                        sp.dma_start(bias[:, a], column(w[name], DT)).then_inc(w_loaded, DMA)
                    for a, name in enumerate(("mu_r", "mu_k")):
                        sp.dma_start(mu[:, a], column(w[name], DT)).then_inc(w_loaded, DMA)
                sp.dma_start(bv[:, :], w["bv"].partition_broadcast(P)).then_inc(w_loaded, DMA)
                sp.wait_ge(filled, 1)
                load_head_columns(sp, wo_cols, w["wo"], w_loaded, 0)
                for stored in (v_stored, gate_stored):
                    sp.sem_inc(stored, DMA)
                sp.sem_inc(norm_stored, 2 * DMA)
                split.sp_setup(sp)

                def body(b, ahead):
                    if ahead > 1:
                        sp.wait_ge(ln.ready, b * TT + 2 * TT)
                        load_x(b + 2)
                    for n in range(split.TILES):
                        split.sp(sp, b, n)
                    sp.wait_ge(v_copied, b * 2 + 4)
                    sp.dma_start(token_tiles(v_out, b), v[:, :, :, :].rearrange("p i h e -> p i (h e)")).then_inc(v_stored, DMA)
                    for side, to in enumerate((q2_out, k2_out)):
                        sp.wait_ge(norm_ready, b * 2 + side + 1)
                        sp.dma_start(to[b].rearrange("a (h t) -> h a t", h=NH), norm_parts[:, side]).then_inc(norm_stored, DMA)
                    sp.wait_ge(gate_ready, b + 1)
                    sp.dma_start(token_tiles(gate_out, b), gate[:, :, :]).then_inc(gate_stored, DMA)

                sp.wait_ge(ln.ready, TT)
                load_x(1)
                with sp.Fori(0, NB - 2) as b:
                    body(b, 2)
                body(NB - 2, 1)
                body(NB - 1, 0)
                for stored, per_batch in ((v_stored, 1), (gate_stored, 1), (norm_stored, 2)):
                    sp.wait_ge(stored, (NB + 1) * per_batch * DMA)
                sp.wait_ge(split.stored, (NB + 1) * split.STORES * DMA)

            @block.gpsimd
            def _(pool):
                make_identity(pool, ident, ident_made)
                pool.wait_ge(filled, FILLS - 2)
                pool.affine_select(out=head_of[:, :, :], in_=head_of[:, :, :], compare_op=ALU.is_ge, fill=0.0, base=0,
                                   pattern=[[P, DT], [-HD, NH]], channel_multiplier=1).then_inc(made, 1)
                pool.wait_ge(made, 1)
                pool.affine_select(out=head_of[:, :, :], in_=head_of[:, :, :], compare_op=ALU.is_ge, fill=0.0, base=HD - 1,
                                   pattern=[[-P, DT], [HD, NH]], channel_multiplier=-1).then_inc(made, 1)
                pool.wait_ge(made, MADE)
                constant = in_turn(pool, attention.made)
                for stack in (attention.qs, attention.ks):
                    for g in range(NG):
                        constant(pool.memset(stack[KQK:KD, g], 1.0))
                split.pool_setup(pool)
                with pool.Fori(0, NB) as b:
                    for n in range(split.TILES):
                        split.pool(pool, b, n)
                    pool.wait_ge(sig_ready, b + 1)
                    pool.wait_ge(gate_stored, b * DMA + DMA)
                    pool.tensor_tensor(gate[:, :, :], gate[:, :, :], ffn[:, :, :], ALU.mult).then_inc(gate_ready, 1)

            @block.scalar
            def _(act):
                ln.act_setup(act)
                all_made(act)
                turned.act(act)
                split.act_setup(act)
                act.sem_inc(relu_ready, DT)
                act.sem_inc(r_ready, 2)
                act.sem_inc(norm_copied, 2)

                def turn_copies(b):
                    for m in range(DT):
                        act.wait_ge(xt_done, b * DT + m + 3)
                        act.copy(xn_t[:, m, 1:], ps[:, m]).then_inc(xt_copied, 1)

                def qk_copies(b, tiles):
                    for n in tiles:
                        act.wait_ge(qk_done, b * split.TILES + n + 1)
                        side, m = divmod(n, DT)
                        split.act(act, b, n, ps[:, 2 + n], bias=bias[:, side, m:m + 1], scale=1.0 if side == 0 else -2.0)

                def body(b, more):
                    qk_copies(b, (0, 1))
                    if more:
                        ln.act(act, b + 1)
                    qk_copies(b, (2, 3))
                    for m in range(DT):
                        act.wait_ge(mix_k_done, b * DT + m + 1)
                        act.activation(act_k[:, m], ps[:, m], ACT.Relu).then_inc(relu_ready, 1)
                    for m in range(DT):
                        act.wait_ge(relu_ready, b * DT + m + 1 + DT)
                        act.activation(act_k[:, m], act_k[:, m], ACT.Square).then_inc(act_k_ready, 1)
                    split.act_middle(act, b)
                    for n in range(split.TILES):
                        act.wait_ge(split.copied, b * split.TILES + n + 1 + split.TILES)
                        act.activation(squares[:, n], split.full[:, n], ACT.Square).then_inc(squared, 1)
                    if more:
                        turn_copies(b + 1)
                    for j in range(2):
                        act.wait_ge(mix_r_done, b * 2 + j + 1)
                        act.activation(r[:, 2 * j:2 * j + 2, :], ps[:, 2 + j].rearrange("p (i d) -> p i d", d=D),
                                       ACT.Sigmoid).then_inc(r_ready, 1)
                    for side in range(2):
                        act.wait_ge(norm_done, b * 2 + side + 1)
                        act.activation(norm[:, side], ps[0:NH, 4 + side], ACT.Identity,
                                       scale=1.0 if side == 0 else 0.25).then_inc(norm_copied, 1)
                    act.wait_ge(ffn_ready, b * 2 + 4)
                    act.wait_ge(gate_stored, b * DMA + DMA)
                    act.activation(gate[:, :, :], ffn[:, :, :], ACT.Sigmoid).then_inc(sig_ready, 1)

                ln.act(act, 0)
                turn_copies(0)
                batches(act, body)

            @block.vector
            def _(dve):
                count = [0]

                def step(ins):
                    ins.then_inc(filled, 1)
                    count[0] += 1
                    dve.wait_ge(filled, count[0])

                step(dve.memset(wo_cols[:, :, :, :], 0.0))
                step(dve.memset(v[:, :, :, :], 0.0))
                step(dve.memset(v[:, :, :, HD:HD + 1], 1.0))
                step(dve.memset(xn_t[:, :, 0:1], 0.0))
                step(dve.memset(head_of[:, :, :], 1.0))
                dve.wait_ge(w_loaded, LOADS * DMA)
                step(dve.tensor_scalar(mu_not[:, :, :], mu[:, :, :], -1.0, 1.0, ALU.mult, ALU.add))
                step(dve.tensor_scalar(bias[:, 1], bias[:, 1], -2.0, None, ALU.mult))
                assert count[0] == FILLS
                ln.dve_setup(dve)
                all_made(dve)
                split.dve_setup(dve)
                dve.sem_inc(v_copied, 2)
                dve.sem_inc(ffn_ready, 2)

                def norm_x(b):
                    dve.wait_ge(x_loaded, b * DMA + DMA)
                    dve.wait_ge(xt_done, b * DT + 2)
                    ln.dve(dve, b, x)

                def body(b, more):
                    dve.wait_ge(xt_copied, b * DT + DT)
                    for a in range(2):
                        for m in range(DT):
                            dve.tensor_scalar(mixed[:, a, m], xn_t[:, m, 0:T], mu_not[:, a, m:m + 1], None,
                                              ALU.mult).then_inc(mix_half, 1)
                    for a in range(2):
                        for m in range(DT):
                            dve.wait_ge(mix_half, b * 2 * DT + a * DT + m + 1)
                            dve.scalar_tensor_tensor(mixed[:, a, m], xn_t[:, m, 1:], mu[:, a, m:m + 1], mixed[:, a, m], ALU.mult,
                                                     ALU.add).then_inc(mixed_ready, 1)
                    if more:
                        norm_x(b + 1)
                    for n in range(split.TILES):
                        split.dve(dve, b, n)
                    dve.wait_ge(v_stored, b * DMA + DMA)
                    for j in range(2):
                        dve.wait_ge(v_done, b * 2 + j + 1)
                        dve.tensor_tensor(v[:, 2 * j:2 * j + 2, :, 0:HD],
                                          ps[:, 6 + j].rearrange("p (i h e) -> p i h e", i=2, h=NH),
                                          bv[:, :].rearrange("p (h e) -> p h e", h=NH).unsqueeze(1).broadcast_to([P, 2, NH, HD]),
                                          ALU.add).then_inc(v_copied, 1)
                    dve.wait_ge(norm_stored, b * 2 * DMA + 2 * DMA)
                    for side in range(2):
                        dve.wait_ge(norm_copied, b * 2 + side + 3)
                        chain = (b * 2 + side) * 3
                        dve.tensor_copy(norm_parts[:, side, 0], norm[:, side]).then_inc(norm_step, 1)
                        dve.wait_ge(norm_step, chain + 1)
                        dve.tensor_tensor(norm_rest[:, side], norm[:, side], norm_parts[:, side, 0], ALU.subtract).then_inc(norm_step, 1)
                        dve.wait_ge(norm_step, chain + 2)
                        dve.tensor_copy(norm_parts[:, side, 1], norm_rest[:, side]).then_inc(norm_step, 1)
                        dve.wait_ge(norm_step, chain + 3)
                        dve.tensor_tensor(norm_parts[:, side, 2], norm_rest[:, side], norm_parts[:, side, 1],
                                          ALU.subtract).then_inc(norm_ready, 1)
                    wait_past(dve, gate_ready, b)
                    for j in range(2):
                        dve.wait_ge(r_ready, b * 2 + j + 3)
                        dve.wait_ge(mix_v_done, b * 2 + j + 1)
                        tiles = slice(2 * j, 2 * j + 2)
                        dve.tensor_tensor(ffn[:, tiles, :], r[:, tiles, :], ps[:, 6 + j].rearrange("p (i d) -> p i d", d=D),
                                          ALU.mult).then_inc(ffn_ready, 1)

                norm_x(0)
                batches(dve, body)

            @block.tensor
            def _(pe):
                all_made(pe)
                turned.pe(pe)
                pe.sem_inc(xt_done, 2)

                def turn(b):
                    pe.wait_ge(ln.ready, b * TT + TT)
                    pe.wait_ge(relu_ready, b * DT + DT)
                    for m in range(DT):
                        for i in range(TT):
                            last = pe.transpose(ps[:, m, i * P:(i + 1) * P], xn[:, i, m * P:(m + 1) * P], ident[:, :])
                        last.then_inc(xt_done, 1)

                def body(b, more):
                    pe.wait_ge(xt_copied, b * DT + DT)
                    pe.wait_ge(r_ready, b * 2 + 2)
                    pe.wait_ge(norm_copied, b * 2 + 2)
                    for n in range(split.TILES):
                        split.bank_free(pe, b, n)
                        side, n2 = divmod(n, DT)
                        for m in range(DT):
                            last = pe.matmul(ps[:, 2 + n], w_t[:, Q + side, m, n2 * P:(n2 + 1) * P], xn_t[:, m, 1:], start=(m == 0),
                                             stop=(m == DT - 1))
                        last.then_inc(qk_done, 1)
                    for j in range(2):
                        pe.wait_ge(v_copied, b * 2 + j + 1)
                        pe.wait_ge(ffn_ready, b * 2 + j + 1)
                        for i in (2 * j, 2 * j + 1):
                            for m in range(DT):
                                last = pe.matmul(ps[:, 6 + j, i % 2 * D:(i % 2 + 1) * D], xn_t[:, m, 1 + i * P:1 + (i + 1) * P],
                                                 w_t[:, V, m], start=(m == 0), stop=(m == DT - 1))
                        last.then_inc(v_done, 1)
                    pe.wait_ge(mixed_ready, (b + 1) * 2 * DT)
                    for n in range(DT):
                        for m in range(DT):
                            last = pe.matmul(ps[:, n], w_t[:, MIX_K, m, n * P:(n + 1) * P], mixed[:, 1, m], start=(m == 0),
                                             stop=(m == DT - 1))
                        last.then_inc(mix_k_done, 1)
                    for j in range(2):
                        pe.wait_ge(split.copied, b * split.TILES + j + 1 + split.TILES)
                        for i in (2 * j, 2 * j + 1):
                            for m in range(DT):
                                last = pe.matmul(ps[:, 2 + j, i % 2 * D:(i % 2 + 1) * D], mixed[:, 0, m, i * P:(i + 1) * P],
                                                 w_t[:, MIX_R, m], start=(m == 0), stop=(m == DT - 1))
                        last.then_inc(mix_r_done, 1)
                    if more:
                        turn(b + 1)
                    for side in range(2):
                        pe.wait_ge(squared, b * 2 * DT + (side + 1) * DT)
                        pe.wait_ge(split.copied, b * split.TILES + DT + side + 1 + split.TILES)
                        for m in range(DT):
                            last = pe.matmul(ps[0:NH, 4 + side], head_of[:, m], squares[:, side * DT + m], start=(m == 0),
                                             stop=(m == DT - 1))
                        last.then_inc(norm_done, 1)
                    pe.wait_ge(act_k_ready, b * DT + DT)
                    for j in range(2):
                        pe.wait_ge(v_copied, b * 2 + j + 3)
                        for i in (2 * j, 2 * j + 1):
                            for m in range(DT):
                                last = pe.matmul(ps[:, 6 + j, i % 2 * D:(i % 2 + 1) * D], act_k[:, m, i * P:(i + 1) * P],
                                                 w_t[:, MIX_V, m], start=(m == 0), stop=(m == DT - 1))
                        last.then_inc(mix_v_done, 1)

                turn(0)
                batches(pe, body)


D2_MIN = 1e-12


def stage_distance_attend(nc, w, attention, x_in, q_in, k_in, q2_in, k2_in, v_in, gate_in, x_out):
    with Chip(nc, "distance") as c:
        ident = c.sb("ident", [P, P])
        qs, ks, wo = attention.qs, attention.ks, attention.wo
        bo = c.sb("bo", [P, D])
        v = c.sb("v", [P, NG, TT, GH * QUAD])
        floor = c.sb("floor", [P, 1])
        minus_floor = c.sb("minus_floor", [P, 1])
        least = c.sb("least", [P, 2, GH * TT])
        least_t = c.sb("least_t", [GH * TT, 2, P])
        least_all = c.sb("least_all", [P, 2, GH * T])
        dist = c.sb("dist", [P, 2, TT, GH * T])
        context = Context(c)
        gate = c.sb("gate", [P, TT, D])
        x = c.sb("x", [P, TT, D])
        xo = c.sb("xo", [P, TT, D])
        least_dram = nc.dram_tensor("distance_least_rows", (2, GH * TT, P), F32, kind="Internal").ap()
        ps = c.psum()

        bo_loaded, ident_made, floor_set = c.sem("bo_loaded"), c.sem("ident_made"), c.sem("floor_set")
        qk_loaded, v_loaded = ([c.sem(f"{n}_loaded{g}") for g in range(NG)] for n in ("qk", "v"))
        least_stored, least_loaded = ([c.sem(f"{n}{g}") for g in range(2)] for n in ("least_stored", "least_loaded"))
        a_done, a_min, least_clamped, least_ready, least_turned, least_copied = (
            c.sem(n) for n in ("a_done", "a_min", "least_clamped", "least_ready", "least_turned", "least_copied"))
        s_done, above_floor, clamped, sqrt_ready, shifted, p_ready, pv_done = (
            c.sem(n) for n in ("s_done", "above_floor", "clamped", "sqrt_ready", "shifted", "p_ready", "pv_done"))
        gx_loaded, proj_done, proj_copied, gated, xo_ready, xo_stored = (
            c.sem(n) for n in ("gx_loaded", "proj_done", "proj_copied", "gated", "xo", "xo_stored"))

        UNITS = GH * TT // 2
        ACT_UNITS = 2
        DVE_UNITS = UNITS - ACT_UNITS
        BUFFERS = 3
        K_LOADS = 2 * (len(STACK) + 1)

        def load_side(eng, b, g, k_side):
            stack, parts, squares, row = (ks, k_in, k2_in, KQK + NPART) if k_side else (qs, q_in, q2_in, KQK)
            load_stack(eng, stack[:, g], parts, b, g, k_side, qk_loaded[g])
            eng.dma_start(stack[row:row + NPART, g], squares[b][:, g * GH * T:(g + 1) * GH * T].rearrange(
                "a (h t) -> a h t", h=GH)).then_inc(qk_loaded[g], DMA)

        def load_v(eng, b, g):
            eng.dma_start(v[:, g], token_tiles(v_in, b)[:, :, g * GH * QUAD:(g + 1) * GH * QUAD]).then_inc(v_loaded[g], DMA)

        def pair(u):
            n = u % BUFFERS if u < 2 * UNITS - 1 else (u - 2) % BUFFERS
            return slice(2 * n, 2 * n + 2)

        def run(eng, step):
            step(None, (0, 0), (0, 1), None, None)
            step((0, 0), (0, 1), (0, 2), None, None)
            step((0, 1), (0, 2), (0, 3), (0, 0), None)
            with eng.Fori(0, NB - 1) as b:
                step((b, 2), (b, 3), (b + 1, 0), (b, 1), None)
                step((b, 3), (b + 1, 0), (b + 1, 1), (b, 2), None)
                step((b + 1, 0), (b + 1, 1), (b + 1, 2), (b, 3), None)
                step((b + 1, 1), (b + 1, 2), (b + 1, 3), (b + 1, 0), b)
            step((NB - 1, 2), (NB - 1, 3), None, (NB - 1, 1), None)
            step((NB - 1, 3), None, None, (NB - 1, 2), None)
            step(None, None, None, (NB - 1, 3), None)
            step(None, None, None, None, NB - 1)

        with nc.Block() as block:

            @block.sync
            def _(sp):
                for g in range(NG):
                    load_side(sp, 0, g, False)
                    load_v(sp, 0, g)
                sp.dma_start(bo[:, :], w["bo"].partition_broadcast(P)).then_inc(bo_loaded, DMA)

                def spread_least(b, g):
                    sp.wait_ge(least_copied, b * NG + g + 1)
                    sp.wait_ge(shifted, (b * NG + g) * TT + TT)
                    sp.dma_start(least_dram[g % 2], least_t[:, g % 2]).then_inc(least_stored[g % 2], DMA)
                    sp.wait_ge(least_stored[g % 2], (b * 2 + g // 2 + 1) * DMA)
                    sp.dma_start(least_all[:, g % 2], least_dram[g % 2].rearrange("n q -> (n q)").partition_broadcast(P)).then_inc(
                        least_loaded[g % 2], DMA)

                def store(b):
                    sp.wait_ge(xo_ready, b * 2 + 4)
                    sp.dma_start(token_tiles(x_out, b), xo[:, :, :]).then_inc(xo_stored, DMA)

                sp.sem_inc(xo_stored, DMA)
                for g in range(3):
                    spread_least(0, g)
                with sp.Fori(0, NB - 1) as b:
                    spread_least(b, 3)
                    for g in range(3):
                        spread_least(b + 1, g)
                    store(b)
                spread_least(NB - 1, 3)
                store(NB - 1)
                sp.wait_ge(xo_stored, (NB + 1) * DMA)

            @block.gpsimd
            def _(pool):
                make_identity(pool, ident, ident_made)
                pool.sem_inc(shifted, 2 * TT)
                pool.sem_inc(xo_ready, 2)

                def step(out, mid, first, before, proj):
                    if mid is not None:
                        b, g = mid
                        pool.wait_ge(least_loaded[g % 2], (b * 2 + g // 2 + 1) * DMA)
                        for kt in range(TT):
                            pool.wait_ge(sqrt_ready, (b * NG + g) * TT + kt + 1)
                            pool.tensor_tensor(dist[:, g % 2, kt], dist[:, g % 2, kt], least_all[:, g % 2],
                                               ALU.subtract).then_inc(shifted, 1)
                    if proj is not None:
                        b = proj
                        pool.wait_ge(gx_loaded, b * 2 * DMA + 2 * DMA)
                        for j in range(2):
                            tiles = slice(2 * j, 2 * j + 2)
                            pool.wait_ge(proj_copied, b * 2 + j + 2)
                            pool.tensor_tensor(xo[:, tiles], xo[:, tiles], gate[:, tiles], ALU.mult).then_inc(gated, 1)
                        for j in range(2):
                            tiles = slice(2 * j, 2 * j + 2)
                            pool.wait_ge(gated, b * 2 + j + 1)
                            pool.tensor_tensor(xo[:, tiles], xo[:, tiles], x[:, tiles], ALU.add).then_inc(xo_ready, 1)

                run(pool, step)

            @block.scalar
            def _(act):
                def load_ahead(b, q_k, values):
                    for g in q_k:
                        act.wait_ge(s_done, (b * NG + g - NG) * UNITS + UNITS)
                        load_side(act, b, g, False)
                        load_side(act, b, g, True)
                    for g in values:
                        act.wait_ge(pv_done, (b * NG + g - NG) * TT + 3 * TT)
                        load_v(act, b, g)

                def load_gx(b):
                    act.wait_ge(xo_ready, b * 2 + 2)
                    act.dma_start(gate[:, :, :], token_tiles(gate_in, b)).then_inc(gx_loaded, DMA)
                    act.dma_start(x[:, :, :], token_tiles(x_in, b)).then_inc(gx_loaded, DMA)

                def step(out, mid, first, before, proj):
                    if first is not None and not isinstance(first[0], int):
                        b = first[0]
                        load_ahead(b, ((0, 1), (2,), (3,), ())[first[1]], ((), (0,), (1,), (2, 3))[first[1]])
                    if proj is not None and not isinstance(proj, int):
                        load_gx(proj)
                    if first is None and mid is not None:
                        load_gx(NB - 1)
                    if mid is not None:
                        b, g = mid
                        n = b * NG + g
                        act.wait_ge(least_clamped, n + 1)
                        act.activation(least[:, g % 2], least[:, g % 2], ACT.Sqrt).then_inc(least_ready, 1)
                    if mid is not None:
                        for u in range(ACT_UNITS):
                            act.wait_ge(s_done, n * UNITS + u + 1)
                            if u == 0:
                                act.wait_ge(pv_done, n * TT + 1)
                            act.activation(dist[:, g % 2, 0, u * 2 * T:(u + 1) * 2 * T], ps[:, pair(u)].rearrange("p h t -> p (h t)"),
                                           ACT.Relu, bias=minus_floor[:, 0:1]).then_inc(above_floor, 1)
                        for kt in range(TT):
                            if kt == 0:
                                act.wait_ge(above_floor, (n + 1) * ACT_UNITS)
                                act.activation(dist[:, g % 2, kt], dist[:, g % 2, kt], ACT.Sqrt, bias=floor[:, 0:1]).then_inc(sqrt_ready, 1)
                            else:
                                act.wait_ge(clamped, n * DVE_UNITS + 2 * kt + 2 - ACT_UNITS + 2)
                                act.activation(dist[:, g % 2, kt], dist[:, g % 2, kt], ACT.Sqrt).then_inc(sqrt_ready, 1)
                            if kt == 0:
                                act.wait_ge(least_turned, n + 3)
                                act.copy(least_t[:, g % 2], ps[0:GH * TT, 7, 0:P]).then_inc(least_copied, 1)
                    if out is not None:
                        b, g = out
                        for kt in range(TT):
                            act.wait_ge(shifted, (b * NG + g) * TT + kt + 1 + 2 * TT)
                            act.activation(dist[:, g % 2, kt], dist[:, g % 2, kt], ACT.Exp, scale=-1.0).then_inc(p_ready, 1)

                for g in range(NG):
                    load_side(act, 0, g, True)
                act.wait_ge(floor_set, 2)
                run(act, step)

            @block.vector
            def _(dve):
                dve.memset(floor[:, :], D2_MIN).then_inc(floor_set, 1)
                dve.memset(minus_floor[:, :], -D2_MIN).then_inc(floor_set, 1)
                dve.sem_inc(a_min, 1)
                dve.sem_inc(clamped, 2)
                context.dve_setup(dve)
                dve.sem_inc(proj_copied, 1)

                def minima(b, g):
                    n = b * NG + g
                    for u in range(UNITS):
                        h, j = divmod(u, 2)
                        dve.wait_ge(a_done, n * UNITS + u + 1)
                        if u == 0:
                            dve.wait_ge(least_turned, n + 1)
                        dve.tensor_reduce(least[:, g % 2, h * TT + 2 * j:h * TT + 2 * j + 2], ps[:, pair(UNITS + u)], op=ALU.min,
                                          axis=AX.X).then_inc(a_min, 1)
                    dve.wait_ge(a_min, n * UNITS + UNITS + 1)
                    dve.tensor_scalar(least[:, g % 2], least[:, g % 2], D2_MIN, None, ALU.max).then_inc(least_clamped, 1)

                def add_bias(b, j):
                    dve.wait_ge(proj_done, b * 4 + 2 * j + 2)
                    if j == 0:
                        dve.wait_ge(xo_stored, b * DMA + DMA)
                    dve.tensor_tensor(xo[:, 2 * j:2 * j + 2, :], ps[:, 7].rearrange("p (i n) -> p i n", n=D),
                                      bo[:, :].unsqueeze(1).broadcast_to([P, 2, D]), ALU.add).then_inc(proj_copied, 1)

                def step(out, mid, first, before, proj):
                    for u in range(ACT_UNITS, UNITS):
                        if mid is not None:
                            b, g = mid
                            kt, j = divmod(u, 2)
                            dve.wait_ge(s_done, (b * NG + g) * UNITS + u + 1)
                            if j == 0:
                                dve.wait_ge(pv_done, (b * NG + g) * TT + kt + 1)
                            dve.tensor_scalar(dist[:, g % 2, kt, j * 2 * T:(j + 1) * 2 * T],
                                              ps[:, pair(u)].rearrange("p h t -> p (h t)"), D2_MIN, None,
                                              ALU.max).then_inc(clamped, 1)
                    if proj is not None:
                        add_bias(proj, 0)
                    if before is not None:
                        b, g = before
                        dve.wait_ge(pv_done, (b * NG + g) * TT + 3 * TT)
                        context.turn(dve, ps[:, 6])
                        context.scale(dve, b * NG + g)
                    if first is not None:
                        minima(*first)
                    if before is not None:
                        if g == 0 and not (isinstance(b, int) and b == 0):
                            dve.wait_ge(proj_done, b * 4)
                        context.turn_back(dve, b * NG + g, g)
                    if proj is not None:
                        add_bias(proj, 1)

                minima(0, 0)
                dve.wait_ge(bo_loaded, DMA)
                run(dve, step)

            @block.tensor
            def _(pe):
                pe.wait_ge(ident_made, 2)
                pe.sem_inc(pv_done, 2 * TT)
                pe.sem_inc(least_turned, 2)

                def first_scores(b, g, u, after_second=True):
                    h, j = divmod(u, 2)
                    n = b * NG + g
                    if u == 0:
                        pe.wait_ge(qk_loaded[g], (b + 1) * K_LOADS * DMA)
                    if u == UNITS - 1:
                        pe.wait_ge(a_min, n * UNITS + u)
                    elif u >= BUFFERS:
                        pe.wait_ge(a_min, n * UNITS + u - BUFFERS + 2)
                    elif after_second:
                        pe.wait_ge(clamped, n * DVE_UNITS - BUFFERS + u + 3)
                    for i in range(2):
                        last = pe.matmul(ps[:, pair(UNITS + u)][:, i], qs[0:KD, g, h, (2 * j + i) * P:(2 * j + i + 1) * P],
                                         ks[0:KD, g, h, :], start=True, stop=True)
                    last.then_inc(a_done, 1)

                def second_scores(b, g, u):
                    kt, j = divmod(u, 2)
                    n = b * NG + g
                    if u >= BUFFERS + ACT_UNITS:
                        pe.wait_ge(clamped, n * DVE_UNITS + u - BUFFERS - ACT_UNITS + 3)
                    elif u >= BUFFERS:
                        pe.wait_ge(above_floor, n * ACT_UNITS + u - BUFFERS + 1)
                    elif u < 2:
                        pe.wait_ge(a_min, n * UNITS + UNITS + (-2, 1)[u])
                    for i in range(2):
                        h = 2 * j + i
                        last = pe.matmul(ps[:, pair(u)][:, i], ks[0:KD, g, h, kt * P:(kt + 1) * P], qs[0:KD, g, h, :],
                                         start=True, stop=True)
                    last.then_inc(s_done, 1)

                def turn_least(b, g):
                    pe.wait_ge(least_ready, b * NG + g + 1)
                    due = 1 if g == 3 else -1
                    if due > 0 or not isinstance(b, int):
                        pe.wait_ge(proj_copied, b * 2 + due)
                    if not (isinstance(b, int) and b == 0 and g == 0):
                        pe.wait_ge(least_copied, b * NG + g)
                    pe.transpose(ps[0:GH * TT, 7, 0:P], least[:, g % 2], ident[:, :]).then_inc(least_turned, 1)

                def output(b, g, kt):
                    n = b * NG + g
                    if kt == 0:
                        pe.wait_ge(v_loaded[g], (b + 1) * DMA)
                        context.bank_free(pe, n)
                    pe.wait_ge(p_ready, n * TT + kt + 1)
                    for h in range(GH):
                        last = pe.matmul(ps[h * QUAD:(h + 1) * QUAD, 6], v[:, g, kt, h * QUAD:(h + 1) * QUAD],
                                         dist[:, g % 2, kt, h * T:(h + 1) * T], start=(kt == 0), stop=(kt == TT - 1))
                    last.then_inc(pv_done, 1)

                def project(b, i, mid):
                    if i == 0:
                        pe.wait_ge(context.ready, b * NG + NG)
                        if mid is not None:
                            pe.wait_ge(least_copied, mid[0] * NG + mid[1] + 1)
                    if i % 2 == 0:
                        pe.wait_ge(proj_copied, b * 2 + i // 2 + 1)
                    for g in range(NG):
                        last = pe.matmul(ps[:, 7, i % 2 * D:(i % 2 + 1) * D], context.ctx[:, g, i * P:(i + 1) * P], wo[:, g],
                                         start=(g == 0), stop=(g == NG - 1))
                    last.then_inc(proj_done, 1)

                def step(out, mid, first, before, proj):
                    for u in range(UNITS):
                        if mid is not None:
                            second_scores(*mid, u)
                            if u == 2:
                                turn_least(*mid)
                        if before is not None and u in (2, 3):
                            output(*before, u)
                        if proj is not None and u in (4, 5):
                            project(proj, u - 4, mid)
                    for u in range(UNITS):
                        if first is not None:
                            first_scores(*first, u)
                        if proj is not None and u in (1, 2):
                            project(proj, u + 1, mid)
                        if out is not None and u >= UNITS - 2:
                            output(*out, u - UNITS + 2)

                for u in range(UNITS):
                    first_scores(0, 0, u, False)
                run(pe, step)


def build(nc, a, out):
    def scratch(name, shape):
        return nc.dram_tensor(name, shape, F32, kind="Internal").ap()

    def weights(prefix, names):
        return {n: a[f"{prefix}_{n}"] for n in names}

    x1, x2, x3, xn1, chunks, gate1, xn2, s2, gate3 = (
        scratch(n, (NB, T, D)) for n in ("x1", "x2", "x3", "xn1", "chunks", "gate1", "xn2", "s2", "gate3"))
    means, context = (scratch(n, (NB, NC, D)) for n in ("means", "context"))
    probs2 = scratch("probs2", (NB * NE2, T))
    v1, v2, v3 = (scratch(n, (NB, T, V_WIDTH)) for n in ("v1", "v2", "v3"))
    q1, k1, q2, k2, q3, k3 = (parts_tensor(nc, f"{n}_parts") for n in ("q1", "k1", "q2", "k2", "q3", "k3"))
    q3_norm, k3_norm = (norms_tensor(nc, n) for n in ("q3_norm", "k3_norm"))

    xc, z, dt = (channels_tensor(nc, n) for n in ("xc", "z", "dt"))
    bc, low = scratch("bc", (NB, 2 * DS, T)), scratch("low", (NB, R0, T))

    stage_mamba_in(nc, weights("L0_attn", ("W_in", "conv_w", "conv_b", "W_x", "W_dt", "b_dt")) | weights("L0_ffn", ("U1",)),
                   a["L0_attn_x"], xc, z, dt, bc, low)
    stage_mamba_scan(nc, weights("L0_attn", ("A_log", "D", "W_out")) | weights("L0_ffn", ("V1", "b1", "U2", "V2", "b2")),
                     a["L0_attn_x"], xc, z, dt, bc, low, x1)
    weights1 = weights("L1_attn", ("Wq_l", "Wk_l", "Wv_l", "Wo_l", "Wq_g", "Wk_g", "Wv_g", "Wo_g")) | weights("L1_ffn", ("Wr", "We"))
    stage_chunks(nc, weights1, x1, xn1, q1, k1, v1, gate1, chunks, means)
    stage_chunk_means(nc, weights1, means.rearrange("b n d -> (b n) d"), context.rearrange("b n d -> (b n) d"))
    stage_causal(nc, weights("L2_attn", ("w_qkv", "w_out")) | weights("L2_ffn", ("gate_w",)), x1, chunks, context, gate1,
                 x2, xn2, q2, k2, v2, s2, probs2)
    stage_experts(nc, weights("L2_ffn", ("w1", "w2")), x2, xn2, s2, probs2, x3)
    stage_distance(nc, weights("L3_attn", ("wq", "bq", "wk", "bk", "wv", "bv", "wo", "bo"))
                   | weights("L3_ffn", ("W_r", "W_k", "W_v", "mu_r", "mu_k")), x3, q3, k3, q3_norm, k3_norm, v3, gate3, out)


def kernel(**inputs):
    import numpy as np
    import concourse.bacc as bacc
    from concourse.bass_utils import run_bass_kernel_spmd

    nc = bacc.Bacc("TRN2", target_bir_lowering=False, num_devices=1)
    arrays, handles = {}, {}
    for name, value in inputs.items():
        arrays[name] = np.ascontiguousarray(value)
        handles[name] = nc.dram_tensor(name, arrays[name].shape, mybir.dt.from_np(arrays[name].dtype), kind="ExternalInput").ap()
    out = nc.dram_tensor("out", (NB, T, D), F32, kind="ExternalOutput").ap()
    build(nc, handles, out)
    return run_bass_kernel_spmd(nc, [arrays], core_ids=[0]).results[0]["out"]
```
